# Optimizing a Trainium2 kernel written in Bass

```python
import numpy as np
import jax
import jax.numpy as jnp

def _softmax(x, axis=-1):
    return jax.nn.softmax(x, axis=axis)

def _gelu(x):
    return jax.nn.gelu(x, approximate=True)

def _silu(x):
    return jax.nn.silu(x)

def _sigmoid(x):
    return jax.nn.sigmoid(x)

def _layernorm(x, axis=-1, eps=1e-05):
    m = jnp.mean(x, axis=axis, keepdims=True)
    v = jnp.var(x, axis=axis, keepdims=True)
    return (x - m) / jnp.sqrt(v + eps)

def _scatter_add(tgt, idx, src, axis=0):
    return tgt.at[idx].add(src)

def _segment_sum(src, seg, n):
    return jax.ops.segment_sum(src, seg, n)
kernel_name = 'mk_flamingo_gated_d4_seqx_r4_8dfb14'

def setup_inputs(seed: int=0):
    np.random.seed(seed)
    _w = jnp.asarray

    def _rec_inputs():
        import jax
        import jax.numpy as jnp
        _rk = jax.random.key(seed)
        x = 7.22e-05 + 1 * jax.random.normal(jax.random.fold_in(_rk, 1), (8, 256, 512), jnp.float32)
        _lenS = 256 - jax.random.randint(jax.random.fold_in(_rk, 7), (8,), 0, max(1, 256 // 4) + 1, jnp.int32)
        _lenS2 = 256 - jax.random.randint(jax.random.fold_in(_rk, 8), (8,), 0, max(1, 256 // 4) + 1, jnp.int32)
        _ctx_2048P = jax.random.normal(jax.random.fold_in(_rk, 11), (8, 16, 512), jnp.float32)
        _ctx_2048c = jax.random.dirichlet(jax.random.fold_in(_rk, 511), 0.3 * jnp.ones((16,), jnp.float32), (8, 256))
        _ctx_2048t = jnp.einsum('bsk,bkd->bsd', _ctx_2048c, _ctx_2048P)
        _ctx_2048t = _ctx_2048t * jax.lax.rsqrt(jnp.mean(jnp.square(_ctx_2048t)) + 1e-12) * 0.953939
        ctx_2048 = 4.13588e-05 + 0.999923 * (_ctx_2048t + 0.3 * jax.random.normal(jax.random.fold_in(_rk, 611), (8, 256, 512), jnp.float32))
        fside_S2_0 = -0.00337071 + 1.01897 * jax.random.normal(jax.random.fold_in(_rk, 13), (256,), jnp.float32)
        _validS = jnp.arange(256)[None, :] < _lenS[:, None]
        _validS2 = jnp.arange(256)[None, :] < _lenS2[:, None]
        _causal = jnp.tril(jnp.ones((256, 256), dtype=bool))
        mask_BxS2_ff1 = jnp.where(jnp.ones((8, 256), dtype=bool), 1.0, 0.0).astype(jnp.float32)
        _g = jax.random.normal(jax.random.fold_in(_rk, 9001), (2, 4), jnp.float32)
        _g = jnp.sign(_g) * jnp.maximum(jnp.abs(_g), 1.0) + (_g == 0) * 1.0
        g_xattn = _g[0]
        g_ffn = _g[1]
        return (x, ctx_2048, fside_S2_0, mask_BxS2_ff1, g_xattn, g_ffn)
    x, ctx_2048, fside_S2_0, mask_BxS2_ff1, g_xattn, g_ffn = _rec_inputs()

    def _L0_xattn_setup():
        import jax, jax.numpy as jnp
        import numpy as np
        N_HEAD = 8
        key = jax.random.key(seed)
        k1, k2, k3 = jax.random.split(key, 3)
        B, D, L = (4, 256, 512)
        q = jax.random.normal(k1, (B, D, L), dtype=jnp.float32)
        k = jax.random.normal(k2, (B, D, L), dtype=jnp.float32)
        v = jax.random.normal(k3, (B, D, L), dtype=jnp.float32)
        gamma = jnp.ones((), dtype=jnp.float32)
        return {'q': q, 'k': k, 'v': v, 'gamma': gamma}
    _L0_xattn_all = _L0_xattn_setup()
    _L0_xattn_in = {k: v for k, v in _L0_xattn_all.items() if k in ('gamma',)}
    del _L0_xattn_all

    def _L0_ffn_setup():
        import jax, jax.numpy as jnp
        import numpy as np
        TOPK = 6
        CAP = 256
        ROUTE_SCALE = 1.0
        key = jax.random.key(seed)
        k = jax.random.split(key, 6)
        B, T, C = (2, 512, 512)
        E, H, HS = (64, 64, 128)
        std = 0.01
        return {'x': jax.random.normal(k[0], (B, T, C), jnp.float32), 'w_gate': jax.random.normal(k[1], (C, E), jnp.float32) * std, 'w_shared_up': jax.random.normal(k[2], (C, 2 * HS), jnp.float32) * std, 'w_shared_down': jax.random.normal(k[3], (HS, C), jnp.float32) * std, 'w_up': jax.random.normal(k[4], (E, C, 2 * H), jnp.float32) * std, 'w_down': jax.random.normal(k[5], (E, H, C), jnp.float32) * std}
    _L0_ffn_all = _L0_ffn_setup()
    _L0_ffn_in = {k: v for k, v in _L0_ffn_all.items() if k in ('w_gate', 'w_shared_up', 'w_shared_down', 'w_up', 'w_down')}
    del _L0_ffn_all

    def _L1_xattn_setup():
        import jax, jax.numpy as jnp
        import numpy as np
        H = 512
        NH = 16
        HD = H // NH
        FD = 64
        key = jax.random.key(seed)
        ks = jax.random.split(key, 12)
        B, S = (4, 1024)
        s = 1.0 / np.sqrt(H)
        sf = 1.0 / np.sqrt(HD)
        return {'query': jax.random.normal(ks[0], (B, S, H), jnp.float32), 'key': jax.random.normal(ks[1], (B, S, H), jnp.float32), 'value': jax.random.normal(ks[2], (B, S, H), jnp.float32), 'attention_mask': jnp.ones((B, S), jnp.float32), 'Wq': jax.random.normal(ks[3], (H, H), jnp.float32) * s, 'bq': jnp.zeros((H,), jnp.float32), 'Wk': jax.random.normal(ks[4], (H, H), jnp.float32) * s, 'bk': jnp.zeros((H,), jnp.float32), 'Wv': jax.random.normal(ks[5], (H, H), jnp.float32) * s, 'bv': jnp.zeros((H,), jnp.float32), 'Wqf': jax.random.normal(ks[6], (FD, HD), jnp.float32) * sf, 'Wkf': jax.random.normal(ks[7], (FD, HD), jnp.float32) * sf, 'Wo': jax.random.normal(ks[8], (H, H), jnp.float32) * s, 'bo': jnp.zeros((H,), jnp.float32)}
    _L1_xattn_all = _L1_xattn_setup()
    _L1_xattn_in = {k: v for k, v in _L1_xattn_all.items() if k in ('Wq', 'bq', 'Wk', 'bk', 'Wv', 'bv', 'Wqf', 'Wkf', 'Wo', 'bo')}
    del _L1_xattn_all

    def _L1_ffn_setup():
        import jax, jax.numpy as jnp
        import numpy as np
        D_MODEL = 512
        HIDDEN = int(2 * D_MODEL * 4 / 3)

        def ternary_quant(w):
            s = jnp.mean(jnp.abs(w))
            q = jnp.clip(jnp.round(w / s), -1.0, 1.0) * s
            return w + jax.lax.stop_gradient(q - w)
        key = jax.random.key(seed)
        k0, k1, k2, k3 = jax.random.split(key, 4)
        x = jax.random.normal(k0, (4, 1024, D_MODEL), dtype=jnp.float32)
        std_in = 1.0 / np.sqrt(D_MODEL)
        std_h = 1.0 / np.sqrt(HIDDEN)
        w1 = jax.random.uniform(k1, (HIDDEN, D_MODEL), jnp.float32, -std_in, std_in)
        w3 = jax.random.uniform(k2, (HIDDEN, D_MODEL), jnp.float32, -std_in, std_in)
        w2 = jax.random.uniform(k3, (D_MODEL, HIDDEN), jnp.float32, -std_h, std_h)
        return {'x': x, 'w1': w1, 'w3': w3, 'w2': w2}
    _L1_ffn_all = _L1_ffn_setup()
    _L1_ffn_in = {k: v for k, v in _L1_ffn_all.items() if k in ('w1', 'w3', 'w2')}
    del _L1_ffn_all

    def _L2_xattn_setup():
        import jax, jax.numpy as jnp
        import numpy as np
        BS, S, DK = (8, 128, 512)
        key = jax.random.key(seed)
        kq, kk, kv = jax.random.split(key, 3)
        q = jax.random.normal(kq, (BS, S, DK), dtype=jnp.float32)
        k = jax.random.normal(kk, (BS, S, DK), dtype=jnp.float32)
        v = jax.random.normal(kv, (BS, S, DK), dtype=jnp.float32)
        return {'q': q, 'k': k, 'v': v}
    _L2_xattn_all = _L2_xattn_setup()
    _L2_xattn_in = {k: v for k, v in _L2_xattn_all.items() if k in ()}
    del _L2_xattn_all

    def _L2_ffn_setup():
        import jax, jax.numpy as jnp
        import numpy as np
        B, S, DIM = (2, 512, 512)
        INTER = 352
        E = 8
        K = 2
        SHARED = 1
        ROUTE_SCALE = 1.0

        def _expert(xt, w1, w2, w3, cw=None):
            h = jax.nn.silu((xt @ w1.T).astype(jnp.float32)) * (xt @ w3.T).astype(jnp.float32)
            if cw is not None:
                h = cw[:, None] * h
            return h.astype(xt.dtype) @ w2.T
        key = jax.random.key(seed)
        ks = jax.random.split(key, 9)
        bf = lambda k, shape: (jax.random.normal(k, shape, dtype=jnp.float32) * 0.02).astype(jnp.bfloat16)
        return {'x': jax.random.normal(ks[0], (B, S, DIM), dtype=jnp.float32).astype(jnp.bfloat16), 'gate_w': jax.random.normal(ks[1], (E, DIM), dtype=jnp.float32) * 0.02, 'gate_b': jax.random.normal(ks[2], (E,), dtype=jnp.float32) * 0.01, 'w1': bf(ks[3], (E, INTER, DIM)), 'w2': bf(ks[4], (E, DIM, INTER)), 'w3': bf(ks[5], (E, INTER, DIM)), 'sw1': bf(ks[6], (SHARED * INTER, DIM)), 'sw2': bf(ks[7], (DIM, SHARED * INTER)), 'sw3': bf(ks[8], (SHARED * INTER, DIM))}
    _L2_ffn_all = _L2_ffn_setup()
    _L2_ffn_in = {k: v for k, v in _L2_ffn_all.items() if k in ('gate_w', 'gate_b', 'w1', 'w2', 'w3', 'sw1', 'sw2', 'sw3')}
    del _L2_ffn_all

    def _L3_xattn_setup():
        import jax, jax.numpy as jnp
        import numpy as np
        key = jax.random.key(seed)
        ks = jax.random.split(key, 5)
        B, D, L, NH = (2, 256, 512, 8)
        H = D // NH
        return {'v': jax.random.normal(ks[0], (B, D, L), jnp.float32), 'k': jax.random.normal(ks[1], (H, L), jnp.float32) * 0.1, 'bias': jax.random.normal(ks[2], (D,), jnp.float32), 'x1': jax.random.normal(ks[3], (B, D, L), jnp.float32), 'x2': jax.random.normal(ks[4], (B, D, L), jnp.float32), 'num_heads': NH}
    _L3_xattn_all = _L3_xattn_setup()
    _L3_xattn_in = {k: v for k, v in _L3_xattn_all.items() if k in ('k',)}
    del _L3_xattn_all

    def _L3_ffn_setup():
        import jax, jax.numpy as jnp
        import numpy as np
        HIDDEN = 512
        INTER = 1376
        LUT_SIZE = 16

        def _ghost_linear(x, idx, lut):
            w = lut[idx]
            return jnp.einsum('bsh,oh->bso', x, w)
        key = jax.random.key(seed)
        k_x, k_lut, k_g, k_u, k_d = jax.random.split(key, 5)
        x = jax.random.normal(k_x, (2, 1024, HIDDEN), dtype=jnp.float32)
        lut = jax.random.normal(k_lut, (LUT_SIZE,), dtype=jnp.float32) * 0.02
        gate_idx = jax.random.randint(k_g, (INTER, HIDDEN), 0, LUT_SIZE, dtype=jnp.int32)
        up_idx = jax.random.randint(k_u, (INTER, HIDDEN), 0, LUT_SIZE, dtype=jnp.int32)
        down_idx = jax.random.randint(k_d, (HIDDEN, INTER), 0, LUT_SIZE, dtype=jnp.int32)
        return {'x': x, 'lut': lut, 'gate_idx': gate_idx, 'up_idx': up_idx, 'down_idx': down_idx}
    _L3_ffn_all = _L3_ffn_setup()
    _L3_ffn_in = {k: v for k, v in _L3_ffn_all.items() if k in ('lut', 'gate_idx', 'up_idx', 'down_idx')}
    del _L3_ffn_all
    return {'x': x, 'ctx_2048': ctx_2048, 'fside_S2_0': fside_S2_0, 'mask_BxS2_ff1': mask_BxS2_ff1, 'g_xattn': g_xattn, 'g_ffn': g_ffn, 'L0_xattn_gamma': _L0_xattn_in['gamma'], 'L0_ffn_w_gate': _L0_ffn_in['w_gate'], 'L0_ffn_w_shared_up': _L0_ffn_in['w_shared_up'], 'L0_ffn_w_shared_down': _L0_ffn_in['w_shared_down'], 'L0_ffn_w_up': _L0_ffn_in['w_up'], 'L0_ffn_w_down': _L0_ffn_in['w_down'], 'L1_xattn_Wq': _L1_xattn_in['Wq'], 'L1_xattn_bq': _L1_xattn_in['bq'], 'L1_xattn_Wk': _L1_xattn_in['Wk'], 'L1_xattn_bk': _L1_xattn_in['bk'], 'L1_xattn_Wv': _L1_xattn_in['Wv'], 'L1_xattn_bv': _L1_xattn_in['bv'], 'L1_xattn_Wqf': _L1_xattn_in['Wqf'], 'L1_xattn_Wkf': _L1_xattn_in['Wkf'], 'L1_xattn_Wo': _L1_xattn_in['Wo'], 'L1_xattn_bo': _L1_xattn_in['bo'], 'L1_ffn_w1': _L1_ffn_in['w1'], 'L1_ffn_w3': _L1_ffn_in['w3'], 'L1_ffn_w2': _L1_ffn_in['w2'], 'L2_ffn_gate_w': _L2_ffn_in['gate_w'], 'L2_ffn_gate_b': _L2_ffn_in['gate_b'], 'L2_ffn_w1': _L2_ffn_in['w1'], 'L2_ffn_w2': _L2_ffn_in['w2'], 'L2_ffn_w3': _L2_ffn_in['w3'], 'L2_ffn_sw1': _L2_ffn_in['sw1'], 'L2_ffn_sw2': _L2_ffn_in['sw2'], 'L2_ffn_sw3': _L2_ffn_in['sw3'], 'L3_xattn_k': _L3_xattn_in['k'], 'L3_ffn_lut': _L3_ffn_in['lut'], 'L3_ffn_gate_idx': _L3_ffn_in['gate_idx'], 'L3_ffn_up_idx': _L3_ffn_in['up_idx'], 'L3_ffn_down_idx': _L3_ffn_in['down_idx']}

def reference(x, ctx_2048, fside_S2_0, mask_BxS2_ff1, g_xattn, g_ffn, L0_xattn_gamma, L0_ffn_w_gate, L0_ffn_w_shared_up, L0_ffn_w_shared_down, L0_ffn_w_up, L0_ffn_w_down, L1_xattn_Wq, L1_xattn_bq, L1_xattn_Wk, L1_xattn_bk, L1_xattn_Wv, L1_xattn_bv, L1_xattn_Wqf, L1_xattn_Wkf, L1_xattn_Wo, L1_xattn_bo, L1_ffn_w1, L1_ffn_w3, L1_ffn_w2, L2_ffn_gate_w, L2_ffn_gate_b, L2_ffn_w1, L2_ffn_w2, L2_ffn_w3, L2_ffn_sw1, L2_ffn_sw2, L2_ffn_sw3, L3_xattn_k, L3_ffn_lut, L3_ffn_gate_idx, L3_ffn_up_idx, L3_ffn_down_idx):
    import jax
    import jax.numpy as jnp

    def _L0_xattn_ref(q, k, v, gamma):
        import jax, jax.numpy as jnp
        import numpy as np
        N_HEAD = 8
        B, Dq, Lq = q.shape
        Dv, Lk = (v.shape[-2], v.shape[-1])
        h = N_HEAD
        dq = Dq // h
        dv = Dv // h
        qh = q.reshape(B, h, dq, Lq)
        kh = k.reshape(B, h, dq, Lk)
        vh = v.reshape(B, h, dv, Lk)
        scale = 1.0 / jnp.sqrt(jnp.asarray(dq, dtype=q.dtype))
        qk = jnp.einsum('bhdq,bhdl->bhql', qh, kh) * scale
        sm = jax.nn.softmax(qk, axis=-1)
        ret = jnp.einsum('bhql,bhdl->bhdq', sm, vh)
        ret = ret.reshape(B, Dv, Lq)
        return gamma * ret

    def _L0_ffn_ref(x, w_gate, w_shared_up, w_shared_down, w_up, w_down):
        import jax, jax.numpy as jnp
        import numpy as np
        TOPK = 6
        CAP = 256
        ROUTE_SCALE = 1.0
        B, T, C = x.shape
        E = w_gate.shape[1]
        x_flat = x.reshape(-1, C)
        N = x_flat.shape[0]
        su = x_flat @ w_shared_up
        y_s, g_s = jnp.split(su, 2, axis=-1)
        shared = jax.nn.silu(g_s) * y_s @ w_shared_down
        scores = jax.nn.sigmoid(x_flat @ w_gate)
        _, topk_idx = jax.lax.top_k(scores, TOPK)
        w = jnp.take_along_axis(scores, topk_idx, axis=-1)
        w = w / w.sum(-1, keepdims=True) * ROUTE_SCALE
        flat_e = topk_idx.reshape(-1)
        oh = jax.nn.one_hot(flat_e, E, dtype=jnp.int32)
        pos = jnp.take_along_axis(jnp.cumsum(oh, axis=0), flat_e[:, None], axis=1)[:, 0] - 1
        valid = pos < CAP
        pos_c = jnp.where(valid, pos, CAP - 1)
        token_ids = jnp.repeat(jnp.arange(N), TOPK)
        x_disp = jnp.zeros((E, CAP, C), x.dtype).at[flat_e, pos].set(x_flat[token_ids], mode='drop')
        up = jnp.einsum('ecd,edh->ech', x_disp, w_up)
        g_r, v_r = jnp.split(up, 2, axis=-1)
        h_r = jax.nn.silu(g_r) * v_r
        out_r = jnp.einsum('ech,ehd->ecd', h_r, w_down)
        y_ts = out_r[flat_e, pos_c]
        y_ts = jnp.where(valid[:, None], y_ts, 0.0)
        routed = (y_ts.reshape(N, TOPK, C) * w[:, :, None]).sum(axis=1)
        return (shared + routed).reshape(B, T, C)

    def _L1_xattn_ref(query, key, value, attention_mask, Wq, bq, Wk, bk, Wv, bv, Wqf, Wkf, Wo, bo):
        import jax, jax.numpy as jnp
        import numpy as np
        H = 512
        NH = 16
        HD = H // NH
        FD = 64
        B, Sq, _ = query.shape
        Sk = key.shape[1]

        def heads(x, W, b, S):
            return (x @ W.T + b).reshape(B, S, NH, HD).transpose(0, 2, 1, 3)
        q = heads(query, Wq, bq, Sq)
        k = heads(key, Wk, bk, Sk)
        v = heads(value, Wv, bv, Sk)
        q_prime = jax.nn.relu(jnp.einsum('bhnd,fd->bhnf', q, Wqf))
        k_prime = jax.nn.relu(jnp.einsum('bhnd,fd->bhnf', k, Wkf))
        k_prime = k_prime * attention_mask[:, None, :, None]
        kv = jnp.einsum('bhnf,bhne->bhfe', k_prime, v)
        qkv = jnp.einsum('bhmf,bhfe->bhme', q_prime, kv)
        k_sum = jnp.sum(k_prime, axis=2)
        qk_sum = jnp.einsum('bhmf,bhf->bhm', q_prime, k_sum)[..., None]
        out = qkv / (qk_sum + 1e-08)
        out = out.transpose(0, 2, 1, 3).reshape(B, Sq, H)
        return out @ Wo.T + bo

    def _L1_ffn_ref(x, w1, w3, w2):
        import jax, jax.numpy as jnp
        import numpy as np
        D_MODEL = 512
        HIDDEN = int(2 * D_MODEL * 4 / 3)

        def ternary_quant(w):
            s = jnp.mean(jnp.abs(w))
            q = jnp.clip(jnp.round(w / s), -1.0, 1.0) * s
            return w + jax.lax.stop_gradient(q - w)
        w1q = ternary_quant(w1)
        w3q = ternary_quant(w3)
        w2q = ternary_quant(w2)
        h1 = jnp.einsum('bsd,hd->bsh', x, w1q)
        h3 = jnp.einsum('bsd,hd->bsh', x, w3q)
        g = jax.nn.silu(h1) * h3
        return jnp.einsum('bsh,dh->bsd', g, w2q)

    def _L2_xattn_ref(q, k, v):
        import jax, jax.numpy as jnp
        import numpy as np
        BS, S, DK = (8, 128, 512)
        dk = q.shape[-1]
        scale = 1.0 / jnp.sqrt(jnp.asarray(dk, dtype=q.dtype))
        scaled = jnp.einsum('bsd,bse->bde', q, k) * scale
        attn = jax.nn.softmax(scaled, axis=1)
        out = jnp.einsum('bde,bse->bsd', attn, v)
        return out

    def _L2_ffn_ref(x, gate_w, gate_b, w1, w2, w3, sw1, sw2, sw3):
        import jax, jax.numpy as jnp
        import numpy as np
        B, S, DIM = (2, 512, 512)
        INTER = 352
        E = 8
        K = 2
        SHARED = 1
        ROUTE_SCALE = 1.0

        def _expert(xt, w1, w2, w3, cw=None):
            h = jax.nn.silu((xt @ w1.T).astype(jnp.float32)) * (xt @ w3.T).astype(jnp.float32)
            if cw is not None:
                h = cw[:, None] * h
            return h.astype(xt.dtype) @ w2.T
        Bx, Sx, D = x.shape
        xt = x.reshape(-1, D)
        T = xt.shape[0]
        scores = xt.astype(jnp.float32) @ gate_w.T
        scores = jnp.sqrt(jax.nn.softplus(scores))
        biased = scores + gate_b
        _, idx = jax.lax.top_k(biased, K)
        weights = jnp.take_along_axis(scores, idx, axis=1) * ROUTE_SCALE
        cw = jnp.einsum('tk,tke->te', weights, jax.nn.one_hot(idx, E, dtype=jnp.float32))
        y = jnp.zeros((T, D), dtype=xt.dtype)
        for e in range(E):
            y = y + _expert(xt, w1[e], w2[e], w3[e], cw[:, e])
        z = _expert(xt, sw1, sw2, sw3)
        return (y + z).reshape(Bx, Sx, D)

    def _L3_xattn_ref(v, k, bias, x1, x2, num_heads):
        import jax, jax.numpy as jnp
        import numpy as np
        B, D, L = v.shape
        H = D // num_heads
        fft_size = 2 * L
        vr = v.reshape(B, H, num_heads, L)
        x1r = x1.reshape(B, H, num_heads, L)
        x2r = x2.reshape(B, H, num_heads, L)
        kv = vr[:, :, :, None, :] * x2r[:, :, None, :, :]
        k_f = jnp.fft.rfft(k.astype(jnp.float32), n=fft_size)
        y = jnp.fft.irfft(jnp.fft.rfft(kv, n=fft_size) * k_f[None, :, None, None, :], n=fft_size)[..., :L]
        skip = bias.astype(jnp.float32).reshape(H, num_heads)[None, :, :, None, None]
        y = y + kv * skip
        out = jnp.einsum('bhijl,bhil->bhjl', y, x1r)
        return out.reshape(B, D, L)

    def _L3_ffn_ref(x, lut, gate_idx, up_idx, down_idx):
        import jax, jax.numpy as jnp
        import numpy as np
        HIDDEN = 512
        INTER = 1376
        LUT_SIZE = 16

        def _ghost_linear(x, idx, lut):
            w = lut[idx]
            return jnp.einsum('bsh,oh->bso', x, w)
        gate = _ghost_linear(x, gate_idx, lut)
        up = _ghost_linear(x, up_idx, lut)
        h = jax.nn.silu(gate) * up
        return _ghost_linear(h, down_idx, lut)
    x = x + jnp.tanh(g_xattn[0]) * _L0_xattn_ref(_layernorm(x, axis=-1), ctx_2048, ctx_2048, L0_xattn_gamma)
    x = x + jnp.tanh(g_ffn[0]) * _L0_ffn_ref(_layernorm(x, axis=-1), L0_ffn_w_gate, L0_ffn_w_shared_up, L0_ffn_w_shared_down, L0_ffn_w_up, L0_ffn_w_down)
    x = x + jnp.tanh(g_xattn[1]) * _L1_xattn_ref(_layernorm(x, axis=-1), ctx_2048, ctx_2048, mask_BxS2_ff1, L1_xattn_Wq, L1_xattn_bq, L1_xattn_Wk, L1_xattn_bk, L1_xattn_Wv, L1_xattn_bv, L1_xattn_Wqf, L1_xattn_Wkf, L1_xattn_Wo, L1_xattn_bo)
    x = x + jnp.tanh(g_ffn[1]) * _L1_ffn_ref(_layernorm(x, axis=-1), L1_ffn_w1, L1_ffn_w3, L1_ffn_w2)
    x = x + jnp.tanh(g_xattn[2]) * _L2_xattn_ref(_layernorm(x, axis=-1), ctx_2048, ctx_2048)
    x = x + jnp.tanh(g_ffn[2]) * _L2_ffn_ref(_layernorm(x, axis=-1), L2_ffn_gate_w, L2_ffn_gate_b, L2_ffn_w1, L2_ffn_w2, L2_ffn_w3, L2_ffn_sw1, L2_ffn_sw2, L2_ffn_sw3)
    x = x + jnp.tanh(g_xattn[3]) * _L3_xattn_ref(_layernorm(x, axis=-1), L3_xattn_k, fside_S2_0, ctx_2048, ctx_2048, 8)
    x = x + jnp.tanh(g_ffn[3]) * _L3_ffn_ref(_layernorm(x, axis=-1), L3_ffn_lut, L3_ffn_gate_idx, L3_ffn_up_idx, L3_ffn_down_idx)
    return x

_drawn_inputs = setup_inputs


def setup_inputs(seed=0):
    import zlib

    import numpy as np

    out = dict(_drawn_inputs(seed))
    spreads = {'L1_xattn_bq': (0.0, 0.526),
     'L1_xattn_bk': (0.0, 0.626),
     'L1_xattn_bv': (0.0, 0.1),
     'L1_xattn_bo': (0.0, 0.1)}
    factors = {'g_ffn': 8.0,
     'L0_ffn_w_gate': 8.0,
     'L0_ffn_w_shared_up': 8.0,
     'L0_ffn_w_shared_down': 8.0,
     'L0_ffn_w_up': 8.0,
     'L0_ffn_w_down': 8.0,
     'L2_ffn_gate_w': 3.004,
     'L2_ffn_gate_b': 8.0,
     'L2_ffn_sw1': 3.337,
     'L2_ffn_sw2': 3.239,
     'L2_ffn_sw3': 3.252,
     'L3_ffn_lut': 2.972}
    for name, (base, spread) in spreads.items():
        noise = np.random.default_rng([zlib.crc32(name.encode()), seed]).standard_normal(out[name].shape)
        drawn = base * np.exp(spread * noise) if base else spread * noise
        out[name] = jnp.asarray(drawn.astype(out[name].dtype))
    for name, factor in factors.items():
        out[name] = (out[name] * factor).astype(out[name].dtype)
    return out
```

```python
from contextlib import ExitStack

import numpy as np
import concourse.bass as bass
from concourse import mybir

PHASES = range(8)

ALU = mybir.AluOpType
ACT = mybir.ActivationFunctionType
AX = mybir.AxisListType
F32 = mybir.dt.float32
BF16 = mybir.dt.bfloat16
I32 = mybir.dt.int32
U32 = mybir.dt.uint32

P = 128
B, S, D = 8, 256, 512
N = B * S
DC = D // P
LN_EPS = 1e-5


class Scope:

    def __init__(self, nc, ctx, name):
        self.nc, self.ctx, self.name = nc, ctx, name
        self.held = []
        ctx.callback(self.release)

    def release(self):
        if self.held:
            self.nc.clear_and_free_semaphores(self.held)
            self.nc.all_engine_barrier()

    def sb(self, name, shape, dt=F32):
        return self.ctx.enter_context(self.nc.sbuf_tensor(f"{self.name}_{name}", shape, dt))

    def ps(self, name, shape, dt=F32):
        return self.ctx.enter_context(self.nc.psum_tensor(f"{self.name}_{name}", shape, dt))

    def sem(self, name):
        self.held.append(self.nc.alloc_semaphore(f"{self.name}_{name}"))
        return self.held[-1]

    def sems(self, name, n):
        return [self.sem(f"{name}{i}") for i in range(n)]


def hold(eng, sem, val, passed):
    eng.wait_ge(sem, val)
    eng.sem_inc(passed, 1)


def rows(ap, start, count):
    return ap[bass.ds(start, count), :]


def build_setup(nc, io, keep):
    with ExitStack() as ctx:
        sc = Scope(nc, ctx, "setup")
        g_raw = sc.sb("g_raw", [P, 8])
        gamma = sc.sb("gamma", [P, 1])
        iota_i = sc.sb("iota_i", [P, 64], I32)
        spare_i = sc.sb("spare_i", [P, 1], I32)
        ints_done = sc.sem("ints_done")
        g_loaded = sc.sem("g_loaded")
        tanh_done = sc.sem("tanh_done")
        zeroed = sc.sem("zeroed")
        const_done = sc.sem("const_done")
        with nc.Block() as block:

            @block.sync
            def _(sp):
                sp.dma_start(g_raw[:, 0:4], io["g_xattn"].rearrange("(a g) -> a g", a=1).broadcast_to([P, 4])).then_inc(g_loaded, 16)
                sp.dma_start(g_raw[:, 4:8], io["g_ffn"].rearrange("(a g) -> a g", a=1).broadcast_to([P, 4])).then_inc(g_loaded, 16)
                sp.dma_start(gamma[:, :], io["gamma"].broadcast_to([P, 1])).then_inc(g_loaded, 16)

            @block.scalar
            def _(act):
                act.wait_ge(g_loaded, 48)
                nc.scalar.activation(keep["gates"][:, :], g_raw[:, :], ACT.Tanh).then_inc(tanh_done, 1)

            @block.vector
            def _(dve):
                nc.vector.memset(keep["neg_half"][:, :], -0.5)
                nc.vector.memset(keep["half"][:, :], 0.5)
                nc.vector.memset(keep["ones"][:, :], 1.0)
                dve.wait_ge(tanh_done, 1)
                nc.vector.tensor_tensor(keep["gate0"][:, :], keep["gates"][:, 0:1], gamma[:, :], ALU.mult)
                dve.wait_ge(const_done, 1)
                nc.vector.tensor_copy(keep["ident_bf"][:, :], keep["ident"][:, :])
                nc.vector.memset(keep["ones_bf"][:, :], 1.0)
                nc.vector.memset(keep["zeros_i"][:, :], 0)
                dve.wait_ge(ints_done, 4)
                nc.vector.tensor_copy(keep["earlier"][:, :], keep["earlier_f"][:, :])
                nc.vector.tensor_copy(keep["iota"][:, :], iota_i[:, :])
                nc.vector.tensor_copy(keep["spare"][:, :], spare_i[:, :])

            @block.gpsimd
            def _(pool):
                nc.gpsimd.memset(keep["ident"][:, :], 0.0).then_inc(zeroed, 1)
                nc.gpsimd.memset(keep["anti"][:, :], 0.0).then_inc(zeroed, 1)
                nc.gpsimd.memset(keep["earlier_f"][:, :], 1.0).then_inc(zeroed, 1)
                pool.wait_ge(zeroed, 3)
                nc.gpsimd.affine_select(out=keep["earlier_f"][:, :], in_=keep["earlier_f"][:, :], compare_op=ALU.is_gt, fill=0.0,
                                        base=0, pattern=[[1, P]], channel_multiplier=-1).then_inc(ints_done, 1)
                nc.gpsimd.iota(iota_i[:, :], pattern=[[1, 64]], base=0, channel_multiplier=0).then_inc(ints_done, 1)
                nc.gpsimd.iota(spare_i[:, :], pattern=[[1, 1]], base=64 * CAP, channel_multiplier=1).then_inc(ints_done, 1)
                nc.gpsimd.iota(keep["row_id"][:, :], pattern=[[P, N // P]], base=0, channel_multiplier=1).then_inc(ints_done, 1)
                nc.gpsimd.affine_select(out=keep["ident"][:, :], in_=keep["ident"][:, :], compare_op=ALU.not_equal, fill=1.0,
                                        base=0, pattern=[[-1, P]], channel_multiplier=1).then_inc(const_done, 1)
                nc.gpsimd.affine_select(out=keep["anti"][:, :], in_=keep["anti"][:, :], compare_op=ALU.not_equal, fill=1.0,
                                        base=-(P - 1), pattern=[[1, P]], channel_multiplier=1)


def build_feature_attention(nc, io, keep, x_in, x_out):
    T = S // P
    scale = float(D) ** -0.5
    with ExitStack() as ctx:
        sc = Scope(nc, ctx, "fattn")
        x_sb = sc.sb("x", [P, 2, T, D])
        k_sb = sc.sb("k", [P, 2, T, D])
        vt_sb = sc.sb("vt", [P, 2, DC, S])
        xn = sc.sb("xn", [P, 2, T, D])
        stats = sc.sb("stats", [P, T, 6])
        mv = sc.sb("mv", [P, T, 2])
        ve = sc.sb("ve", [P, T])
        rstd = sc.sb("rstd", [P, T])
        negmax = sc.sb("negmax", [P, DC])
        bias = sc.sb("bias", [P, DC])
        sums = sc.sb("sums", [P, DC])
        rsum = sc.sb("rsum", [P, DC])
        prob = sc.sb("prob", [P, DC, D])
        vs = sc.sb("vs", [P, DC, S])
        x_new = sc.sb("x_new", [P, 2, T, D])
        scores = sc.ps("scores", [P, DC, D])
        mixed = sc.ps("mixed", [P, T, D])

        loaded = sc.sems("loaded", 2)
        stored = sc.sems("stored", 2)
        inputs_free = sc.sem("inputs_free")
        passed = sc.sem("passed")
        stats_done = sc.sem("stats_done")
        var_done = sc.sem("var_done")
        ve_done = sc.sem("ve_done")
        rstd_done = sc.sem("rstd_done")
        xn_done = sc.sem("xn_done")
        scores_done = sc.sem("scores_done")
        max_done = sc.sem("max_done")
        bias_done = sc.sem("bias_done")
        prob_done = sc.sem("prob_done")
        rsum_done = sc.sem("rsum_done")
        vs_done = sc.sem("vs_done")
        mixed_done = sc.sem("mixed_done")
        out_done = sc.sem("out_done")

        with nc.Block() as block:

            @block.sync
            def _(sp):
                with sp.Fori(0, B // 2) as i:
                    for u in range(2):
                        sp.wait_ge(inputs_free, 2 * i + u + 1)
                        sp.dma_start(x_sb[:, u], rows(x_in, (2 * i + u) * S, S).rearrange("(t p) d -> p t d", p=P)).then_inc(loaded[u], 16)
                        sp.dma_start(k_sb[:, u], rows(io["ctx"], (2 * i + u) * S, S).rearrange("(t p) d -> p t d", p=P)).then_inc(loaded[u], 16)
                        sp.dma_start(vt_sb[:, u], io["ctxT"][bass.ds(2 * i + u, 1)].rearrange("b p c s -> p (b c) s")).then_inc(loaded[u], 16)

            @block.tensor
            def _(pe):
                with pe.Fori(0, B // 2) as i:
                    for u in range(2):
                        b = 2 * i + u
                        pe.wait_ge(xn_done, T * b + T)
                        for e in range(DC):
                            pe.wait_ge(prob_done, DC * b + e + 1)
                            for t in range(T):
                                mm = nc.tensor.matmul(scores[:, e, :], k_sb[:, u, t, e * P:(e + 1) * P], xn[:, u, t, :], start=t == 0, stop=t == T - 1)
                            mm.then_inc(scores_done, 1)
                        pe.wait_ge(out_done, T * b + T)
                        for e in range(DC):
                            pe.wait_ge(vs_done, DC * b + e + 1)
                            for t in range(T):
                                mm = nc.tensor.matmul(mixed[:, t, :], vs[:, e, t * P:(t + 1) * P], prob[:, e, :], start=e == 0, stop=e == DC - 1)
                        mm.then_inc(mixed_done, 1)

            @block.vector
            def _(dve):
                dve.sem_inc(inputs_free, 2)
                dve.sem_inc(out_done, T)
                dve.sem_inc(stored[0], 16)
                dve.sem_inc(stored[1], 16)

                with dve.Fori(0, B // 2) as i:
                    for u in range(2):
                        b = 2 * i + u
                        dve.wait_ge(loaded[u], 48 * i + 48)
                        for t in range(T):
                            nc.vector.bn_stats(stats[:, t, :], x_sb[:, u, t, :]).then_inc(stats_done, 1)
                        for t in range(T):
                            hold(dve, stats_done, T * b + t + 1, passed)
                            nc.vector.bn_aggr(mv[:, t, :], stats[:, t, :]).then_inc(var_done, 1)
                        dve.wait_ge(var_done, T * b + T)
                        nc.vector.tensor_scalar(ve[:, :], mv[:, :, 1], LN_EPS, None, ALU.add).then_inc(ve_done, 1)
                        dve.wait_ge(rstd_done, b + 1)
                        for t in range(T):
                            nc.vector.tensor_scalar(xn[:, u, t, :], x_sb[:, u, t, :], mv[:, t, 0:1], rstd[:, t:t + 1], ALU.subtract, ALU.mult).then_inc(xn_done, 1)
                        for e in range(DC):
                            dve.wait_ge(scores_done, DC * b + e + 1)
                            nc.vector.tensor_reduce(negmax[:, e:e + 1], scores[:, e, :], AX.X, ALU.max, negate=True).then_inc(max_done, 1)
                            dve.wait_ge(max_done, DC * b + e + 1)
                            nc.vector.tensor_scalar(bias[:, e:e + 1], negmax[:, e:e + 1], scale, None, ALU.mult).then_inc(bias_done, 1)
                        if True:
                            dve.wait_ge(mixed_done, b + 1)
                        for e in range(DC):
                            dve.wait_ge(prob_done, DC * b + DC + e + 1)
                            nc.vector.reciprocal(rsum[:, e:e + 1], sums[:, e:e + 1]).then_inc(rsum_done, 1)
                            dve.wait_ge(rsum_done, DC * b + e + 1)
                            nc.vector.tensor_scalar(vs[:, e, :], vt_sb[:, u, e, :], rsum[:, e:e + 1], None, ALU.mult).then_inc(vs_done, 1)
                        dve.wait_ge(mixed_done, b + 2)
                        dve.wait_ge(stored[u], 16 * i + 16)
                        for t in range(T):
                            nc.vector.scalar_tensor_tensor(out=x_new[:, u, t, :], in0=mixed[:, t, :], scalar=keep["gates"][:, 2:3], in1=x_sb[:, u, t, :],
                                                           op0=ALU.mult, op1=ALU.add).then_inc(out_done, 1)
                        dve.wait_ge(out_done, T * b + 2 * T)
                        dve.sem_inc(inputs_free, 1)

            @block.gpsimd
            def _(pool):
                pool.sem_inc(mixed_done, 1)
                with pool.Fori(0, B) as b:
                    pool.wait_ge(ve_done, b + 1)
                    nc.gpsimd.tensor_tensor(rstd[:, :], ve[:, :], keep["neg_half"][:, 0:T], ALU.pow).then_inc(rstd_done, 1)

            @block.scalar
            def _(act):
                act.sem_inc(prob_done, DC)
                with act.Fori(0, B // 2) as i:
                    for u in range(2):
                        b = 2 * i + u
                        act.wait_ge(mixed_done, b + 1)
                        for e in range(DC):
                            act.wait_ge(bias_done, DC * b + e + 1)
                            nc.scalar.activation(prob[:, e, :], scores[:, e, :], ACT.Exp, bias=bias[:, e:e + 1], scale=scale, accum_out=sums[:, e:e + 1]).then_inc(prob_done, 1)
                        act.wait_ge(out_done, T * b + 2 * T)
                        act.dma_start(rows(x_out, b * S, S).rearrange("(t p) d -> p t d", p=P), x_new[:, u]).then_inc(stored[u], 16)
                for u in range(2):
                    act.wait_ge(stored[u], 16 * (B // 2) + 16)


def build_channel_attention(nc, io, keep, x_in, x_out):
    T = S // P
    H4 = 4
    HDIM = S // 8
    QC = D // P
    GROUPS = T * QC
    UB = GROUPS * H4
    scale = float(HDIM) ** -0.5
    with ExitStack() as ctx:
        sc = Scope(nc, ctx, "cattn")
        x_sb = sc.sb("x", [P, 2, T, D])
        k_sb = sc.sb("k", [P, 2, T, D])
        vT = sc.sb("vT", [P, 2, DC, S])
        xn = sc.sb("xn", [P, 2, T, H4, D])
        stats = sc.sb("stats", [P, T, 6])
        mv = sc.sb("mv", [P, T, 2])
        ve = sc.sb("ve", [P, T])
        rstd = sc.sb("rstd", [P, T])
        rstd_h = sc.sb("rstd_h", [P, T, H4])
        head_scale = sc.sb("head_scale", [P, T, H4])
        negmax = sc.sb("negmax", [P, 2, H4])
        sums = sc.sb("sums", [P, 2, H4])
        rsum = sc.sb("rsum", [P, 2, H4, HDIM])
        prob = sc.sb("prob", [P, 2, H4, D])
        probT = sc.sb("probT", [P, T, H4, DC, D])
        rsumT_sb = sc.sb("rsumT_sb", [P, T, D])
        o_sb = sc.sb("o", [P, D])
        x_new = sc.sb("x_new", [P, T, D])
        scores = sc.ps("scores", [P, H4, D])
        turn = sc.ps("turn", [P, 2, DC, P])
        pv = sc.ps("pv", [P, D])
        rsumT = sc.ps("rsumT", [P, D])

        loaded = sc.sems("loaded", 2)
        stored = sc.sems("stored", T)
        stats_done = sc.sem("stats_done")
        var_done = sc.sem("var_done")
        ve_done = sc.sem("ve_done")
        pow_done = sc.sem("pow_done")
        rstd_done = sc.sem("rstd_done")
        xn_done = sc.sem("xn_done")
        scores_done = sc.sem("scores_done")
        max_done = sc.sem("max_done")
        exp_done = sc.sem("exp_done")
        turned = sc.sem("turned")
        act_out = sc.sem("act_out")
        dve_out = sc.sem("dve_out")
        pv_done = sc.sem("pv_done")
        rsum_done = sc.sem("rsum_done")
        rsumT_done = sc.sem("rsumT_done")
        rsumT_moved = sc.sem("rsumT_moved")
        o_done = sc.sem("o_done")
        out_done = sc.sem("out_done")
        const_done = sc.sem("const_done")
        passed = sc.sem("passed")

        def await_if(eng, sem, value):
            if not isinstance(value, int) or value > 0:
                eng.wait_ge(sem, value)

        def elements(eng, element):
            element(0, 0, 0)
            with eng.Fori(0, B // 2 - 1) as i:
                element(2 * i + 1, 1, i + 1)
                element(2 * i + 2, 0, i + 1)
            element(B - 1, 1, None)

        with nc.Block() as block:

            @block.sync
            def _(sp):
                def load(b, u):
                    sp.dma_start(x_sb[:, u], rows(x_in, b * S, S).rearrange("(t p) d -> p t d", p=P)).then_inc(loaded[u], 16)
                    sp.dma_start(k_sb[:, u], rows(io["ctx"], b * S, S).rearrange("(t p) d -> p t d", p=P)).then_inc(loaded[u], 16)
                    sp.dma_start(vT[:, u], io["ctxT"][bass.ds(b, 1)].rearrange("b p c s -> p (b c) s")).then_inc(loaded[u], 16)

                def store(b):
                    for t in range(T):
                        sp.wait_ge(out_done, T * b + t + 1)
                        sp.dma_start(rows(x_out, b * S + t * P, P), x_new[:, t]).then_inc(stored[t], 16)

                load(0, 0)
                load(1, 1)
                with sp.Fori(0, B // 2 - 1) as i:
                    for u in range(2):
                        store(2 * i + u)
                        load(2 * i + u + 2, u)
                for b in range(B - 2, B):
                    store(b)
                for t in range(T):
                    sp.wait_ge(stored[t], 16 * B + 16)

            @block.tensor
            def _(pe):
                def score(b, u, g, h):
                    n = UB * b + H4 * g + h
                    t, qc = g // QC, g % QC
                    pe.wait_ge(xn_done, T * H4 * b + H4 * t + h + 1)
                    await_if(pe, exp_done, n + 1 - H4)
                    nc.tensor.matmul(scores[:, h, :], xn[:, u, t, h, qc * P:(qc + 1) * P], k_sb[:, u, t, :], start=True, stop=True).then_inc(scores_done, 1)

                def transpose(b, g, h):
                    n = UB * b + H4 * g + h
                    pe.wait_ge(exp_done, n + 1)
                    await_if(pe, dve_out if h % 2 else act_out, 2 * (GROUPS * b + g) + h // 2)
                    for c in range(DC):
                        mm = nc.tensor.transpose(turn[:, h % 2, c, :], prob[:, g % 2, h, c * P:(c + 1) * P], keep["ident"][:, :])
                    mm.then_inc(turned, 1)

                def turn_sums(b, g):
                    q = g % QC
                    pe.wait_ge(rsum_done, GROUPS * b + g + 1)
                    if q == 0:
                        await_if(pe, rsumT_moved, T * b + g // QC)
                    nc.tensor.transpose(rsumT[:, q * P:(q + 1) * P], rsum[:, q % 2, :, :].rearrange("p h e -> p (h e)"), keep["ident"][:, :]).then_inc(rsumT_done, 1)

                def values(half, u, t, c):
                    if c == 0:
                        pe.wait_ge(act_out, 2 * QC * half + 2 * QC)
                        pe.wait_ge(dve_out, 2 * QC * half + 2 * QC)
                        await_if(pe, out_done, half)
                    for h in range(H4):
                        head = H4 * t + h
                        mm = nc.tensor.matmul(pv[h * HDIM:(h + 1) * HDIM, :], vT[:, u, c, head * HDIM:(head + 1) * HDIM], probT[:, t, h, c, :],
                                              start=c == 0, stop=c == DC - 1, tile_position=(0, h * HDIM))
                    if c == DC - 1:
                        mm.then_inc(pv_done, 1)

                def element(b, u, next_load):
                    first, last = isinstance(b, int) and b == 0, isinstance(b, int) and b == B - 1
                    for g in range(GROUPS):
                        t, q = g // QC, g % QC
                        for h in range(H4):
                            if g < GROUPS - 1:
                                score(b, u, g + 1, h)
                            elif not last:
                                score(b + 1, 1 - u, 0, h)
                            if h == 0 and not (first and g == 0):
                                turn_sums(b, g - 1)
                            transpose(b, g, h)
                            if h % 2 and q < 2 and not (first and t == 0):
                                values(T * b + t - 1, u if t else 1 - u, 1 - t, 2 * q + h // 2)

                for h in range(H4):
                    score(0, 0, 0, h)
                elements(pe, element)
                turn_sums(B - 1, GROUPS - 1)
                for c in range(DC):
                    values(T * B - 1, 1, 1, c)

            @block.vector
            def _(dve):
                def norm_stats(b, u, load):
                    dve.wait_ge(loaded[u], 48 * load + 48)
                    for t in range(T):
                        nc.vector.bn_stats(stats[:, t, :], x_sb[:, u, t, :]).then_inc(stats_done, 1)
                    hold(dve, stats_done, T * b + T, passed)
                    for t in range(T):
                        nc.vector.bn_aggr(mv[:, t, :], stats[:, t, :]).then_inc(var_done, 1)
                    dve.wait_ge(var_done, T * b + T)
                    nc.vector.tensor_scalar(ve[:, :], mv[:, :, 1], LN_EPS, None, ALU.add).then_inc(ve_done, 1)

                def norm(b, u, j):
                    t, h = j // H4, j % H4
                    dve.wait_ge(rstd_done, b + 1)
                    nc.vector.tensor_scalar(xn[:, u, t, h, :], x_sb[:, u, t, :], mv[:, t, 0:1], rstd_h[:, t, h:h + 1], ALU.subtract, ALU.mult).then_inc(xn_done, 1)

                def maximum(b, g, h):
                    dve.wait_ge(scores_done, UB * b + H4 * g + h + 1)
                    nc.vector.tensor_reduce(negmax[:, g % 2, h:h + 1], scores[:, h, :], AX.X, ALU.max, negate=True).then_inc(max_done, 1)

                def evacuate(b, g, h):
                    t, q = g // QC, g % QC
                    dve.wait_ge(turned, UB * b + H4 * g + h + 1)
                    await_if(dve, pv_done, T * b + t - 1)
                    nc.vector.tensor_copy(probT[:, t, h, :, q * P:(q + 1) * P], turn[:, h % 2, :, :]).then_inc(dve_out, 1)

                def invert(b, g):
                    G = GROUPS * b + g
                    dve.wait_ge(exp_done, H4 * G + H4)
                    await_if(dve, rsumT_done, G - 1)
                    nc.vector.reciprocal(rsum[:, g % 2, :, :], sums[:, g % 2, :].rearrange("p (h e) -> p h e", e=1).broadcast_to([P, H4, HDIM])).then_inc(rsum_done, 1)

                def finish(b, u, t):
                    half = T * b + t
                    dve.wait_ge(pv_done, half + 1)
                    dve.wait_ge(rsumT_moved, half + 1)
                    await_if(dve, out_done, half)
                    nc.vector.tensor_tensor(o_sb[:, :], pv[:, :], rsumT_sb[:, t, :], ALU.mult).then_inc(o_done, 1)
                    dve.wait_ge(o_done, half + 1)
                    dve.wait_ge(stored[t], 16 * b + 16)
                    nc.vector.scalar_tensor_tensor(out=x_new[:, t, :], in0=o_sb[:, :], scalar=keep["gate0"][:, 0:1], in1=x_sb[:, u, t, :],
                                                   op0=ALU.mult, op1=ALU.add).then_inc(out_done, 1)

                def element(b, u, next_load):
                    first, last = isinstance(b, int) and b == 0, isinstance(b, int) and b == B - 1
                    for g in range(GROUPS):
                        if g == QC and not last:
                            norm_stats(b + 1, 1 - u, next_load)
                        for h in range(H4):
                            if h % 2:
                                evacuate(b, g, h)
                            if g < GROUPS - 1:
                                maximum(b, g + 1, h)
                            elif not last:
                                maximum(b + 1, 0, h)
                            if g > QC and not last and h < H4 - 1:
                                j = (g - QC - 1) * (H4 - 1) + h
                                if j < T * H4:
                                    norm(b + 1, 1 - u, j)
                        invert(b, g)
                        if g == 1 and not first:
                            finish(b - 1, 1 - u, 1)
                        if g == QC + 1:
                            finish(b, u, 0)

                for t in range(T):
                    dve.sem_inc(stored[t], 16)
                nc.vector.memset(head_scale[:, :, :], 0.0).then_inc(const_done, 1)
                dve.wait_ge(const_done, 1)
                for h in range(H4):
                    nc.vector.memset(head_scale[h * HDIM:(h + 1) * HDIM, :, h:h + 1], scale).then_inc(const_done, 1)
                norm_stats(0, 0, 0)
                for j in range(T * H4):
                    norm(0, 0, j)
                for h in range(H4):
                    maximum(0, 0, h)
                elements(dve, element)
                finish(B - 1, 1, 1)

            @block.gpsimd
            def _(pool):
                pool.wait_ge(const_done, 1 + H4)
                with pool.Fori(0, B) as b:
                    pool.wait_ge(ve_done, b + 1)
                    nc.gpsimd.tensor_tensor(rstd[:, :], ve[:, :], keep["neg_half"][:, 0:T], ALU.pow).then_inc(pow_done, 1)
                    pool.wait_ge(pow_done, b + 1)
                    nc.gpsimd.tensor_tensor(rstd_h[:, :, :], rstd[:, :].rearrange("p (t e) -> p t e", e=1).broadcast_to([P, T, H4]),
                                            head_scale[:, :, :], ALU.mult).then_inc(rstd_done, 1)

            @block.scalar
            def _(act):
                def exponential(b, g, h):
                    n = UB * b + H4 * g + h
                    if h == 0:
                        await_if(act, rsum_done, GROUPS * b + g - 1)
                    await_if(act, turned, n + 1 - 2 * H4)
                    act.wait_ge(max_done, n + 1)
                    nc.scalar.activation(prob[:, g % 2, h, :], scores[:, h, :], ACT.Exp, bias=negmax[:, g % 2, h:h + 1], accum_out=sums[:, g % 2, h:h + 1]).then_inc(exp_done, 1)

                def evacuate(b, g, h):
                    t, q = g // QC, g % QC
                    act.wait_ge(turned, UB * b + H4 * g + h + 1)
                    await_if(act, pv_done, T * b + t - 1)
                    nc.scalar.activation(probT[:, t, h, :, q * P:(q + 1) * P], turn[:, h % 2, :, :], ACT.Copy).then_inc(act_out, 1)

                def move_sums(b, t):
                    half = T * b + t
                    act.wait_ge(rsumT_done, QC * half + QC)
                    await_if(act, out_done, half - 1)
                    nc.scalar.activation(rsumT_sb[:, t, :], rsumT[:, :], ACT.Copy).then_inc(rsumT_moved, 1)

                def element(b, u, next_load):
                    first, last = isinstance(b, int) and b == 0, isinstance(b, int) and b == B - 1
                    for g in range(GROUPS):
                        for h in range(H4):
                            if h % 2 == 0:
                                evacuate(b, g, h)
                            if g < GROUPS - 1:
                                exponential(b, g + 1, h)
                            elif not last:
                                exponential(b + 1, 0, h)
                        if g == 0 and not first:
                            move_sums(b - 1, 1)
                        if g == QC:
                            move_sums(b, 0)

                for h in range(H4):
                    exponential(0, 0, h)
                elements(act, element)
                move_sums(B - 1, 1)


F32R = mybir.dt.float32r
BLK = 512
NB = N // BLK
TB = BLK // P
HC = 11
HPAD = HC * P
TERNARY_HIDDEN = 1365
LUT_HIDDEN = 1376
LUT_SIZE = 16
WCOLS = DC * HPAD


def build_ternary_weights(nc, io, keep, weights, scales):
    with ExitStack() as ctx:
        sc = Scope(nc, ctx, "tern")
        raw = sc.sb("raw", [P, 2, WCOLS])
        low = sc.sb("low", [P, WCOLS], BF16)
        part = sc.sb("part", [P, 3])
        thr = sc.sb("thr", [P, 3])
        nthr = sc.sb("nthr", [P, 3])
        total = sc.ps("total", [P, 512])
        loaded = sc.sems("loaded", 2)
        part_done = sc.sem("part_done")
        total_done = sc.sem("total_done")
        scale_done = sc.sem("scale_done")
        thr_done = sc.sem("thr_done")
        low_done = sc.sem("low_done")
        weight_done = sc.sem("weight_done")
        with nc.Block() as block:

            @block.sync
            def _(sp):
                for m, name in enumerate(("w1t", "w3t", "w2t")):
                    if m == 2:
                        sp.wait_ge(weight_done, 1)
                    sp.dma_start(raw[:, m % 2, :], io[name]).then_inc(loaded[m % 2], 16)

            @block.tensor
            def _(pe):
                for m in range(3):
                    pe.wait_ge(part_done, m + 1)
                    nc.tensor.matmul(total[:, m:m + 1], keep["ones"][:, :], part[:, m:m + 1], start=True, stop=True).then_inc(total_done, 1)

            @block.vector
            def _(dve):
                for m in range(3):
                    w = raw[:, m % 2, :]
                    dve.wait_ge(loaded[m % 2], 16 * (m // 2) + 16)
                    nc.vector.tensor_reduce(part[:, m:m + 1], w, AX.X, ALU.add, apply_absolute_value=True).then_inc(part_done, 1)
                    dve.wait_ge(total_done, m + 1)
                    nc.vector.tensor_scalar(scales[:, m:m + 1], total[:, m:m + 1], 1.0 / (TERNARY_HIDDEN * D), None, ALU.mult).then_inc(scale_done, 1)
                    dve.wait_ge(scale_done, m + 1)
                    nc.vector.tensor_scalar(thr[:, m:m + 1], scales[:, m:m + 1], 0.5, None, ALU.mult).then_inc(thr_done, 1)
                    nc.vector.tensor_scalar(nthr[:, m:m + 1], scales[:, m:m + 1], -0.5, None, ALU.mult).then_inc(thr_done, 1)
                    dve.wait_ge(thr_done, 2 * m + 2)
                    nc.vector.tensor_scalar(low[:, :], w, nthr[:, m:m + 1], None, ALU.is_lt).then_inc(low_done, 1)
                    dve.wait_ge(low_done, m + 1)
                    nc.vector.scalar_tensor_tensor(out=weights[:, m, :], in0=w, scalar=thr[:, m:m + 1], in1=low[:, :], op0=ALU.is_gt, op1=ALU.subtract).then_inc(weight_done, 1)


def build_lut_weights(nc, io, keep, weights):
    CH = 1408
    CHUNKS = 3 * WCOLS // CH
    flat = weights[:, :, :].rearrange("p m c -> p (m c)")
    with ExitStack() as ctx:
        sc = Scope(nc, ctx, "lut")
        lut = sc.sb("lut", [P, LUT_SIZE])
        idx = sc.sb("idx", [P, 2, CH], I32)
        idxb = sc.sb("idxb", [P, CH], BF16)
        mask = sc.sb("mask", [P, 2, CH], BF16)
        acc = sc.sb("acc", [P, 2, CH])
        lut_loaded = sc.sem("lut_loaded")
        loaded = sc.sems("loaded", 2)
        idx_free = sc.sem("idx_free")
        small_done = sc.sem("small_done")
        mask_done = sc.sem("mask_done")
        acc_done = sc.sem("acc_done")
        K = LUT_SIZE
        with nc.Block() as block:

            @block.sync
            def _(sp):
                sp.dma_start(lut[:, :], io["lut"].rearrange("(a g) -> a g", a=1).broadcast_to([P, LUT_SIZE])).then_inc(lut_loaded, 16)
                with sp.Fori(0, CHUNKS // 2) as i:
                    for u in range(2):
                        sp.wait_ge(idx_free, 2 * i + u + 1)
                        sp.dma_start(idx[:, u, :], io["lut_idx"][:, bass.ds((2 * i + u) * CH, CH)]).then_inc(loaded[u], 16)

            @block.vector
            def _(dve):
                dve.sem_inc(idx_free, 2)
                dve.sem_inc(mask_done, 1)
                dve.sem_inc(acc_done, 2)
                dve.wait_ge(lut_loaded, 16)
                with dve.Fori(0, CHUNKS // 2) as i:
                    for u in range(2):
                        c = 2 * i + u
                        dve.wait_ge(mask_done, K * c + 1)
                        dve.wait_ge(loaded[u], 16 * i + 16)
                        nc.vector.tensor_copy(idxb[:, :], idx[:, u, :]).then_inc(small_done, 1)
                        for k in range(K):
                            if k == 0:
                                dve.wait_ge(small_done, c + 1)
                            dve.wait_ge(acc_done, K * c + k + 1)
                            nc.vector.tensor_scalar(mask[:, k % 2, :], idxb[:, :], float(k), None, ALU.is_equal).then_inc(mask_done, 1)
                            dve.wait_ge(mask_done, K * c + k + 2)
                            dve.wait_ge(acc_done, K * c + k + 2)
                            if k == 0:
                                nc.vector.tensor_scalar(acc[:, 0, :], mask[:, 0, :], lut[:, 0:1], None, ALU.mult).then_inc(acc_done, 1)
                            else:
                                out = acc[:, k % 2, :] if k < K - 1 else flat[:, bass.ds(c * CH, CH)]
                                nc.vector.scalar_tensor_tensor(out=out, in0=mask[:, k % 2, :], scalar=lut[:, k:k + 1], in1=acc[:, (k - 1) % 2, :],
                                                               op0=ALU.mult, op1=ALU.add).then_inc(acc_done, 1)
                        dve.wait_ge(small_done, c + 1)
                        dve.sem_inc(idx_free, 1)


def build_ffn(nc, io, keep, x_in, x_out, ternary):
    name = "tffn" if ternary else "lffn"
    hidden = TERNARY_HIDDEN if ternary else LUT_HIDDEN
    gate = keep["gates"][:, 5:6] if ternary else keep["gates"][:, 7:8]
    parts = 2 if ternary else 1
    WDT = F32R if ternary else F32
    with ExitStack() as outer:
        osc = Scope(nc, outer, name)
        weights = osc.sb("weights", [P, 3, WCOLS], WDT)
        scales = osc.sb("scales", [P, 3])
        if ternary:
            build_ternary_weights(nc, io, keep, weights, scales)
        else:
            build_lut_weights(nc, io, keep, weights)
        w1 = weights[:, 0, :].rearrange("p (c h) -> p c h", c=DC)
        w3 = weights[:, 1, :].rearrange("p (c h) -> p c h", c=DC)
        w2 = weights[:, 2, :].rearrange("p (j d) -> p j d", j=HC)
        HM = [min(P, (P * HC if ternary else hidden) - P * j) for j in range(HC)]
        with ExitStack() as ctx:
            sc = Scope(nc, ctx, name)
            x_ln = sc.sb("x_ln", [P, TB, D])
            x_res = sc.sb("x_res", [P, TB, D])
            xn = sc.sb("xn", [P, TB, D])
            xnT = [sc.sb(f"xnT{q}", [P, DC, BLK], WDT) for q in range(parts)]
            stats = sc.sb("stats", [P, TB, 6])
            mv = sc.sb("mv", [P, TB, 2])
            ve = sc.sb("ve", [P, TB])
            rstd = sc.sb("rstd", [P, TB])
            sil = sc.sb("sil", [P, 2, BLK])
            g32 = sc.sb("g32", [P, 2, BLK])
            gp = [sc.sb(f"g_part{q}", [P, 2, BLK], WDT) for q in range(parts)] if ternary else [g32]
            x_new = sc.sb("x_new", [P, TB, D])
            out_scale = sc.sb("out_scale", [P, 1])
            s23 = sc.sb("s23", [P, 1])
            h1 = sc.ps("h1", [P, 2, BLK])
            h3 = sc.ps("h3", [P, 2, BLK])
            y = sc.ps("y", [P, TB, D])

            ln_loaded = sc.sem("ln_loaded")
            res_loaded = sc.sem("res_loaded")
            stored = sc.sem("stored")
            ln_free = sc.sem("ln_free")
            res_free = sc.sem("res_free")
            stats_done = sc.sem("stats_done")
            var_done = sc.sem("var_done")
            ve_done = sc.sem("ve_done")
            rstd_done = sc.sem("rstd_done")
            xn_done = sc.sem("xn_done")
            turned = sc.sem("turned")
            hi_done = sc.sem("hi_done")
            lo_done = sc.sem("lo_done")
            h1_done = sc.sem("h1_done")
            h3_done = sc.sem("h3_done")
            sil_done = sc.sem("sil_done")
            g_done = sc.sem("g_done")
            ghi_done = sc.sem("ghi_done")
            glo_done = sc.sem("glo_done")
            y_step = sc.sem("y_step")
            out_done = sc.sem("out_done")
            scale_done = sc.sem("scale_done")
            passed = sc.sem("passed")
            dve_passed = sc.sem("dve_passed")
            g_ready = glo_done if ternary else g_done

            def left(i, j):
                return HC * i + j + 1 + (j == 0)

            with nc.Block() as block:

                @block.sync
                def _(sp):
                    with sp.Fori(0, NB) as i:
                        sp.wait_ge(ln_free, i + 1)
                        sp.dma_start(x_ln[:, :, :], rows(x_in, i * BLK, BLK).rearrange("(t p) d -> p t d", p=P)).then_inc(ln_loaded, 16)
                        sp.wait_ge(res_free, i + 1)
                        sp.dma_start(x_res[:, :, :], rows(x_in, i * BLK, BLK).rearrange("(t p) d -> p t d", p=P)).then_inc(res_loaded, 16)

                @block.tensor
                def _(pe):
                    def turn(i):
                        pe.wait_ge(sil_done, HC * i + 2)
                        pe.wait_ge(g_done, HC * i + 2)
                        for c in range(DC):
                            bank = (h1, h3)[c // 2][:, c % 2, :]
                            for t in range(TB):
                                if c == 0:
                                    pe.wait_ge(xn_done, TB * i + t + 1)
                                mm = nc.tensor.transpose(bank[:, t * P:(t + 1) * P], xn[:, t, c * P:(c + 1) * P], keep["ident"][:, :])
                            mm.then_inc(turned, 1)

                    def down(i, j):
                        if j == 0:
                            pe.wait_ge(out_done, TB * i + TB)
                        pe.wait_ge(g_ready, HC * i + j + 1 + (0 if ternary else 2))
                        for t in range(TB):
                            for q in range(parts):
                                mm = nc.tensor.matmul(y[:, t, :], gp[q][0:HM[j], j % 2, t * P:(t + 1) * P], w2[0:HM[j], j, :],
                                                      start=j == 0 and q == 0, stop=j == HC - 1 and q == parts - 1)
                        mm.then_inc(y_step, 1)

                    def main(i):
                        pe.wait_ge(lo_done if ternary else hi_done, DC * i + DC)
                        for j in range(HC):
                            for w, h, done, used in ((w1, h1, h1_done, sil_done), (w3, h3, h3_done, g_done)):
                                pe.wait_ge(used, left(i, j))
                                n = 0
                                for c in range(DC):
                                    for q in range(parts):
                                        mm = nc.tensor.matmul(h[0:HM[j], j % 2, :], w[:, c, j * P:j * P + HM[j]], xnT[q][:, c, :],
                                                              start=n == 0, stop=n == DC * parts - 1)
                                        n += 1
                                mm.then_inc(done, 1)
                            if j >= 1:
                                down(i, j - 1)
                        down(i, HC - 1)

                    turn(0)
                    with pe.Fori(0, NB - 1) as i:
                        main(i)
                        turn(i + 1)
                    main(NB - 1)

                @block.vector
                def _(dve):
                    def norm(i):
                        dve.wait_ge(ln_loaded, 16 * i + 16)
                        for t in range(TB):
                            nc.vector.bn_stats(stats[:, t, :], x_ln[:, t, :]).then_inc(stats_done, 1)
                        hold(dve, stats_done, TB * i + TB, dve_passed)
                        for t in range(TB):
                            nc.vector.bn_aggr(mv[:, t, :], stats[:, t, :]).then_inc(var_done, 1)
                        dve.wait_ge(var_done, TB * i + TB)
                        nc.vector.tensor_scalar(ve[:, :], mv[:, :, 1], LN_EPS, None, ALU.add).then_inc(ve_done, 1)
                        dve.wait_ge(rstd_done, i + 1)
                        dve.wait_ge(turned, DC * i + 1)
                        for t in range(TB):
                            nc.vector.tensor_scalar(xn[:, t, :], x_ln[:, t, :], mv[:, t, 0:1], rstd[:, t:t + 1], ALU.subtract, ALU.mult).then_inc(xn_done, 1)
                        dve.wait_ge(xn_done, TB * i + TB)
                        dve.sem_inc(ln_free, 1)

                    def evacuate_low(i):
                        for c in range(DC):
                            dve.wait_ge(turned, DC * i + c + 2)
                            dve.wait_ge(hi_done, DC * i + c + 1)
                            nc.vector.tensor_tensor(xnT[1][:, c, :], (h1, h3)[c // 2][:, c % 2, :], xnT[0][:, c, :].bitcast(F32), ALU.subtract).then_inc(lo_done, 1)

                    def main(i, next_norm):
                        for j in range(HC):
                            m = HM[j]
                            dve.wait_ge(sil_done, HC * i + j + 3)
                            dve.wait_ge(h3_done, HC * i + j + 1)
                            if not ternary:
                                dve.wait_ge(y_step, left(i, j))
                            nc.vector.tensor_tensor(g32[0:m, j % 2, :], sil[0:m, j % 2, :], h3[0:m, j % 2, :], ALU.mult).then_inc(g_done, 1)
                            if ternary:
                                dve.wait_ge(y_step, left(i, j))
                                dve.wait_ge(ghi_done, HC * i + j + 1)
                                nc.vector.tensor_tensor(gp[1][0:m, j % 2, :], g32[0:m, j % 2, :], gp[0][0:m, j % 2, :].bitcast(F32), ALU.subtract).then_inc(glo_done, 1)
                            if j == 2 and next_norm:
                                norm(i + 1)

                    def finish(i):
                        dve.wait_ge(res_loaded, 16 * i + 16)
                        dve.wait_ge(stored, 16 * i + 16)
                        dve.wait_ge(y_step, HC * i + HC + 2)
                        for t in range(TB):
                            nc.vector.scalar_tensor_tensor(out=x_new[:, t, :], in0=y[:, t, :], scalar=out_scale[:, 0:1], in1=x_res[:, t, :],
                                                           op0=ALU.mult, op1=ALU.add).then_inc(out_done, 1)
                        dve.wait_ge(out_done, TB * i + 2 * TB)
                        dve.sem_inc(res_free, 1)

                    for sem, n in ((ln_free, 1), (res_free, 1), (out_done, TB), (turned, 1), (g_done, 2), (sil_done, 2), (y_step, 2), (stored, 16)):
                        dve.sem_inc(sem, n)
                    if ternary:
                        nc.vector.tensor_tensor(s23[:, :], scales[:, 1:2], scales[:, 2:3], ALU.mult).then_inc(scale_done, 1)
                        dve.wait_ge(scale_done, 1)
                        nc.vector.tensor_tensor(out_scale[:, :], s23[:, :], gate, ALU.mult)
                    else:
                        nc.vector.tensor_copy(out_scale[:, :], gate)
                    norm(0)
                    if ternary:
                        evacuate_low(0)
                    with dve.Fori(0, NB - 1) as i:
                        main(i, True)
                        if ternary:
                            evacuate_low(i + 1)
                        finish(i)
                    main(NB - 1, False)
                    finish(NB - 1)

                @block.gpsimd
                def _(pool):
                    with pool.Fori(0, NB) as i:
                        pool.wait_ge(ve_done, i + 1)
                        nc.gpsimd.tensor_tensor(rstd[:, :], ve[:, :], keep["neg_half"][:, 0:TB], ALU.pow).then_inc(rstd_done, 1)

                @block.scalar
                def _(act):
                    def evacuate(i):
                        for c in range(DC):
                            act.wait_ge(turned, DC * i + c + 2)
                            nc.scalar.activation(xnT[0][:, c, :], (h1, h3)[c // 2][:, c % 2, :], ACT.Copy).then_inc(hi_done, 1)

                    def main(i):
                        for j in range(HC):
                            m = HM[j]
                            act.wait_ge(h1_done, HC * i + j + 1)
                            act.wait_ge(g_done, left(i, j))
                            nc.scalar.activation(sil[0:m, j % 2, :], h1[0:m, j % 2, :], ACT.Silu, scale=scales[0:m, 0:1] if ternary else 1.0).then_inc(sil_done, 1)
                            if ternary:
                                act.wait_ge(y_step, left(i, j))
                                act.wait_ge(g_done, HC * i + j + 3)
                                nc.scalar.activation(gp[0][0:m, j % 2, :], g32[0:m, j % 2, :], ACT.Copy).then_inc(ghi_done, 1)

                    def store(i):
                        act.wait_ge(out_done, TB * i + 2 * TB)
                        act.dma_start(rows(x_out, i * BLK, BLK).rearrange("(t p) d -> p t d", p=P), x_new[:, :, :]).then_inc(stored, 16)

                    evacuate(0)
                    with act.Fori(0, NB - 1) as i:
                        main(i)
                        evacuate(i + 1)
                        store(i)
                    main(NB - 1)
                    store(NB - 1)
                    act.wait_ge(stored, 16 * NB + 16)


def build_ternary_ffn(nc, io, keep, x_in, x_out):
    build_ffn(nc, io, keep, x_in, x_out, True)


def build_lut_ffn(nc, io, keep, x_in, x_out):
    build_ffn(nc, io, keep, x_in, x_out, False)


HEADS = 16
HD = D // HEADS
FD = 64
VE = HD + 1
LB = 512
LT = LB // P


class Fills:

    def __init__(self, plan):
        self.names = [name for name, _ in plan]
        self.engine = [e for _, e in plan]
        self.count = len(plan)
        self.per = {e: self.engine.count(e) for e in ("act", "dve")}
        self.place = {name: n for n, name in enumerate(self.names)}

    def filled(self, i, name):
        return self.count * i + self.place[name] + 1

    def emptied(self, i, name):
        n = self.place[name]
        e = self.engine[n]
        return e, self.per[e] * (i + 1) + self.engine[:n].count(e) + 1

    def bank_free(self, i, name):
        n = self.place[name]
        if n >= 8:
            return self.emptied(i, self.names[n - 8])
        before = max(m for m in range(self.count) if m % 8 == n % 8)
        return self.emptied(i - 1, self.names[before])


def build_linear_attention(nc, io, keep, x_in, x_out):
    PAIRS = HEADS // 2
    EB = LB // S
    NIT = N // LB
    with ExitStack() as ctx:
        sc = Scope(nc, ctx, "lin")
        wq, wk, wv, wo = (sc.sb(n, [P, DC, D]) for n in ("wq", "wk", "wv", "wo"))
        bq, bk = (sc.sb(n, [P, DC]) for n in ("bq", "bk"))
        bv, bo = (sc.sb(n, [P, D]) for n in ("bv", "bo"))
        fmap_q = sc.sb("fmap_q", [P, 4 * FD])
        fmap_k = sc.sb("fmap_k", [P, 4 * FD])
        mask = sc.sb("mask", [P, N // P])
        x_sb = sc.sb("x", [P, LT, D])
        x_res = sc.sb("x_res", [P, LT, D])
        cT = sc.sb("cT", [P, EB, DC, S])
        xn = sc.sb("xn", [P, LT, D])
        xnT = sc.sb("xnT", [P, DC, LB])
        qT = sc.sb("qT", [P, DC, LB])
        kT = sc.sb("kT", [P, DC, LB])
        v = sc.sb("v", [P, LT, HEADS, VE])
        qf = sc.sb("qf", [P, PAIRS, LB])
        kf = sc.sb("kf", [P, LT, HEADS * FD])
        kvd = sc.sb("kvd", [P, EB, PAIRS, 2 * VE])
        den = sc.sb("den", [P, LT, HEADS])
        rden = sc.sb("rden", [P, LT, HEADS])
        att = sc.sb("att", [P, LT, D])
        attT = sc.sb("attT", [P, DC, LB])
        proj = sc.sb("proj", [P, LT, D])
        x_new = proj
        stats = sc.sb("stats", [P, LT, 6])
        mv = sc.sb("mv", [P, LT, 2])
        ve = sc.sb("ve", [P, LT])
        rstd = sc.sb("rstd", [P, LT])
        bank = sc.ps("bank", [P, 8, 512])

        weights_loaded = sc.sem("weights_loaded")
        x_loaded = sc.sem("x_loaded")
        res_loaded = sc.sem("res_loaded")
        c_loaded = sc.sem("c_loaded")
        x_free = sc.sem("x_free")
        c_free = sc.sem("c_free")
        res_free = sc.sem("res_free")
        stored = sc.sem("stored")
        stats_done = sc.sem("stats_done")
        var_done = sc.sem("var_done")
        ve_done = sc.sem("ve_done")
        rstd_done = sc.sem("rstd_done")
        xn_done = sc.sem("xn_done")
        setup_done = sc.sem("setup_done")
        filled = sc.sem("filled")
        emptied = {"act": sc.sem("act_emptied"), "dve": sc.sem("dve_emptied")}
        den_done = sc.sem("den_done")
        rden_done = sc.sem("rden_done")
        add_done = sc.sem("add_done")
        out_done = sc.sem("out_done")
        passed = sc.sem("passed")
        pe_passed = sc.sem("pe_passed")

        plan = Fills([(("kT", o), "act") for o in range(DC)] + [(("v", t), "dve") for t in range(LT)] + [(("xnT", c), "act") for c in range(DC)]
                     + [(("qT", o), "act") for o in range(DC)] + [(("kf", t, h), "dve") for t in range(LT) for h in range(2)]
                     + [(("qf", p), "act") for p in range(PAIRS)] + [(("kv", e, h), "act") for e in range(EB) for h in range(2)]
                     + [(("att", t, h), "dve") for t in range(LT) for h in range(2)] + [(("attT", c), "act") for c in range(DC)]
                     + [(("out", t), "dve") for t in range(LT)])

        def at(name):
            return bank[:, plan.place[name] % 8, :]

        def wait_emptied(eng, i, *names):
            for name in names:
                e, value = plan.emptied(i, name)
                eng.wait_ge(emptied[e], value)

        with nc.Block() as block:

            @block.sync
            def _(sp):
                for w, n in ((wq, "wq"), (wk, "wk"), (wv, "wv"), (wo, "wo")):
                    sp.dma_start(w[:, :, :], io[n].rearrange("p (c o) -> p c o", c=DC)).then_inc(weights_loaded, 16)
                for w, n in ((bq, "bq"), (bk, "bk")):
                    sp.dma_start(w[:, :], io[n]).then_inc(weights_loaded, 16)
                for w, n in ((bv, "bv"), (bo, "bo")):
                    sp.dma_start(w[:, :], io[n].broadcast_to([P, D])).then_inc(weights_loaded, 16)
                sp.dma_start(mask[:, :], io["mask"]).then_inc(weights_loaded, 16)
                sp.wait_ge(setup_done, 4)
                for m, n in ((fmap_q, "wqf"), (fmap_k, "wkf")):
                    for h in range(4):
                        sp.dma_start(m[h * HD:(h + 1) * HD, h * FD:(h + 1) * FD], io[n]).then_inc(weights_loaded, 16)
                with sp.Fori(0, NIT) as i:
                    sp.wait_ge(c_free, i + 1)
                    sp.dma_start(cT[:, :, :, :], io["ctxT"][bass.ds(EB * i, EB)].rearrange("b p c s -> p b c s")).then_inc(c_loaded, 16)
                    sp.wait_ge(x_free, i + 1)
                    sp.dma_start(x_sb[:, :, :], rows(x_in, i * LB, LB).rearrange("(t p) d -> p t d", p=P)).then_inc(x_loaded, 16)
                    sp.wait_ge(res_free, i + 1)
                    sp.dma_start(x_res[:, :, :], rows(x_in, i * LB, LB).rearrange("(t p) d -> p t d", p=P)).then_inc(res_loaded, 16)

            @block.tensor
            def _(pe):
                def begin(i, name):
                    e, value = plan.bank_free(i, name)
                    pe.wait_ge(emptied[e], value)
                    return at(name)

                def projection(i, name, lhsT, rhs):
                    out = begin(i, name)
                    for c in range(DC):
                        mm = nc.tensor.matmul(out, lhsT(c), rhs(c), start=c == 0, stop=c == DC - 1)
                    mm.then_inc(filled, 1)

                pe.wait_ge(weights_loaded, 16 * 17)
                pe.wait_ge(setup_done, 6)
                with pe.Fori(0, NIT) as i:
                    pe.wait_ge(c_loaded, 16 * i + 16)
                    for o in range(DC):
                        projection(i, ("kT", o), lambda c: wk[:, c, o * P:(o + 1) * P], lambda c: cT[:, :, c, :])
                    for t in range(LT):
                        projection(i, ("v", t), lambda c: cT[:, t // 2, c, (t % 2) * P:(t % 2 + 1) * P], lambda c: wv[:, c, :])
                    pe.wait_ge(xn_done, LT * i + LT)
                    for c in range(DC):
                        out = begin(i, ("xnT", c))
                        for t in range(LT):
                            mm = nc.tensor.transpose(out[:, t * P:(t + 1) * P], xn[:, t, c * P:(c + 1) * P], keep["ident"][:, :])
                        mm.then_inc(filled, 1)
                    wait_emptied(pe, i, ("xnT", DC - 1))
                    for o in range(DC):
                        projection(i, ("qT", o), lambda c: wq[:, c, o * P:(o + 1) * P], lambda c: xnT[:, c, :])
                    wait_emptied(pe, i, ("kT", DC - 1))
                    for t in range(LT):
                        for h in range(2):
                            out = begin(i, ("kf", t, h))
                            for q in range(2):
                                mm = nc.tensor.matmul(out[:, q * 256:(q + 1) * 256], kT[:, 2 * h + q, t * P:(t + 1) * P], fmap_k[:, :], start=True, stop=True)
                            mm.then_inc(filled, 1)
                    for p in range(PAIRS):
                        wait_emptied(pe, i, ("qT", p // 2))
                        out = begin(i, ("qf", p))
                        nc.tensor.matmul(out, fmap_q[:, (p % 2) * P:(p % 2 + 1) * P], qT[:, p // 2, :], start=True, stop=True).then_inc(filled, 1)
                    for e in range(EB):
                        wait_emptied(pe, i, ("v", LT - 1), ("kf", 2 * e + 1, 1))
                        for h in range(2):
                            out = begin(i, ("kv", e, h))
                            for q in range(4):
                                p = 4 * h + q
                                for t in (2 * e, 2 * e + 1):
                                    mm = nc.tensor.matmul(out[:, q * 2 * VE:(q + 1) * 2 * VE], kf[:, t, p * P:(p + 1) * P],
                                                          v[:, t, 2 * p:2 * p + 2, :].rearrange("p h e -> p (h e)"), start=t == 2 * e, stop=t == 2 * e + 1)
                            mm.then_inc(filled, 1)
                    for t in range(LT):
                        wait_emptied(pe, i, ("kv", t // 2, 1), ("qf", PAIRS - 1))
                        for h in range(2):
                            out = begin(i, ("att", t, h))
                            for q in range(4):
                                p = 4 * h + q
                                mm = nc.tensor.matmul(out[:, q * 2 * VE:(q + 1) * 2 * VE], qf[:, p, t * P:(t + 1) * P], kvd[:, t // 2, p, :], start=True, stop=True)
                            mm.then_inc(filled, 1)
                    wait_emptied(pe, i, ("att", LT - 1, 1))
                    for c in range(DC):
                        out = begin(i, ("attT", c))
                        for t in range(LT):
                            mm = nc.tensor.transpose(out[:, t * P:(t + 1) * P], att[:, t, c * P:(c + 1) * P], keep["ident"][:, :])
                        mm.then_inc(filled, 1)
                    wait_emptied(pe, i, ("attT", DC - 1))
                    for t in range(LT):
                        projection(i, ("out", t), lambda c: attT[:, c, t * P:(t + 1) * P], lambda c: wo[:, c, :])

            @block.scalar
            def _(act):
                def evacuate(i, name, out, func, bias=0.0, src=None, inc=True):
                    act.wait_ge(filled, plan.filled(i, name))
                    ins = nc.scalar.activation(out, at(name) if src is None else src, func, bias=bias)
                    if inc:
                        ins.then_inc(emptied["act"], 1)

                act.sem_inc(emptied["act"], plan.per["act"])
                act.wait_ge(weights_loaded, 16 * 17)
                with act.Fori(0, NIT) as i:
                    for o in range(DC):
                        evacuate(i, ("kT", o), kT[:, o, :], ACT.Identity, bk[:, o:o + 1])
                    for c in range(DC):
                        evacuate(i, ("xnT", c), xnT[:, c, :], ACT.Identity)
                    for o in range(DC):
                        evacuate(i, ("qT", o), qT[:, o, :], ACT.Identity, bq[:, o:o + 1])
                    for p in range(PAIRS):
                        evacuate(i, ("qf", p), qf[:, p, :], ACT.Relu)
                    for e in range(EB):
                        for h in range(2):
                            for r in range(2):
                                src = at(("kv", e, h))[r * FD:(r + 1) * FD, 0:4 * 2 * VE].rearrange("p (q w) -> p q w", q=4)[:, :, r * VE:(r + 1) * VE]
                                evacuate(i, ("kv", e, h), kvd[r * FD:(r + 1) * FD, e, 4 * h:4 * h + 4, r * VE:(r + 1) * VE], ACT.Identity, src=src, inc=r == 1)
                    for c in range(DC):
                        evacuate(i, ("attT", c), attT[:, c, :], ACT.Identity)
                    act.wait_ge(out_done, LT * i + 2 * LT)
                    act.dma_start(rows(x_out, i * LB, LB).rearrange("(t p) d -> p t d", p=P), x_new[:, :, :]).then_inc(stored, 16)
                act.wait_ge(stored, 16 * NIT + 16)

            @block.vector
            def _(dve):
                def norm(i):
                    dve.wait_ge(x_loaded, 16 * i + 16)
                    for t in range(LT):
                        nc.vector.bn_stats(stats[:, t, :], x_sb[:, t, :]).then_inc(stats_done, 1)
                    hold(dve, stats_done, LT * i + LT, passed)
                    for t in range(LT):
                        nc.vector.bn_aggr(mv[:, t, :], stats[:, t, :]).then_inc(var_done, 1)
                    dve.wait_ge(var_done, LT * i + LT)
                    nc.vector.tensor_scalar(ve[:, :], mv[:, :, 1], LN_EPS, None, ALU.add).then_inc(ve_done, 1)
                    dve.wait_ge(rstd_done, i + 1)
                    for t in range(LT):
                        nc.vector.tensor_scalar(xn[:, t, :], x_sb[:, t, :], mv[:, t, 0:1], rstd[:, t:t + 1], ALU.subtract, ALU.mult).then_inc(xn_done, 1)
                    dve.wait_ge(xn_done, LT * i + LT)
                    dve.sem_inc(x_free, 1)

                def main(i, next_norm):
                    for t in range(LT):
                        dve.wait_ge(filled, plan.filled(i, ("v", t)))
                        nc.vector.tensor_tensor(v[:, t, :, 0:HD], at(("v", t)).rearrange("p (h e) -> p h e", h=HEADS),
                                                bv[:, :].rearrange("p (h e) -> p h e", h=HEADS), ALU.add).then_inc(emptied["dve"], 1)
                    dve.sem_inc(c_free, 1)
                    for t in range(LT):
                        for h in range(2):
                            dve.wait_ge(filled, plan.filled(i, ("kf", t, h)))
                            nc.vector.tensor_scalar(kf[:, t, h * 512:(h + 1) * 512], at(("kf", t, h)), 0.0, mask[:, bass.ds(LT * i + t, 1)], ALU.max, ALU.mult)\
                                .then_inc(emptied["dve"], 1)
                    if next_norm:
                        norm(i + 1)
                    for t in range(LT):
                        for h in range(2):
                            n = 2 * LT * i + 2 * t + h + 1
                            src = at(("att", t, h))[:, 0:8 * VE].rearrange("p (h e) -> p h e", h=8)
                            dve.wait_ge(filled, plan.filled(i, ("att", t, h)))
                            nc.vector.tensor_scalar(den[:, t, 8 * h:8 * h + 8], src[:, :, HD], 1e-8, None, ALU.add).then_inc(den_done, 1)
                            dve.wait_ge(den_done, n)
                            nc.vector.reciprocal(rden[:, t, 8 * h:8 * h + 8], den[:, t, 8 * h:8 * h + 8]).then_inc(rden_done, 1)
                            dve.wait_ge(rden_done, n)
                            nc.vector.tensor_tensor(att[:, t, h * 256:(h + 1) * 256].rearrange("p (h e) -> p h e", h=8), src[:, :, 0:HD],
                                                    rden[:, t, 8 * h:8 * h + 8].rearrange("p (h e) -> p h e", e=1).broadcast_to([P, 8, HD]), ALU.mult).then_inc(emptied["dve"], 1)
                    dve.wait_ge(stored, 16 * i + 16)
                    dve.wait_ge(res_loaded, 16 * i + 16)
                    for t in range(LT):
                        dve.wait_ge(filled, plan.filled(i, ("out", t)))
                        nc.vector.tensor_tensor(proj[:, t, :], at(("out", t)), bo[:, :], ALU.add).then_inc(emptied["dve"], 1)
                        dve.wait_ge(*(emptied["dve"], plan.emptied(i, ("out", t))[1]))
                        nc.vector.scalar_tensor_tensor(out=x_new[:, t, :], in0=proj[:, t, :], scalar=keep["gates"][:, 1:2], in1=x_res[:, t, :],
                                                       op0=ALU.mult, op1=ALU.add).then_inc(out_done, 1)
                    dve.wait_ge(out_done, LT * i + 2 * LT)
                    dve.sem_inc(res_free, 1)

                for sem, n in ((c_free, 1), (x_free, 1), (res_free, 1), (out_done, LT), (stored, 16), (emptied["dve"], plan.per["dve"])):
                    dve.sem_inc(sem, n)
                nc.vector.memset(fmap_q[0:64, :], 0.0).then_inc(setup_done, 1)
                nc.vector.memset(fmap_q[64:128, :], 0.0).then_inc(setup_done, 1)
                nc.vector.memset(fmap_k[0:64, :], 0.0).then_inc(setup_done, 1)
                nc.vector.memset(fmap_k[64:128, :], 0.0).then_inc(setup_done, 1)
                nc.vector.memset(kvd[:, :, :, :], 0.0).then_inc(setup_done, 1)
                nc.vector.memset(v[:, :, :, HD:VE], 1.0).then_inc(setup_done, 1)
                dve.wait_ge(weights_loaded, 16 * 17)
                norm(0)
                with dve.Fori(0, NIT - 1) as i:
                    main(i, True)
                main(NIT - 1, False)

            @block.gpsimd
            def _(pool):
                with pool.Fori(0, NIT) as i:
                    pool.wait_ge(ve_done, i + 1)
                    nc.gpsimd.tensor_tensor(rstd[:, :], ve[:, :], keep["neg_half"][:, 0:LT], ALU.pow).then_inc(rstd_done, 1)


CAP = 256


class Routing:

    def __init__(self, nc, sc, name, experts, topk, slots, spare):
        self.nc, self.name, self.experts, self.topk, self.slots = nc, name, experts, topk, slots
        NT = N // P
        self.slot_of = sc.sb("slot_of", [P, NT, topk], U32)
        self.weight = sc.sb("weight", [P, NT, topk])
        self.xn = nc.dram_tensor(f"{name}_xn", [N, D], F32, kind="Internal").ap()
        self.token_of = nc.dram_tensor(f"{name}_token_of", [slots + spare, 1], I32, kind="Internal").ap()
        self.y = nc.dram_tensor(f"{name}_y", [slots, D], F32, kind="Internal").ap()


def build_route(nc, io, keep, x_in, x_mid, r, shared, gate, late):
    E, K = r.experts, r.topk
    (n1, n3, n2), hidden, split = shared
    SC = -(-hidden // P)
    HM = [min(P, hidden - P * j) for j in range(SC)]
    parts = 2 if split else 1
    WDT = F32R if split else F32
    with ExitStack() as ctx:
        sc = Scope(nc, ctx, r.name + "_route")
        w1 = sc.sb("w1", [P, DC, hidden], WDT)
        w3 = sc.sb("w3", [P, DC, hidden], WDT)
        w2 = sc.sb("w2", [P, SC, D], WDT)
        raw = [sc.sb("w1b", [P, DC, hidden], BF16), sc.sb("w3b", [P, DC, hidden], BF16), sc.sb("w2b", [P, SC, D], BF16)] if split else [w1, w3, w2]
        wg = sc.sb("wg", [P, DC, E])
        bias = sc.sb("bias", [P, E])
        x_ln = sc.sb("x_ln", [P, TB, D])
        x_res = sc.sb("x_res", [P, TB, D])
        x_new = sc.sb("x_new", [P, TB, D])
        xn = sc.sb("xn", [P, TB, D])
        xnT = sc.sb("xnT", [P, DC, BLK])
        xp = [sc.sb(f"x_part{q}", [P, DC, BLK], WDT) for q in range(parts)] if split else [xnT]
        g32 = sc.sb("g32", [P, SC, BLK])
        gp = [sc.sb(f"g_part{q}", [P, SC, BLK], WDT) for q in range(parts)] if split else [g32]
        sil = sc.sb("sil", [P, SC, BLK])
        stats = sc.sb("stats", [P, TB, 6])
        mv = sc.sb("mv", [P, TB, 2])
        ve = sc.sb("ve", [P, TB])
        rstd = sc.sb("rstd", [P, TB])
        score = sc.sb("score", [P, TB, E])
        biased = sc.sb("biased", [P, TB, E]) if late else score
        tmp1 = sc.sb("tmp1", [P, TB, E])
        tmp2 = sc.sb("tmp2", [P, TB, E])
        top = sc.sb("top", [P, TB, 8])
        top_at = sc.sb("top_at", [P, TB, 8], U32)
        idx = sc.sb("idx", [P, TB, 8])
        chosen = sc.sb("chosen", [P, TB, E], BF16)
        before = sc.sb("before", [P, E], BF16)
        pos = sc.sb("pos", [P, TB, K])
        junk = sc.sb("junk", [P, 2, E])
        decay = sc.sb("decay", [P, TB, E])
        wraw = sc.sb("wraw", [P, TB, K])
        wsum = sc.sb("wsum", [P, TB])
        wrec = sc.sb("wrec", [P, TB])
        valid = sc.sb("valid", [P, TB, K])
        wnorm = sc.sb("wnorm", [P, TB, K])
        posc = sc.sb("posc", [P, TB, K])
        slotf = sc.sb("slotf", [P, TB, K])
        slotd = sc.sb("slotd", [P, TB, K])
        slot_now = sc.sb("slot_now", [P, TB, K], U32)
        token_now = sc.sb("token_now", [P, TB], I32)
        turn = sc.ps("turn", [P, 2, BLK])
        h = sc.ps("h", [P, 2, BLK])
        y = sc.ps("y", [P, 2, D])
        logits = sc.ps("logits", [P, TB, P])
        places = sc.ps("places", [P, TB, P])

        names = ("w_loaded raw_done ln_loaded res_loaded ln_free res_free xn_stored stored stats_done var_done ve_done rstd_done xn_done turned "
                 "xnT_done hi_done lo_done logits_done h1_done h3_done sil_done g_done ghi_done glo_done y_done out_done abs_done exp_done ln_done "
                 "soft_done score_done biased_done top_done top_at_done idx_done chosen_done init_done places_done pos_done weight_done "
                 "before_done before_step small_done slots_ready slots_free scattered passed pool_passed").split()
        s = {n: sc.sem(n) for n in names}

        with nc.Block() as block:

            @block.sync
            def _(sp):
                for w, n in zip(raw, (n1, n3, n2)):
                    sp.dma_start(w[:, :, :], io[n].rearrange("p (c h) -> p c h", c=w.shape[1])).then_inc(s["w_loaded"], 16)
                sp.dma_start(wg[:, :, :], io[r.name + "_wg"].rearrange("p (c e) -> p c e", c=DC)).then_inc(s["w_loaded"], 16)
                if late:
                    sp.dma_start(bias[:, :], io[r.name + "_bias"].broadcast_to([P, E])).then_inc(s["w_loaded"], 16)
                rows_total = r.token_of.shape[0]
                sp.wait_ge(s["init_done"], 1)
                sp.dma_start(r.token_of.rearrange("(p c) a -> p (c a)", p=P), keep["zeros_i"][:, 0:rows_total // P]).then_inc(s["w_loaded"], 16)
                with sp.Fori(0, NB) as i:
                    sp.wait_ge(s["ln_free"], i + 1)
                    sp.dma_start(x_ln[:, :, :], rows(x_in, i * BLK, BLK).rearrange("(t p) d -> p t d", p=P)).then_inc(s["ln_loaded"], 16)
                    sp.wait_ge(s["res_free"], i + 1)
                    sp.dma_start(x_res[:, :, :], rows(x_in, i * BLK, BLK).rearrange("(t p) d -> p t d", p=P)).then_inc(s["res_loaded"], 16)
                    sp.wait_ge(s["xn_done"], TB * i + TB)
                    sp.dma_start(rows(r.xn, i * BLK, BLK).rearrange("(t p) d -> p t d", p=P), xn[:, :, :]).then_inc(s["xn_stored"], 16)
                sp.wait_ge(s["xn_stored"], 16 * NB + 16)

            NW = 16 * (6 if late else 5)

            @block.tensor
            def _(pe):
                pe.wait_ge(s["w_loaded"], NW)
                if split:
                    pe.wait_ge(s["raw_done"], 3)
                pe.wait_ge(s["init_done"], 1)
                with pe.Fori(0, NB) as i:
                    pe.wait_ge(s["xn_done"], TB * i + TB)
                    for c in range(DC):
                        pe.wait_ge(s["xnT_done"], DC * i + c + 1)
                        if split:
                            pe.wait_ge(s["hi_done"], DC * i + c + 1)
                        for t in range(TB):
                            mm = nc.tensor.transpose(turn[:, c % 2, t * P:(t + 1) * P], xn[:, t, c * P:(c + 1) * P], keep["ident"][:, :])
                        mm.then_inc(s["turned"], 1)
                    pe.wait_ge(s["xnT_done"], DC * i + DC + 2)
                    pe.wait_ge(s["score_done"], i + 1)
                    for t in range(TB):
                        for c in range(DC):
                            mm = nc.tensor.matmul(logits[:, t, 0:E], xnT[:, c, t * P:(t + 1) * P], wg[:, c, :], start=c == 0, stop=c == DC - 1)
                    mm.then_inc(s["logits_done"], 1)
                    if split:
                        pe.wait_ge(s["lo_done"], DC * i + DC)
                    for j in range(SC):
                        m = HM[j]
                        for which, w, done, used in ((0, w1, "h1_done", "sil_done"), (1, w3, "h3_done", "g_done")):
                            pe.wait_ge(s[used], SC * i + j + 1)
                            n = 0
                            for c in range(DC):
                                for q in range(parts):
                                    mm = nc.tensor.matmul(h[0:m, which, :], w[:, c, j * P:j * P + m], xp[q][:, c, :], start=n == 0, stop=n == DC * parts - 1)
                                    n += 1
                            mm.then_inc(s[done], 1)
                    for t in range(TB):
                        pe.wait_ge(s["out_done"], TB * i + t + 1)
                        n = 0
                        for j in range(SC):
                            pe.wait_ge(s["glo_done" if split else "g_done"], SC * i + j + 1 + (0 if split else 1))
                            for q in range(parts):
                                mm = nc.tensor.matmul(y[:, t % 2, :], gp[q][0:HM[j], j, t * P:(t + 1) * P], w2[0:HM[j], j, :], start=n == 0, stop=n == SC * parts - 1)
                                n += 1
                        mm.then_inc(s["y_done"], 1)
                    pe.wait_ge(s["pos_done"], TB * K * i + 1)
                    for t in range(TB):
                        pe.wait_ge(s["chosen_done"], TB * i + t + 1)
                        pe.wait_ge(s["before_done"], i + 1)
                        nc.tensor.matmul(places[:, t, 0:E], keep["ones_bf"][:, :], before[:, :], start=True, stop=False)
                        for e in range(t):
                            nc.tensor.matmul(places[:, t, 0:E], keep["ones_bf"][:, :], chosen[:, e, :], start=False, stop=False)
                        mm = nc.tensor.matmul(places[:, t, 0:E], keep["earlier"][:, :], chosen[:, t, :], start=False, stop=True)
                    mm.then_inc(s["places_done"], 1)

            @block.vector
            def _(dve):
                def norm(i):
                    dve.wait_ge(s["ln_loaded"], 16 * i + 16)
                    for t in range(TB):
                        nc.vector.bn_stats(stats[:, t, :], x_ln[:, t, :]).then_inc(s["stats_done"], 1)
                    hold(dve, s["stats_done"], TB * i + TB, s["passed"])
                    for t in range(TB):
                        nc.vector.bn_aggr(mv[:, t, :], stats[:, t, :]).then_inc(s["var_done"], 1)
                    dve.wait_ge(s["var_done"], TB * i + TB)
                    nc.vector.tensor_scalar(ve[:, :], mv[:, :, 1], LN_EPS, None, ALU.add).then_inc(s["ve_done"], 1)
                    dve.wait_ge(s["rstd_done"], i + 1)
                    dve.wait_ge(s["turned"], DC * i + 1)
                    dve.wait_ge(s["xn_stored"], 16 * i + 16)
                    for t in range(TB):
                        nc.vector.tensor_scalar(xn[:, t, :], x_ln[:, t, :], mv[:, t, 0:1], rstd[:, t:t + 1], ALU.subtract, ALU.mult).then_inc(s["xn_done"], 1)
                    dve.wait_ge(s["xn_done"], TB * i + TB)
                    dve.sem_inc(s["ln_free"], 1)

                def hidden_product(i, j):
                    m = HM[j]
                    dve.wait_ge(s["sil_done"], SC * i + j + 2)
                    dve.wait_ge(s["h3_done"], SC * i + j + 1)
                    if j == 0:
                        dve.wait_ge(s["y_done"], TB * i + 1)
                    nc.vector.tensor_tensor(g32[0:m, j, :], sil[0:m, j, :], h[0:m, 1, :], ALU.mult).then_inc(s["g_done"], 1)
                    if split:
                        dve.wait_ge(s["ghi_done"], SC * i + j + 1)
                        nc.vector.tensor_tensor(gp[1][0:m, j, :], g32[0:m, j, :], gp[0][0:m, j, :].bitcast(F32), ALU.subtract).then_inc(s["glo_done"], 1)

                def choose(i):
                    if late:
                        dve.wait_ge(s["ln_done"], i + 1)
                        nc.vector.scalar_tensor_tensor(out=tmp1[:, :, :], in0=logits[:, :, 0:E], scalar=0.0, in1=tmp2[:, :, :], op0=ALU.max, op1=ALU.add).then_inc(s["soft_done"], 1)
                        dve.wait_ge(s["score_done"], i + 2)
                        for t in range(TB):
                            nc.vector.tensor_tensor(biased[:, t, :], score[:, t, :], bias[:, :], ALU.add).then_inc(s["biased_done"], 1)
                    ready = (s["biased_done"], TB * i + TB) if late else (s["score_done"], i + 2)
                    hold(dve, *ready, s["passed"])
                    for t in range(TB):
                        nc.vector.max(top[:, t, :], biased[:, t, :]).then_inc(s["top_done"], 1)
                    hold(dve, s["top_done"], TB * i + TB, s["passed"])
                    for t in range(TB):
                        nc.vector.max_index(top_at[:, t, :], top[:, t, :], biased[:, t, :]).then_inc(s["top_at_done"], 1)
                    dve.wait_ge(s["top_at_done"], TB * i + TB)
                    nc.vector.tensor_copy(idx[:, :, :], top_at[:, :, :]).then_inc(s["idx_done"], 1)
                    dve.wait_ge(s["idx_done"], i + 1)
                    for k in range(K):
                        for t in range(TB):
                            n = TB * K * i + TB * k + t
                            dve.wait_ge(s["small_done"], n + 1)
                            if k == 0:
                                nc.vector.tensor_scalar(chosen[:, t, :], keep["iota"][:, 0:E], idx[:, t, 0:1], None, ALU.is_equal).then_inc(s["small_done"], 1)
                            else:
                                ins = nc.vector.scalar_tensor_tensor(out=chosen[:, t, :], in0=keep["iota"][:, 0:E], scalar=idx[:, t, k:k + 1], in1=chosen[:, t, :],
                                                                     op0=ALU.is_equal, op1=ALU.add).then_inc(s["small_done"], 1)
                                if k == K - 1:
                                    dve.wait_ge(s["small_done"], n + TB + 1)
                                    dve.sem_inc(s["chosen_done"], 1)

                def place(i):
                    dve.wait_ge(s["places_done"], i + 1)
                    for t in range(TB):
                        for k in range(K):
                            n = TB * K * i + K * t + k
                            dve.wait_ge(s["pos_done"], n + 1)
                            nc.vector.scalar_tensor_tensor(out=junk[:, 0, :], in0=keep["iota"][:, 0:E], scalar=idx[:, t, k:k + 1], in1=places[:, t, 0:E],
                                                           op0=ALU.is_equal, op1=ALU.mult, accum_out=pos[:, t, k:k + 1]).then_inc(s["pos_done"], 1)
                            if late:
                                dve.wait_ge(s["weight_done"], n + 1)
                                nc.vector.scalar_tensor_tensor(out=junk[:, 1, :], in0=keep["iota"][:, 0:E], scalar=idx[:, t, k:k + 1], in1=score[:, t, :],
                                                               op0=ALU.is_equal, op1=ALU.mult, accum_out=wraw[:, t, k:k + 1]).then_inc(s["weight_done"], 1)
                    dve.wait_ge(s["pos_done"], TB * K * (i + 1) + 1)
                    for t in range(TB):
                        last = t == TB - 1
                        nc.vector.tensor_tensor(before[:, :], before[:, :], chosen[:, t, :], ALU.add).then_inc(s["before_step"], 1)
                        dve.wait_ge(s["before_step"], TB * i + t + 1)
                        if last:
                            dve.sem_inc(s["before_done"], 1)
                    ti = bass.ds(TB * i, TB)
                    step = [0]

                    def then(ins):
                        step[0] += 1
                        ins.then_inc(s["slots_ready"], 1)
                        dve.wait_ge(s["slots_ready"], per_block * i + step[0])

                    def over_k(ap):
                        return ap.rearrange("p (t k) -> p t k", k=1).broadcast_to([P, TB, K])

                    if late:
                        per_block = 3
                        then(nc.vector.tensor_copy(late["idx"][:, ti, :], idx[:, :, 0:K]))
                        then(nc.vector.tensor_copy(late["pos"][:, ti, :], pos[:, :, :]))
                        dve.wait_ge(s["weight_done"], TB * K * (i + 1) + 1)
                        then(nc.vector.tensor_scalar(r.weight[:, ti, :], wraw[:, :, :], gate, None, ALU.mult))
                    else:
                        per_block = 11
                        then(nc.vector.tensor_reduce(wsum[:, :], top[:, :, 0:K], AX.X, ALU.add))
                        then(nc.vector.reciprocal(wrec[:, :], wsum[:, :]))
                        then(nc.vector.tensor_tensor(wnorm[:, :, :], top[:, :, 0:K], over_k(wrec[:, :]), ALU.mult))
                        then(nc.vector.tensor_scalar(valid[:, :, :], pos[:, :, :], float(CAP), None, ALU.is_lt))
                        then(nc.vector.scalar_tensor_tensor(out=r.weight[:, ti, :], in0=wnorm[:, :, :], scalar=gate, in1=valid[:, :, :], op0=ALU.mult, op1=ALU.mult))
                        then(nc.vector.tensor_scalar(posc[:, :, :], pos[:, :, :], float(CAP - 1), None, ALU.min))
                        then(nc.vector.scalar_tensor_tensor(out=slotf[:, :, :], in0=idx[:, :, 0:K], scalar=float(CAP), in1=posc[:, :, :], op0=ALU.mult, op1=ALU.add))
                        then(nc.vector.tensor_copy(r.slot_of[:, ti, :], slotf[:, :, :]))
                        then(nc.vector.scalar_tensor_tensor(out=slotd[:, :, :], in0=slotf[:, :, :], scalar=keep["spare"][:, 0:1], in1=valid[:, :, :], op0=ALU.subtract, op1=ALU.mult))
                        dve.wait_ge(s["slots_free"], i + 1)
                        then(nc.vector.tensor_copy(token_now[:, :], keep["row_id"][:, ti]))
                        then(nc.vector.tensor_scalar(slot_now[:, :, :], slotd[:, :, :], keep["spare"][:, 0:1], None, ALU.add))

                def finish(i):
                    dve.wait_ge(s["res_loaded"], 16 * i + 16)
                    dve.wait_ge(s["stored"], 16 * i + 16)
                    for t in range(TB):
                        dve.wait_ge(s["y_done"], TB * i + t + 2)
                        nc.vector.scalar_tensor_tensor(out=x_new[:, t, :], in0=y[:, t % 2, :], scalar=gate, in1=x_res[:, t, :], op0=ALU.mult, op1=ALU.add).then_inc(s["out_done"], 1)
                    dve.wait_ge(s["out_done"], TB * i + TB + 2)
                    dve.sem_inc(s["res_free"], 1)

                def main(i, next_norm):
                    if split:
                        for c in range(DC):
                            dve.wait_ge(s["hi_done"], DC * i + c + 1 + 2)
                            dve.wait_ge(s["xnT_done"], DC * i + c + 1 + 2)
                            nc.vector.tensor_tensor(xp[1][:, c, :], xnT[:, c, :], xp[0][:, c, :].bitcast(F32), ALU.subtract).then_inc(s["lo_done"], 1)
                    hidden_product(i, 0)
                    choose(i)
                    for j in range(1, SC):
                        hidden_product(i, j)
                    if next_norm:
                        norm(i + 1)
                    finish(i)
                    place(i)

                for name, n in (("ln_free", 1), ("res_free", 1), ("xn_stored", 16), ("stored", 16), ("turned", 1), ("out_done", 2), ("y_done", 1),
                                ("g_done", 1), ("sil_done", 1), ("small_done", TB), ("pos_done", 1), ("weight_done", 1), ("slots_free", 1)):
                    dve.sem_inc(s[name], n)
                nc.vector.memset(before[:, :], 0.0).then_inc(s["before_done"], 1)
                dve.sem_inc(s["init_done"], 1)
                dve.wait_ge(s["before_done"], 1)
                dve.wait_ge(s["w_loaded"], NW)
                if split:
                    for src, dst in zip(raw, (w1, w3, w2)):
                        nc.vector.tensor_copy(dst[:, :, :], src[:, :, :]).then_inc(s["raw_done"], 1)
                norm(0)
                with dve.Fori(0, NB - 1) as i:
                    main(i, True)
                main(NB - 1, False)
                if late:
                    dve.wait_ge(s["before_done"], NB + 1)
                    nc.vector.tensor_copy(late["counts"][:, :], before[:, :])

            @block.scalar
            def _(act):
                act.sem_inc(s["xnT_done"], 2)
                act.sem_inc(s["hi_done"], 2)
                if not late:
                    act.sem_inc(s["score_done"], 1)
                with act.Fori(0, NB) as i:
                    for c in range(DC):
                        act.wait_ge(s["turned"], DC * i + c + 2)
                        nc.scalar.activation(xnT[:, c, :], turn[:, c % 2, :], ACT.Copy).then_inc(s["xnT_done"], 1)
                        if split:
                            nc.scalar.activation(xp[0][:, c, :], turn[:, c % 2, :], ACT.Copy).then_inc(s["hi_done"], 1)
                    act.wait_ge(s["logits_done"], i + 1)
                    if late:
                        act.wait_ge(s["soft_done"], i + 1)
                        nc.scalar.activation(tmp2[:, :, :], logits[:, :, 0:E], ACT.Abs).then_inc(s["abs_done"], 1)
                        act.wait_ge(s["abs_done"], i + 1)
                        nc.scalar.activation(decay[:, :, :], tmp2[:, :, :], ACT.Exp, scale=-1.0).then_inc(s["exp_done"], 1)
                        act.wait_ge(s["exp_done"], i + 1)
                        nc.scalar.activation(tmp2[:, :, :], decay[:, :, :], ACT.Ln, bias=1.0).then_inc(s["ln_done"], 1)
                    else:
                        act.wait_ge(s["pos_done"], TB * K * i + 1)
                        nc.scalar.activation(score[:, :, :], logits[:, :, 0:E], ACT.Sigmoid).then_inc(s["score_done"], 1)
                    for j in range(SC):
                        m = HM[j]
                        act.wait_ge(s["h1_done"], SC * i + j + 1)
                        act.wait_ge(s["g_done"], SC * i + j + 1)
                        nc.scalar.activation(sil[0:m, j, :], h[0:m, 0, :], ACT.Silu).then_inc(s["sil_done"], 1)
                        if split:
                            act.wait_ge(s["g_done"], SC * i + j + 2)
                            nc.scalar.activation(gp[0][0:m, j, :], g32[0:m, j, :], ACT.Copy).then_inc(s["ghi_done"], 1)
                    act.wait_ge(s["out_done"], TB * i + TB + 2)
                    act.dma_start(rows(x_mid, i * BLK, BLK).rearrange("(t p) d -> p t d", p=P), x_new[:, :, :]).then_inc(s["stored"], 16)
                act.wait_ge(s["stored"], 16 * NB + 16)

            @block.gpsimd
            def _(pool):
                def root(i):
                    pool.wait_ge(s["ve_done"], i + 1)
                    nc.gpsimd.tensor_tensor(rstd[:, :], ve[:, :], keep["neg_half"][:, 0:TB], ALU.pow).then_inc(s["rstd_done"], 1)

                def square_root(i):
                    pool.wait_ge(s["weight_done"], TB * K * i + 1)
                    pool.wait_ge(s["soft_done"], i + 2)
                    nc.gpsimd.tensor_tensor(score[:, :, :], tmp1[:, :, :], keep["half"][:, :].rearrange("p (t e) -> p t e", t=TB), ALU.pow).then_inc(s["score_done"], 1)

                def scatter(i):
                    hold(pool, s["slots_ready"], 11 * i + 11, s["pool_passed"])
                    for t in range(TB):
                        for k in range(K):
                            nc.gpsimd.indirect_dma_start(out=r.token_of, out_offset=bass.IndirectOffsetOnAxis(ap=slot_now[:, t, k:k + 1], axis=0),
                                                         in_=token_now[:, t:t + 1], in_offset=None).then_inc(s["scattered"], 16)
                    pool.wait_ge(s["scattered"], 16 * TB * K * (i + 1))
                    pool.sem_inc(s["slots_free"], 1)

                if late:
                    pool.sem_inc(s["score_done"], 1)
                    pool.sem_inc(s["soft_done"], 1)
                root(0)
                with pool.Fori(0, NB - 1) as i:
                    if late:
                        square_root(i)
                        root(i + 1)
                    else:
                        root(i + 1)
                        scatter(i)
                if late:
                    square_root(NB - 1)
                else:
                    scatter(NB - 1)


def load_tokens(nc, r, tokens):
    tiles = r.slots // P
    with ExitStack() as ctx:
        sc = Scope(nc, ctx, r.name + "_tokens")
        raw = sc.sb("raw", [tiles, P], I32)
        asf = sc.sb("asf", [tiles, P])
        turned = sc.ps("turned", [P, 512])
        loaded, asf_done, turn_done, done = (sc.sem(n) for n in ("loaded", "asf_done", "turn_done", "done"))
        with nc.Block() as block:

            @block.sync
            def _(sp):
                sp.dma_start(raw[:, :], r.token_of[0:r.slots, :].rearrange("(n p) a -> n (p a)", p=P)).then_inc(loaded, 16)

            @block.vector
            def _(dve):
                dve.wait_ge(loaded, 16)
                nc.vector.tensor_copy(asf[:, :], raw[:, :]).then_inc(asf_done, 1)
                dve.wait_ge(turn_done, 1)
                nc.vector.tensor_copy(tokens[:, :], turned[:, 0:tiles]).then_inc(done, 1)

            @block.tensor
            def _(pe):
                pe.wait_ge(asf_done, 1)
                nc.tensor.transpose(turned[:, 0:tiles], asf[:, :], r.ident[0:tiles, 0:tiles]).then_inc(turn_done, 1)


def build_small_experts(nc, io, keep, r):
    TT = CAP // P
    HU = 64
    NI = r.experts // 2
    with ExitStack() as ctx:
        sc = Scope(nc, ctx, "small")
        tokens = sc.sb("tokens", [P, r.slots // P], U32)
        load_tokens(nc, r, tokens)
        now = sc.sb("now", [P, 2, TT], U32)
        w_up = sc.sb("w_up", [P, 2, DC, 2 * HU])
        w_down = sc.sb("w_down", [HU, 2, D])
        xg = sc.sb("xg", [P, 2, TT, D])
        xgT = sc.sb("xgT", [P, 2, DC, CAP])
        sil = sc.sb("sil", [P, 2, TT, HU])
        hid = sc.sb("hid", [P, 2, TT, HU])
        hidT = sc.sb("hidT", [HU, 2, CAP])
        y_sb = sc.sb("y", [P, 2, TT, D])
        wide = sc.ps("wide", [P, 2, 2, 512])
        narrow = sc.ps("narrow", [P, 2, 512])
        w_loaded = sc.sems("w_loaded", 2)
        gathered = sc.sems("gathered", 2)
        stored = sc.sems("stored", 2)
        names = "now_done turned xT_act xT_dve up_done sil_done hid_done hturned hidT_done y_done y_act y_dve pool_passed pe_passed".split()
        s = {n: sc.sem(n) for n in names}
        with nc.Block() as block:

            @block.sync
            def _(sp):
                with sp.Fori(0, NI) as i:
                    for u in range(2):
                        e = 2 * i + u
                        sp.wait_ge(s["y_done"], TT * e + TT)
                        sp.dma_start(w_up[:, u], io["w_up"][bass.ds(e, 1)].rearrange("e p (c h) -> p (e c) h", c=DC)).then_inc(w_loaded[u], 16)
                        sp.dma_start(w_down[:, u], io["w_down"][bass.ds(e, 1)].rearrange("e p d -> p (e d)")).then_inc(w_loaded[u], 16)

            @block.gpsimd
            def _(pool):
                with pool.Fori(0, NI) as i:
                    for u in range(2):
                        e = 2 * i + u
                        hold(pool, s["turned"], 2 * e + 4, s["pool_passed"])
                        nc.gpsimd.tensor_copy(now[:, u, :], tokens[:, bass.ds(TT * e, TT)]).then_inc(s["now_done"], 1)
                        hold(pool, s["now_done"], e + 1, s["pool_passed"])
                        for t in range(TT):
                            nc.gpsimd.indirect_dma_start(out=xg[:, u, t, :], out_offset=None, in_=r.xn, in_offset=bass.IndirectOffsetOnAxis(ap=now[:, u, t:t + 1], axis=0))\
                                .then_inc(gathered[u], 16)

            @block.tensor
            def _(pe):
                pe.sem_inc(s["turned"], 4)
                pe.sem_inc(s["y_done"], 2 * TT)
                with pe.Fori(0, NI) as i:
                    for u in range(2):
                        e = 2 * i + u
                        pe.wait_ge(gathered[u], 32 * i + 32)
                        for half in range(2):
                            pe.wait_ge(s["y_dve" if half else "y_act"], e + 1)
                            for c in (2 * half, 2 * half + 1):
                                for t in range(TT):
                                    at = (c % 2) * CAP + t * P
                                    mm = nc.tensor.transpose(wide[:, u, half, at:at + P], xg[:, u, t, c * P:(c + 1) * P], keep["ident"][:, :])
                            mm.then_inc(s["turned"], 1)
                    for u in range(2):
                        e = 2 * i + u
                        pe.wait_ge(w_loaded[u], 32 * i + 32)
                        pe.wait_ge(s["hidT_done"], e + 1)
                        pe.wait_ge(s["xT_act"], e + 1)
                        pe.wait_ge(s["xT_dve"], e + 1)
                        for t in range(TT):
                            for c in range(DC):
                                mm = nc.tensor.matmul(narrow[:, u, t * P:(t + 1) * P], xgT[:, u, c, t * P:(t + 1) * P], w_up[:, u, c, :], start=c == 0, stop=c == DC - 1)
                        mm.then_inc(s["up_done"], 1)
                    for u in range(2):
                        e = 2 * i + u
                        hold(pe, s["hid_done"], e + 1, s["pe_passed"])
                        for t in range(TT):
                            mm = nc.tensor.transpose(narrow[0:HU, u, t * P:(t + 1) * P], hid[:, u, t, :], keep["ident"][:, :])
                        mm.then_inc(s["hturned"], 1)
                    for u in range(2):
                        e = 2 * i + u
                        pe.wait_ge(s["hidT_done"], e + 3)
                        for t in range(TT):
                            nc.tensor.matmul(wide[:, u, t, :], hidT[:, u, t * P:(t + 1) * P], w_down[:, u, :], start=True, stop=True).then_inc(s["y_done"], 1)

            @block.scalar
            def _(act):
                act.sem_inc(s["y_act"], 2)
                with act.Fori(0, NI) as i:
                    for u in range(2):
                        e = 2 * i + u
                        act.wait_ge(s["turned"], 2 * e + 1 + 4)
                        nc.scalar.activation(xgT[:, u, 0:2, :], wide[:, u, 0, :].rearrange("p (c s) -> p c s", c=2), ACT.Copy).then_inc(s["xT_act"], 1)
                    for u in range(2):
                        e = 2 * i + u
                        act.wait_ge(s["up_done"], e + 1)
                        nc.scalar.activation(sil[:, u, :, :], narrow[:, u, 0:2 * P].rearrange("p (t h) -> p t h", t=TT)[:, :, 0:HU], ACT.Silu).then_inc(s["sil_done"], 1)
                    for u in range(2):
                        e = 2 * i + u
                        act.wait_ge(stored[u], 16 * i + 16)
                        act.wait_ge(s["y_done"], TT * e + 1 + 2 * TT)
                        nc.scalar.activation(y_sb[:, u, 0, :], wide[:, u, 0, :], ACT.Copy).then_inc(s["y_act"], 1)
                        act.wait_ge(s["y_act"], e + 3)
                        act.wait_ge(s["y_dve"], e + 3)
                        act.dma_start(rows(r.y, e * CAP, CAP).rearrange("(t p) d -> p t d", p=P), y_sb[:, u]).then_inc(stored[u], 16)
                for u in range(2):
                    act.wait_ge(stored[u], 16 * NI + 16)

            @block.vector
            def _(dve):
                for sem, n in ((s["y_dve"], 2), (s["hidT_done"], 2), (stored[0], 16), (stored[1], 16)):
                    dve.sem_inc(sem, n)
                with dve.Fori(0, NI) as i:
                    for u in range(2):
                        e = 2 * i + u
                        dve.wait_ge(s["turned"], 2 * e + 2 + 4)
                        nc.vector.tensor_copy(xgT[:, u, 2:4, :], wide[:, u, 1, :].rearrange("p (c s) -> p c s", c=2)).then_inc(s["xT_dve"], 1)
                    for u in range(2):
                        e = 2 * i + u
                        dve.wait_ge(s["sil_done"], e + 1)
                        nc.vector.tensor_tensor(hid[:, u, :, :], sil[:, u, :, :], narrow[:, u, 0:2 * P].rearrange("p (t h) -> p t h", t=TT)[:, :, HU:2 * HU], ALU.mult)\
                            .then_inc(s["hid_done"], 1)
                    for u in range(2):
                        e = 2 * i + u
                        dve.wait_ge(s["hturned"], e + 1)
                        nc.vector.tensor_copy(hidT[:, u, :], narrow[0:HU, u, 0:CAP]).then_inc(s["hidT_done"], 1)
                    for u in range(2):
                        e = 2 * i + u
                        dve.wait_ge(stored[u], 16 * i + 16)
                        dve.wait_ge(s["y_done"], TT * e + 2 + 2 * TT)
                        nc.vector.tensor_copy(y_sb[:, u, 1, :], wide[:, u, 1, :]).then_inc(s["y_dve"], 1)


def build_combine(nc, keep, r, x_mid, x_out):
    K = r.topk
    NT = N // P
    with ExitStack() as ctx:
        sc = Scope(nc, ctx, r.name + "_comb")
        now = sc.sb("now", [P, 2, K], U32)
        x_sb = sc.sb("x", [P, 2, D])
        yk = sc.sb("yk", [P, 2, K, D])
        acc = sc.sb("acc", [P, 2, D])
        x_new = sc.sb("x_new", [P, 2, D])
        loaded = sc.sems("loaded", 2)
        gathered = sc.sems("gathered", 2)
        stored = sc.sems("stored", 2)
        x_free, now_done, acc_done, pool_passed = (sc.sem(n) for n in ("x_free", "now_done", "acc_done", "pool_passed"))
        with nc.Block() as block:

            @block.sync
            def _(sp):
                with sp.Fori(0, NT // 2) as i:
                    for u in range(2):
                        sp.wait_ge(x_free, 2 * i + u + 1)
                        sp.dma_start(x_sb[:, u, :], rows(x_mid, (2 * i + u) * P, P)).then_inc(loaded[u], 16)

            @block.gpsimd
            def _(pool):
                with pool.Fori(0, NT // 2) as i:
                    for u in range(2):
                        t = 2 * i + u
                        hold(pool, x_free, t + 1, pool_passed)
                        nc.gpsimd.tensor_copy(now[:, u, :], r.slot_of[:, bass.ds(t, 1), :].rearrange("p a k -> p (a k)")).then_inc(now_done, 1)
                        hold(pool, now_done, t + 1, pool_passed)
                        for k in range(K):
                            nc.gpsimd.indirect_dma_start(out=yk[:, u, k, :], out_offset=None, in_=r.y, in_offset=bass.IndirectOffsetOnAxis(ap=now[:, u, k:k + 1], axis=0))\
                                .then_inc(gathered[u], 16)

            @block.vector
            def _(dve):
                for sem, n in ((x_free, 2), (stored[0], 16), (stored[1], 16)):
                    dve.sem_inc(sem, n)
                with dve.Fori(0, NT // 2) as i:
                    for u in range(2):
                        t = 2 * i + u
                        dve.wait_ge(loaded[u], 16 * i + 16)
                        dve.wait_ge(gathered[u], 16 * K * i + 16 * K)
                        dve.wait_ge(stored[u], 16 * i + 16)
                        for k in range(K):
                            if k:
                                dve.wait_ge(acc_done, K * t + k)
                            src = x_sb[:, u, :] if k == 0 else acc[:, (k - 1) % 2, :]
                            dst = x_new[:, u, :] if k == K - 1 else acc[:, k % 2, :]
                            nc.vector.scalar_tensor_tensor(out=dst, in0=yk[:, u, k, :], scalar=r.weight[:, bass.ds(t, 1), k:k + 1].rearrange("p a k -> p (a k)"), in1=src,
                                                           op0=ALU.mult, op1=ALU.add).then_inc(acc_done, 1)
                        dve.wait_ge(acc_done, K * t + K)
                        dve.sem_inc(x_free, 1)

            @block.scalar
            def _(act):
                with act.Fori(0, NT // 2) as i:
                    for u in range(2):
                        act.wait_ge(acc_done, K * (2 * i + u) + K)
                        act.dma_start(rows(x_out, (2 * i + u) * P, P), x_new[:, u, :]).then_inc(stored[u], 16)
                for u in range(2):
                    act.wait_ge(stored[u], 16 * (NT // 2) + 16)


def build_small_mixture(nc, io, keep, x_in, x_out):
    with ExitStack() as ctx:
        gate = keep["gates"][:, 4:5]
        r = Routing(nc, Scope(nc, ctx, "moe0"), "moe0", 64, 6, 64 * CAP, P)
        r.ident = keep["ident"]
        x_mid = nc.dram_tensor("moe0_x_mid", [N, D], F32, kind="Internal").ap()
        build_route(nc, io, keep, x_in, x_mid, r, (("moe0_w1", "moe0_w3", "moe0_w2"), 128, False), gate, None)
        build_small_experts(nc, io, keep, r)
        build_combine(nc, keep, r, x_mid, x_out)


INTER = 352
INTER_C = 3
WIDE_TILES = N * 2 // P + 8


def build_late_slots(nc, keep, r, late, tile_expert):
    E, K, NT = r.experts, r.topk, N // P
    with ExitStack() as ctx:
        sc = Scope(nc, ctx, r.name + "_slots")
        counts_ps = sc.ps("counts_ps", [P, 512])
        counts = sc.sb("counts", [P, E])
        steps = sc.sb("steps", [P, NT])
        over = sc.sb("over", [P, E, NT])
        tiles = sc.sb("tiles", [P, E])
        start = sc.sb("start", [P, E])
        start_slot = sc.sb("start_slot", [P, E])
        first = sc.sb("first", [P, NT, K])
        slotf = sc.sb("slotf", [P, 2, NT, K])
        te = sc.sb("te", [P, 2, WIDE_TILES])
        slot_now = sc.sb("slot_now", [P, TB, K], U32)
        token_now = sc.sb("token_now", [P, TB], I32)
        counted, dve_step, slots_ready, slots_free, scattered, pool_passed = (sc.sem(n) for n in ("counted", "dve_step", "slots_ready", "slots_free", "scattered", "pool_passed"))
        with nc.Block() as block:

            @block.tensor
            def _(pe):
                nc.tensor.matmul(counts_ps[:, 0:E], keep["ones_bf"][:, :], late["counts"][:, :], start=True, stop=True).then_inc(counted, 1)

            @block.vector
            def _(dve):
                n = [0]

                def then(ins):
                    n[0] += 1
                    ins.then_inc(dve_step, 1)
                    dve.wait_ge(dve_step, n[0])

                dve.sem_inc(slots_free, 1)
                then(nc.vector.tensor_scalar(steps[:, :], keep["iota"][:, 0:NT], float(P), None, ALU.mult))
                dve.wait_ge(counted, 1)
                then(nc.vector.tensor_copy(counts[:, :], counts_ps[:, 0:E]))
                then(nc.vector.tensor_tensor(over[:, :, :], counts[:, :].rearrange("p (e m) -> p e m", m=1).broadcast_to([P, E, NT]),
                                             steps[:, :].rearrange("p (e m) -> p e m", e=1).broadcast_to([P, E, NT]), ALU.is_gt))
                then(nc.vector.tensor_reduce(tiles[:, :], over[:, :, :], AX.X, ALU.add))
                then(nc.vector.memset(start[:, 0:1], 0.0))
                for e in range(1, E):
                    then(nc.vector.tensor_tensor(start[:, e:e + 1], start[:, e - 1:e], tiles[:, e - 1:e], ALU.add))
                then(nc.vector.tensor_scalar(start_slot[:, :], start[:, :], float(P), None, ALU.mult))
                for e in range(E):
                    src = late["pos"] if e == 0 else slotf[:, (e - 1) % 2]
                    then(nc.vector.tensor_scalar(first[:, :, :], late["idx"][:, :, :], float(e), start_slot[:, e:e + 1], ALU.is_equal, ALU.mult))
                    then(nc.vector.tensor_tensor(slotf[:, e % 2], src[:, :, :], first[:, :, :], ALU.add))
                then(nc.vector.tensor_copy(r.slot_of[:, :, :], slotf[:, (E - 1) % 2]))
                then(nc.vector.memset(te[:, 0, :], 0.0))
                for e in range(1, E):
                    then(nc.vector.scalar_tensor_tensor(out=te[:, e % 2, :], in0=keep["iota"][:, 0:WIDE_TILES], scalar=start[:, e:e + 1], in1=te[:, (e - 1) % 2, :],
                                                        op0=ALU.is_ge, op1=ALU.add))
                then(nc.vector.tensor_copy(tile_expert[:, :], te[:, (E - 1) % 2, :]))
                with dve.Fori(0, NB) as i:
                    dve.wait_ge(slots_free, i + 1)
                    nc.vector.tensor_copy(token_now[:, :], keep["row_id"][:, bass.ds(TB * i, TB)]).then_inc(slots_ready, 1)
                    nc.vector.tensor_copy(slot_now[:, :, :], r.slot_of[:, bass.ds(TB * i, TB), :]).then_inc(slots_ready, 1)

            @block.gpsimd
            def _(pool):
                with pool.Fori(0, NB) as i:
                    hold(pool, slots_ready, 2 * i + 2, pool_passed)
                    for t in range(TB):
                        for k in range(K):
                            nc.gpsimd.indirect_dma_start(out=r.token_of, out_offset=bass.IndirectOffsetOnAxis(ap=slot_now[:, t, k:k + 1], axis=0),
                                                         in_=token_now[:, t:t + 1], in_offset=None).then_inc(scattered, 16)
                    pool.wait_ge(scattered, 16 * TB * K * (i + 1))
                    pool.sem_inc(slots_free, 1)


def build_wide_experts(nc, io, keep, r, tile_expert):
    E = r.experts
    UPC = DC * INTER
    WC = 2 * UPC + INTER_C * D
    NI = WIDE_TILES // 2
    HM = [min(P, INTER - P * j) for j in range(INTER_C)]
    with ExitStack() as ctx:
        sc = Scope(nc, ctx, "wide")
        tokens = sc.sb("tokens", [P, WIDE_TILES], U32)
        load_tokens(nc, r, tokens)
        weights = sc.sb("weights", [P, E * WC], F32R)
        raw = sc.sb("raw", [P, 2, WC], BF16)
        now = sc.sb("now", [P, 2, 1], U32)
        xg = sc.sb("xg", [P, 2, D])
        xT = [sc.sb(f"xT{q}", [P, 2, DC, P], F32R) for q in range(2)]
        sil = sc.sb("sil", [P, 2, INTER])
        hid = sc.sb("hid", [P, 2, INTER])
        hT = [sc.sb(f"hT{q}", [P, 2, INTER_C, P], F32R) for q in range(2)]
        y_sb = sc.sb("y", [P, 2, D])
        turn = sc.ps("turn", [P, 2, 512])
        up1 = sc.ps("up1", [P, 2, 512])
        up3 = sc.ps("up3", [P, 2, 512])
        out = sc.ps("out", [P, 2, 512])
        raw_loaded = sc.sems("raw_loaded", 2)
        gathered = sc.sems("gathered", 2)
        stored = sc.sems("stored", 2)
        names = ("raw_free weights_done now_done turned hi_done lo_done up_done sil_done hid_done hturned hhi_done hlo_done y_done y_moved "
                 "pool_passed").split()
        s = {n: sc.sem(n) for n in names}
        with nc.Block() as block:

            @block.sync
            def _(sp):
                with sp.Fori(0, E // 2) as i:
                    for u in range(2):
                        e = 2 * i + u
                        sp.wait_ge(s["raw_free"], e + 1)
                        sp.dma_start(raw[:, u, :], io["moe2_w"][bass.ds(e, 1)].rearrange("e p c -> p (e c)")).then_inc(raw_loaded[u], 16)

            @block.gpsimd
            def _(pool):
                with pool.Fori(0, NI) as i:
                    for u in range(2):
                        j = 2 * i + u
                        hold(pool, s["turned"], j + 1, s["pool_passed"])
                        nc.gpsimd.tensor_copy(now[:, u, :], tokens[:, bass.ds(j, 1)]).then_inc(s["now_done"], 1)
                        hold(pool, s["now_done"], j + 1, s["pool_passed"])
                        nc.gpsimd.indirect_dma_start(out=xg[:, u, :], out_offset=None, in_=r.xn, in_offset=bass.IndirectOffsetOnAxis(ap=now[:, u, 0:1], axis=0))\
                            .then_inc(gathered[u], 16)

            @block.tensor
            def _(pe):
                pe.sem_inc(s["turned"], 2)
                pe.wait_ge(s["weights_done"], E)
                with pe.Fori(0, NI) as i:
                    base = []
                    for u in range(2):
                        j = 2 * i + u
                        base.append(nc.tensor.value_load(tile_expert[0:1, bass.ds(j, 1)], min_val=0, max_val=E - 1) * WC)
                    for u in range(2):
                        j = 2 * i + u
                        pe.wait_ge(gathered[u], 16 * i + 16)
                        pe.wait_ge(s["hlo_done"], j + 1)
                        for c in range(DC):
                            mm = nc.tensor.transpose(turn[:, u, c * P:(c + 1) * P], xg[:, u, c * P:(c + 1) * P], keep["ident"][:, :])
                        mm.then_inc(s["turned"], 1)
                    for u in range(2):
                        j = 2 * i + u
                        pe.wait_ge(s["hid_done"], j + 1)
                        pe.wait_ge(s["lo_done"], j + 1)
                        for bank, at in ((up1, 0), (up3, UPC)):
                            n = 0
                            for c in range(DC):
                                for q in range(2):
                                    mm = nc.tensor.matmul(bank[:, u, 0:INTER], xT[q][:, u, c, :], weights[:, bass.ds(base[u] + (at + c * INTER), INTER)], start=n == 0, stop=n == 2 * DC - 1)
                                    n += 1
                        mm.then_inc(s["up_done"], 1)
                    for u in range(2):
                        j = 2 * i + u
                        pe.wait_ge(s["hid_done"], j + 3)
                        for k in range(INTER_C):
                            mm = nc.tensor.transpose(turn[0:HM[k], u, k * P:(k + 1) * P], hid[:, u, k * P:k * P + HM[k]], keep["ident"][:, :])
                        mm.then_inc(s["hturned"], 1)
                    for u in range(2):
                        j = 2 * i + u
                        pe.wait_ge(s["hlo_done"], j + 3)
                        pe.wait_ge(s["y_moved"], j + 1)
                        n = 0
                        for k in range(INTER_C):
                            for q in range(2):
                                mm = nc.tensor.matmul(out[:, u, :], hT[q][0:HM[k], u, k, :], weights[0:HM[k], bass.ds(base[u] + (2 * UPC + k * D), D)], start=n == 0, stop=n == 2 * INTER_C - 1)
                                n += 1
                        mm.then_inc(s["y_done"], 1)

            @block.scalar
            def _(act):
                act.sem_inc(s["y_moved"], 2)
                with act.Fori(0, NI) as i:
                    for u in range(2):
                        j = 2 * i + u
                        act.wait_ge(s["turned"], j + 1 + 2)
                        nc.scalar.activation(xT[0][:, u, :, :], turn[:, u, :].rearrange("p (c s) -> p c s", c=DC), ACT.Copy).then_inc(s["hi_done"], 1)
                    for u in range(2):
                        j = 2 * i + u
                        act.wait_ge(s["up_done"], j + 1)
                        nc.scalar.activation(sil[:, u, :], up1[:, u, 0:INTER], ACT.Silu).then_inc(s["sil_done"], 1)
                    for u in range(2):
                        j = 2 * i + u
                        act.wait_ge(s["hturned"], j + 1)
                        nc.scalar.activation(hT[0][:, u, 0:2, :], turn[:, u, 0:2 * P].rearrange("p (c s) -> p c s", c=2), ACT.Copy)
                        nc.scalar.activation(hT[0][0:HM[2], u, 2, :], turn[0:HM[2], u, 2 * P:3 * P], ACT.Copy).then_inc(s["hhi_done"], 1)
                    for u in range(2):
                        j = 2 * i + u
                        act.wait_ge(stored[u], 16 * i + 16)
                        act.wait_ge(s["y_done"], j + 1)
                        nc.scalar.activation(y_sb[:, u, :], out[:, u, :], ACT.Copy).then_inc(s["y_moved"], 1)
                        act.wait_ge(s["y_moved"], j + 3)
                        act.dma_start(rows(r.y, j * P, P), y_sb[:, u, :]).then_inc(stored[u], 16)
                for u in range(2):
                    act.wait_ge(stored[u], 16 * NI + 16)

            @block.vector
            def _(dve):
                for sem, n in ((s["raw_free"], 2), (s["hid_done"], 2), (s["hlo_done"], 2), (stored[0], 16), (stored[1], 16)):
                    dve.sem_inc(sem, n)
                with dve.Fori(0, E // 2) as i:
                    for u in range(2):
                        e = 2 * i + u
                        dve.wait_ge(raw_loaded[u], 16 * i + 16)
                        nc.vector.tensor_copy(weights[:, bass.ds(e * WC, WC)], raw[:, u, :]).then_inc(s["weights_done"], 1)
                        dve.wait_ge(s["weights_done"], e + 1)
                        dve.sem_inc(s["raw_free"], 1)
                with dve.Fori(0, NI) as i:
                    for u in range(2):
                        j = 2 * i + u
                        dve.wait_ge(s["hi_done"], j + 1)
                        nc.vector.tensor_tensor(xT[1][:, u, :, :], turn[:, u, :].rearrange("p (c s) -> p c s", c=DC), xT[0][:, u, :, :].bitcast(F32), ALU.subtract).then_inc(s["lo_done"], 1)
                    for u in range(2):
                        j = 2 * i + u
                        dve.wait_ge(s["sil_done"], j + 1)
                        nc.vector.tensor_tensor(hid[:, u, :], sil[:, u, :], up3[:, u, 0:INTER], ALU.mult).then_inc(s["hid_done"], 1)
                    for u in range(2):
                        j = 2 * i + u
                        dve.wait_ge(s["hhi_done"], j + 1)
                        nc.vector.tensor_tensor(hT[1][:, u, 0:2, :], turn[:, u, 0:2 * P].rearrange("p (c s) -> p c s", c=2), hT[0][:, u, 0:2, :].bitcast(F32), ALU.subtract)
                        nc.vector.tensor_tensor(hT[1][0:HM[2], u, 2, :], turn[0:HM[2], u, 2 * P:3 * P], hT[0][0:HM[2], u, 2, :].bitcast(F32), ALU.subtract).then_inc(s["hlo_done"], 1)


def build_wide_mixture(nc, io, keep, x_in, x_out):
    with ExitStack() as ctx:
        gate = keep["gates"][:, 6:7]
        sc = Scope(nc, ctx, "moe2")
        r = Routing(nc, sc, "moe2", 8, 2, WIDE_TILES * P, 0)
        r.ident = keep["ident"]
        late = {"idx": sc.sb("late_idx", [P, N // P, 2]), "pos": sc.sb("late_pos", [P, N // P, 2]), "counts": sc.sb("late_counts", [P, 8], BF16)}
        tile_expert = sc.sb("tile_expert", [P, WIDE_TILES], I32)
        x_mid = nc.dram_tensor("moe2_x_mid", [N, D], F32, kind="Internal").ap()
        build_route(nc, io, keep, x_in, x_mid, r, (("moe2_w1", "moe2_w3", "moe2_w2"), INTER, True), gate, late)
        build_late_slots(nc, keep, r, late, tile_expert)
        build_wide_experts(nc, io, keep, r, tile_expert)
        build_combine(nc, keep, r, x_mid, x_out)


GN = 8
GROUPS = S // GN
KPAD = D + P


def build_gated_conv(nc, io, keep, x_in, x_out):
    T = S // P
    NS = 2
    with ExitStack() as outer:
        osc = Scope(nc, outer, "conv")
        vT = osc.sb("vT", [P, DC, B, S])
        cT = osc.sb("cT", [P, B, DC, S])
        cTr = osc.sb("cTr", [P, B, DC, S])
        oT = osc.sb("oT", [P, DC, B, S])
        ctx_loaded = osc.sem("ctx_loaded")

        with ExitStack() as ctx:
            sc = Scope(nc, ctx, "skip")
            x_sb = sc.sb("x", [P, 2, T, D])
            c_sb = sc.sb("c", [P, 2, T, D])
            xn = sc.sb("xn", [P, T, D])
            z = sc.sb("z", [P, T, D])
            group8 = sc.sb("group8", [P, P])
            skip = sc.sb("skip", [P, T])
            skip_m = sc.sb("skip_m", [P, T, P])
            sk = sc.sb("sk", [P, T, D])
            x_mid = sc.sb("x_mid", [P, 2, T, D])
            stats = sc.sb("stats", [P, T, 6])
            mv = sc.sb("mv", [P, T, 2])
            ve = sc.sb("ve", [P, T])
            rstd = sc.sb("rstd", [P, T])
            turn = sc.ps("turn", [P, DC, 512])
            ssum = sc.ps("ssum", [P, T, D])
            const_loaded = sc.sem("const_loaded")
            loaded = sc.sems("loaded", 2)
            stored = sc.sems("stored", 2)
            inputs_free = sc.sem("inputs_free")
            stats_done = sc.sem("stats_done")
            var_done = sc.sem("var_done")
            ve_done = sc.sem("ve_done")
            rstd_done = sc.sem("rstd_done")
            xn_done = sc.sem("xn_done")
            z_done = sc.sem("z_done")
            skip_done = sc.sem("skip_done")
            turned = sc.sem("turned")
            vT_done = sc.sem("vT_done")
            ssum_done = sc.sem("ssum_done")
            sk_done = sc.sem("sk_done")
            mid_done = sc.sem("mid_done")
            passed = sc.sem("passed")
            with nc.Block() as block:

                @block.sync
                def _(sp):
                    sp.dma_start(group8[:, :], io["group8"]).then_inc(const_loaded, 16)
                    sp.dma_start(skip[:, :], io["skip"]).then_inc(const_loaded, 16)
                    with sp.Fori(0, B // 2) as i:
                        for u in range(2):
                            b = 2 * i + u
                            sp.wait_ge(inputs_free, b + 1)
                            sp.dma_start(x_sb[:, u], rows(x_in, b * S, S).rearrange("(t p) d -> p t d", p=P)).then_inc(loaded[u], 16)
                            sp.dma_start(c_sb[:, u], rows(io["ctx"], b * S, S).rearrange("(t p) d -> p t d", p=P)).then_inc(loaded[u], 16)
                    sp.dma_start(cT[:, :, :, :], io["ctxT"].rearrange("b p c s -> p b c s")).then_inc(ctx_loaded, 16)
                    sp.dma_start(cTr[:, :, :, :], io["ctxTr"].rearrange("b p c s -> p b c s")).then_inc(ctx_loaded, 16)

                @block.tensor
                def _(pe):
                    pe.wait_ge(skip_done, T)
                    with pe.Fori(0, B) as b:
                        pe.wait_ge(xn_done, T * b + T)
                        for c in range(DC):
                            pe.wait_ge(vT_done, DC * b + c + 1)
                            for t in range(T):
                                mm = nc.tensor.transpose(turn[:, c, t * P:(t + 1) * P], xn[:, t, c * P:(c + 1) * P], keep["ident"][:, :])
                            mm.then_inc(turned, 1)
                        for t in range(T):
                            pe.wait_ge(z_done, T * b + t + 1)
                            pe.wait_ge(sk_done, T * b + t + 1)
                            nc.tensor.matmul(ssum[:, t, :], skip_m[:, t, :], z[:, t, :], start=True, stop=True).then_inc(ssum_done, 1)

                @block.vector
                def _(dve):
                    for sem, n in ((inputs_free, 2), (sk_done, T), (turned, 1), (ssum_done, T), (stored[0], 16), (stored[1], 16)):
                        dve.sem_inc(sem, n)
                    dve.wait_ge(const_loaded, 32)
                    for t in range(T):
                        nc.vector.tensor_scalar(skip_m[:, t, :], group8[:, :], skip[:, t:t + 1], None, ALU.mult).then_inc(skip_done, 1)
                    with dve.Fori(0, B // 2) as i:
                        for u in range(2):
                            b = 2 * i + u
                            dve.wait_ge(loaded[u], 32 * i + 32)
                            for t in range(T):
                                nc.vector.bn_stats(stats[:, t, :], x_sb[:, u, t, :]).then_inc(stats_done, 1)
                            hold(dve, stats_done, T * b + T, passed)
                            for t in range(T):
                                nc.vector.bn_aggr(mv[:, t, :], stats[:, t, :]).then_inc(var_done, 1)
                            dve.wait_ge(var_done, T * b + T)
                            nc.vector.tensor_scalar(ve[:, :], mv[:, :, 1], LN_EPS, None, ALU.add).then_inc(ve_done, 1)
                            dve.wait_ge(rstd_done, b + 1)
                            dve.wait_ge(turned, DC * b + 1)
                            for t in range(T):
                                nc.vector.tensor_scalar(xn[:, t, :], x_sb[:, u, t, :], mv[:, t, 0:1], rstd[:, t:t + 1], ALU.subtract, ALU.mult).then_inc(xn_done, 1)
                            for t in range(T):
                                dve.wait_ge(xn_done, T * b + t + 1)
                                dve.wait_ge(ssum_done, T * b + t + 1)
                                nc.vector.tensor_tensor(z[:, t, :], xn[:, t, :], c_sb[:, u, t, :], ALU.mult).then_inc(z_done, 1)
                            dve.wait_ge(stored[u], 16 * i + 16)
                            for t in range(T):
                                dve.wait_ge(ssum_done, T * b + t + 1 + T)
                                nc.vector.tensor_tensor(sk[:, t, :], ssum[:, t, :], c_sb[:, u, t, :], ALU.mult).then_inc(sk_done, 1)
                                dve.wait_ge(sk_done, T * b + t + 1 + T)
                                nc.vector.scalar_tensor_tensor(out=x_mid[:, u, t, :], in0=sk[:, t, :], scalar=keep["gates"][:, 3:4], in1=x_sb[:, u, t, :],
                                                               op0=ALU.mult, op1=ALU.add).then_inc(mid_done, 1)
                            dve.wait_ge(mid_done, T * b + T)
                            dve.sem_inc(inputs_free, 1)

                @block.gpsimd
                def _(pool):
                    with pool.Fori(0, B) as b:
                        pool.wait_ge(ve_done, b + 1)
                        nc.gpsimd.tensor_tensor(rstd[:, :], ve[:, :], keep["neg_half"][:, 0:T], ALU.pow).then_inc(rstd_done, 1)

                @block.scalar
                def _(act):
                    act.sem_inc(vT_done, DC)
                    with act.Fori(0, B // 2) as i:
                        for u in range(2):
                            b = 2 * i + u
                            for c in range(DC):
                                act.wait_ge(turned, DC * b + c + 2)
                                nc.scalar.activation(vT[:, c, bass.ds(b, 1), :].rearrange("p a s -> p (a s)"), turn[:, c, 0:S], ACT.Copy).then_inc(vT_done, 1)
                            act.wait_ge(mid_done, T * b + T)
                            act.dma_start(rows(x_out, b * S, S).rearrange("(t p) d -> p t d", p=P), x_mid[:, u]).then_inc(stored[u], 16)
                    for u in range(2):
                        act.wait_ge(stored[u], 16 * (B // 2) + 16)

        with ExitStack() as ctx:
            sc = Scope(nc, ctx, "toep")
            toep = sc.sb("toep", [P, NS, D])
            kv = sc.sb("kv", [P, NS, DC, 512])
            gated = sc.sb("gated", [P, 2, 512])
            y = sc.ps("y", [P, NS, DC, 512])
            loaded = sc.sems("loaded", NS)
            kv_done = sc.sem("kv_done")
            y_done = sc.sem("y_done")
            gated_done = sc.sem("gated_done")
            o_done = sc.sem("o_done")
            fourths = [P, B, GN, GN]

            with nc.Block() as block:

                @block.sync
                def _(sp):
                    with sp.Fori(0, GROUPS // NS) as i:
                        for u in range(NS):
                            h = NS * i + u
                            sp.wait_ge(y_done, DC * h + DC)
                            windows = bass.AP(io["filt"].tensor, h * KPAD, [[1, P], [1, D]])
                            sp.dma_start(toep[:, u, :], windows).then_inc(loaded[u], 16)

                @block.tensor
                def _(pe):
                    pe.sem_inc(y_done, NS * DC)
                    with pe.Fori(0, GROUPS // NS) as i:
                        for u in range(NS):
                            h = NS * i + u
                            pe.wait_ge(loaded[u], 16 * i + 16)
                            for lc in range(DC):
                                pe.wait_ge(kv_done, DC * h + lc + 1)
                                pe.wait_ge(gated_done, DC * h + lc + 1)
                                for mc in range(lc + 1):
                                    at = 384 - P * (lc - mc)
                                    mm = nc.tensor.matmul(y[:, u, lc, :], toep[:, u, at:at + P], kv[:, u, mc, :], start=mc == 0, stop=mc == lc)
                                mm.then_inc(y_done, 1)

                @block.vector
                def _(dve):
                    def pairs(h, u, c):
                        dve.wait_ge(y_done, DC * h + DC)
                        nc.vector.tensor_tensor(kv[:, u, c, :].rearrange("p (b i j) -> p b i j", b=B, i=GN),
                                                vT[:, c, :, bass.ds(GN * h, GN)].rearrange("p b (i j) -> p b i j", j=1).broadcast_to(fourths),
                                                cT[:, :, c, bass.ds(GN * h, GN)].rearrange("p b (i j) -> p b i j", i=1).broadcast_to(fourths),
                                                ALU.mult).then_inc(kv_done, 1)

                    def combine(h, u, lc):
                        n = DC * h + lc
                        dve.wait_ge(y_done, n + 1 + NS * DC)
                        dve.wait_ge(o_done, n + 1)
                        nc.vector.tensor_tensor(gated[:, lc % 2, :].rearrange("p (b i j) -> p b i j", b=B, i=GN), y[:, u, lc, :].rearrange("p (b i j) -> p b i j", b=B, i=GN),
                                                cTr[:, :, lc, bass.ds(GN * h, GN)].rearrange("p b (i j) -> p b i j", j=1).broadcast_to(fourths),
                                                ALU.mult).then_inc(gated_done, 1)
                        dve.wait_ge(gated_done, n + 1 + NS * DC)
                        nc.vector.tensor_reduce(oT[:, lc, :, bass.ds(GN * h, GN)], gated[:, lc % 2, :].rearrange("p (b i j) -> p b j i", b=B, i=GN), AX.X, ALU.add)\
                            .then_inc(o_done, 1)

                    dve.sem_inc(gated_done, NS * DC)
                    dve.sem_inc(o_done, 2)
                    dve.wait_ge(ctx_loaded, 32)
                    for c in range(DC):
                        pairs(0, 0, c)
                    with dve.Fori(0, GROUPS // NS - 1) as i:
                        for u in range(NS):
                            for c in range(DC):
                                pairs(NS * i + u + 1, 1 - u, c)
                                combine(NS * i + u, u, c)
                    for c in range(DC):
                        pairs(GROUPS - 1, 1, c)
                        combine(GROUPS - 2, 0, c)
                    for c in range(DC):
                        combine(GROUPS - 1, 1, c)

        with ExitStack() as ctx:
            sc = Scope(nc, ctx, "back")
            o_b = sc.sb("o_b", [P, 2, DC, S])
            x_mid = sc.sb("x_mid", [P, 2, T, D])
            x_new = sc.sb("x_new", [P, 2, T, D])
            rows_ps = sc.ps("rows", [P, 2, T, D])
            loaded = sc.sems("loaded", 2)
            stored = sc.sems("stored", 2)
            mid_free = sc.sem("mid_free")
            o_copied = sc.sem("o_copied")
            rows_done = sc.sem("rows_done")
            out_done = sc.sem("out_done")
            with nc.Block() as block:

                @block.sync
                def _(sp):
                    with sp.Fori(0, B // 2) as i:
                        for u in range(2):
                            b = 2 * i + u
                            sp.wait_ge(mid_free, b + 1)
                            sp.dma_start(x_mid[:, u], rows(x_out, b * S, S).rearrange("(t p) d -> p t d", p=P)).then_inc(loaded[u], 16)

                @block.tensor
                def _(pe):
                    with pe.Fori(0, B // 2) as i:
                        for u in range(2):
                            b = 2 * i + u
                            pe.wait_ge(o_copied, b + 1)
                            pe.wait_ge(out_done, T * b + T)
                            for t in range(T):
                                for c in range(DC):
                                    mm = nc.tensor.matmul(rows_ps[:, u, t, c * P:(c + 1) * P], o_b[:, u, c, t * P:(t + 1) * P], keep["anti"][:, :], start=True, stop=True)
                                mm.then_inc(rows_done, 1)

                @block.vector
                def _(dve):
                    for sem, n in ((mid_free, 2), (out_done, 2 * T), (rows_done, 2 * T), (stored[0], 16), (stored[1], 16)):
                        dve.sem_inc(sem, n)
                    with dve.Fori(0, B // 2) as i:
                        for u in range(2):
                            b = 2 * i + u
                            dve.wait_ge(loaded[u], 16 * i + 16)
                            dve.wait_ge(stored[u], 16 * i + 16)
                            for t in range(T):
                                dve.wait_ge(rows_done, T * b + t + 1 + 2 * T)
                                nc.vector.scalar_tensor_tensor(out=x_new[:, u, t, :], in0=rows_ps[:, u, t, :], scalar=keep["gates"][:, 3:4], in1=x_mid[:, u, t, :],
                                                               op0=ALU.mult, op1=ALU.add).then_inc(out_done, 1)
                            dve.wait_ge(out_done, T * b + 3 * T)
                            dve.sem_inc(mid_free, 1)

                @block.scalar
                def _(act):
                    with act.Fori(0, B // 2) as i:
                        for u in range(2):
                            b = 2 * i + u
                            act.wait_ge(rows_done, T * b + T)
                            nc.scalar.activation(o_b[:, u, :, :], oT[:, :, bass.ds(b, 1), :].rearrange("p c a s -> p c (a s)"), ACT.Copy).then_inc(o_copied, 1)
                            act.wait_ge(out_done, T * b + 3 * T)
                            act.dma_start(rows(x_out, b * S, S).rearrange("(t p) d -> p t d", p=P), x_new[:, u]).then_inc(stored[u], 16)
                    for u in range(2):
                        act.wait_ge(stored[u], 16 * (B // 2) + 16)


STAGES = [build_channel_attention, build_small_mixture, build_linear_attention, build_ternary_ffn, build_feature_attention, build_wide_mixture, build_gated_conv, build_lut_ffn]

INPUTS = {"x": "x", "ctx": "ctx_2048", "g_xattn": "g_xattn", "g_ffn": "g_ffn", "gamma": "L0_xattn_gamma"}


def build(nc, io, out):
    with ExitStack() as ctx:
        keep = {name: ctx.enter_context(nc.sbuf_tensor(f"keep_{name}", shape, dt)) for name, shape, dt in [
            ("ident", [P, P], F32), ("anti", [P, P], F32), ("ident_bf", [P, P], BF16), ("gates", [P, 8], F32), ("gate0", [P, 1], F32),
            ("neg_half", [P, 16], F32), ("half", [P, 32], F32), ("ones", [P, P], F32), ("ones_bf", [P, P], BF16),
            ("earlier_f", [P, P], F32), ("earlier", [P, P], BF16), ("iota", [P, 64], F32), ("spare", [P, 1], F32), ("row_id", [P, N // P], I32), ("zeros_i", [P, 136], I32)]}
        state = nc.dram_tensor("x_state", [N, D], F32, kind="Internal").ap()
        build_setup(nc, io, keep)
        todo = list(PHASES)
        for s in todo:
            STAGES[s](nc, io, keep, io["x"] if s == todo[0] else state, out if s == todo[-1] else state)


def kernel(**inputs):
    import concourse.bacc as _bacc
    from concourse.bass_utils import run_bass_kernel_spmd as _run

    a = {k: np.asarray(v) for k, v in inputs.items()}
    ctx = a["ctx_2048"]
    arrays = {
        "x": a["x"].reshape(N, D), "ctx": ctx.reshape(N, D),
        "ctxT": ctx.transpose(0, 2, 1).reshape(B, DC, P, S).transpose(0, 2, 1, 3),
        "g_xattn": a["g_xattn"], "g_ffn": a["g_ffn"], "gamma": a["L0_xattn_gamma"].reshape(1, 1),
    }

    def contraction_first(w, pad):
        w = np.concatenate([w, np.zeros((pad - w.shape[0], D), w.dtype)])
        return w.T.reshape(DC, P, pad).transpose(1, 0, 2).reshape(P, DC * pad)

    def units_first(w, pad):
        w = np.concatenate([w.T, np.zeros((pad - w.shape[1], D), w.dtype)])
        return w.reshape(pad // P, P, D).transpose(1, 0, 2).reshape(P, pad // P * D)

    def square(w):
        return w.T.reshape(DC, P, D).transpose(1, 0, 2).reshape(P, DC * D)

    filt = a["L3_xattn_k"][:, ::-1]
    arrays |= {
        "filt": np.concatenate([filt, np.zeros((filt.shape[0], P), filt.dtype)], axis=1).reshape(-1),
        "ctxTr": arrays["ctxT"][:, ::-1],
        "skip": a["fside_S2_0"].reshape(S // P, P).T,
        "group8": np.kron(np.eye(P // GN, dtype=np.float32), np.ones((GN, GN), np.float32)),
    }
    def chunks(w):
        return w.reshape(-1, P, w.shape[1]).transpose(1, 0, 2).reshape(P, -1)

    up = a["L0_ffn_w_shared_up"]
    arrays |= {
        "moe0_w1": chunks(up[:, 128:]), "moe0_w3": chunks(up[:, :128]), "moe0_w2": chunks(a["L0_ffn_w_shared_down"]), "moe0_wg": chunks(a["L0_ffn_w_gate"]),
        "w_up": a["L0_ffn_w_up"].reshape(64, DC, P, 128).transpose(0, 2, 1, 3).reshape(64, P, DC * 128), "w_down": a["L0_ffn_w_down"],
    }
    def padded_rows(w):
        return np.concatenate([w, np.zeros((-w.shape[0] % P, w.shape[1]), w.dtype)])

    arrays |= {
        "moe2_w1": chunks(a["L2_ffn_sw1"].T), "moe2_w3": chunks(a["L2_ffn_sw3"].T), "moe2_w2": chunks(padded_rows(a["L2_ffn_sw2"].T)),
        "moe2_wg": chunks(a["L2_ffn_gate_w"].T), "moe2_bias": a["L2_ffn_gate_b"].reshape(1, -1),
        "moe2_w": np.stack([np.concatenate([chunks(a["L2_ffn_w1"][e].T), chunks(a["L2_ffn_w3"][e].T), chunks(padded_rows(a["L2_ffn_w2"][e].T))], axis=1)
                            for e in range(8)]),
    }
    arrays |= {n.lower(): square(a[f"L1_xattn_{n}"]) for n in ("Wq", "Wk", "Wv", "Wo")}
    arrays |= {n: a[f"L1_xattn_{n}"].reshape(DC, P).T for n in ("bq", "bk")}
    arrays |= {n: a[f"L1_xattn_{n}"].reshape(1, D) for n in ("bv", "bo")}
    arrays |= {"wqf": a["L1_xattn_Wqf"].T, "wkf": a["L1_xattn_Wkf"].T, "mask": a["mask_BxS2_ff1"].reshape(N // P, P).T}
    arrays |= {
        "w1t": contraction_first(a["L1_ffn_w1"], HPAD), "w3t": contraction_first(a["L1_ffn_w3"], HPAD), "w2t": units_first(a["L1_ffn_w2"], HPAD),
        "lut": a["L3_ffn_lut"],
        "lut_idx": np.concatenate([contraction_first(a["L3_ffn_gate_idx"], HPAD), contraction_first(a["L3_ffn_up_idx"], HPAD),
                                   units_first(a["L3_ffn_down_idx"], HPAD)], axis=1),
    }
    arrays = {f"in_{k}": np.ascontiguousarray(v) for k, v in arrays.items()}
    nc = _bacc.Bacc("TRN2", target_bir_lowering=False, num_devices=1)
    io = {k[3:]: nc.dram_tensor(k, v.shape, mybir.dt.from_np(v.dtype), kind="ExternalInput").ap() for k, v in arrays.items()}
    out = nc.dram_tensor("x_out", [N, D], F32, kind="ExternalOutput").ap()
    build(nc, io, out)
    r = _run(nc, [arrays], core_ids=[0])
    return r.results[0]["x_out"].reshape(B, S, D)
```

```python
from contextlib import ExitStack

import numpy as np
import concourse.bass as bass
from concourse import mybir

PHASES = range(8)

ALU = mybir.AluOpType
ACT = mybir.ActivationFunctionType
AX = mybir.AxisListType
F32 = mybir.dt.float32
BF16 = mybir.dt.bfloat16
I32 = mybir.dt.int32
U32 = mybir.dt.uint32

P = 128
B, S, D = 8, 256, 512
N = B * S
DC = D // P
LN_EPS = 1e-5


class Scope:

    def __init__(self, nc, ctx, name):
        self.nc, self.ctx, self.name = nc, ctx, name
        self.held = []
        ctx.callback(self.release)

    def release(self):
        if self.held:
            self.nc.clear_and_free_semaphores(self.held)
            self.nc.all_engine_barrier()

    def sb(self, name, shape, dt=F32):
        return self.ctx.enter_context(self.nc.sbuf_tensor(f"{self.name}_{name}", shape, dt))

    def ps(self, name, shape, dt=F32):
        return self.ctx.enter_context(self.nc.psum_tensor(f"{self.name}_{name}", shape, dt))

    def sem(self, name):
        self.held.append(self.nc.alloc_semaphore(f"{self.name}_{name}"))
        return self.held[-1]

    def sems(self, name, n):
        return [self.sem(f"{name}{i}") for i in range(n)]


def hold(eng, sem, val, passed):
    eng.wait_ge(sem, val)
    eng.sem_inc(passed, 1)


def rows(ap, start, count):
    return ap[bass.ds(start, count), :]


def build_setup(nc, io, keep):
    with ExitStack() as ctx:
        sc = Scope(nc, ctx, "setup")
        g_raw = sc.sb("g_raw", [P, 8])
        gamma = sc.sb("gamma", [P, 1])
        iota_i = sc.sb("iota_i", [P, 64], I32)
        spare_i = sc.sb("spare_i", [P, 1], I32)
        ints_done = sc.sem("ints_done")
        g_loaded = sc.sem("g_loaded")
        tanh_done = sc.sem("tanh_done")
        zeroed = sc.sem("zeroed")
        const_done = sc.sem("const_done")
        with nc.Block() as block:

            @block.sync
            def _(sp):
                sp.dma_start(g_raw[:, 0:4], io["g_xattn"].rearrange("(a g) -> a g", a=1).broadcast_to([P, 4])).then_inc(g_loaded, 16)
                sp.dma_start(g_raw[:, 4:8], io["g_ffn"].rearrange("(a g) -> a g", a=1).broadcast_to([P, 4])).then_inc(g_loaded, 16)
                sp.dma_start(gamma[:, :], io["gamma"].broadcast_to([P, 1])).then_inc(g_loaded, 16)

            @block.scalar
            def _(act):
                act.wait_ge(g_loaded, 48)
                nc.scalar.activation(keep["gates"][:, :], g_raw[:, :], ACT.Tanh).then_inc(tanh_done, 1)

            @block.vector
            def _(dve):
                nc.vector.memset(keep["neg_half"][:, :], -0.5)
                nc.vector.memset(keep["half"][:, :], 0.5)
                nc.vector.memset(keep["ones"][:, :], 1.0)
                dve.wait_ge(tanh_done, 1)
                nc.vector.tensor_tensor(keep["gate0"][:, :], keep["gates"][:, 0:1], gamma[:, :], ALU.mult)
                dve.wait_ge(const_done, 1)
                nc.vector.tensor_copy(keep["ident_bf"][:, :], keep["ident"][:, :])
                nc.vector.memset(keep["ones_bf"][:, :], 1.0)
                nc.vector.memset(keep["zeros_i"][:, :], 0)
                dve.wait_ge(ints_done, 4)
                nc.vector.tensor_copy(keep["earlier"][:, :], keep["earlier_f"][:, :])
                nc.vector.tensor_copy(keep["iota"][:, :], iota_i[:, :])
                nc.vector.tensor_copy(keep["spare"][:, :], spare_i[:, :])

            @block.gpsimd
            def _(pool):
                nc.gpsimd.memset(keep["ident"][:, :], 0.0).then_inc(zeroed, 1)
                nc.gpsimd.memset(keep["anti"][:, :], 0.0).then_inc(zeroed, 1)
                nc.gpsimd.memset(keep["earlier_f"][:, :], 1.0).then_inc(zeroed, 1)
                pool.wait_ge(zeroed, 3)
                nc.gpsimd.affine_select(out=keep["earlier_f"][:, :], in_=keep["earlier_f"][:, :], compare_op=ALU.is_gt, fill=0.0,
                                        base=0, pattern=[[1, P]], channel_multiplier=-1).then_inc(ints_done, 1)
                nc.gpsimd.iota(iota_i[:, :], pattern=[[1, 64]], base=0, channel_multiplier=0).then_inc(ints_done, 1)
                nc.gpsimd.iota(spare_i[:, :], pattern=[[1, 1]], base=64 * CAP, channel_multiplier=1).then_inc(ints_done, 1)
                nc.gpsimd.iota(keep["row_id"][:, :], pattern=[[P, N // P]], base=0, channel_multiplier=1).then_inc(ints_done, 1)
                nc.gpsimd.affine_select(out=keep["ident"][:, :], in_=keep["ident"][:, :], compare_op=ALU.not_equal, fill=1.0,
                                        base=0, pattern=[[-1, P]], channel_multiplier=1).then_inc(const_done, 1)
                nc.gpsimd.affine_select(out=keep["anti"][:, :], in_=keep["anti"][:, :], compare_op=ALU.not_equal, fill=1.0,
                                        base=-(P - 1), pattern=[[1, P]], channel_multiplier=1)


def build_feature_attention(nc, io, keep, x_in, x_out):
    T = S // P
    scale = float(D) ** -0.5
    with ExitStack() as ctx:
        sc = Scope(nc, ctx, "fattn")
        x_sb = sc.sb("x", [P, 2, T, D])
        k_sb = sc.sb("k", [P, 2, T, D])
        vt_sb = sc.sb("vt", [P, 2, DC, S])
        xn = sc.sb("xn", [P, 2, T, D])
        stats = sc.sb("stats", [P, T, 6])
        mv = sc.sb("mv", [P, T, 2])
        ve = sc.sb("ve", [P, T])
        rstd = sc.sb("rstd", [P, T])
        negmax = sc.sb("negmax", [P, DC])
        bias = sc.sb("bias", [P, DC])
        sums = sc.sb("sums", [P, DC])
        rsum = sc.sb("rsum", [P, DC])
        prob = sc.sb("prob", [P, DC, D])
        vs = sc.sb("vs", [P, DC, S])
        x_new = sc.sb("x_new", [P, 2, T, D])
        scores = sc.ps("scores", [P, DC, D])
        mixed = sc.ps("mixed", [P, T, D])

        loaded = sc.sems("loaded", 2)
        stored = sc.sems("stored", 2)
        inputs_free = sc.sem("inputs_free")
        passed = sc.sem("passed")
        stats_done = sc.sem("stats_done")
        var_done = sc.sem("var_done")
        ve_done = sc.sem("ve_done")
        rstd_done = sc.sem("rstd_done")
        xn_done = sc.sem("xn_done")
        scores_done = sc.sem("scores_done")
        max_done = sc.sem("max_done")
        bias_done = sc.sem("bias_done")
        prob_done = sc.sem("prob_done")
        rsum_done = sc.sem("rsum_done")
        vs_done = sc.sem("vs_done")
        mixed_done = sc.sem("mixed_done")
        out_done = sc.sem("out_done")

        with nc.Block() as block:

            @block.sync
            def _(sp):
                def load(b, u):
                    sp.wait_ge(inputs_free, b + 1)
                    sp.dma_start(x_sb[:, u], rows(x_in, b * S, S).rearrange("(t p) d -> p t d", p=P)).then_inc(loaded[u], 16)
                    sp.dma_start(k_sb[:, u], rows(io["ctx"], b * S, S).rearrange("(t p) d -> p t d", p=P)).then_inc(loaded[u], 16)
                    sp.dma_start(vt_sb[:, u], io["ctxT"][bass.ds(b, 1)].rearrange("b p c s -> p (b c) s")).then_inc(loaded[u], 16)

                load(0, 0)
                load(1, 1)
                with sp.Fori(0, B // 2 - 1) as i:
                    load(2 * i + 2, 0)
                    load(2 * i + 3, 1)

            @block.tensor
            def _(pe):
                with pe.Fori(0, B // 2) as i:
                    for u in range(2):
                        b = 2 * i + u
                        pe.wait_ge(xn_done, T * b + T)
                        for e in range(DC):
                            pe.wait_ge(prob_done, DC * b + e + 1)
                            for t in range(T):
                                mm = nc.tensor.matmul(scores[:, e, :], k_sb[:, u, t, e * P:(e + 1) * P], xn[:, u, t, :], start=t == 0, stop=t == T - 1)
                            mm.then_inc(scores_done, 1)
                        pe.wait_ge(out_done, T * b + T)
                        for e in range(DC):
                            pe.wait_ge(vs_done, DC * b + e + 1)
                            for t in range(T):
                                mm = nc.tensor.matmul(mixed[:, t, :], vs[:, e, t * P:(t + 1) * P], prob[:, e, :], start=e == 0, stop=e == DC - 1)
                        mm.then_inc(mixed_done, 1)

            @block.vector
            def _(dve):
                dve.sem_inc(inputs_free, 2)
                dve.sem_inc(out_done, T)
                dve.sem_inc(stored[0], 16)
                dve.sem_inc(stored[1], 16)
                with dve.Fori(0, B // 2) as i:
                    for u in range(2):
                        b = 2 * i + u
                        dve.wait_ge(loaded[u], 48 * i + 48)
                        for t in range(T):
                            nc.vector.bn_stats(stats[:, t, :], x_sb[:, u, t, :]).then_inc(stats_done, 1)
                        for t in range(T):
                            hold(dve, stats_done, T * b + t + 1, passed)
                            nc.vector.bn_aggr(mv[:, t, :], stats[:, t, :]).then_inc(var_done, 1)
                        dve.wait_ge(var_done, T * b + T)
                        nc.vector.tensor_scalar(ve[:, :], mv[:, :, 1], LN_EPS, None, ALU.add).then_inc(ve_done, 1)
                        dve.wait_ge(rstd_done, b + 1)
                        for t in range(T):
                            nc.vector.tensor_scalar(xn[:, u, t, :], x_sb[:, u, t, :], mv[:, t, 0:1], rstd[:, t:t + 1], ALU.subtract, ALU.mult).then_inc(xn_done, 1)
                        for e in range(DC):
                            dve.wait_ge(scores_done, DC * b + e + 1)
                            nc.vector.tensor_reduce(negmax[:, e:e + 1], scores[:, e, :], AX.X, ALU.max, negate=True).then_inc(max_done, 1)
                            dve.wait_ge(max_done, DC * b + e + 1)
                            nc.vector.tensor_scalar(bias[:, e:e + 1], negmax[:, e:e + 1], scale, None, ALU.mult).then_inc(bias_done, 1)
                        dve.wait_ge(mixed_done, b + 1)
                        for e in range(DC):
                            dve.wait_ge(prob_done, DC * b + DC + e + 1)
                            nc.vector.reciprocal(rsum[:, e:e + 1], sums[:, e:e + 1]).then_inc(rsum_done, 1)
                            dve.wait_ge(rsum_done, DC * b + e + 1)
                            nc.vector.tensor_scalar(vs[:, e, :], vt_sb[:, u, e, :], rsum[:, e:e + 1], None, ALU.mult).then_inc(vs_done, 1)
                        dve.wait_ge(mixed_done, b + 2)
                        dve.wait_ge(stored[u], 16 * i + 16)
                        for t in range(T):
                            nc.vector.scalar_tensor_tensor(out=x_new[:, u, t, :], in0=mixed[:, t, :], scalar=keep["gates"][:, 2:3], in1=x_sb[:, u, t, :],
                                                           op0=ALU.mult, op1=ALU.add).then_inc(out_done, 1)
                        dve.wait_ge(out_done, T * b + 2 * T)
                        dve.sem_inc(inputs_free, 1)

            @block.gpsimd
            def _(pool):
                pool.sem_inc(mixed_done, 1)
                with pool.Fori(0, B) as b:
                    pool.wait_ge(ve_done, b + 1)
                    nc.gpsimd.tensor_tensor(rstd[:, :], ve[:, :], keep["neg_half"][:, 0:T], ALU.pow).then_inc(rstd_done, 1)

            @block.scalar
            def _(act):
                act.sem_inc(prob_done, DC)
                with act.Fori(0, B // 2) as i:
                    for u in range(2):
                        b = 2 * i + u
                        act.wait_ge(mixed_done, b + 1)
                        for e in range(DC):
                            act.wait_ge(bias_done, DC * b + e + 1)
                            nc.scalar.activation(prob[:, e, :], scores[:, e, :], ACT.Exp, bias=bias[:, e:e + 1], scale=scale, accum_out=sums[:, e:e + 1]).then_inc(prob_done, 1)
                        act.wait_ge(out_done, T * b + 2 * T)
                        act.dma_start(rows(x_out, b * S, S).rearrange("(t p) d -> p t d", p=P), x_new[:, u]).then_inc(stored[u], 16)
                for u in range(2):
                    act.wait_ge(stored[u], 16 * (B // 2) + 16)


def build_channel_attention(nc, io, keep, x_in, x_out):
    T = S // P
    H4 = 4
    HDIM = S // 8
    QC = D // P
    GROUPS = T * QC
    UB = GROUPS * H4
    scale = float(HDIM) ** -0.5
    with ExitStack() as ctx:
        sc = Scope(nc, ctx, "cattn")
        x_sb = sc.sb("x", [P, 2, T, D])
        k_sb = sc.sb("k", [P, 2, T, D])
        vT = sc.sb("vT", [P, 2, DC, S])
        xn = sc.sb("xn", [P, 2, T, H4, D])
        stats = sc.sb("stats", [P, T, 6])
        mv = sc.sb("mv", [P, T, 2])
        ve = sc.sb("ve", [P, T])
        rstd = sc.sb("rstd", [P, T])
        rstd_h = sc.sb("rstd_h", [P, T, H4])
        head_scale = sc.sb("head_scale", [P, T, H4])
        negmax = sc.sb("negmax", [P, 2, H4])
        sums = sc.sb("sums", [P, 2, H4])
        rsum = sc.sb("rsum", [P, 2, H4, HDIM])
        prob = sc.sb("prob", [P, 2, H4, D])
        probT = sc.sb("probT", [P, T, H4, DC, D])
        rsumT_sb = sc.sb("rsumT_sb", [P, T, D])
        o_sb = sc.sb("o", [P, D])
        x_new = sc.sb("x_new", [P, T, D])
        scores = sc.ps("scores", [P, H4, D])
        turn = sc.ps("turn", [P, 2, DC, P])
        pv = sc.ps("pv", [P, D])
        rsumT = sc.ps("rsumT", [P, D])

        loaded = sc.sems("loaded", 2)
        stored = sc.sems("stored", T)
        stats_done = sc.sem("stats_done")
        var_done = sc.sem("var_done")
        ve_done = sc.sem("ve_done")
        pow_done = sc.sem("pow_done")
        rstd_done = sc.sem("rstd_done")
        xn_done = sc.sem("xn_done")
        scores_done = sc.sem("scores_done")
        max_done = sc.sem("max_done")
        exp_done = sc.sem("exp_done")
        turned = sc.sem("turned")
        act_out = sc.sem("act_out")
        dve_out = sc.sem("dve_out")
        pv_done = sc.sem("pv_done")
        rsum_done = sc.sem("rsum_done")
        rsumT_done = sc.sem("rsumT_done")
        rsumT_moved = sc.sem("rsumT_moved")
        o_done = sc.sem("o_done")
        out_done = sc.sem("out_done")
        const_done = sc.sem("const_done")
        passed = sc.sem("passed")

        def await_if(eng, sem, value):
            if not isinstance(value, int) or value > 0:
                eng.wait_ge(sem, value)

        def elements(eng, element):
            element(0, 0, 0)
            with eng.Fori(0, B // 2 - 1) as i:
                element(2 * i + 1, 1, i + 1)
                element(2 * i + 2, 0, i + 1)
            element(B - 1, 1, None)

        with nc.Block() as block:

            @block.sync
            def _(sp):
                def load(b, u):
                    sp.dma_start(x_sb[:, u], rows(x_in, b * S, S).rearrange("(t p) d -> p t d", p=P)).then_inc(loaded[u], 16)
                    sp.dma_start(k_sb[:, u], rows(io["ctx"], b * S, S).rearrange("(t p) d -> p t d", p=P)).then_inc(loaded[u], 16)
                    sp.dma_start(vT[:, u], io["ctxT"][bass.ds(b, 1)].rearrange("b p c s -> p (b c) s")).then_inc(loaded[u], 16)

                def store(b):
                    for t in range(T):
                        sp.wait_ge(out_done, T * b + t + 1)
                        sp.dma_start(rows(x_out, b * S + t * P, P), x_new[:, t]).then_inc(stored[t], 16)

                load(0, 0)
                load(1, 1)
                with sp.Fori(0, B // 2 - 1) as i:
                    for u in range(2):
                        store(2 * i + u)
                        load(2 * i + u + 2, u)
                for b in range(B - 2, B):
                    store(b)
                for t in range(T):
                    sp.wait_ge(stored[t], 16 * B + 16)

            @block.tensor
            def _(pe):
                def score(b, u, g, h):
                    n = UB * b + H4 * g + h
                    t, qc = g // QC, g % QC
                    pe.wait_ge(xn_done, T * H4 * b + H4 * t + h + 1)
                    await_if(pe, exp_done, n + 1 - H4)
                    nc.tensor.matmul(scores[:, h, :], xn[:, u, t, h, qc * P:(qc + 1) * P], k_sb[:, u, t, :], start=True, stop=True).then_inc(scores_done, 1)

                def transpose(b, g, h):
                    n = UB * b + H4 * g + h
                    pe.wait_ge(exp_done, n + 1)
                    await_if(pe, dve_out if h % 2 else act_out, 2 * (GROUPS * b + g) + h // 2)
                    for c in range(DC):
                        mm = nc.tensor.transpose(turn[:, h % 2, c, :], prob[:, g % 2, h, c * P:(c + 1) * P], keep["ident"][:, :])
                    mm.then_inc(turned, 1)

                def turn_sums(b, g):
                    q = g % QC
                    pe.wait_ge(rsum_done, GROUPS * b + g + 1)
                    if q == 0:
                        await_if(pe, rsumT_moved, T * b + g // QC)
                    nc.tensor.transpose(rsumT[:, q * P:(q + 1) * P], rsum[:, q % 2, :, :].rearrange("p h e -> p (h e)"), keep["ident"][:, :]).then_inc(rsumT_done, 1)

                def values(half, u, t, c):
                    if c == 0:
                        pe.wait_ge(act_out, 2 * QC * half + 2 * QC)
                        pe.wait_ge(dve_out, 2 * QC * half + 2 * QC)
                        await_if(pe, out_done, half)
                    for h in range(H4):
                        head = H4 * t + h
                        mm = nc.tensor.matmul(pv[h * HDIM:(h + 1) * HDIM, :], vT[:, u, c, head * HDIM:(head + 1) * HDIM], probT[:, t, h, c, :],
                                              start=c == 0, stop=c == DC - 1, tile_position=(0, h * HDIM))
                    if c == DC - 1:
                        mm.then_inc(pv_done, 1)

                def element(b, u, next_load):
                    first, last = isinstance(b, int) and b == 0, isinstance(b, int) and b == B - 1
                    for g in range(GROUPS):
                        t, q = g // QC, g % QC
                        for h in range(H4):
                            if g < GROUPS - 1:
                                score(b, u, g + 1, h)
                            elif not last:
                                score(b + 1, 1 - u, 0, h)
                            if h == 0 and not (first and g == 0):
                                turn_sums(b, g - 1)
                            transpose(b, g, h)
                            if h % 2 and q < 2 and not (first and t == 0):
                                values(T * b + t - 1, u if t else 1 - u, 1 - t, 2 * q + h // 2)

                for h in range(H4):
                    score(0, 0, 0, h)
                elements(pe, element)
                turn_sums(B - 1, GROUPS - 1)
                for c in range(DC):
                    values(T * B - 1, 1, 1, c)

            @block.vector
            def _(dve):
                def norm_stats(b, u, load):
                    dve.wait_ge(loaded[u], 48 * load + 48)
                    for t in range(T):
                        nc.vector.bn_stats(stats[:, t, :], x_sb[:, u, t, :]).then_inc(stats_done, 1)
                    hold(dve, stats_done, T * b + T, passed)
                    for t in range(T):
                        nc.vector.bn_aggr(mv[:, t, :], stats[:, t, :]).then_inc(var_done, 1)
                    dve.wait_ge(var_done, T * b + T)
                    nc.vector.tensor_scalar(ve[:, :], mv[:, :, 1], LN_EPS, None, ALU.add).then_inc(ve_done, 1)

                def norm(b, u, j):
                    t, h = j // H4, j % H4
                    dve.wait_ge(rstd_done, b + 1)
                    nc.vector.tensor_scalar(xn[:, u, t, h, :], x_sb[:, u, t, :], mv[:, t, 0:1], rstd_h[:, t, h:h + 1], ALU.subtract, ALU.mult).then_inc(xn_done, 1)

                def maximum(b, g, h):
                    dve.wait_ge(scores_done, UB * b + H4 * g + h + 1)
                    nc.vector.tensor_reduce(negmax[:, g % 2, h:h + 1], scores[:, h, :], AX.X, ALU.max, negate=True).then_inc(max_done, 1)

                def evacuate(b, g, h):
                    t, q = g // QC, g % QC
                    dve.wait_ge(turned, UB * b + H4 * g + h + 1)
                    await_if(dve, pv_done, T * b + t - 1)
                    nc.vector.tensor_copy(probT[:, t, h, :, q * P:(q + 1) * P], turn[:, h % 2, :, :]).then_inc(dve_out, 1)

                def invert(b, g):
                    G = GROUPS * b + g
                    dve.wait_ge(exp_done, H4 * G + H4)
                    await_if(dve, rsumT_done, G - 1)
                    nc.vector.reciprocal(rsum[:, g % 2, :, :], sums[:, g % 2, :].rearrange("p (h e) -> p h e", e=1).broadcast_to([P, H4, HDIM])).then_inc(rsum_done, 1)

                def finish(b, u, t):
                    half = T * b + t
                    dve.wait_ge(pv_done, half + 1)
                    dve.wait_ge(rsumT_moved, half + 1)
                    await_if(dve, out_done, half)
                    nc.vector.tensor_tensor(o_sb[:, :], pv[:, :], rsumT_sb[:, t, :], ALU.mult).then_inc(o_done, 1)
                    dve.wait_ge(o_done, half + 1)
                    dve.wait_ge(stored[t], 16 * b + 16)
                    nc.vector.scalar_tensor_tensor(out=x_new[:, t, :], in0=o_sb[:, :], scalar=keep["gate0"][:, 0:1], in1=x_sb[:, u, t, :],
                                                   op0=ALU.mult, op1=ALU.add).then_inc(out_done, 1)

                def element(b, u, next_load):
                    first, last = isinstance(b, int) and b == 0, isinstance(b, int) and b == B - 1
                    for g in range(GROUPS):
                        if g == QC and not last:
                            norm_stats(b + 1, 1 - u, next_load)
                        for h in range(H4):
                            if h % 2:
                                evacuate(b, g, h)
                            if g < GROUPS - 1:
                                maximum(b, g + 1, h)
                            elif not last:
                                maximum(b + 1, 0, h)
                            if g > QC and not last and h < H4 - 1:
                                j = (g - QC - 1) * (H4 - 1) + h
                                if j < T * H4:
                                    norm(b + 1, 1 - u, j)
                        invert(b, g)
                        if g == 1 and not first:
                            finish(b - 1, 1 - u, 1)
                        if g == QC + 1:
                            finish(b, u, 0)

                for t in range(T):
                    dve.sem_inc(stored[t], 16)
                nc.vector.memset(head_scale[:, :, :], 0.0).then_inc(const_done, 1)
                dve.wait_ge(const_done, 1)
                for h in range(H4):
                    nc.vector.memset(head_scale[h * HDIM:(h + 1) * HDIM, :, h:h + 1], scale).then_inc(const_done, 1)
                norm_stats(0, 0, 0)
                for j in range(T * H4):
                    norm(0, 0, j)
                for h in range(H4):
                    maximum(0, 0, h)
                elements(dve, element)
                finish(B - 1, 1, 1)

            @block.gpsimd
            def _(pool):
                pool.wait_ge(const_done, 1 + H4)
                with pool.Fori(0, B) as b:
                    pool.wait_ge(ve_done, b + 1)
                    nc.gpsimd.tensor_tensor(rstd[:, :], ve[:, :], keep["neg_half"][:, 0:T], ALU.pow).then_inc(pow_done, 1)
                    pool.wait_ge(pow_done, b + 1)
                    nc.gpsimd.tensor_tensor(rstd_h[:, :, :], rstd[:, :].rearrange("p (t e) -> p t e", e=1).broadcast_to([P, T, H4]),
                                            head_scale[:, :, :], ALU.mult).then_inc(rstd_done, 1)

            @block.scalar
            def _(act):
                def exponential(b, g, h):
                    n = UB * b + H4 * g + h
                    if h == 0:
                        await_if(act, rsum_done, GROUPS * b + g - 1)
                    await_if(act, turned, n + 1 - 2 * H4)
                    act.wait_ge(max_done, n + 1)
                    nc.scalar.activation(prob[:, g % 2, h, :], scores[:, h, :], ACT.Exp, bias=negmax[:, g % 2, h:h + 1], accum_out=sums[:, g % 2, h:h + 1]).then_inc(exp_done, 1)

                def evacuate(b, g, h):
                    t, q = g // QC, g % QC
                    act.wait_ge(turned, UB * b + H4 * g + h + 1)
                    await_if(act, pv_done, T * b + t - 1)
                    nc.scalar.activation(probT[:, t, h, :, q * P:(q + 1) * P], turn[:, h % 2, :, :], ACT.Copy).then_inc(act_out, 1)

                def move_sums(b, t):
                    half = T * b + t
                    act.wait_ge(rsumT_done, QC * half + QC)
                    await_if(act, out_done, half - 1)
                    nc.scalar.activation(rsumT_sb[:, t, :], rsumT[:, :], ACT.Copy).then_inc(rsumT_moved, 1)

                def element(b, u, next_load):
                    first, last = isinstance(b, int) and b == 0, isinstance(b, int) and b == B - 1
                    for g in range(GROUPS):
                        for h in range(H4):
                            if h % 2 == 0:
                                evacuate(b, g, h)
                            if g < GROUPS - 1:
                                exponential(b, g + 1, h)
                            elif not last:
                                exponential(b + 1, 0, h)
                        if g == 0 and not first:
                            move_sums(b - 1, 1)
                        if g == QC:
                            move_sums(b, 0)

                for h in range(H4):
                    exponential(0, 0, h)
                elements(act, element)
                move_sums(B - 1, 1)


F32R = mybir.dt.float32r
BLK = 512
NB = N // BLK
TB = BLK // P
HC = 11
HPAD = HC * P
TERNARY_HIDDEN = 1365
LUT_HIDDEN = 1376
LUT_SIZE = 16
LUT_FIRST = {"experts": 0, "combine": 8, 2: 12, 3: 20, "end": 24}
WCOLS = DC * HPAD


def build_ternary_weights(nc, io, keep, weights, scales):
    with ExitStack() as ctx:
        sc = Scope(nc, ctx, "tern")
        raw = sc.sb("raw", [P, 2, WCOLS])
        low = sc.sb("low", [P, WCOLS], BF16)
        part = sc.sb("part", [P, 3])
        thr = sc.sb("thr", [P, 3])
        nthr = sc.sb("nthr", [P, 3])
        total = sc.ps("total", [P, 512])
        loaded = sc.sems("loaded", 2)
        part_done = sc.sem("part_done")
        total_done = sc.sem("total_done")
        scale_done = sc.sem("scale_done")
        thr_done = sc.sem("thr_done")
        low_done = sc.sem("low_done")
        weight_done = sc.sem("weight_done")
        with nc.Block() as block:

            @block.sync
            def _(sp):
                for m, name in enumerate(("w1t", "w3t", "w2t")):
                    if m == 2:
                        sp.wait_ge(weight_done, 1)
                    sp.dma_start(raw[:, m % 2, :], io[name]).then_inc(loaded[m % 2], 16)

            @block.tensor
            def _(pe):
                for m in range(3):
                    pe.wait_ge(part_done, m + 1)
                    nc.tensor.matmul(total[:, m:m + 1], keep["ones"][:, :], part[:, m:m + 1], start=True, stop=True).then_inc(total_done, 1)

            @block.vector
            def _(dve):
                for m in range(3):
                    w = raw[:, m % 2, :]
                    dve.wait_ge(loaded[m % 2], 16 * (m // 2) + 16)
                    nc.vector.tensor_reduce(part[:, m:m + 1], w, AX.X, ALU.add, apply_absolute_value=True).then_inc(part_done, 1)
                    dve.wait_ge(total_done, m + 1)
                    nc.vector.tensor_scalar(scales[:, m:m + 1], total[:, m:m + 1], 1.0 / (TERNARY_HIDDEN * D), None, ALU.mult).then_inc(scale_done, 1)
                    dve.wait_ge(scale_done, m + 1)
                    nc.vector.tensor_scalar(thr[:, m:m + 1], scales[:, m:m + 1], 0.5, None, ALU.mult).then_inc(thr_done, 1)
                    nc.vector.tensor_scalar(nthr[:, m:m + 1], scales[:, m:m + 1], -0.5, None, ALU.mult).then_inc(thr_done, 1)
                    dve.wait_ge(thr_done, 2 * m + 2)
                    nc.vector.tensor_scalar(low[:, :], w, nthr[:, m:m + 1], None, ALU.is_lt).then_inc(low_done, 1)
                    dve.wait_ge(low_done, m + 1)
                    nc.vector.scalar_tensor_tensor(out=weights[:, m, :], in0=w, scalar=thr[:, m:m + 1], in1=low[:, :], op0=ALU.is_gt, op1=ALU.subtract).then_inc(weight_done, 1)


class LutDecoder:
    CH = 704
    CHUNKS = 3 * WCOLS // CH
    K = LUT_SIZE

    def __init__(self, nc, io, sc, first):
        self.nc, self.io, self.first = nc, io, first
        self.lut = sc.sb("lut", [P, self.K])
        self.idx = sc.sb("lut_idx", [P, self.CH], I32)
        self.idxb = sc.sb("lut_idxb", [P, self.CH], BF16)
        self.mask = sc.sb("lut_mask", [P, 2, self.CH], BF16)
        self.acc = sc.sb("lut_acc", [P, 2, self.CH])
        self.out = sc.sb("lut_out", [P, self.CH])
        self.table_loaded = sc.sem("lut_table_loaded")
        self.idx_loaded = sc.sem("lut_idx_loaded")
        self.idxb_done = sc.sem("lut_idxb_done")
        self.mask_done = sc.sem("lut_mask_done")
        self.acc_done = sc.sem("lut_acc_done")
        self.stored = sc.sem("lut_stored")

    def columns(self, c):
        return bass.ds((self.first + c) * self.CH, self.CH)

    def load_table(self, sp):
        sp.dma_start(self.lut[:, :], self.io["lut"].rearrange("(a g) -> a g", a=1).broadcast_to([P, self.K])).then_inc(self.table_loaded, 16)

    def load(self, sp, c):
        sp.wait_ge(self.idxb_done, c + 1)
        sp.dma_start(self.idx[:, :], self.io["lut_idx"][:, self.columns(c)]).then_inc(self.idx_loaded, 16)

    def store(self, sp, c):
        sp.wait_ge(self.acc_done, self.K * (c + 1) + 2)
        sp.dma_start(self.io["lut_weights"][:, self.columns(c)], self.out[:, :]).then_inc(self.stored, 16)

    def finish(self, sp, chunks):
        sp.wait_ge(self.stored, 16 * chunks + 16)

    def begin(self, dve):
        for sem, n in ((self.idxb_done, 1), (self.mask_done, 1), (self.acc_done, 2), (self.stored, 16)):
            dve.sem_inc(sem, n)
        dve.wait_ge(self.table_loaded, 16)

    def step(self, dve, c, k):
        nc, K = self.nc, self.K
        if k == 0:
            dve.wait_ge(self.idx_loaded, 16 * c + 16)
            dve.wait_ge(self.mask_done, K * c + 1)
            nc.vector.tensor_copy(self.idxb[:, :], self.idx[:, :]).then_inc(self.idxb_done, 1)
            dve.wait_ge(self.idxb_done, c + 2)
        dve.wait_ge(self.acc_done, K * c + k + 1)
        nc.vector.tensor_scalar(self.mask[:, k % 2, :], self.idxb[:, :], float(k), None, ALU.is_equal).then_inc(self.mask_done, 1)
        dve.wait_ge(self.mask_done, K * c + k + 2)
        dve.wait_ge(self.acc_done, K * c + k + 2)
        if k == 0:
            nc.vector.tensor_scalar(self.acc[:, 0, :], self.mask[:, 0, :], self.lut[:, 0:1], None, ALU.mult).then_inc(self.acc_done, 1)
        else:
            if k == K - 1:
                dve.wait_ge(self.stored, 16 * c + 16)
            out = self.acc[:, k % 2, :] if k < K - 1 else self.out[:, :]
            nc.vector.scalar_tensor_tensor(out=out, in0=self.mask[:, k % 2, :], scalar=self.lut[:, k:k + 1], in1=self.acc[:, (k - 1) % 2, :],
                                           op0=ALU.mult, op1=ALU.add).then_inc(self.acc_done, 1)

    def steps(self, dve, first, begin, end):
        for n in range(begin, end):
            self.step(dve, first + n // self.K, n % self.K)


def build_ffn(nc, io, keep, x_in, x_out, ternary):
    name = "tffn" if ternary else "lffn"
    hidden = TERNARY_HIDDEN if ternary else LUT_HIDDEN
    gate = keep["gates"][:, 5:6] if ternary else keep["gates"][:, 7:8]
    parts = 2 if ternary else 1
    WDT = F32R if ternary else F32
    with ExitStack() as outer:
        osc = Scope(nc, outer, name)
        weights = osc.sb("weights", [P, 3, WCOLS], WDT)
        scales = osc.sb("scales", [P, 3])
        if ternary:
            build_ternary_weights(nc, io, keep, weights, scales)
        w1 = weights[:, 0, :].rearrange("p (c h) -> p c h", c=DC)
        w3 = weights[:, 1, :].rearrange("p (c h) -> p c h", c=DC)
        w2 = weights[:, 2, :].rearrange("p (j d) -> p j d", j=HC)
        HM = [min(P, (P * HC if ternary else hidden) - P * j) for j in range(HC)]
        with ExitStack() as ctx:
            sc = Scope(nc, ctx, name)
            x_ln = sc.sb("x_ln", [P, TB, D])
            x_res = sc.sb("x_res", [P, TB, D])
            xn = sc.sb("xn", [P, TB, D])
            xnT = [sc.sb(f"xnT{q}", [P, DC, BLK], WDT) for q in range(parts)]
            stats = sc.sb("stats", [P, TB, 6])
            mv = sc.sb("mv", [P, TB, 2])
            ve = sc.sb("ve", [P, TB])
            rstd = sc.sb("rstd", [P, TB])
            sil = sc.sb("sil", [P, 2, BLK])
            g32 = sc.sb("g32", [P, 2, BLK])
            gp = [sc.sb(f"g_part{q}", [P, 2, BLK], WDT) for q in range(parts)] if ternary else [g32]
            x_new = sc.sb("x_new", [P, TB, D])
            lut = LutDecoder(nc, io, sc, LUT_FIRST[3]) if ternary else None
            LC = LUT_FIRST["end"] - LUT_FIRST[3]
            LI = LC // NB
            out_scale = sc.sb("out_scale", [P, 1])
            s23 = sc.sb("s23", [P, 1])
            h1 = sc.ps("h1", [P, 2, BLK])
            h3 = sc.ps("h3", [P, 2, BLK])
            y = sc.ps("y", [P, TB, D])

            w_loaded = sc.sems("w_loaded", 3)
            ln_loaded = sc.sem("ln_loaded")
            res_loaded = sc.sem("res_loaded")
            stored = sc.sem("stored")
            ln_free = sc.sem("ln_free")
            res_free = sc.sem("res_free")
            stats_done = sc.sem("stats_done")
            var_done = sc.sem("var_done")
            ve_done = sc.sem("ve_done")
            rstd_done = sc.sem("rstd_done")
            xn_done = sc.sem("xn_done")
            turned = sc.sem("turned")
            hi_done = sc.sem("hi_done")
            lo_done = sc.sem("lo_done")
            h1_done = sc.sem("h1_done")
            h3_done = sc.sem("h3_done")
            sil_done = sc.sem("sil_done")
            g_done = sc.sem("g_done")
            ghi_done = sc.sem("ghi_done")
            glo_done = sc.sem("glo_done")
            y_step = sc.sem("y_step")
            out_done = sc.sem("out_done")
            scale_done = sc.sem("scale_done")
            passed = sc.sem("passed")
            dve_passed = sc.sem("dve_passed")
            g_ready = glo_done if ternary else g_done

            def left(i, j):
                return HC * i + j + 1 + (j == 0)

            with nc.Block() as block:

                @block.sync
                def _(sp):
                    def load_ln(i):
                        sp.wait_ge(ln_free, i + 1)
                        sp.dma_start(x_ln[:, :, :], rows(x_in, i * BLK, BLK).rearrange("(t p) d -> p t d", p=P)).then_inc(ln_loaded, 16)

                    def load_res(i):
                        sp.wait_ge(res_free, i + 1)
                        sp.dma_start(x_res[:, :, :], rows(x_in, i * BLK, BLK).rearrange("(t p) d -> p t d", p=P)).then_inc(res_loaded, 16)

                    def iteration(i, last):
                        if not last:
                            load_ln(i + 1)
                        if ternary:
                            for n in range(LI):
                                if not (last and n == LI - 1):
                                    lut.load(sp, LI * i + n + 1)
                                lut.store(sp, LI * i + n)
                        if not last:
                            load_res(i + 1)

                    load_ln(0)
                    if ternary:
                        lut.load_table(sp)
                        lut.load(sp, 0)
                    else:
                        for m in range(3):
                            sp.dma_start(weights[:, m, :], io["lut_weights"][:, m * WCOLS:(m + 1) * WCOLS]).then_inc(w_loaded[m], 16)
                    load_res(0)
                    with sp.Fori(0, NB - 1) as i:
                        iteration(i, False)
                    iteration(NB - 1, True)
                    if ternary:
                        lut.finish(sp, LC)

                @block.tensor
                def _(pe):
                    def turn(i):
                        pe.wait_ge(sil_done, HC * i + 2)
                        pe.wait_ge(g_done, HC * i + 2)
                        for c in range(DC):
                            bank = (h1, h3)[c // 2][:, c % 2, :]
                            for t in range(TB):
                                if c == 0:
                                    pe.wait_ge(xn_done, TB * i + t + 1)
                                mm = nc.tensor.transpose(bank[:, t * P:(t + 1) * P], xn[:, t, c * P:(c + 1) * P], keep["ident"][:, :])
                            mm.then_inc(turned, 1)

                    def down(i, j):
                        if j == 0:
                            pe.wait_ge(out_done, TB * i + TB)
                        pe.wait_ge(g_ready, HC * i + j + 1 + (0 if ternary else 2))
                        for t in range(TB):
                            for q in range(parts):
                                mm = nc.tensor.matmul(y[:, t, :], gp[q][0:HM[j], j % 2, t * P:(t + 1) * P], w2[0:HM[j], j, :],
                                                      start=j == 0 and q == 0, stop=j == HC - 1 and q == parts - 1)
                        mm.then_inc(y_step, 1)

                    def main(i):
                        pe.wait_ge(lo_done if ternary else hi_done, DC * i + DC)
                        for j in range(HC):
                            for w, h, done, used in ((w1, h1, h1_done, sil_done), (w3, h3, h3_done, g_done)):
                                pe.wait_ge(used, left(i, j))
                                n = 0
                                for c in range(DC):
                                    for q in range(parts):
                                        mm = nc.tensor.matmul(h[0:HM[j], j % 2, :], w[:, c, j * P:j * P + HM[j]], xnT[q][:, c, :],
                                                              start=n == 0, stop=n == DC * parts - 1)
                                        n += 1
                                mm.then_inc(done, 1)
                            if j >= 1:
                                down(i, j - 1)
                        down(i, HC - 1)

                    turn(0)
                    if not ternary:
                        for m in range(3):
                            pe.wait_ge(w_loaded[m], 16)
                    with pe.Fori(0, NB - 1) as i:
                        main(i)
                        turn(i + 1)
                    main(NB - 1)

                @block.vector
                def _(dve):
                    def norm(i):
                        dve.wait_ge(ln_loaded, 16 * i + 16)
                        for t in range(TB):
                            nc.vector.bn_stats(stats[:, t, :], x_ln[:, t, :]).then_inc(stats_done, 1)
                        hold(dve, stats_done, TB * i + TB, dve_passed)
                        for t in range(TB):
                            nc.vector.bn_aggr(mv[:, t, :], stats[:, t, :]).then_inc(var_done, 1)
                        dve.wait_ge(var_done, TB * i + TB)
                        nc.vector.tensor_scalar(ve[:, :], mv[:, :, 1], LN_EPS, None, ALU.add).then_inc(ve_done, 1)
                        dve.wait_ge(rstd_done, i + 1)
                        dve.wait_ge(turned, DC * i + 1)
                        for t in range(TB):
                            nc.vector.tensor_scalar(xn[:, t, :], x_ln[:, t, :], mv[:, t, 0:1], rstd[:, t:t + 1], ALU.subtract, ALU.mult).then_inc(xn_done, 1)
                        dve.wait_ge(xn_done, TB * i + TB)
                        dve.sem_inc(ln_free, 1)

                    def evacuate_low(i):
                        for c in range(DC):
                            dve.wait_ge(turned, DC * i + c + 2)
                            dve.wait_ge(hi_done, DC * i + c + 1)
                            nc.vector.tensor_tensor(xnT[1][:, c, :], (h1, h3)[c // 2][:, c % 2, :], xnT[0][:, c, :].bitcast(F32), ALU.subtract).then_inc(lo_done, 1)

                    def main(i, next_norm):
                        for j in range(HC):
                            m = HM[j]
                            dve.wait_ge(sil_done, HC * i + j + 3)
                            dve.wait_ge(h3_done, HC * i + j + 1)
                            if not ternary:
                                dve.wait_ge(y_step, left(i, j))
                            nc.vector.tensor_tensor(g32[0:m, j % 2, :], sil[0:m, j % 2, :], h3[0:m, j % 2, :], ALU.mult).then_inc(g_done, 1)
                            if ternary:
                                dve.wait_ge(y_step, left(i, j))
                                dve.wait_ge(ghi_done, HC * i + j + 1)
                                nc.vector.tensor_tensor(gp[1][0:m, j % 2, :], g32[0:m, j % 2, :], gp[0][0:m, j % 2, :].bitcast(F32), ALU.subtract).then_inc(glo_done, 1)
                            if ternary:
                                lut.steps(dve, LI * i, LI * LUT_SIZE * j // HC, LI * LUT_SIZE * (j + 1) // HC)
                            if j == 2 and next_norm:
                                norm(i + 1)

                    def finish(i):
                        dve.wait_ge(res_loaded, 16 * i + 16)
                        dve.wait_ge(stored, 16 * i + 16)
                        dve.wait_ge(y_step, HC * i + HC + 2)
                        for t in range(TB):
                            nc.vector.scalar_tensor_tensor(out=x_new[:, t, :], in0=y[:, t, :], scalar=out_scale[:, 0:1], in1=x_res[:, t, :],
                                                           op0=ALU.mult, op1=ALU.add).then_inc(out_done, 1)
                        dve.wait_ge(out_done, TB * i + 2 * TB)
                        dve.sem_inc(res_free, 1)

                    for sem, n in ((ln_free, 1), (res_free, 1), (out_done, TB), (turned, 1), (g_done, 2), (sil_done, 2), (y_step, 2), (stored, 16)):
                        dve.sem_inc(sem, n)
                    if ternary:
                        nc.vector.tensor_tensor(s23[:, :], scales[:, 1:2], scales[:, 2:3], ALU.mult).then_inc(scale_done, 1)
                        dve.wait_ge(scale_done, 1)
                        nc.vector.tensor_tensor(out_scale[:, :], s23[:, :], gate, ALU.mult)
                    else:
                        nc.vector.tensor_copy(out_scale[:, :], gate)
                    norm(0)
                    if ternary:
                        lut.begin(dve)
                        evacuate_low(0)
                    with dve.Fori(0, NB - 1) as i:
                        main(i, True)
                        if ternary:
                            evacuate_low(i + 1)
                        finish(i)
                    main(NB - 1, False)
                    finish(NB - 1)

                @block.gpsimd
                def _(pool):
                    with pool.Fori(0, NB) as i:
                        pool.wait_ge(ve_done, i + 1)
                        nc.gpsimd.tensor_tensor(rstd[:, :], ve[:, :], keep["neg_half"][:, 0:TB], ALU.pow).then_inc(rstd_done, 1)

                @block.scalar
                def _(act):
                    def evacuate(i):
                        for c in range(DC):
                            act.wait_ge(turned, DC * i + c + 2)
                            nc.scalar.activation(xnT[0][:, c, :], (h1, h3)[c // 2][:, c % 2, :], ACT.Copy).then_inc(hi_done, 1)

                    def main(i):
                        for j in range(HC):
                            m = HM[j]
                            act.wait_ge(h1_done, HC * i + j + 1)
                            act.wait_ge(g_done, left(i, j))
                            nc.scalar.activation(sil[0:m, j % 2, :], h1[0:m, j % 2, :], ACT.Silu, scale=scales[0:m, 0:1] if ternary else 1.0).then_inc(sil_done, 1)
                            if ternary:
                                act.wait_ge(y_step, left(i, j))
                                act.wait_ge(g_done, HC * i + j + 3)
                                nc.scalar.activation(gp[0][0:m, j % 2, :], g32[0:m, j % 2, :], ACT.Copy).then_inc(ghi_done, 1)

                    def store(i):
                        act.wait_ge(out_done, TB * i + 2 * TB)
                        act.dma_start(rows(x_out, i * BLK, BLK).rearrange("(t p) d -> p t d", p=P), x_new[:, :, :]).then_inc(stored, 16)

                    evacuate(0)
                    with act.Fori(0, NB - 1) as i:
                        main(i)
                        evacuate(i + 1)
                        store(i)
                    main(NB - 1)
                    store(NB - 1)
                    act.wait_ge(stored, 16 * NB + 16)


def build_ternary_ffn(nc, io, keep, x_in, x_out):
    build_ffn(nc, io, keep, x_in, x_out, True)


def build_lut_ffn(nc, io, keep, x_in, x_out):
    build_ffn(nc, io, keep, x_in, x_out, False)


HEADS = 16
HD = D // HEADS
FD = 64
VE = HD + 1
LB = 512
LT = LB // P


class Fills:

    def __init__(self, plan):
        self.names = [name for name, _ in plan]
        self.engine = [e for _, e in plan]
        self.count = len(plan)
        self.per = {e: self.engine.count(e) for e in ("act", "dve")}
        self.place = {name: n for n, name in enumerate(self.names)}

    def filled(self, i, name):
        return self.count * i + self.place[name] + 1

    def emptied(self, i, name):
        n = self.place[name]
        e = self.engine[n]
        return e, self.per[e] * (i + 1) + self.engine[:n].count(e) + 1

    def bank_free(self, i, name):
        n = self.place[name]
        if n >= 8:
            return self.emptied(i, self.names[n - 8])
        before = max(m for m in range(self.count) if m % 8 == n % 8)
        return self.emptied(i - 1, self.names[before])


def build_linear_attention(nc, io, keep, x_in, x_out):
    PAIRS = HEADS // 2
    EB = LB // S
    NIT = N // LB
    with ExitStack() as ctx:
        sc = Scope(nc, ctx, "lin")
        wq, wk, wv, wo = (sc.sb(n, [P, DC, D]) for n in ("wq", "wk", "wv", "wo"))
        bq, bk = (sc.sb(n, [P, DC]) for n in ("bq", "bk"))
        bv, bo = (sc.sb(n, [P, D]) for n in ("bv", "bo"))
        fmap_q = sc.sb("fmap_q", [P, 4 * FD])
        fmap_k = sc.sb("fmap_k", [P, 4 * FD])
        mask = sc.sb("mask", [P, N // P])
        x_sb = sc.sb("x", [P, LT, D])
        x_res = sc.sb("x_res", [P, LT, D])
        cT = sc.sb("cT", [P, EB, DC, S])
        xn = sc.sb("xn", [P, LT, D])
        xnT = sc.sb("xnT", [P, DC, LB])
        qT = sc.sb("qT", [P, DC, LB])
        kT = sc.sb("kT", [P, DC, LB])
        v = sc.sb("v", [P, LT, HEADS, VE])
        qf = sc.sb("qf", [P, PAIRS, LB])
        kf = sc.sb("kf", [P, LT, HEADS * FD])
        kvd = sc.sb("kvd", [P, EB, PAIRS, 2 * VE])
        den = sc.sb("den", [P, LT, HEADS])
        rden = sc.sb("rden", [P, LT, HEADS])
        att = sc.sb("att", [P, LT, D])
        attT = sc.sb("attT", [P, DC, LB])
        proj = sc.sb("proj", [P, LT, D])
        x_new = proj
        stats = sc.sb("stats", [P, LT, 6])
        mv = sc.sb("mv", [P, LT, 2])
        ve = sc.sb("ve", [P, LT])
        rstd = sc.sb("rstd", [P, LT])
        bank = sc.ps("bank", [P, 8, 512])
        lut = LutDecoder(nc, io, sc, LUT_FIRST[2])
        LI = (LUT_FIRST[3] - LUT_FIRST[2]) // NIT

        weights_loaded = sc.sem("weights_loaded")
        x_loaded = sc.sem("x_loaded")
        res_loaded = sc.sem("res_loaded")
        c_loaded = sc.sem("c_loaded")
        x_free = sc.sem("x_free")
        c_free = sc.sem("c_free")
        res_free = sc.sem("res_free")
        stored = sc.sem("stored")
        stats_done = sc.sem("stats_done")
        var_done = sc.sem("var_done")
        ve_done = sc.sem("ve_done")
        rstd_done = sc.sem("rstd_done")
        xn_done = sc.sem("xn_done")
        setup_done = sc.sem("setup_done")
        filled = sc.sem("filled")
        emptied = {"act": sc.sem("act_emptied"), "dve": sc.sem("dve_emptied")}
        den_done = sc.sem("den_done")
        rden_done = sc.sem("rden_done")
        add_done = sc.sem("add_done")
        out_done = sc.sem("out_done")
        passed = sc.sem("passed")
        pe_passed = sc.sem("pe_passed")

        plan = Fills([(("kT", o), "act") for o in range(DC)] + [(("v", t), "dve") for t in range(LT)] + [(("xnT", c), "act") for c in range(DC)]
                     + [(("qT", o), "act") for o in range(DC)] + [(("kf", t, h), "dve") for t in range(LT) for h in range(2)]
                     + [(("qf", p), "act") for p in range(PAIRS)] + [(("kv", e, h), "act") for e in range(EB) for h in range(2)]
                     + [(("att", t, h), "dve") for t in range(LT) for h in range(2)] + [(("attT", c), "act") for c in range(DC)]
                     + [(("out", t), "dve") for t in range(LT)])

        def at(name):
            return bank[:, plan.place[name] % 8, :]

        def wait_emptied(eng, i, *names):
            for name in names:
                e, value = plan.emptied(i, name)
                eng.wait_ge(emptied[e], value)

        with nc.Block() as block:

            @block.sync
            def _(sp):
                sp.dma_start(x_sb[:, :, :], rows(x_in, 0, LB).rearrange("(t p) d -> p t d", p=P)).then_inc(x_loaded, 16)
                sp.dma_start(cT[:, :, :, :], io["ctxT"][0:EB].rearrange("b p c s -> p b c s")).then_inc(c_loaded, 16)
                for w, n in ((wk, "wk"), (wv, "wv"), (wq, "wq"), (wo, "wo")):
                    sp.dma_start(w[:, :, :], io[n].rearrange("p (c o) -> p c o", c=DC)).then_inc(weights_loaded, 16)
                for w, n in ((bq, "bq"), (bk, "bk")):
                    sp.dma_start(w[:, :], io[n]).then_inc(weights_loaded, 16)
                for w, n in ((bv, "bv"), (bo, "bo")):
                    sp.dma_start(w[:, :], io[n].broadcast_to([P, D])).then_inc(weights_loaded, 16)
                sp.dma_start(mask[:, :], io["mask"]).then_inc(weights_loaded, 16)
                sp.wait_ge(setup_done, 4)
                for m, n in ((fmap_q, "wqf"), (fmap_k, "wkf")):
                    for h in range(4):
                        sp.dma_start(m[h * HD:(h + 1) * HD, h * FD:(h + 1) * FD], io[n]).then_inc(weights_loaded, 16)
                def load_c(i):
                    sp.wait_ge(c_free, i)
                    sp.dma_start(cT[:, :, :, :], io["ctxT"][bass.ds(EB * i, EB)].rearrange("b p c s -> p b c s")).then_inc(c_loaded, 16)

                def load_x(i):
                    sp.wait_ge(x_free, i)
                    sp.dma_start(x_sb[:, :, :], rows(x_in, i * LB, LB).rearrange("(t p) d -> p t d", p=P)).then_inc(x_loaded, 16)

                def load_res(i):
                    sp.wait_ge(res_free, i + 1)
                    sp.dma_start(x_res[:, :, :], rows(x_in, i * LB, LB).rearrange("(t p) d -> p t d", p=P)).then_inc(res_loaded, 16)

                def iteration(i, last):
                    if not last:
                        load_x(i + 1)
                    for n in range(LI):
                        if n == 1 and not last:
                            load_c(i + 1)
                        if not (last and n == LI - 1):
                            lut.load(sp, LI * i + n + 1)
                        lut.store(sp, LI * i + n)
                    if not last:
                        load_res(i + 1)

                lut.load_table(sp)
                lut.load(sp, 0)
                load_res(0)
                with sp.Fori(0, NIT - 1) as i:
                    iteration(i, False)
                iteration(NIT - 1, True)
                lut.finish(sp, LI * NIT)

            @block.tensor
            def _(pe):
                def begin(i, name):
                    e, value = plan.bank_free(i, name)
                    pe.wait_ge(emptied[e], value)
                    return at(name)

                def projection(i, name, lhsT, rhs):
                    out = begin(i, name)
                    for c in range(DC):
                        mm = nc.tensor.matmul(out, lhsT(c), rhs(c), start=c == 0, stop=c == DC - 1)
                    mm.then_inc(filled, 1)

                pe.wait_ge(weights_loaded, 16 * 17)
                pe.wait_ge(setup_done, 6)
                with pe.Fori(0, NIT) as i:
                    pe.wait_ge(c_loaded, 16 * i + 16)
                    for o in range(DC):
                        projection(i, ("kT", o), lambda c: wk[:, c, o * P:(o + 1) * P], lambda c: cT[:, :, c, :])
                    for t in range(LT):
                        projection(i, ("v", t), lambda c: cT[:, t // 2, c, (t % 2) * P:(t % 2 + 1) * P], lambda c: wv[:, c, :])
                    pe.wait_ge(xn_done, LT * i + LT)
                    for c in range(DC):
                        out = begin(i, ("xnT", c))
                        for t in range(LT):
                            mm = nc.tensor.transpose(out[:, t * P:(t + 1) * P], xn[:, t, c * P:(c + 1) * P], keep["ident"][:, :])
                        mm.then_inc(filled, 1)
                    wait_emptied(pe, i, ("xnT", DC - 1))
                    for o in range(DC):
                        projection(i, ("qT", o), lambda c: wq[:, c, o * P:(o + 1) * P], lambda c: xnT[:, c, :])
                    wait_emptied(pe, i, ("kT", DC - 1))
                    for t in range(LT):
                        for h in range(2):
                            out = begin(i, ("kf", t, h))
                            for q in range(2):
                                mm = nc.tensor.matmul(out[:, q * 256:(q + 1) * 256], kT[:, 2 * h + q, t * P:(t + 1) * P], fmap_k[:, :], start=True, stop=True)
                            mm.then_inc(filled, 1)
                    for p in range(PAIRS):
                        wait_emptied(pe, i, ("qT", p // 2))
                        out = begin(i, ("qf", p))
                        nc.tensor.matmul(out, fmap_q[:, (p % 2) * P:(p % 2 + 1) * P], qT[:, p // 2, :], start=True, stop=True).then_inc(filled, 1)
                    for e in range(EB):
                        wait_emptied(pe, i, ("v", LT - 1), ("kf", 2 * e + 1, 1))
                        for h in range(2):
                            out = begin(i, ("kv", e, h))
                            for q in range(4):
                                p = 4 * h + q
                                for t in (2 * e, 2 * e + 1):
                                    mm = nc.tensor.matmul(out[:, q * 2 * VE:(q + 1) * 2 * VE], kf[:, t, p * P:(p + 1) * P],
                                                          v[:, t, 2 * p:2 * p + 2, :].rearrange("p h e -> p (h e)"), start=t == 2 * e, stop=t == 2 * e + 1)
                            mm.then_inc(filled, 1)
                    for t in range(LT):
                        wait_emptied(pe, i, ("kv", t // 2, 1), ("qf", PAIRS - 1))
                        for h in range(2):
                            out = begin(i, ("att", t, h))
                            for q in range(4):
                                p = 4 * h + q
                                mm = nc.tensor.matmul(out[:, q * 2 * VE:(q + 1) * 2 * VE], qf[:, p, t * P:(t + 1) * P], kvd[:, t // 2, p, :], start=True, stop=True)
                            mm.then_inc(filled, 1)
                    wait_emptied(pe, i, ("att", LT - 1, 1))
                    for c in range(DC):
                        out = begin(i, ("attT", c))
                        for t in range(LT):
                            mm = nc.tensor.transpose(out[:, t * P:(t + 1) * P], att[:, t, c * P:(c + 1) * P], keep["ident"][:, :])
                        mm.then_inc(filled, 1)
                    wait_emptied(pe, i, ("attT", DC - 1))
                    for t in range(LT):
                        projection(i, ("out", t), lambda c: attT[:, c, t * P:(t + 1) * P], lambda c: wo[:, c, :])

            @block.scalar
            def _(act):
                def evacuate(i, name, out, func, bias=0.0, src=None, inc=True):
                    act.wait_ge(filled, plan.filled(i, name))
                    ins = nc.scalar.activation(out, at(name) if src is None else src, func, bias=bias)
                    if inc:
                        ins.then_inc(emptied["act"], 1)

                act.sem_inc(emptied["act"], plan.per["act"])
                act.wait_ge(weights_loaded, 16 * 17)
                with act.Fori(0, NIT) as i:
                    for o in range(DC):
                        evacuate(i, ("kT", o), kT[:, o, :], ACT.Identity, bk[:, o:o + 1])
                    for c in range(DC):
                        evacuate(i, ("xnT", c), xnT[:, c, :], ACT.Identity)
                    for o in range(DC):
                        evacuate(i, ("qT", o), qT[:, o, :], ACT.Identity, bq[:, o:o + 1])
                    for p in range(PAIRS):
                        evacuate(i, ("qf", p), qf[:, p, :], ACT.Relu)
                    for e in range(EB):
                        for h in range(2):
                            for r in range(2):
                                src = at(("kv", e, h))[r * FD:(r + 1) * FD, 0:4 * 2 * VE].rearrange("p (q w) -> p q w", q=4)[:, :, r * VE:(r + 1) * VE]
                                evacuate(i, ("kv", e, h), kvd[r * FD:(r + 1) * FD, e, 4 * h:4 * h + 4, r * VE:(r + 1) * VE], ACT.Identity, src=src, inc=r == 1)
                    for c in range(DC):
                        evacuate(i, ("attT", c), attT[:, c, :], ACT.Identity)
                    act.wait_ge(out_done, LT * i + 2 * LT)
                    act.dma_start(rows(x_out, i * LB, LB).rearrange("(t p) d -> p t d", p=P), x_new[:, :, :]).then_inc(stored, 16)
                act.wait_ge(stored, 16 * NIT + 16)

            @block.vector
            def _(dve):
                def norm(i):
                    dve.wait_ge(x_loaded, 16 * i + 16)
                    for t in range(LT):
                        nc.vector.bn_stats(stats[:, t, :], x_sb[:, t, :]).then_inc(stats_done, 1)
                    hold(dve, stats_done, LT * i + LT, passed)
                    for t in range(LT):
                        nc.vector.bn_aggr(mv[:, t, :], stats[:, t, :]).then_inc(var_done, 1)
                    dve.wait_ge(var_done, LT * i + LT)
                    nc.vector.tensor_scalar(ve[:, :], mv[:, :, 1], LN_EPS, None, ALU.add).then_inc(ve_done, 1)
                    dve.wait_ge(rstd_done, i + 1)
                    for t in range(LT):
                        nc.vector.tensor_scalar(xn[:, t, :], x_sb[:, t, :], mv[:, t, 0:1], rstd[:, t:t + 1], ALU.subtract, ALU.mult).then_inc(xn_done, 1)
                    dve.wait_ge(xn_done, LT * i + LT)
                    dve.sem_inc(x_free, 1)

                def main(i, next_norm):
                    place = [0]

                    def decode(n):
                        lut.steps(dve, LI * i, place[0], place[0] + n)
                        place[0] += n

                    decode(8)
                    for t in range(LT):
                        decode(1)
                        dve.wait_ge(filled, plan.filled(i, ("v", t)))
                        nc.vector.tensor_tensor(v[:, t, :, 0:HD], at(("v", t)).rearrange("p (h e) -> p h e", h=HEADS),
                                                bv[:, :].rearrange("p (h e) -> p h e", h=HEADS), ALU.add).then_inc(emptied["dve"], 1)
                    dve.sem_inc(c_free, 1)
                    decode(11)
                    for t in range(LT):
                        for h in range(2):
                            dve.wait_ge(filled, plan.filled(i, ("kf", t, h)))
                            nc.vector.tensor_scalar(kf[:, t, h * 512:(h + 1) * 512], at(("kf", t, h)), 0.0, mask[:, bass.ds(LT * i + t, 1)], ALU.max, ALU.mult)\
                                .then_inc(emptied["dve"], 1)
                    if next_norm:
                        norm(i + 1)
                    decode(1)
                    for t in range(LT):
                        for h in range(2):
                            n = 2 * LT * i + 2 * t + h + 1
                            src = at(("att", t, h))[:, 0:8 * VE].rearrange("p (h e) -> p h e", h=8)
                            dve.wait_ge(filled, plan.filled(i, ("att", t, h)))
                            nc.vector.tensor_scalar(den[:, t, 8 * h:8 * h + 8], src[:, :, HD], 1e-8, None, ALU.add).then_inc(den_done, 1)
                            dve.wait_ge(den_done, n)
                            nc.vector.reciprocal(rden[:, t, 8 * h:8 * h + 8], den[:, t, 8 * h:8 * h + 8]).then_inc(rden_done, 1)
                            dve.wait_ge(rden_done, n)
                            nc.vector.tensor_tensor(att[:, t, h * 256:(h + 1) * 256].rearrange("p (h e) -> p h e", h=8), src[:, :, 0:HD],
                                                    rden[:, t, 8 * h:8 * h + 8].rearrange("p (h e) -> p h e", e=1).broadcast_to([P, 8, HD]), ALU.mult).then_inc(emptied["dve"], 1)
                    dve.wait_ge(stored, 16 * i + 16)
                    dve.wait_ge(res_loaded, 16 * i + 16)
                    for t in range(LT):
                        decode(2)
                        dve.wait_ge(filled, plan.filled(i, ("out", t)))
                        nc.vector.tensor_tensor(proj[:, t, :], at(("out", t)), bo[:, :], ALU.add).then_inc(emptied["dve"], 1)
                        dve.wait_ge(emptied["dve"], plan.emptied(i, ("out", t))[1])
                        nc.vector.scalar_tensor_tensor(out=x_new[:, t, :], in0=proj[:, t, :], scalar=keep["gates"][:, 1:2], in1=x_res[:, t, :],
                                                       op0=ALU.mult, op1=ALU.add).then_inc(out_done, 1)
                    dve.wait_ge(out_done, LT * i + 2 * LT)
                    dve.sem_inc(res_free, 1)

                for sem, n in ((res_free, 1), (out_done, LT), (stored, 16), (emptied["dve"], plan.per["dve"])):
                    dve.sem_inc(sem, n)
                nc.vector.memset(fmap_q[0:64, :], 0.0).then_inc(setup_done, 1)
                nc.vector.memset(fmap_q[64:128, :], 0.0).then_inc(setup_done, 1)
                nc.vector.memset(fmap_k[0:64, :], 0.0).then_inc(setup_done, 1)
                nc.vector.memset(fmap_k[64:128, :], 0.0).then_inc(setup_done, 1)
                nc.vector.memset(kvd[:, :, :, :], 0.0).then_inc(setup_done, 1)
                nc.vector.memset(v[:, :, :, HD:VE], 1.0).then_inc(setup_done, 1)
                norm(0)
                dve.wait_ge(weights_loaded, 16 * 17)
                lut.begin(dve)
                with dve.Fori(0, NIT - 1) as i:
                    main(i, True)
                main(NIT - 1, False)

            @block.gpsimd
            def _(pool):
                with pool.Fori(0, NIT) as i:
                    pool.wait_ge(ve_done, i + 1)
                    nc.gpsimd.tensor_tensor(rstd[:, :], ve[:, :], keep["neg_half"][:, 0:LT], ALU.pow).then_inc(rstd_done, 1)


CAP = 256


class Routing:

    def __init__(self, nc, sc, name, experts, topk, slots, spare):
        self.nc, self.name, self.experts, self.topk, self.slots = nc, name, experts, topk, slots
        NT = N // P
        self.slot_of = sc.sb("slot_of", [P, NT, topk], U32)
        self.weight = sc.sb("weight", [P, NT, topk])
        self.xn = nc.dram_tensor(f"{name}_xn", [N, D], F32, kind="Internal").ap()
        self.token_of = nc.dram_tensor(f"{name}_token_of", [slots + spare, 1], I32, kind="Internal").ap()
        self.y = nc.dram_tensor(f"{name}_y", [slots, D], F32, kind="Internal").ap()


def build_route(nc, io, keep, x_in, x_mid, r, shared, gate, late):
    E, K = r.experts, r.topk
    (n1, n3, n2), hidden, split = shared
    SC = -(-hidden // P)
    HM = [min(P, hidden - P * j) for j in range(SC)]
    parts = 2 if split else 1
    WDT = F32R if split else F32
    with ExitStack() as ctx:
        sc = Scope(nc, ctx, r.name + "_route")
        w1 = sc.sb("w1", [P, DC, hidden], WDT)
        w3 = sc.sb("w3", [P, DC, hidden], WDT)
        w2 = sc.sb("w2", [P, SC, D], WDT)
        raw = [sc.sb("w1b", [P, DC, hidden], BF16), sc.sb("w3b", [P, DC, hidden], BF16), sc.sb("w2b", [P, SC, D], BF16)] if split else [w1, w3, w2]
        wg = sc.sb("wg", [P, DC, E])
        bias = sc.sb("bias", [P, E])
        x_all = sc.sb("x_all", [P, NB * TB, D])
        x_new = sc.sb("x_new", [P, TB, D])
        xn = sc.sb("xn", [P, TB, D])
        xnT = sc.sb("xnT", [P, DC, BLK])
        xp = [sc.sb(f"x_part{q}", [P, DC, BLK], WDT) for q in range(parts)] if split else [xnT]
        g32 = sc.sb("g32", [P, SC, BLK])
        gp = [sc.sb(f"g_part{q}", [P, SC, BLK], WDT) for q in range(parts)] if split else [g32]
        sil = sc.sb("sil", [P, SC, BLK])
        stats = sc.sb("stats", [P, NB * TB, 6])
        mv = sc.sb("mv", [P, NB * TB, 2])
        ve = sc.sb("ve", [P, NB * TB])
        rstd = sc.sb("rstd", [P, NB * TB])
        score = sc.sb("score", [P, TB, E])
        biased = sc.sb("biased", [P, TB, E]) if late else score
        tmp1 = sc.sb("tmp1", [P, TB, E])
        tmp2 = sc.sb("tmp2", [P, TB, E])
        top = sc.sb("top", [P, TB, 8])
        top_at = sc.sb("top_at", [P, TB, 8], U32)
        idx = sc.sb("idx", [P, TB, 8])
        is_kth = sc.sb("is_kth", [P, TB, K, E])
        at_kth = sc.sb("at_kth", [P, TB, K, E])
        at_kth_w = sc.sb("at_kth_w", [P, TB, K, E]) if late else None
        chosen = sc.sb("chosen", [P, TB, E], BF16)
        before = sc.sb("before", [P, E], BF16)
        pos = sc.sb("pos", [P, TB, K])
        decay = sc.sb("decay", [P, TB, E])
        wraw = sc.sb("wraw", [P, TB, K])
        wsum = sc.sb("wsum", [P, TB])
        wrec = sc.sb("wrec", [P, TB])
        valid = sc.sb("valid", [P, TB, K])
        wnorm = sc.sb("wnorm", [P, TB, K])
        posc = sc.sb("posc", [P, TB, K])
        slotf = sc.sb("slotf", [P, TB, K])
        slotd = sc.sb("slotd", [P, TB, K])
        slot_now = sc.sb("slot_now", [P, TB, K], U32)
        token_now = sc.sb("token_now", [P, TB], I32)
        turn = sc.ps("turn", [P, 2, BLK])
        h = sc.ps("h", [P, 2, BLK])
        y = sc.ps("y", [P, 2, D])
        logits = sc.ps("logits", [P, TB, P])
        places = sc.ps("places", [P, TB, P])

        x_loaded = sc.sems("x_loaded", NB)
        names = ("w_loaded raw_done xn_stored stored stats_done var_done ve_done rstd_done xn_done turned "
                 "xnT_done hi_done lo_done logits_done h1_done h3_done sil_done g_done ghi_done glo_done y_done out_done abs_done exp_done ln_done "
                 "soft_done score_done biased_done top_done top_at_done idx_done is_kth_done chosen_done init_done places_done at_kth_done pos_done weight_done "
                 "before_done before_step slots_ready slots_free scattered passed pool_passed").split()
        s = {n: sc.sem(n) for n in names}

        with nc.Block() as block:

            @block.sync
            def _(sp):
                for i in range(NB):
                    sp.dma_start(x_all[:, TB * i:TB * i + TB, :], rows(x_in, i * BLK, BLK).rearrange("(t p) d -> p t d", p=P)).then_inc(x_loaded[i], 16)
                sp.dma_start(wg[:, :, :], io[r.name + "_wg"].rearrange("p (c e) -> p c e", c=DC)).then_inc(s["w_loaded"], 16)
                for w, n in zip(raw, (n1, n3, n2)):
                    sp.dma_start(w[:, :, :], io[n].rearrange("p (c h) -> p c h", c=w.shape[1])).then_inc(s["w_loaded"], 16)
                if late:
                    sp.dma_start(bias[:, :], io[r.name + "_bias"].broadcast_to([P, E])).then_inc(s["w_loaded"], 16)
                rows_total = r.token_of.shape[0]
                sp.wait_ge(s["init_done"], 1)
                sp.dma_start(r.token_of.rearrange("(p c) a -> p (c a)", p=P), keep["zeros_i"][:, 0:rows_total // P]).then_inc(s["w_loaded"], 16)
                with sp.Fori(0, NB) as i:
                    sp.wait_ge(s["xn_done"], TB * i + TB)
                    sp.dma_start(rows(r.xn, i * BLK, BLK).rearrange("(t p) d -> p t d", p=P), xn[:, :, :]).then_inc(s["xn_stored"], 16)
                sp.wait_ge(s["xn_stored"], 16 * NB + 16)

            NW = 16 * (6 if late else 5)

            @block.tensor
            def _(pe):
                pe.wait_ge(s["w_loaded"], NW)
                if split:
                    pe.wait_ge(s["raw_done"], 3)
                pe.wait_ge(s["init_done"], 1)

                def turn_rows(i):
                    for c in range(DC):
                        pe.wait_ge(s["xnT_done"], DC * i + c + 1)
                        if split:
                            pe.wait_ge(s["hi_done"], DC * i + c + 1)
                        for t in range(TB):
                            if c == 0:
                                pe.wait_ge(s["xn_done"], TB * i + t + 1)
                            mm = nc.tensor.transpose(turn[:, c % 2, t * P:(t + 1) * P], xn[:, t, c * P:(c + 1) * P], keep["ident"][:, :])
                        mm.then_inc(s["turned"], 1)

                def main(i, last):
                    pe.wait_ge(s["xnT_done"], DC * i + DC + 2)
                    pe.wait_ge(s["score_done"], i + 1)
                    for t in range(TB):
                        for c in range(DC):
                            mm = nc.tensor.matmul(logits[:, t, 0:E], xnT[:, c, t * P:(t + 1) * P], wg[:, c, :], start=c == 0, stop=c == DC - 1)
                    mm.then_inc(s["logits_done"], 1)
                    if split:
                        pe.wait_ge(s["lo_done"], DC * i + DC)
                    for j in range(SC):
                        m = HM[j]
                        for which, w, done, used in ((0, w1, "h1_done", "sil_done"), (1, w3, "h3_done", "g_done")):
                            pe.wait_ge(s[used], SC * i + j + 1)
                            n = 0
                            for c in range(DC):
                                for q in range(parts):
                                    mm = nc.tensor.matmul(h[0:m, which, :], w[:, c, j * P:j * P + m], xp[q][:, c, :], start=n == 0, stop=n == DC * parts - 1)
                                    n += 1
                            mm.then_inc(s[done], 1)
                    if not last:
                        turn_rows(i + 1)
                    for t in range(TB):
                        pe.wait_ge(s["out_done"], TB * i + t + 1)
                        n = 0
                        for j in range(SC):
                            pe.wait_ge(s["glo_done" if split else "g_done"], SC * i + j + 1 + (0 if split else 1))
                            for q in range(parts):
                                mm = nc.tensor.matmul(y[:, t % 2, :], gp[q][0:HM[j], j, t * P:(t + 1) * P], w2[0:HM[j], j, :], start=n == 0, stop=n == SC * parts - 1)
                                n += 1
                        mm.then_inc(s["y_done"], 1)
                    pe.wait_ge(s["at_kth_done"], i + 1)
                    pe.wait_ge(s["chosen_done"], i + 1)
                    pe.wait_ge(s["before_done"], i + 1)
                    for t in range(TB):
                        nc.tensor.matmul(places[:, t, 0:E], keep["ones_bf"][:, :], before[:, :], start=True, stop=False)
                        for e in range(t):
                            nc.tensor.matmul(places[:, t, 0:E], keep["ones_bf"][:, :], chosen[:, e, :], start=False, stop=False)
                        mm = nc.tensor.matmul(places[:, t, 0:E], keep["earlier"][:, :], chosen[:, t, :], start=False, stop=True)
                    mm.then_inc(s["places_done"], 1)

                turn_rows(0)
                with pe.Fori(0, NB - 1) as i:
                    main(i, False)
                main(NB - 1, True)

            @block.vector
            def _(dve):
                def statistics():
                    for i in range(NB):
                        dve.wait_ge(x_loaded[i], 16)
                        for t in range(TB * i, TB * i + TB):
                            nc.vector.bn_stats(stats[:, t, :], x_all[:, t, :]).then_inc(s["stats_done"], 1)
                    hold(dve, s["stats_done"], NB * TB, s["passed"])
                    for t in range(NB * TB):
                        nc.vector.bn_aggr(mv[:, t, :], stats[:, t, :]).then_inc(s["var_done"], 1)
                    dve.wait_ge(s["var_done"], NB * TB)
                    nc.vector.tensor_scalar(ve[:, :], mv[:, :, 1], LN_EPS, None, ALU.add).then_inc(s["ve_done"], 1)
                    dve.wait_ge(s["rstd_done"], 1)

                def norm(i):
                    dve.wait_ge(s["turned"], DC * i + 1)
                    dve.wait_ge(s["xn_stored"], 16 * i + 16)
                    for t in range(TB):
                        at = bass.ds(TB * i + t, 1)
                        nc.vector.tensor_scalar(xn[:, t, :], x_all[:, at, :].rearrange("p a d -> p (a d)"), mv[:, at, 0:1].rearrange("p a b -> p (a b)"),
                                                rstd[:, at], ALU.subtract, ALU.mult).then_inc(s["xn_done"], 1)

                def hidden_product(i, j):
                    m = HM[j]
                    dve.wait_ge(s["sil_done"], SC * i + j + 2)
                    dve.wait_ge(s["h3_done"], SC * i + j + 1)
                    if j == 0:
                        dve.wait_ge(s["y_done"], TB * i + 1)
                    nc.vector.tensor_tensor(g32[0:m, j, :], sil[0:m, j, :], h[0:m, 1, :], ALU.mult).then_inc(s["g_done"], 1)
                    if split:
                        dve.wait_ge(s["ghi_done"], SC * i + j + 1)
                        nc.vector.tensor_tensor(gp[1][0:m, j, :], g32[0:m, j, :], gp[0][0:m, j, :].bitcast(F32), ALU.subtract).then_inc(s["glo_done"], 1)

                def softplus(i):
                    dve.wait_ge(s["ln_done"], i + 1)
                    nc.vector.scalar_tensor_tensor(out=tmp1[:, :, :], in0=logits[:, :, 0:E], scalar=0.0, in1=tmp2[:, :, :], op0=ALU.max, op1=ALU.add).then_inc(s["soft_done"], 1)

                def choose(i):
                    if late:
                        dve.wait_ge(s["score_done"], i + 2)
                        for t in range(TB):
                            nc.vector.tensor_tensor(biased[:, t, :], score[:, t, :], bias[:, :], ALU.add).then_inc(s["biased_done"], 1)
                    ready = (s["biased_done"], TB * i + TB) if late else (s["score_done"], i + 2)
                    hold(dve, *ready, s["passed"])
                    for t in range(TB):
                        nc.vector.max(top[:, t, :], biased[:, t, :]).then_inc(s["top_done"], 1)
                    hold(dve, s["top_done"], TB * i + TB, s["passed"])
                    for t in range(TB):
                        nc.vector.max_index(top_at[:, t, :], top[:, t, :], biased[:, t, :]).then_inc(s["top_at_done"], 1)
                    dve.wait_ge(s["top_at_done"], TB * i + TB)
                    nc.vector.tensor_copy(idx[:, :, :], top_at[:, :, :]).then_inc(s["idx_done"], 1)
                    dve.wait_ge(s["idx_done"], i + 1)
                    nc.vector.tensor_tensor(is_kth[:, :, :, :], keep["iota"][:, 0:E].rearrange("p (t k e) -> p t k e", t=1, k=1).broadcast_to([P, TB, K, E]),
                                            idx[:, :, 0:K].rearrange("p t (k e) -> p t k e", e=1).broadcast_to([P, TB, K, E]), ALU.is_equal).then_inc(s["is_kth_done"], 1)
                    dve.wait_ge(s["is_kth_done"], i + 1)
                    with nc.allow_low_precision(reason="sums of zeros and at most a one"):
                        nc.vector.tensor_reduce(chosen[:, :, :], is_kth[:, :, :, :].rearrange("p t k e -> p t e k"), AX.X, ALU.add).then_inc(s["chosen_done"], 1)

                def place(i):
                    def over_k4(ap):
                        return ap.rearrange("p t (k e) -> p t k e", k=1).broadcast_to([P, TB, K, E])

                    dve.wait_ge(s["places_done"], i + 1)
                    nc.vector.tensor_tensor(at_kth[:, :, :, :], is_kth[:, :, :, :], over_k4(places[:, :, 0:E]), ALU.mult).then_inc(s["at_kth_done"], 1)
                    if late:
                        nc.vector.tensor_tensor(at_kth_w[:, :, :, :], is_kth[:, :, :, :], over_k4(score[:, :, :]), ALU.mult).then_inc(s["weight_done"], 1)
                    dve.wait_ge(s["at_kth_done"], i + 2)
                    nc.vector.tensor_reduce(pos[:, :, :], at_kth[:, :, :, :], AX.X, ALU.add).then_inc(s["pos_done"], 1)
                    if late:
                        dve.wait_ge(s["weight_done"], i + 2)
                        nc.vector.tensor_reduce(wraw[:, :, :], at_kth_w[:, :, :, :], AX.X, ALU.add).then_inc(s["pos_done"], 1)
                    dve.wait_ge(s["pos_done"], (2 if late else 1) * (i + 1))
                    for t in range(TB):
                        last = t == TB - 1
                        nc.vector.tensor_tensor(before[:, :], before[:, :], chosen[:, t, :], ALU.add).then_inc(s["before_step"], 1)
                        dve.wait_ge(s["before_step"], TB * i + t + 1)
                        if last:
                            dve.sem_inc(s["before_done"], 1)
                    ti = bass.ds(TB * i, TB)
                    step = [0]

                    def then(ins):
                        step[0] += 1
                        ins.then_inc(s["slots_ready"], 1)
                        dve.wait_ge(s["slots_ready"], per_block * i + step[0])

                    def over_k(ap):
                        return ap.rearrange("p (t k) -> p t k", k=1).broadcast_to([P, TB, K])

                    if late:
                        per_block = 3
                        then(nc.vector.tensor_copy(late["idx"][:, ti, :], idx[:, :, 0:K]))
                        then(nc.vector.tensor_copy(late["pos"][:, ti, :], pos[:, :, :]))
                        then(nc.vector.tensor_scalar(r.weight[:, ti, :], wraw[:, :, :], gate, None, ALU.mult))
                    else:
                        per_block = 11
                        then(nc.vector.tensor_reduce(wsum[:, :], top[:, :, 0:K], AX.X, ALU.add))
                        then(nc.vector.reciprocal(wrec[:, :], wsum[:, :]))
                        then(nc.vector.tensor_tensor(wnorm[:, :, :], top[:, :, 0:K], over_k(wrec[:, :]), ALU.mult))
                        then(nc.vector.tensor_scalar(valid[:, :, :], pos[:, :, :], float(CAP), None, ALU.is_lt))
                        then(nc.vector.scalar_tensor_tensor(out=r.weight[:, ti, :], in0=wnorm[:, :, :], scalar=gate, in1=valid[:, :, :], op0=ALU.mult, op1=ALU.mult))
                        then(nc.vector.tensor_scalar(posc[:, :, :], pos[:, :, :], float(CAP - 1), None, ALU.min))
                        then(nc.vector.scalar_tensor_tensor(out=slotf[:, :, :], in0=idx[:, :, 0:K], scalar=float(CAP), in1=posc[:, :, :], op0=ALU.mult, op1=ALU.add))
                        then(nc.vector.tensor_copy(r.slot_of[:, ti, :], slotf[:, :, :]))
                        then(nc.vector.scalar_tensor_tensor(out=slotd[:, :, :], in0=slotf[:, :, :], scalar=keep["spare"][:, 0:1], in1=valid[:, :, :], op0=ALU.subtract, op1=ALU.mult))
                        dve.wait_ge(s["slots_free"], i + 1)
                        then(nc.vector.tensor_copy(token_now[:, :], keep["row_id"][:, ti]))
                        then(nc.vector.tensor_scalar(slot_now[:, :, :], slotd[:, :, :], keep["spare"][:, 0:1], None, ALU.add))

                def finish(i):
                    dve.wait_ge(s["stored"], 16 * i + 16)
                    for t in range(TB):
                        dve.wait_ge(s["y_done"], TB * i + t + 2)
                        nc.vector.scalar_tensor_tensor(out=x_new[:, t, :], in0=y[:, t % 2, :], scalar=gate,
                                                       in1=x_all[:, bass.ds(TB * i + t, 1), :].rearrange("p a d -> p (a d)"), op0=ALU.mult, op1=ALU.add).then_inc(s["out_done"], 1)

                def main(i, next_norm):
                    if split:
                        for c in range(DC):
                            dve.wait_ge(s["hi_done"], DC * i + c + 1 + 2)
                            dve.wait_ge(s["xnT_done"], DC * i + c + 1 + 2)
                            nc.vector.tensor_tensor(xp[1][:, c, :], xnT[:, c, :], xp[0][:, c, :].bitcast(F32), ALU.subtract).then_inc(s["lo_done"], 1)
                    if next_norm:
                        norm(i + 1)
                    if late:
                        softplus(i)
                    first = SC - 1 if late else 0
                    for j in range(first):
                        hidden_product(i, j)
                    choose(i)
                    for j in range(first, SC):
                        hidden_product(i, j)
                    finish(i)
                    place(i)

                for name, n in (("xn_stored", 16), ("stored", 16), ("turned", 1), ("out_done", 2), ("y_done", 1),
                                ("g_done", 1), ("sil_done", 1), ("at_kth_done", 1), ("weight_done", 1), ("slots_free", 1)):
                    dve.sem_inc(s[name], n)
                nc.vector.memset(before[:, :], 0.0).then_inc(s["before_done"], 1)
                dve.sem_inc(s["init_done"], 1)
                dve.wait_ge(s["before_done"], 1)
                statistics()
                norm(0)
                dve.wait_ge(s["w_loaded"], NW)
                if split:
                    for src, dst in zip(raw, (w1, w3, w2)):
                        nc.vector.tensor_copy(dst[:, :, :], src[:, :, :]).then_inc(s["raw_done"], 1)
                with dve.Fori(0, NB - 1) as i:
                    main(i, True)
                main(NB - 1, False)
                if late:
                    dve.wait_ge(s["before_done"], NB + 1)
                    nc.vector.tensor_copy(late["counts"][:, :], before[:, :])

            @block.scalar
            def _(act):
                act.sem_inc(s["xnT_done"], 2)
                act.sem_inc(s["hi_done"], 2)
                if not late:
                    act.sem_inc(s["score_done"], 1)
                def move_rows(i):
                    for c in range(DC):
                        act.wait_ge(s["turned"], DC * i + c + 2)
                        nc.scalar.activation(xnT[:, c, :], turn[:, c % 2, :], ACT.Copy).then_inc(s["xnT_done"], 1)
                        if split:
                            nc.scalar.activation(xp[0][:, c, :], turn[:, c % 2, :], ACT.Copy).then_inc(s["hi_done"], 1)

                def main(i, last):
                    act.wait_ge(s["logits_done"], i + 1)
                    if late:
                        act.wait_ge(s["soft_done"], i + 1)
                        nc.scalar.activation(tmp2[:, :, :], logits[:, :, 0:E], ACT.Abs).then_inc(s["abs_done"], 1)
                        act.wait_ge(s["abs_done"], i + 1)
                        nc.scalar.activation(decay[:, :, :], tmp2[:, :, :], ACT.Exp, scale=-1.0).then_inc(s["exp_done"], 1)
                        act.wait_ge(s["exp_done"], i + 1)
                        nc.scalar.activation(tmp2[:, :, :], decay[:, :, :], ACT.Ln, bias=1.0).then_inc(s["ln_done"], 1)
                    else:
                        nc.scalar.activation(score[:, :, :], logits[:, :, 0:E], ACT.Sigmoid).then_inc(s["score_done"], 1)
                    for j in range(SC):
                        m = HM[j]
                        act.wait_ge(s["h1_done"], SC * i + j + 1)
                        act.wait_ge(s["g_done"], SC * i + j + 1)
                        nc.scalar.activation(sil[0:m, j, :], h[0:m, 0, :], ACT.Silu).then_inc(s["sil_done"], 1)
                        if split:
                            act.wait_ge(s["g_done"], SC * i + j + 2)
                            nc.scalar.activation(gp[0][0:m, j, :], g32[0:m, j, :], ACT.Copy).then_inc(s["ghi_done"], 1)
                    if not last:
                        move_rows(i + 1)
                    act.wait_ge(s["out_done"], TB * i + TB + 2)
                    act.dma_start(rows(x_mid, i * BLK, BLK).rearrange("(t p) d -> p t d", p=P), x_new[:, :, :]).then_inc(s["stored"], 16)

                move_rows(0)
                with act.Fori(0, NB - 1) as i:
                    main(i, False)
                main(NB - 1, True)
                act.wait_ge(s["stored"], 16 * NB + 16)

            @block.gpsimd
            def _(pool):
                def root():
                    pool.wait_ge(s["ve_done"], 1)
                    nc.gpsimd.tensor_tensor(rstd[:, :], ve[:, :], keep["neg_half"][:, 0:NB * TB], ALU.pow).then_inc(s["rstd_done"], 1)

                def square_root(i):
                    pool.wait_ge(s["weight_done"], i + 1)
                    pool.wait_ge(s["soft_done"], i + 2)
                    nc.gpsimd.tensor_tensor(score[:, :, :], tmp1[:, :, :], keep["half"][:, :].rearrange("p (t e) -> p t e", t=TB), ALU.pow).then_inc(s["score_done"], 1)

                def scatter(i):
                    hold(pool, s["slots_ready"], 11 * i + 11, s["pool_passed"])
                    for t in range(TB):
                        for k in range(K):
                            nc.gpsimd.indirect_dma_start(out=r.token_of, out_offset=bass.IndirectOffsetOnAxis(ap=slot_now[:, t, k:k + 1], axis=0),
                                                         in_=token_now[:, t:t + 1], in_offset=None).then_inc(s["scattered"], 16)
                    pool.wait_ge(s["scattered"], 16 * TB * K * (i + 1))
                    pool.sem_inc(s["slots_free"], 1)

                if late:
                    pool.sem_inc(s["score_done"], 1)
                    pool.sem_inc(s["soft_done"], 1)
                root()
                with pool.Fori(0, NB) as i:
                    if late:
                        square_root(i)
                    else:
                        scatter(i)


def load_tokens(nc, r, tokens):
    tiles = r.slots // P
    with ExitStack() as ctx:
        sc = Scope(nc, ctx, r.name + "_tokens")
        raw = sc.sb("raw", [tiles, P], I32)
        asf = sc.sb("asf", [tiles, P])
        turned = sc.ps("turned", [P, 512])
        loaded, asf_done, turn_done, done = (sc.sem(n) for n in ("loaded", "asf_done", "turn_done", "done"))
        with nc.Block() as block:

            @block.sync
            def _(sp):
                sp.dma_start(raw[:, :], r.token_of[0:r.slots, :].rearrange("(n p) a -> n (p a)", p=P)).then_inc(loaded, 16)

            @block.vector
            def _(dve):
                dve.wait_ge(loaded, 16)
                nc.vector.tensor_copy(asf[:, :], raw[:, :]).then_inc(asf_done, 1)
                dve.wait_ge(turn_done, 1)
                nc.vector.tensor_copy(tokens[:, :], turned[:, 0:tiles]).then_inc(done, 1)

            @block.tensor
            def _(pe):
                pe.wait_ge(asf_done, 1)
                nc.tensor.transpose(turned[:, 0:tiles], asf[:, :], r.ident[0:tiles, 0:tiles]).then_inc(turn_done, 1)


def build_small_experts(nc, io, keep, r):
    TT = CAP // P
    HU = 64
    PAIRS = r.experts // 2
    QUADS = PAIRS // 4
    OUTS = 2 * TT
    with ExitStack() as ctx:
        sc = Scope(nc, ctx, "small")
        tokens = sc.sb("tokens", [P, r.slots // P], U32)
        load_tokens(nc, r, tokens)
        now = sc.sb("now", [P, 2, OUTS], U32)
        w_up = sc.sb("w_up", [P, 2, 2, DC, 2 * HU])
        w_down = sc.sb("w_down", [P, 2, 2, D])
        xg = sc.sb("xg", [P, 2, 2, TT, D])
        xgT = sc.sb("xgT", [P, 2, DC, CAP])
        sil = sc.sb("sil", [P, CAP])
        hid = sc.sb("hid", [P, CAP])
        y_sb = sc.sb("y", [P, 2, 2, TT, D])
        wide = sc.ps("wide", [P, 2, 2, 512])
        narrow = sc.ps("narrow", [P, 2, CAP])
        out = sc.ps("out", [P, 3, 512])
        w_loaded = sc.sems("w_loaded", 2)
        gathered = sc.sems("gathered", 2)
        stored = sc.sems("stored", 2)
        names = "zeroed now_done turned xT_act xT_dve up_done sil_done hid_done y_done y_act y_dve pool_passed".split()
        s = {n: sc.sem(n) for n in names}

        lut = LutDecoder(nc, io, sc, LUT_FIRST["experts"])

        def pairs(eng, pair):
            def four(q, last):
                for n in range(4):
                    pair(4 * q + n, n % 2, 2 * q + n // 2, last and n == 3, q, n)

            with eng.Fori(0, QUADS - 1) as q:
                four(q, False)
            four(QUADS - 1, True)

        with nc.Block() as block:

            @block.sync
            def _(sp):
                def load(i, par):
                    sp.dma_start(w_up[:, par], io["w_up"][bass.ds(2 * i, 2)].rearrange("e p (c h) -> p e c h", c=DC)).then_inc(w_loaded[par], 16)
                    for u in range(2):
                        sp.dma_start(w_down[u * HU:(u + 1) * HU, par, u, :], io["w_down"][bass.ds(2 * i + u, 1)].rearrange("e p d -> p (e d)")).then_inc(w_loaded[par], 16)

                def store(i, par):
                    for u in range(2):
                        sp.wait_ge(s["y_act"], 2 * i + u + 3)
                        sp.wait_ge(s["y_dve"], 2 * i + u + 3)
                        sp.dma_start(rows(r.y, (2 * i + u) * CAP, CAP).rearrange("(t p) d -> p t d", p=P), y_sb[:, par, u]).then_inc(stored[par], 16)

                def four(q, last):
                    for n in range(4):
                        store(4 * q + n, n % 2)
                        if not (last and n >= 2):
                            load(4 * q + n + 2, n % 2)
                        if n == 0 and not last:
                            lut.load(sp, q + 1)
                    lut.store(sp, q)

                load(0, 0)
                load(1, 1)
                lut.load_table(sp)
                lut.load(sp, 0)
                with sp.Fori(0, QUADS - 1) as q:
                    four(q, False)
                four(QUADS - 1, True)
                for par in range(2):
                    sp.wait_ge(stored[par], 16 * PAIRS + 32)
                lut.finish(sp, QUADS)

            @block.gpsimd
            def _(pool):
                with pool.Fori(0, PAIRS // 2) as k:
                    for par in range(2):
                        i = 2 * k + par
                        hold(pool, s["turned"], 4 * i + 4, s["pool_passed"])
                        nc.gpsimd.tensor_copy(now[:, par, :], tokens[:, bass.ds(OUTS * i, OUTS)]).then_inc(s["now_done"], 1)
                        hold(pool, s["now_done"], i + 1, s["pool_passed"])
                        for n in range(OUTS):
                            nc.gpsimd.indirect_dma_start(out=xg[:, par, n // TT, n % TT, :], out_offset=None, in_=r.xn,
                                                         in_offset=bass.IndirectOffsetOnAxis(ap=now[:, par, n:n + 1], axis=0)).then_inc(gathered[par], 16)

            @block.tensor
            def _(pe):
                def turn(par, k):
                    pe.wait_ge(gathered[par], 16 * OUTS * (k + 1))
                    for u in range(2):
                        for half in range(2):
                            for c in (2 * half, 2 * half + 1):
                                for t in range(TT):
                                    at = (c % 2) * CAP + t * P
                                    mm = nc.tensor.transpose(wide[:, u, half, at:at + P], xg[:, par, u, t, c * P:(c + 1) * P], keep["ident"][:, :])
                            mm.then_inc(s["turned"], 1)

                def pair(i, par, k, last, q, n):
                    pe.wait_ge(w_loaded[par], 48 * k + 48)
                    pe.wait_ge(s["xT_act"], 2 * i + 2)
                    pe.wait_ge(s["xT_dve"], 2 * i + 2)
                    for which in range(2):
                        for c in range(DC):
                            for u in range(2):
                                mm = nc.tensor.matmul(narrow[u * HU:(u + 1) * HU, which, :], w_up[:, par, u, c, which * HU:(which + 1) * HU], xgT[:, u, c, :],
                                                      start=c == 0, stop=c == DC - 1, tile_position=(0, u * HU))
                    mm.then_inc(s["up_done"], 1)
                    if not last:
                        turn(1 - par, k + par)
                    pe.wait_ge(s["hid_done"], i + 1)
                    for o in range(OUTS):
                        if o == 0:
                            pe.wait_ge(s["y_dve"], 2 * i + 2)
                        elif o == 2:
                            pe.wait_ge(s["y_act"], 2 * i + 2)
                        elif o == 3:
                            pe.wait_ge(s["y_act"], 2 * i + 3)
                        u, t = o // TT, o % TT
                        nc.tensor.matmul(out[:, o % 3, :], hid[:, t * P:(t + 1) * P], w_down[:, par, u, :], start=True, stop=True).then_inc(s["y_done"], 1)

                pe.sem_inc(s["turned"], 8)
                pe.wait_ge(s["zeroed"], 2)
                turn(0, 0)
                pairs(pe, pair)

            def turned(eng, i, u, half, move):
                eng.wait_ge(s["turned"], 4 * i + 2 * u + half + 1 + 8)
                move(xgT[:, u, 2 * half:2 * half + 2, :], wide[:, u, half, :].rearrange("p (c s) -> p c s", c=2)).then_inc(s["xT_dve" if half else "xT_act"], 1)

            @block.scalar
            def _(act):
                def copy(to, of):
                    return nc.scalar.activation(to, of, ACT.Copy)

                def pair(i, par, k, last, q, n):
                    act.wait_ge(s["up_done"], i + 1)
                    nc.scalar.activation(sil[:, :], narrow[:, 0, :], ACT.Silu).then_inc(s["sil_done"], 1)
                    if not last:
                        for u in range(2):
                            turned(act, i + 1, u, 0, copy)
                    act.wait_ge(stored[par], 32 * k + 32)
                    for n in (0, 2):
                        act.wait_ge(s["y_done"], OUTS * i + n + 1)
                        copy(y_sb[:, par, n // TT, n % TT, :], out[:, n % 3, :]).then_inc(s["y_act"], 1)

                act.sem_inc(s["y_act"], 2)
                for u in range(2):
                    turned(act, 0, u, 0, copy)
                pairs(act, pair)

            @block.vector
            def _(dve):
                def pair(i, par, k, last, q, n):
                    dve.wait_ge(s["sil_done"], i + 1)
                    nc.vector.tensor_tensor(hid[:, :], sil[:, :], narrow[:, 1, :], ALU.mult).then_inc(s["hid_done"], 1)
                    if not last:
                        for u in range(2):
                            turned(dve, i + 1, u, 1, nc.vector.tensor_copy)
                    dve.wait_ge(stored[par], 32 * k + 32)
                    lut.steps(dve, q, 4 * n, 4 * n + 2)
                    for out_n in (1, 3):
                        dve.wait_ge(s["y_done"], OUTS * i + out_n + 1)
                        nc.vector.tensor_copy(y_sb[:, par, out_n // TT, out_n % TT, :], out[:, out_n % 3, :]).then_inc(s["y_dve"], 1)
                    lut.steps(dve, q, 4 * n + 2, 4 * n + 4)

                for sem, n in ((s["y_dve"], 2), (stored[0], 32), (stored[1], 32)):
                    dve.sem_inc(sem, n)
                lut.begin(dve)
                nc.vector.memset(w_down[HU:P, :, 0, :], 0.0).then_inc(s["zeroed"], 1)
                nc.vector.memset(w_down[0:HU, :, 1, :], 0.0).then_inc(s["zeroed"], 1)
                for u in range(2):
                    turned(dve, 0, u, 1, nc.vector.tensor_copy)
                pairs(dve, pair)


def build_combine(nc, io, keep, r, x_mid, x_out, first):
    K = r.topk
    NT = N // P
    with ExitStack() as ctx:
        sc = Scope(nc, ctx, r.name + "_comb")
        AHEAD = 4
        now = sc.sb("now", [P, AHEAD, K], U32)
        x_sb = sc.sb("x", [P, AHEAD, D])
        yk = sc.sb("yk", [P, AHEAD, K, D])
        acc = sc.sb("acc", [P, 2, D])
        x_new = sc.sb("x_new", [P, AHEAD, D])
        loaded = sc.sems("loaded", AHEAD)
        gathered = sc.sems("gathered", AHEAD)
        stored = sc.sems("stored", AHEAD)
        x_free, now_done, acc_done, pool_passed = (sc.sem(n) for n in ("x_free", "now_done", "acc_done", "pool_passed"))
        lut = LutDecoder(nc, io, sc, first) if first is not None else None
        ROUNDS = NT // AHEAD

        with nc.Block() as block:

            @block.sync
            def _(sp):
                def load(t, u):
                    sp.wait_ge(x_free, t + 1)
                    sp.dma_start(x_sb[:, u, :], rows(x_mid, t * P, P)).then_inc(loaded[u], 16)

                if lut:
                    lut.load_table(sp)
                    lut.load(sp, 0)
                for u in range(AHEAD):
                    load(u, u)
                with sp.Fori(0, ROUNDS - 1) as q:
                    if lut:
                        lut.load(sp, q + 1)
                    for u in range(AHEAD):
                        load(AHEAD * (q + 1) + u, u)
                    if lut:
                        lut.store(sp, q)
                if lut:
                    lut.store(sp, ROUNDS - 1)
                    lut.finish(sp, ROUNDS)

            @block.gpsimd
            def _(pool):
                with pool.Fori(0, ROUNDS) as q:
                    for u in range(AHEAD):
                        t = AHEAD * q + u
                        hold(pool, x_free, t + 1, pool_passed)
                        nc.gpsimd.tensor_copy(now[:, u, :], r.slot_of[:, bass.ds(t, 1), :].rearrange("p a k -> p (a k)")).then_inc(now_done, 1)
                        hold(pool, now_done, t + 1, pool_passed)
                        for k in range(K):
                            nc.gpsimd.indirect_dma_start(out=yk[:, u, k, :], out_offset=None, in_=r.y, in_offset=bass.IndirectOffsetOnAxis(ap=now[:, u, k:k + 1], axis=0))\
                                .then_inc(gathered[u], 16)

            @block.vector
            def _(dve):
                def tile(q, u):
                    t = AHEAD * q + u
                    dve.wait_ge(loaded[u], 16 * q + 16)
                    dve.wait_ge(gathered[u], 16 * K * q + 16 * K)
                    dve.wait_ge(stored[u], 16 * q + 16)
                    for k in range(K):
                        if k:
                            dve.wait_ge(acc_done, K * t + k)
                        src = x_sb[:, u, :] if k == 0 else acc[:, (k - 1) % 2, :]
                        dst = x_new[:, u, :] if k == K - 1 else acc[:, k % 2, :]
                        nc.vector.scalar_tensor_tensor(out=dst, in0=yk[:, u, k, :], scalar=r.weight[:, bass.ds(t, 1), k:k + 1].rearrange("p a k -> p (a k)"), in1=src,
                                                       op0=ALU.mult, op1=ALU.add).then_inc(acc_done, 1)
                        if lut and k < LUT_SIZE // AHEAD:
                            lut.step(dve, q, LUT_SIZE // AHEAD * u + k)
                    dve.wait_ge(acc_done, K * t + K)
                    dve.sem_inc(x_free, 1)

                dve.sem_inc(x_free, AHEAD)
                for u in range(AHEAD):
                    dve.sem_inc(stored[u], 16)
                if lut:
                    lut.begin(dve)
                with dve.Fori(0, ROUNDS) as q:
                    for u in range(AHEAD):
                        tile(q, u)

            @block.scalar
            def _(act):
                with act.Fori(0, ROUNDS) as q:
                    for u in range(AHEAD):
                        t = AHEAD * q + u
                        act.wait_ge(acc_done, K * t + K)
                        act.dma_start(rows(x_out, t * P, P), x_new[:, u, :]).then_inc(stored[u], 16)
                for u in range(AHEAD):
                    act.wait_ge(stored[u], 16 * ROUNDS + 16)


def build_small_mixture(nc, io, keep, x_in, x_out):
    with ExitStack() as ctx:
        gate = keep["gates"][:, 4:5]
        r = Routing(nc, Scope(nc, ctx, "moe0"), "moe0", 64, 6, 64 * CAP, P)
        r.ident = keep["ident"]
        x_mid = nc.dram_tensor("moe0_x_mid", [N, D], F32, kind="Internal").ap()
        build_route(nc, io, keep, x_in, x_mid, r, (("moe0_w1", "moe0_w3", "moe0_w2"), 128, False), gate, None)
        build_small_experts(nc, io, keep, r)
        build_combine(nc, io, keep, r, x_mid, x_out, LUT_FIRST["combine"])


INTER = 352
INTER_C = 3
WIDE_TILES = N * 2 // P + 8


def build_late_slots(nc, io, keep, r, late, tile_expert, weights):
    E, K, NT = r.experts, r.topk, N // P
    WC = weights.shape[1] // E
    with ExitStack() as ctx:
        sc = Scope(nc, ctx, r.name + "_slots")
        counts_ps = sc.ps("counts_ps", [P, 512])
        counts = sc.sb("counts", [P, E])
        steps = sc.sb("steps", [P, NT])
        over = sc.sb("over", [P, E, NT])
        tiles = sc.sb("tiles", [P, E])
        start = sc.sb("start", [P, E])
        start_slot = sc.sb("start_slot", [P, E])
        first = sc.sb("first", [P, NT, K])
        slotf = sc.sb("slotf", [P, 2, NT, K])
        te = sc.sb("te", [P, 2, WIDE_TILES])
        slot_now = sc.sb("slot_now", [P, TB, K], U32)
        token_now = sc.sb("token_now", [P, TB], I32)
        raw = sc.sb("raw", [P, 2, WC], BF16)
        raw_loaded = sc.sems("raw_loaded", 2)
        weights_done = sc.sem("weights_done")
        counted, dve_step, slots_ready, slots_free, scattered, pool_passed = (sc.sem(n) for n in ("counted", "dve_step", "slots_ready", "slots_free", "scattered", "pool_passed"))
        with nc.Block() as block:

            @block.sync
            def _(sp):
                with sp.Fori(0, E // 2) as i:
                    for u in range(2):
                        e = 2 * i + u
                        sp.wait_ge(weights_done, e + 1)
                        sp.dma_start(raw[:, u, :], io["moe2_w"][bass.ds(e, 1)].rearrange("e p c -> p (e c)")).then_inc(raw_loaded[u], 16)

            @block.scalar
            def _(act):
                act.sem_inc(weights_done, 2)
                with act.Fori(0, E // 2) as i:
                    for u in range(2):
                        e = 2 * i + u
                        act.wait_ge(raw_loaded[u], 16 * i + 16)
                        nc.scalar.activation(weights[:, bass.ds(e * WC, WC)], raw[:, u, :], ACT.Copy).then_inc(weights_done, 1)

            @block.tensor
            def _(pe):
                nc.tensor.matmul(counts_ps[:, 0:E], keep["ones_bf"][:, :], late["counts"][:, :], start=True, stop=True).then_inc(counted, 1)

            @block.vector
            def _(dve):
                n = [0]

                def then(ins):
                    n[0] += 1
                    ins.then_inc(dve_step, 1)
                    dve.wait_ge(dve_step, n[0])

                dve.sem_inc(slots_free, 1)
                then(nc.vector.tensor_scalar(steps[:, :], keep["iota"][:, 0:NT], float(P), None, ALU.mult))
                dve.wait_ge(counted, 1)
                then(nc.vector.tensor_copy(counts[:, :], counts_ps[:, 0:E]))
                then(nc.vector.tensor_tensor(over[:, :, :], counts[:, :].rearrange("p (e m) -> p e m", m=1).broadcast_to([P, E, NT]),
                                             steps[:, :].rearrange("p (e m) -> p e m", e=1).broadcast_to([P, E, NT]), ALU.is_gt))
                then(nc.vector.tensor_reduce(tiles[:, :], over[:, :, :], AX.X, ALU.add))
                then(nc.vector.memset(start[:, 0:1], 0.0))
                for e in range(1, E):
                    then(nc.vector.tensor_tensor(start[:, e:e + 1], start[:, e - 1:e], tiles[:, e - 1:e], ALU.add))
                then(nc.vector.tensor_scalar(start_slot[:, :], start[:, :], float(P), None, ALU.mult))
                for e in range(E):
                    src = late["pos"] if e == 0 else slotf[:, (e - 1) % 2]
                    then(nc.vector.tensor_scalar(first[:, :, :], late["idx"][:, :, :], float(e), start_slot[:, e:e + 1], ALU.is_equal, ALU.mult))
                    then(nc.vector.tensor_tensor(slotf[:, e % 2], src[:, :, :], first[:, :, :], ALU.add))
                then(nc.vector.tensor_copy(r.slot_of[:, :, :], slotf[:, (E - 1) % 2]))
                then(nc.vector.memset(te[:, 0, :], 0.0))
                for e in range(1, E):
                    then(nc.vector.scalar_tensor_tensor(out=te[:, e % 2, :], in0=keep["iota"][:, 0:WIDE_TILES], scalar=start[:, e:e + 1], in1=te[:, (e - 1) % 2, :],
                                                        op0=ALU.is_ge, op1=ALU.add))
                then(nc.vector.tensor_copy(tile_expert[:, :], te[:, (E - 1) % 2, :]))
                with dve.Fori(0, NB) as i:
                    dve.wait_ge(slots_free, i + 1)
                    nc.vector.tensor_copy(token_now[:, :], keep["row_id"][:, bass.ds(TB * i, TB)]).then_inc(slots_ready, 1)
                    nc.vector.tensor_copy(slot_now[:, :, :], r.slot_of[:, bass.ds(TB * i, TB), :]).then_inc(slots_ready, 1)

            @block.gpsimd
            def _(pool):
                with pool.Fori(0, NB) as i:
                    hold(pool, slots_ready, 2 * i + 2, pool_passed)
                    for t in range(TB):
                        for k in range(K):
                            nc.gpsimd.indirect_dma_start(out=r.token_of, out_offset=bass.IndirectOffsetOnAxis(ap=slot_now[:, t, k:k + 1], axis=0),
                                                         in_=token_now[:, t:t + 1], in_offset=None).then_inc(scattered, 16)
                    pool.wait_ge(scattered, 16 * TB * K * (i + 1))
                    pool.sem_inc(slots_free, 1)


def build_wide_experts(nc, io, keep, r, tile_expert, weights):
    E = r.experts
    UPC = DC * INTER
    WC = 2 * UPC + INTER_C * D
    PAIRS = WIDE_TILES // 2
    HM = [min(P, INTER - P * j) for j in range(INTER_C)]
    with ExitStack() as ctx:
        sc = Scope(nc, ctx, "wide")
        tokens = sc.sb("tokens", [P, WIDE_TILES], U32)
        load_tokens(nc, r, tokens)
        now = sc.sb("now", [P, 2, 2], U32)
        xg = sc.sb("xg", [P, 2, 2, D])
        xT = [sc.sb(f"xT{q}", [P, 2, DC, P], F32R) for q in range(2)]
        sil = sc.sb("sil", [P, 2, INTER])
        hid = sc.sb("hid", [P, 2, INTER])
        hT = [sc.sb(f"hT{q}", [P, 2, INTER_C, P], F32R) for q in range(2)]
        y_sb = sc.sb("y", [P, 2, D])
        turn = sc.ps("turn", [P, 2, 512])
        up1 = sc.ps("up1", [P, 2, 512])
        up3 = sc.ps("up3", [P, 2, 512])
        out = sc.ps("out", [P, 2, 512])
        gathered = sc.sems("gathered", 2)
        stored = sc.sems("stored", 2)
        names = "now_done turned hi_done lo_done up_done sil_done hid_done hturned hhi_done hlo_done y_done y_moved pool_passed".split()
        s = {n: sc.sem(n) for n in names}

        def pairs(eng, pair):
            with eng.Fori(0, PAIRS // 2 - 1) as k:
                pair(2 * k, 0, k, False)
                pair(2 * k + 1, 1, k, False)
            pair(PAIRS - 2, 0, PAIRS // 2 - 1, False)
            pair(PAIRS - 1, 1, PAIRS // 2 - 1, True)

        with nc.Block() as block:

            @block.gpsimd
            def _(pool):
                with pool.Fori(0, PAIRS // 2) as k:
                    for par in range(2):
                        i = 2 * k + par
                        hold(pool, s["turned"], 2 * i + 2, s["pool_passed"])
                        nc.gpsimd.tensor_copy(now[:, par, :], tokens[:, bass.ds(2 * i, 2)]).then_inc(s["now_done"], 1)
                        hold(pool, s["now_done"], i + 1, s["pool_passed"])
                        for u in range(2):
                            nc.gpsimd.indirect_dma_start(out=xg[:, par, u, :], out_offset=None, in_=r.xn, in_offset=bass.IndirectOffsetOnAxis(ap=now[:, par, u:u + 1], axis=0))\
                                .then_inc(gathered[par], 16)

            @block.tensor
            def _(pe):
                def turn_slots(par, u, k):
                    pe.wait_ge(gathered[par], 32 * k + 32)
                    for c in range(DC):
                        mm = nc.tensor.transpose(turn[:, u, c * P:(c + 1) * P], xg[:, par, u, c * P:(c + 1) * P], keep["ident"][:, :])
                    mm.then_inc(s["turned"], 1)

                def pair(i, par, k, last):
                    base = [nc.tensor.value_load(tile_expert[0:1, bass.ds(2 * i + u, 1)], min_val=0, max_val=E - 1) * WC for u in range(2)]
                    for u in range(2):
                        j = 2 * i + u
                        pe.wait_ge(s["lo_done"], j + 1)
                        for bank, at in ((up1, 0), (up3, UPC)):
                            n = 0
                            for c in range(DC):
                                for q in range(2):
                                    mm = nc.tensor.matmul(bank[:, u, 0:INTER], xT[q][:, u, c, :], weights[:, bass.ds(base[u] + (at + c * INTER), INTER)], start=n == 0, stop=n == 2 * DC - 1)
                                    n += 1
                        mm.then_inc(s["up_done"], 1)
                    for u in range(2):
                        j = 2 * i + u
                        if not last:
                            turn_slots(1 - par, u, k + par)
                        pe.wait_ge(s["hid_done"], j + 1)
                        pe.wait_ge(s["y_moved"], j + 1)
                        for c in range(INTER_C):
                            mm = nc.tensor.transpose(out[0:HM[c], u, c * P:(c + 1) * P], hid[:, u, c * P:c * P + HM[c]], keep["ident"][:, :])
                        mm.then_inc(s["hturned"], 1)
                    for u in range(2):
                        j = 2 * i + u
                        pe.wait_ge(s["hlo_done"], j + 1)
                        n = 0
                        for c in range(INTER_C):
                            for q in range(2):
                                mm = nc.tensor.matmul(out[:, u, :], hT[q][0:HM[c], u, c, :], weights[0:HM[c], bass.ds(base[u] + (2 * UPC + c * D), D)], start=n == 0, stop=n == 2 * INTER_C - 1)
                                n += 1
                        mm.then_inc(s["y_done"], 1)

                pe.sem_inc(s["turned"], 4)
                for u in range(2):
                    turn_slots(0, u, 0)
                pairs(pe, pair)

            @block.scalar
            def _(act):
                def high(j, u):
                    act.wait_ge(s["turned"], j + 1 + 4)
                    nc.scalar.activation(xT[0][:, u, :, :], turn[:, u, :].rearrange("p (c s) -> p c s", c=DC), ACT.Copy).then_inc(s["hi_done"], 1)

                def pair(i, par, k, last):
                    for u in range(2):
                        act.wait_ge(s["up_done"], 2 * i + u + 1)
                        nc.scalar.activation(sil[:, u, :], up1[:, u, 0:INTER], ACT.Silu).then_inc(s["sil_done"], 1)
                    for u in range(2):
                        if not last:
                            high(2 * i + 2 + u, u)
                        act.wait_ge(s["hturned"], 2 * i + u + 1)
                        nc.scalar.activation(hT[0][:, u, 0:2, :], out[:, u, 0:2 * P].rearrange("p (c s) -> p c s", c=2), ACT.Copy)
                        nc.scalar.activation(hT[0][0:HM[2], u, 2, :], out[0:HM[2], u, 2 * P:3 * P], ACT.Copy).then_inc(s["hhi_done"], 1)
                    for u in range(2):
                        j = 2 * i + u
                        act.wait_ge(stored[u], 16 * i + 16)
                        act.wait_ge(s["y_done"], j + 1)
                        nc.scalar.activation(y_sb[:, u, :], out[:, u, :], ACT.Copy).then_inc(s["y_moved"], 1)
                        act.wait_ge(s["y_moved"], j + 3)
                        act.dma_start(rows(r.y, j * P, P), y_sb[:, u, :]).then_inc(stored[u], 16)

                act.sem_inc(s["y_moved"], 2)
                for u in range(2):
                    high(u, u)
                pairs(act, pair)
                for u in range(2):
                    act.wait_ge(stored[u], 16 * PAIRS + 16)

            @block.vector
            def _(dve):
                def low(j, u):
                    dve.wait_ge(s["hi_done"], j + 1)
                    nc.vector.tensor_tensor(xT[1][:, u, :, :], turn[:, u, :].rearrange("p (c s) -> p c s", c=DC), xT[0][:, u, :, :].bitcast(F32), ALU.subtract).then_inc(s["lo_done"], 1)

                def pair(i, par, k, last):
                    for u in range(2):
                        dve.wait_ge(s["sil_done"], 2 * i + u + 1)
                        nc.vector.tensor_tensor(hid[:, u, :], sil[:, u, :], up3[:, u, 0:INTER], ALU.mult).then_inc(s["hid_done"], 1)
                    for u in range(2):
                        if not last:
                            low(2 * i + 2 + u, u)
                        dve.wait_ge(s["hhi_done"], 2 * i + u + 1)
                        nc.vector.tensor_tensor(hT[1][:, u, 0:2, :], out[:, u, 0:2 * P].rearrange("p (c s) -> p c s", c=2), hT[0][:, u, 0:2, :].bitcast(F32), ALU.subtract)
                        nc.vector.tensor_tensor(hT[1][0:HM[2], u, 2, :], out[0:HM[2], u, 2 * P:3 * P], hT[0][0:HM[2], u, 2, :].bitcast(F32), ALU.subtract).then_inc(s["hlo_done"], 1)

                for u in range(2):
                    dve.sem_inc(stored[u], 16)
                for u in range(2):
                    low(u, u)
                pairs(dve, pair)


def build_wide_mixture(nc, io, keep, x_in, x_out):
    with ExitStack() as ctx:
        gate = keep["gates"][:, 6:7]
        sc = Scope(nc, ctx, "moe2")
        r = Routing(nc, sc, "moe2", 8, 2, WIDE_TILES * P, 0)
        r.ident = keep["ident"]
        late = {"idx": sc.sb("late_idx", [P, N // P, 2]), "pos": sc.sb("late_pos", [P, N // P, 2]), "counts": sc.sb("late_counts", [P, 8], BF16)}
        tile_expert = sc.sb("tile_expert", [P, WIDE_TILES], I32)
        x_mid = nc.dram_tensor("moe2_x_mid", [N, D], F32, kind="Internal").ap()
        build_route(nc, io, keep, x_in, x_mid, r, (("moe2_w1", "moe2_w3", "moe2_w2"), INTER, True), gate, late)
        with ExitStack() as inner:
            WC = 2 * DC * INTER + INTER_C * D
            weights = Scope(nc, inner, "moe2_experts").sb("weights", [P, r.experts * WC], F32R)
            build_late_slots(nc, io, keep, r, late, tile_expert, weights)
            build_wide_experts(nc, io, keep, r, tile_expert, weights)
        build_combine(nc, io, keep, r, x_mid, x_out, None)


GN = 8
GROUPS = S // GN
KPAD = D + P


def build_gated_conv(nc, io, keep, x_in, x_out):
    T = S // P
    NS = 2
    with ExitStack() as outer:
        osc = Scope(nc, outer, "conv")
        vT = osc.sb("vT", [P, DC, B, S])
        cT = osc.sb("cT", [P, B, DC, S])
        cTr = osc.sb("cTr", [P, B, DC, S])
        oT = osc.sb("oT", [P, DC, B, S])
        ctx_loaded = osc.sem("ctx_loaded")

        with ExitStack() as ctx:
            sc = Scope(nc, ctx, "skip")
            x_sb = sc.sb("x", [P, 2, T, D])
            c_sb = sc.sb("c", [P, 2, T, D])
            xn = sc.sb("xn", [P, T, D])
            z = sc.sb("z", [P, T, D])
            group8 = sc.sb("group8", [P, P])
            skip = sc.sb("skip", [P, T])
            skip_m = sc.sb("skip_m", [P, T, P])
            sk = sc.sb("sk", [P, T, D])
            x_mid = sc.sb("x_mid", [P, 2, T, D])
            stats = sc.sb("stats", [P, T, 6])
            mv = sc.sb("mv", [P, T, 2])
            ve = sc.sb("ve", [P, T])
            rstd = sc.sb("rstd", [P, T])
            turn = sc.ps("turn", [P, DC, 512])
            ssum = sc.ps("ssum", [P, T, D])
            const_loaded = sc.sem("const_loaded")
            loaded = sc.sems("loaded", 2)
            stored = sc.sems("stored", 2)
            inputs_free = sc.sem("inputs_free")
            stats_done = sc.sem("stats_done")
            var_done = sc.sem("var_done")
            ve_done = sc.sem("ve_done")
            rstd_done = sc.sem("rstd_done")
            xn_done = sc.sem("xn_done")
            z_done = sc.sem("z_done")
            skip_done = sc.sem("skip_done")
            turned = sc.sem("turned")
            vT_done = sc.sem("vT_done")
            ssum_done = sc.sem("ssum_done")
            sk_done = sc.sem("sk_done")
            mid_done = sc.sem("mid_done")
            passed = sc.sem("passed")
            with nc.Block() as block:

                @block.sync
                def _(sp):
                    sp.dma_start(group8[:, :], io["group8"]).then_inc(const_loaded, 16)
                    sp.dma_start(skip[:, :], io["skip"]).then_inc(const_loaded, 16)
                    with sp.Fori(0, B // 2) as i:
                        for u in range(2):
                            b = 2 * i + u
                            sp.wait_ge(inputs_free, b + 1)
                            sp.dma_start(x_sb[:, u], rows(x_in, b * S, S).rearrange("(t p) d -> p t d", p=P)).then_inc(loaded[u], 16)
                            sp.dma_start(c_sb[:, u], rows(io["ctx"], b * S, S).rearrange("(t p) d -> p t d", p=P)).then_inc(loaded[u], 16)
                    sp.dma_start(cT[:, :, :, :], io["ctxT"].rearrange("b p c s -> p b c s")).then_inc(ctx_loaded, 16)
                    sp.dma_start(cTr[:, :, :, :], io["ctxTr"].rearrange("b p c s -> p b c s")).then_inc(ctx_loaded, 16)

                @block.tensor
                def _(pe):
                    pe.wait_ge(skip_done, T)
                    with pe.Fori(0, B) as b:
                        pe.wait_ge(xn_done, T * b + T)
                        for c in range(DC):
                            pe.wait_ge(vT_done, DC * b + c + 1)
                            for t in range(T):
                                mm = nc.tensor.transpose(turn[:, c, t * P:(t + 1) * P], xn[:, t, c * P:(c + 1) * P], keep["ident"][:, :])
                            mm.then_inc(turned, 1)
                        for t in range(T):
                            pe.wait_ge(z_done, T * b + t + 1)
                            pe.wait_ge(sk_done, T * b + t + 1)
                            nc.tensor.matmul(ssum[:, t, :], skip_m[:, t, :], z[:, t, :], start=True, stop=True).then_inc(ssum_done, 1)

                @block.vector
                def _(dve):
                    for sem, n in ((inputs_free, 2), (sk_done, T), (turned, 1), (ssum_done, T), (stored[0], 16), (stored[1], 16)):
                        dve.sem_inc(sem, n)
                    dve.wait_ge(const_loaded, 32)
                    for t in range(T):
                        nc.vector.tensor_scalar(skip_m[:, t, :], group8[:, :], skip[:, t:t + 1], None, ALU.mult).then_inc(skip_done, 1)
                    with dve.Fori(0, B // 2) as i:
                        for u in range(2):
                            b = 2 * i + u
                            dve.wait_ge(loaded[u], 32 * i + 32)
                            for t in range(T):
                                nc.vector.bn_stats(stats[:, t, :], x_sb[:, u, t, :]).then_inc(stats_done, 1)
                            hold(dve, stats_done, T * b + T, passed)
                            for t in range(T):
                                nc.vector.bn_aggr(mv[:, t, :], stats[:, t, :]).then_inc(var_done, 1)
                            dve.wait_ge(var_done, T * b + T)
                            nc.vector.tensor_scalar(ve[:, :], mv[:, :, 1], LN_EPS, None, ALU.add).then_inc(ve_done, 1)
                            dve.wait_ge(rstd_done, b + 1)
                            dve.wait_ge(turned, DC * b + 1)
                            for t in range(T):
                                nc.vector.tensor_scalar(xn[:, t, :], x_sb[:, u, t, :], mv[:, t, 0:1], rstd[:, t:t + 1], ALU.subtract, ALU.mult).then_inc(xn_done, 1)
                            for t in range(T):
                                dve.wait_ge(xn_done, T * b + t + 1)
                                dve.wait_ge(ssum_done, T * b + t + 1)
                                nc.vector.tensor_tensor(z[:, t, :], xn[:, t, :], c_sb[:, u, t, :], ALU.mult).then_inc(z_done, 1)
                            dve.wait_ge(stored[u], 16 * i + 16)
                            for t in range(T):
                                dve.wait_ge(ssum_done, T * b + t + 1 + T)
                                nc.vector.tensor_tensor(sk[:, t, :], ssum[:, t, :], c_sb[:, u, t, :], ALU.mult).then_inc(sk_done, 1)
                                dve.wait_ge(sk_done, T * b + t + 1 + T)
                                nc.vector.scalar_tensor_tensor(out=x_mid[:, u, t, :], in0=sk[:, t, :], scalar=keep["gates"][:, 3:4], in1=x_sb[:, u, t, :],
                                                               op0=ALU.mult, op1=ALU.add).then_inc(mid_done, 1)
                            dve.wait_ge(mid_done, T * b + T)
                            dve.sem_inc(inputs_free, 1)

                @block.gpsimd
                def _(pool):
                    with pool.Fori(0, B) as b:
                        pool.wait_ge(ve_done, b + 1)
                        nc.gpsimd.tensor_tensor(rstd[:, :], ve[:, :], keep["neg_half"][:, 0:T], ALU.pow).then_inc(rstd_done, 1)

                @block.scalar
                def _(act):
                    act.sem_inc(vT_done, DC)
                    with act.Fori(0, B // 2) as i:
                        for u in range(2):
                            b = 2 * i + u
                            for c in range(DC):
                                act.wait_ge(turned, DC * b + c + 2)
                                nc.scalar.activation(vT[:, c, bass.ds(b, 1), :].rearrange("p a s -> p (a s)"), turn[:, c, 0:S], ACT.Copy).then_inc(vT_done, 1)
                            act.wait_ge(mid_done, T * b + T)
                            act.dma_start(rows(x_out, b * S, S).rearrange("(t p) d -> p t d", p=P), x_mid[:, u]).then_inc(stored[u], 16)
                    for u in range(2):
                        act.wait_ge(stored[u], 16 * (B // 2) + 16)

        with ExitStack() as ctx:
            sc = Scope(nc, ctx, "toep")
            toep = sc.sb("toep", [P, NS, D])
            kv = sc.sb("kv", [P, NS, DC, 512])
            gated = sc.sb("gated", [P, 2, 512])
            y = sc.ps("y", [P, NS, DC, 512])
            loaded = sc.sems("loaded", NS)
            kv_done = sc.sem("kv_done")
            y_done = sc.sem("y_done")
            gated_done = sc.sem("gated_done")
            o_done = sc.sem("o_done")
            fourths = [P, B, GN, GN]

            with nc.Block() as block:

                @block.sync
                def _(sp):
                    with sp.Fori(0, GROUPS // NS) as i:
                        for u in range(NS):
                            h = NS * i + u
                            sp.wait_ge(y_done, DC * h + DC)
                            windows = bass.AP(io["filt"].tensor, h * KPAD, [[1, P], [1, D]])
                            sp.dma_start(toep[:, u, :], windows).then_inc(loaded[u], 16)

                @block.tensor
                def _(pe):
                    pe.sem_inc(y_done, NS * DC)
                    with pe.Fori(0, GROUPS // NS) as i:
                        for u in range(NS):
                            h = NS * i + u
                            pe.wait_ge(loaded[u], 16 * i + 16)
                            for lc in range(DC):
                                pe.wait_ge(kv_done, DC * h + lc + 1)
                                pe.wait_ge(gated_done, DC * h + lc + 1)
                                for mc in range(lc + 1):
                                    at = 384 - P * (lc - mc)
                                    mm = nc.tensor.matmul(y[:, u, lc, :], toep[:, u, at:at + P], kv[:, u, mc, :], start=mc == 0, stop=mc == lc)
                                mm.then_inc(y_done, 1)

                @block.vector
                def _(dve):
                    def pairs(h, u, c):
                        dve.wait_ge(y_done, DC * h + DC)
                        nc.vector.tensor_tensor(kv[:, u, c, :].rearrange("p (b i j) -> p b i j", b=B, i=GN),
                                                vT[:, c, :, bass.ds(GN * h, GN)].rearrange("p b (i j) -> p b i j", j=1).broadcast_to(fourths),
                                                cT[:, :, c, bass.ds(GN * h, GN)].rearrange("p b (i j) -> p b i j", i=1).broadcast_to(fourths),
                                                ALU.mult).then_inc(kv_done, 1)

                    def combine(h, u, lc):
                        n = DC * h + lc
                        dve.wait_ge(y_done, n + 1 + NS * DC)
                        dve.wait_ge(o_done, n + 1)
                        nc.vector.tensor_tensor(gated[:, lc % 2, :].rearrange("p (b i j) -> p b i j", b=B, i=GN), y[:, u, lc, :].rearrange("p (b i j) -> p b i j", b=B, i=GN),
                                                cTr[:, :, lc, bass.ds(GN * h, GN)].rearrange("p b (i j) -> p b i j", j=1).broadcast_to(fourths),
                                                ALU.mult).then_inc(gated_done, 1)
                        dve.wait_ge(gated_done, n + 1 + NS * DC)
                        nc.vector.tensor_reduce(oT[:, lc, :, bass.ds(GN * h, GN)], gated[:, lc % 2, :].rearrange("p (b i j) -> p b j i", b=B, i=GN), AX.X, ALU.add)\
                            .then_inc(o_done, 1)

                    dve.sem_inc(gated_done, NS * DC)
                    dve.sem_inc(o_done, 2)
                    dve.wait_ge(ctx_loaded, 32)
                    for c in range(DC):
                        pairs(0, 0, c)
                    with dve.Fori(0, GROUPS // NS - 1) as i:
                        for u in range(NS):
                            for c in range(DC):
                                pairs(NS * i + u + 1, 1 - u, c)
                                combine(NS * i + u, u, c)
                    for c in range(DC):
                        pairs(GROUPS - 1, 1, c)
                        combine(GROUPS - 2, 0, c)
                    for c in range(DC):
                        combine(GROUPS - 1, 1, c)

        with ExitStack() as ctx:
            sc = Scope(nc, ctx, "back")
            o_b = sc.sb("o_b", [P, 2, DC, S])
            x_mid = sc.sb("x_mid", [P, 2, T, D])
            x_new = sc.sb("x_new", [P, 2, T, D])
            rows_ps = sc.ps("rows", [P, 2, T, D])
            loaded = sc.sems("loaded", 2)
            stored = sc.sems("stored", 2)
            mid_free = sc.sem("mid_free")
            o_copied = sc.sem("o_copied")
            rows_done = sc.sem("rows_done")
            out_done = sc.sem("out_done")
            with nc.Block() as block:

                @block.sync
                def _(sp):
                    with sp.Fori(0, B // 2) as i:
                        for u in range(2):
                            b = 2 * i + u
                            sp.wait_ge(mid_free, b + 1)
                            sp.dma_start(x_mid[:, u], rows(x_out, b * S, S).rearrange("(t p) d -> p t d", p=P)).then_inc(loaded[u], 16)

                @block.tensor
                def _(pe):
                    with pe.Fori(0, B // 2) as i:
                        for u in range(2):
                            b = 2 * i + u
                            pe.wait_ge(o_copied, b + 1)
                            pe.wait_ge(out_done, T * b + T)
                            for t in range(T):
                                for c in range(DC):
                                    mm = nc.tensor.matmul(rows_ps[:, u, t, c * P:(c + 1) * P], o_b[:, u, c, t * P:(t + 1) * P], keep["anti"][:, :], start=True, stop=True)
                                mm.then_inc(rows_done, 1)

                @block.vector
                def _(dve):
                    for sem, n in ((mid_free, 2), (out_done, 2 * T), (rows_done, 2 * T), (stored[0], 16), (stored[1], 16)):
                        dve.sem_inc(sem, n)
                    with dve.Fori(0, B // 2) as i:
                        for u in range(2):
                            b = 2 * i + u
                            dve.wait_ge(loaded[u], 16 * i + 16)
                            dve.wait_ge(stored[u], 16 * i + 16)
                            for t in range(T):
                                dve.wait_ge(rows_done, T * b + t + 1 + 2 * T)
                                nc.vector.scalar_tensor_tensor(out=x_new[:, u, t, :], in0=rows_ps[:, u, t, :], scalar=keep["gates"][:, 3:4], in1=x_mid[:, u, t, :],
                                                               op0=ALU.mult, op1=ALU.add).then_inc(out_done, 1)
                            dve.wait_ge(out_done, T * b + 3 * T)
                            dve.sem_inc(mid_free, 1)

                @block.scalar
                def _(act):
                    with act.Fori(0, B // 2) as i:
                        for u in range(2):
                            b = 2 * i + u
                            act.wait_ge(rows_done, T * b + T)
                            nc.scalar.activation(o_b[:, u, :, :], oT[:, :, bass.ds(b, 1), :].rearrange("p c a s -> p c (a s)"), ACT.Copy).then_inc(o_copied, 1)
                            act.wait_ge(out_done, T * b + 3 * T)
                            act.dma_start(rows(x_out, b * S, S).rearrange("(t p) d -> p t d", p=P), x_new[:, u]).then_inc(stored[u], 16)
                    for u in range(2):
                        act.wait_ge(stored[u], 16 * (B // 2) + 16)


STAGES = [build_channel_attention, build_small_mixture, build_linear_attention, build_ternary_ffn, build_feature_attention, build_wide_mixture, build_gated_conv, build_lut_ffn]

INPUTS = {"x": "x", "ctx": "ctx_2048", "g_xattn": "g_xattn", "g_ffn": "g_ffn", "gamma": "L0_xattn_gamma"}


def build(nc, io, out):
    with ExitStack() as ctx:
        keep = {name: ctx.enter_context(nc.sbuf_tensor(f"keep_{name}", shape, dt)) for name, shape, dt in [
            ("ident", [P, P], F32), ("anti", [P, P], F32), ("ident_bf", [P, P], BF16), ("gates", [P, 8], F32), ("gate0", [P, 1], F32),
            ("neg_half", [P, 16], F32), ("half", [P, 32], F32), ("ones", [P, P], F32), ("ones_bf", [P, P], BF16),
            ("earlier_f", [P, P], F32), ("earlier", [P, P], BF16), ("iota", [P, 64], F32), ("spare", [P, 1], F32), ("row_id", [P, N // P], I32), ("zeros_i", [P, 136], I32)]}
        state = nc.dram_tensor("x_state", [N, D], F32, kind="Internal").ap()
        io = io | {"lut_weights": nc.dram_tensor("lut_weights", [P, 3 * WCOLS], F32, kind="Internal").ap()}
        build_setup(nc, io, keep)
        todo = list(PHASES)
        for s in todo:
            STAGES[s](nc, io, keep, io["x"] if s == todo[0] else state, out if s == todo[-1] else state)


def kernel(**inputs):
    import concourse.bacc as _bacc
    from concourse.bass_utils import run_bass_kernel_spmd as _run

    a = {k: np.asarray(v) for k, v in inputs.items()}
    ctx = a["ctx_2048"]
    arrays = {
        "x": a["x"].reshape(N, D), "ctx": ctx.reshape(N, D),
        "ctxT": ctx.transpose(0, 2, 1).reshape(B, DC, P, S).transpose(0, 2, 1, 3),
        "g_xattn": a["g_xattn"], "g_ffn": a["g_ffn"], "gamma": a["L0_xattn_gamma"].reshape(1, 1),
    }

    def contraction_first(w, pad):
        w = np.concatenate([w, np.zeros((pad - w.shape[0], D), w.dtype)])
        return w.T.reshape(DC, P, pad).transpose(1, 0, 2).reshape(P, DC * pad)

    def units_first(w, pad):
        w = np.concatenate([w.T, np.zeros((pad - w.shape[1], D), w.dtype)])
        return w.reshape(pad // P, P, D).transpose(1, 0, 2).reshape(P, pad // P * D)

    def square(w):
        return w.T.reshape(DC, P, D).transpose(1, 0, 2).reshape(P, DC * D)

    filt = a["L3_xattn_k"][:, ::-1]
    arrays |= {
        "filt": np.concatenate([filt, np.zeros((filt.shape[0], P), filt.dtype)], axis=1).reshape(-1),
        "ctxTr": arrays["ctxT"][:, ::-1],
        "skip": a["fside_S2_0"].reshape(S // P, P).T,
        "group8": np.kron(np.eye(P // GN, dtype=np.float32), np.ones((GN, GN), np.float32)),
    }
    def chunks(w):
        return w.reshape(-1, P, w.shape[1]).transpose(1, 0, 2).reshape(P, -1)

    up = a["L0_ffn_w_shared_up"]
    arrays |= {
        "moe0_w1": chunks(up[:, 128:]), "moe0_w3": chunks(up[:, :128]), "moe0_w2": chunks(a["L0_ffn_w_shared_down"]), "moe0_wg": chunks(a["L0_ffn_w_gate"]),
        "w_up": a["L0_ffn_w_up"].reshape(64, DC, P, 128).transpose(0, 2, 1, 3).reshape(64, P, DC * 128), "w_down": a["L0_ffn_w_down"],
    }
    def padded_rows(w):
        return np.concatenate([w, np.zeros((-w.shape[0] % P, w.shape[1]), w.dtype)])

    arrays |= {
        "moe2_w1": chunks(a["L2_ffn_sw1"].T), "moe2_w3": chunks(a["L2_ffn_sw3"].T), "moe2_w2": chunks(padded_rows(a["L2_ffn_sw2"].T)),
        "moe2_wg": chunks(a["L2_ffn_gate_w"].T), "moe2_bias": a["L2_ffn_gate_b"].reshape(1, -1),
        "moe2_w": np.stack([np.concatenate([chunks(a["L2_ffn_w1"][e].T), chunks(a["L2_ffn_w3"][e].T), chunks(padded_rows(a["L2_ffn_w2"][e].T))], axis=1)
                            for e in range(8)]),
    }
    arrays |= {n.lower(): square(a[f"L1_xattn_{n}"]) for n in ("Wq", "Wk", "Wv", "Wo")}
    arrays |= {n: a[f"L1_xattn_{n}"].reshape(DC, P).T for n in ("bq", "bk")}
    arrays |= {n: a[f"L1_xattn_{n}"].reshape(1, D) for n in ("bv", "bo")}
    arrays |= {"wqf": a["L1_xattn_Wqf"].T, "wkf": a["L1_xattn_Wkf"].T, "mask": a["mask_BxS2_ff1"].reshape(N // P, P).T}
    arrays |= {
        "w1t": contraction_first(a["L1_ffn_w1"], HPAD), "w3t": contraction_first(a["L1_ffn_w3"], HPAD), "w2t": units_first(a["L1_ffn_w2"], HPAD),
        "lut": a["L3_ffn_lut"],
        "lut_idx": np.concatenate([contraction_first(a["L3_ffn_gate_idx"], HPAD), contraction_first(a["L3_ffn_up_idx"], HPAD),
                                   units_first(a["L3_ffn_down_idx"], HPAD)], axis=1),
    }
    arrays = {f"in_{k}": np.ascontiguousarray(v) for k, v in arrays.items()}
    nc = _bacc.Bacc("TRN2", target_bir_lowering=False, num_devices=1)
    io = {k[3:]: nc.dram_tensor(k, v.shape, mybir.dt.from_np(v.dtype), kind="ExternalInput").ap() for k, v in arrays.items()}
    out = nc.dram_tensor("x_out", [N, D], F32, kind="ExternalOutput").ap()
    build(nc, io, out)
    r = _run(nc, [arrays], core_ids=[0])
    return r.results[0]["x_out"].reshape(B, S, D)
```

```python
from contextlib import ExitStack

import numpy as np
import concourse.bass as bass
from concourse import mybir

ALU = mybir.AluOpType
ACT = mybir.ActivationFunctionType
AX = mybir.AxisListType
F32 = mybir.dt.float32
BF16 = mybir.dt.bfloat16
I32 = mybir.dt.int32
U32 = mybir.dt.uint32

P = 128
B, S, D = 8, 256, 512
N = B * S
DC = D // P
LN_EPS = 1e-5


class Scope:

    def __init__(self, nc, ctx, name):
        self.nc, self.ctx, self.name = nc, ctx, name
        self.held = []
        ctx.callback(self.release)

    def release(self):
        if self.held:
            self.nc.clear_and_free_semaphores(self.held)
            self.nc.all_engine_barrier()

    def sb(self, name, shape, dt=F32):
        return self.ctx.enter_context(self.nc.sbuf_tensor(f"{self.name}_{name}", shape, dt))

    def ps(self, name, shape, dt=F32):
        return self.ctx.enter_context(self.nc.psum_tensor(f"{self.name}_{name}", shape, dt))

    def sem(self, name):
        self.held.append(self.nc.alloc_semaphore(f"{self.name}_{name}"))
        return self.held[-1]

    def sems(self, name, n):
        return [self.sem(f"{name}{i}") for i in range(n)]


def hold(eng, sem, val, passed):
    eng.wait_ge(sem, val)
    eng.sem_inc(passed, 1)


def rows(ap, start, count):
    return ap[bass.ds(start, count), :]


def build_setup(nc, io, keep):
    with ExitStack() as ctx:
        sc = Scope(nc, ctx, "setup")
        g_raw = sc.sb("g_raw", [P, 8])
        gamma = sc.sb("gamma", [P, 1])
        iota_i = sc.sb("iota_i", [P, 64], I32)
        spare_i = sc.sb("spare_i", [P, 1], I32)
        ints_done = sc.sem("ints_done")
        g_loaded = sc.sem("g_loaded")
        tanh_done = sc.sem("tanh_done")
        zeroed = sc.sem("zeroed")
        const_done = sc.sem("const_done")
        with nc.Block() as block:

            @block.sync
            def _(sp):
                sp.dma_start(g_raw[:, 0:4], io["g_xattn"].rearrange("(a g) -> a g", a=1).broadcast_to([P, 4])).then_inc(g_loaded, 16)
                sp.dma_start(g_raw[:, 4:8], io["g_ffn"].rearrange("(a g) -> a g", a=1).broadcast_to([P, 4])).then_inc(g_loaded, 16)
                sp.dma_start(gamma[:, :], io["gamma"].broadcast_to([P, 1])).then_inc(g_loaded, 16)

            @block.scalar
            def _(act):
                act.wait_ge(g_loaded, 48)
                nc.scalar.activation(keep["gates"][:, :], g_raw[:, :], ACT.Tanh).then_inc(tanh_done, 1)

            @block.vector
            def _(dve):
                nc.vector.memset(keep["neg_half"][:, :], -0.5)
                nc.vector.memset(keep["half"][:, :], 0.5)
                nc.vector.memset(keep["ones"][:, :], 1.0)
                dve.wait_ge(tanh_done, 1)
                nc.vector.tensor_tensor(keep["gate0"][:, :], keep["gates"][:, 0:1], gamma[:, :], ALU.mult)
                dve.wait_ge(const_done, 1)
                nc.vector.tensor_copy(keep["ident_bf"][:, :], keep["ident"][:, :])
                nc.vector.memset(keep["ones_bf"][:, :], 1.0)
                nc.vector.memset(keep["zeros_i"][:, :], 0)
                dve.wait_ge(ints_done, 4)
                nc.vector.tensor_copy(keep["earlier"][:, :], keep["earlier_f"][:, :])
                nc.vector.tensor_copy(keep["iota"][:, :], iota_i[:, :])
                nc.vector.tensor_copy(keep["spare"][:, :], spare_i[:, :])

            @block.gpsimd
            def _(pool):
                nc.gpsimd.memset(keep["ident"][:, :], 0.0).then_inc(zeroed, 1)
                nc.gpsimd.memset(keep["anti"][:, :], 0.0).then_inc(zeroed, 1)
                nc.gpsimd.memset(keep["earlier_f"][:, :], 1.0).then_inc(zeroed, 1)
                pool.wait_ge(zeroed, 3)
                nc.gpsimd.affine_select(out=keep["earlier_f"][:, :], in_=keep["earlier_f"][:, :], compare_op=ALU.is_gt, fill=0.0,
                                        base=0, pattern=[[1, P]], channel_multiplier=-1).then_inc(ints_done, 1)
                nc.gpsimd.iota(iota_i[:, :], pattern=[[1, 64]], base=0, channel_multiplier=0).then_inc(ints_done, 1)
                nc.gpsimd.iota(spare_i[:, :], pattern=[[1, 1]], base=64 * CAP, channel_multiplier=1).then_inc(ints_done, 1)
                nc.gpsimd.iota(keep["row_id"][:, :], pattern=[[P, N // P]], base=0, channel_multiplier=1).then_inc(ints_done, 1)
                nc.gpsimd.affine_select(out=keep["ident"][:, :], in_=keep["ident"][:, :], compare_op=ALU.not_equal, fill=1.0,
                                        base=0, pattern=[[-1, P]], channel_multiplier=1).then_inc(const_done, 1)
                nc.gpsimd.affine_select(out=keep["anti"][:, :], in_=keep["anti"][:, :], compare_op=ALU.not_equal, fill=1.0,
                                        base=-(P - 1), pattern=[[1, P]], channel_multiplier=1)


def build_feature_attention(nc, io, keep, x_in, x_out):
    T = S // P
    scale = float(D) ** -0.5
    with ExitStack() as ctx:
        sc = Scope(nc, ctx, "fattn")
        x_ln = sc.sb("x_ln", [P, 2, T, D])
        x_res = sc.sb("x_res", [P, 2, T, D])
        k_sb = sc.sb("k", [P, 2, T, D])
        vt_sb = sc.sb("vt", [P, 2, DC, S])
        xn = sc.sb("xn", [P, 2, T, D])
        stats = sc.sb("stats", [P, T, 6])
        mv = sc.sb("mv", [P, T, 2])
        ve = sc.sb("ve", [P, T])
        rstd = sc.sb("rstd", [P, T])
        negmax = sc.sb("negmax", [P, 2, DC])
        bias = sc.sb("bias", [P, 2, DC])
        sums = sc.sb("sums", [P, 2, DC])
        rsum = sc.sb("rsum", [P, 2, DC])
        prob = sc.sb("prob", [P, 2, DC, D])
        vs = sc.sb("vs", [P, 2, DC, S])
        x_new = sc.sb("x_new", [P, 2, T, D])
        scores = sc.ps("scores", [P, DC, D])
        mixed = sc.ps("mixed", [P, 2, T, D])

        ln_loaded = sc.sems("ln_loaded", 2)
        kv_loaded = sc.sems("kv_loaded", 2)
        res_loaded = sc.sems("res_loaded", 2)
        stored = sc.sems("stored", 2)
        passed = sc.sem("passed")
        stats_done = sc.sem("stats_done")
        var_done = sc.sem("var_done")
        ve_done = sc.sem("ve_done")
        rstd_done = sc.sem("rstd_done")
        xn_done = sc.sem("xn_done")
        scores_done = sc.sem("scores_done")
        max_done = sc.sem("max_done")
        bias_done = sc.sem("bias_done")
        prob_done = sc.sem("prob_done")
        rsum_done = sc.sem("rsum_done")
        vs_done = sc.sem("vs_done")
        mixed_done = sc.sem("mixed_done")
        out_done = sc.sem("out_done")

        def elements(eng, element):
            with eng.Fori(0, B // 2 - 1) as i:
                element(2 * i, 0, i)
                element(2 * i + 1, 1, i)
            element(B - 2, 0, B // 2 - 1)
            element(B - 1, 1, B // 2 - 1)

        def is_last(b):
            return isinstance(b, int) and b == B - 1

        with nc.Block() as block:

            @block.sync
            def _(sp):
                def load_ln(b, u):
                    sp.dma_start(x_ln[:, u], rows(x_in, b * S, S).rearrange("(t p) d -> p t d", p=P)).then_inc(ln_loaded[u], 16)

                def load_kv(b, u):
                    sp.dma_start(k_sb[:, u], rows(io["ctx"], b * S, S).rearrange("(t p) d -> p t d", p=P)).then_inc(kv_loaded[u], 16)
                    sp.dma_start(vt_sb[:, u], io["ctxT"][bass.ds(b, 1)].rearrange("b p c s -> p (b c) s")).then_inc(kv_loaded[u], 16)

                def load_res(b, u):
                    sp.dma_start(x_res[:, u], rows(x_in, b * S, S).rearrange("(t p) d -> p t d", p=P)).then_inc(res_loaded[u], 16)

                def element(b, u, ln_ahead):
                    sp.wait_ge(vs_done, DC * b + DC)
                    load_kv(b + 2, u)
                    if ln_ahead:
                        sp.wait_ge(xn_done, T * b + 3 * T)
                        load_ln(b + 4, u)
                    sp.wait_ge(out_done, T * b + 3 * T)
                    load_res(b + 2, u)

                for u in range(2):
                    load_ln(u, u)
                    load_kv(u, u)
                for u in range(2):
                    load_res(u, u)
                    sp.wait_ge(xn_done, T * u + T)
                    load_ln(u + 2, u)
                with sp.Fori(0, B // 2 - 2) as i:
                    element(2 * i, 0, True)
                    element(2 * i + 1, 1, True)
                for u in range(2):
                    element(B - 4 + u, u, False)

            @block.tensor
            def _(pe):
                def score(b, u, e):
                    for t in range(T):
                        mm = nc.tensor.matmul(scores[:, e, :], k_sb[:, u, t, e * P:(e + 1) * P], xn[:, u, t, :], start=t == 0, stop=t == T - 1)
                    mm.then_inc(scores_done, 1)

                def element(b, u, i):
                    if not is_last(b):
                        pe.wait_ge(kv_loaded[1 - u], 32 * (i + u) + 32)
                        pe.wait_ge(xn_done, T * b + 2 * T)
                        for e in range(DC):
                            pe.wait_ge(prob_done, DC * b + e + 1)
                            score(b + 1, 1 - u, e)
                    pe.wait_ge(out_done, T * b + T)
                    for e in range(DC):
                        pe.wait_ge(vs_done, DC * b + e + 1)
                        for t in range(T):
                            mm = nc.tensor.matmul(mixed[:, u, t, :], vs[:, u, e, t * P:(t + 1) * P], prob[:, u, e, :], start=e == 0, stop=e == DC - 1)
                    mm.then_inc(mixed_done, 1)

                pe.wait_ge(kv_loaded[0], 32)
                pe.wait_ge(xn_done, T)
                for e in range(DC):
                    score(0, 0, e)
                elements(pe, element)

            @block.vector
            def _(dve):
                def norm(b, u, i):
                    dve.wait_ge(ln_loaded[u], 16 * i + 16)
                    for t in range(T):
                        nc.vector.bn_stats(stats[:, t, :], x_ln[:, u, t, :]).then_inc(stats_done, 1)
                    hold(dve, stats_done, T * b + T, passed)
                    for t in range(T):
                        nc.vector.bn_aggr(mv[:, t, :], stats[:, t, :]).then_inc(var_done, 1)
                    dve.wait_ge(var_done, T * b + T)
                    nc.vector.tensor_scalar(ve[:, :], mv[:, :, 1], LN_EPS, None, ALU.add).then_inc(ve_done, 1)
                    dve.wait_ge(rstd_done, b + 1)
                    for t in range(T):
                        nc.vector.tensor_scalar(xn[:, u, t, :], x_ln[:, u, t, :], mv[:, t, 0:1], rstd[:, t:t + 1], ALU.subtract, ALU.mult).then_inc(xn_done, 1)

                def maximum(b, u, e):
                    n = DC * b + e + 1
                    dve.wait_ge(scores_done, n)
                    nc.vector.tensor_reduce(negmax[:, u, e:e + 1], scores[:, e, :], AX.X, ALU.max, negate=True).then_inc(max_done, 1)
                    dve.wait_ge(max_done, n)
                    nc.vector.tensor_scalar(bias[:, u, e:e + 1], negmax[:, u, e:e + 1], scale, None, ALU.mult).then_inc(bias_done, 1)

                def values(b, u, e):
                    n = DC * b + e + 1
                    dve.wait_ge(prob_done, n)
                    nc.vector.reciprocal(rsum[:, u, e:e + 1], sums[:, u, e:e + 1]).then_inc(rsum_done, 1)
                    dve.wait_ge(rsum_done, n)
                    nc.vector.tensor_scalar(vs[:, u, e, :], vt_sb[:, u, e, :], rsum[:, u, e:e + 1], None, ALU.mult).then_inc(vs_done, 1)

                def element(b, u, i):
                    dve.wait_ge(kv_loaded[u], 32 * i + 32)
                    dve.wait_ge(mixed_done, b + 1)
                    for e in range(DC):
                        values(b, u, e)
                        if not is_last(b):
                            maximum(b + 1, 1 - u, e)
                    if not (isinstance(b, int) and b >= B - 2):
                        norm(b + 2, u, i + 1)
                    dve.wait_ge(mixed_done, b + 3)
                    dve.wait_ge(res_loaded[u], 16 * i + 16)
                    dve.wait_ge(stored[u], 16 * i + 16)
                    for t in range(T):
                        nc.vector.scalar_tensor_tensor(out=x_new[:, u, t, :], in0=mixed[:, u, t, :], scalar=keep["gates"][:, 2:3], in1=x_res[:, u, t, :],
                                                       op0=ALU.mult, op1=ALU.add).then_inc(out_done, 1)

                for sem, n in ((mixed_done, 2), (out_done, 2 * T), (stored[0], 16), (stored[1], 16)):
                    dve.sem_inc(sem, n)
                norm(0, 0, 0)
                norm(1, 1, 0)
                for e in range(DC):
                    maximum(0, 0, e)
                elements(dve, element)

            @block.gpsimd
            def _(pool):
                with pool.Fori(0, B) as b:
                    pool.wait_ge(ve_done, b + 1)
                    nc.gpsimd.tensor_tensor(rstd[:, :], ve[:, :], keep["neg_half"][:, 0:T], ALU.pow).then_inc(rstd_done, 1)

            @block.scalar
            def _(act):
                def exponentials(b, u):
                    act.wait_ge(mixed_done, b + 1)
                    for e in range(DC):
                        act.wait_ge(bias_done, DC * b + e + 1)
                        nc.scalar.activation(prob[:, u, e, :], scores[:, e, :], ACT.Exp, bias=bias[:, u, e:e + 1], scale=scale, accum_out=sums[:, u, e:e + 1]).then_inc(prob_done, 1)

                def element(b, u, i):
                    if not is_last(b):
                        exponentials(b + 1, 1 - u)
                    act.wait_ge(out_done, T * b + 3 * T)
                    act.dma_start(rows(x_out, b * S, S).rearrange("(t p) d -> p t d", p=P), x_new[:, u]).then_inc(stored[u], 16)

                exponentials(0, 0)
                elements(act, element)
                for u in range(2):
                    act.wait_ge(stored[u], 16 * (B // 2) + 16)


def build_channel_attention(nc, io, keep, x_in, x_out):
    T = S // P
    H4 = 4
    HDIM = S // 8
    QC = D // P
    GROUPS = T * QC
    UB = GROUPS * H4
    scale = float(HDIM) ** -0.5
    with ExitStack() as ctx:
        sc = Scope(nc, ctx, "cattn")
        x_sb = sc.sb("x", [P, 2, T, D])
        k_sb = sc.sb("k", [P, 2, T, D])
        vT = sc.sb("vT", [P, 2, DC, S])
        xn = sc.sb("xn", [P, 2, T, H4, D])
        stats = sc.sb("stats", [P, T, 6])
        mv = sc.sb("mv", [P, T, 2])
        ve = sc.sb("ve", [P, T])
        rstd = sc.sb("rstd", [P, T])
        rstd_h = sc.sb("rstd_h", [P, T, H4])
        head_scale = sc.sb("head_scale", [P, T, H4])
        negmax = sc.sb("negmax", [P, 2, H4])
        sums = sc.sb("sums", [P, 2, H4])
        rsum = sc.sb("rsum", [P, 2, H4, HDIM])
        prob = sc.sb("prob", [P, 2, H4, D])
        probT = sc.sb("probT", [P, T, H4, DC, D])
        rsumT_sb = sc.sb("rsumT_sb", [P, T, D])
        o_sb = sc.sb("o", [P, D])
        x_new = sc.sb("x_new", [P, T, D])
        scores = sc.ps("scores", [P, H4, D])
        turn = sc.ps("turn", [P, 2, DC, P])
        pv = sc.ps("pv", [P, D])
        rsumT = sc.ps("rsumT", [P, D])
        lut = LutDecoder(nc, io, sc, LUT_FIRST[0])

        loaded = sc.sems("loaded", 2)
        stored = sc.sems("stored", T)
        stats_done = sc.sem("stats_done")
        var_done = sc.sem("var_done")
        ve_done = sc.sem("ve_done")
        pow_done = sc.sem("pow_done")
        rstd_done = sc.sem("rstd_done")
        xn_done = sc.sem("xn_done")
        scores_done = sc.sem("scores_done")
        max_done = sc.sem("max_done")
        exp_done = sc.sem("exp_done")
        turned = sc.sem("turned")
        act_out = sc.sem("act_out")
        dve_out = sc.sem("dve_out")
        pv_done = sc.sem("pv_done")
        rsum_done = sc.sem("rsum_done")
        rsumT_done = sc.sem("rsumT_done")
        rsumT_moved = sc.sem("rsumT_moved")
        o_done = sc.sem("o_done")
        out_done = sc.sem("out_done")
        const_done = sc.sem("const_done")
        passed = sc.sem("passed")

        def await_if(eng, sem, value):
            if not isinstance(value, int) or value > 0:
                eng.wait_ge(sem, value)

        def elements(eng, element):
            element(0, 0, 0)
            with eng.Fori(0, B // 2 - 1) as i:
                element(2 * i + 1, 1, i + 1)
                element(2 * i + 2, 0, i + 1)
            element(B - 1, 1, None)

        with nc.Block() as block:

            @block.sync
            def _(sp):
                def load(b, u):
                    sp.dma_start(x_sb[:, u], rows(x_in, b * S, S).rearrange("(t p) d -> p t d", p=P)).then_inc(loaded[u], 16)
                    sp.dma_start(k_sb[:, u], rows(io["ctx"], b * S, S).rearrange("(t p) d -> p t d", p=P)).then_inc(loaded[u], 16)
                    sp.dma_start(vT[:, u], io["ctxT"][bass.ds(b, 1)].rearrange("b p c s -> p (b c) s")).then_inc(loaded[u], 16)

                def store(b):
                    for t in range(T):
                        sp.wait_ge(out_done, T * b + t + 1)
                        sp.dma_start(rows(x_out, b * S + t * P, P), x_new[:, t]).then_inc(stored[t], 16)

                load(0, 0)
                lut.load_table(sp)
                lut.load(sp, 0)
                load(1, 1)
                with sp.Fori(0, B // 2 - 1) as i:
                    lut.load(sp, i + 1)
                    for u in range(2):
                        store(2 * i + u)
                        load(2 * i + u + 2, u)
                    lut.store(sp, i)
                for b in range(B - 2, B):
                    store(b)
                lut.store(sp, B // 2 - 1)
                lut.finish(sp, B // 2)
                for t in range(T):
                    sp.wait_ge(stored[t], 16 * B + 16)

            @block.tensor
            def _(pe):
                def score(b, u, g, h):
                    n = UB * b + H4 * g + h
                    t, qc = g // QC, g % QC
                    pe.wait_ge(xn_done, T * H4 * b + H4 * t + h + 1)
                    await_if(pe, exp_done, n + 1 - H4)
                    nc.tensor.matmul(scores[:, h, :], xn[:, u, t, h, qc * P:(qc + 1) * P], k_sb[:, u, t, :], start=True, stop=True).then_inc(scores_done, 1)

                def transpose(b, g, h):
                    n = UB * b + H4 * g + h
                    pe.wait_ge(exp_done, n + 1)
                    await_if(pe, dve_out if h % 2 else act_out, 2 * (GROUPS * b + g) + h // 2)
                    for c in range(DC):
                        mm = nc.tensor.transpose(turn[:, h % 2, c, :], prob[:, g % 2, h, c * P:(c + 1) * P], keep["ident"][:, :])
                    mm.then_inc(turned, 1)

                def turn_sums(b, g):
                    q = g % QC
                    pe.wait_ge(rsum_done, GROUPS * b + g + 1)
                    if q == 0:
                        await_if(pe, rsumT_moved, T * b + g // QC)
                    nc.tensor.transpose(rsumT[:, q * P:(q + 1) * P], rsum[:, q % 2, :, :].rearrange("p h e -> p (h e)"), keep["ident"][:, :]).then_inc(rsumT_done, 1)

                def values(half, u, t, c):
                    if c == 0:
                        pe.wait_ge(act_out, 2 * QC * half + 2 * QC)
                        pe.wait_ge(dve_out, 2 * QC * half + 2 * QC)
                        await_if(pe, out_done, half)
                    for h in range(H4):
                        head = H4 * t + h
                        mm = nc.tensor.matmul(pv[h * HDIM:(h + 1) * HDIM, :], vT[:, u, c, head * HDIM:(head + 1) * HDIM], probT[:, t, h, c, :],
                                              start=c == 0, stop=c == DC - 1, tile_position=(0, h * HDIM))
                    if c == DC - 1:
                        mm.then_inc(pv_done, 1)

                def element(b, u, next_load):
                    first, last = isinstance(b, int) and b == 0, isinstance(b, int) and b == B - 1
                    for g in range(GROUPS):
                        t, q = g // QC, g % QC
                        for h in range(H4):
                            if g < GROUPS - 1:
                                score(b, u, g + 1, h)
                            elif not last:
                                score(b + 1, 1 - u, 0, h)
                            if h == 0 and not (first and g == 0):
                                turn_sums(b, g - 1)
                            transpose(b, g, h)
                            if h % 2 and q < 2 and not (first and t == 0):
                                values(T * b + t - 1, u if t else 1 - u, 1 - t, 2 * q + h // 2)

                for h in range(H4):
                    score(0, 0, 0, h)
                elements(pe, element)
                turn_sums(B - 1, GROUPS - 1)
                for c in range(DC):
                    values(T * B - 1, 1, 1, c)

            @block.vector
            def _(dve):
                def norm_stats(b, u, load):
                    dve.wait_ge(loaded[u], 48 * load + 48)
                    for t in range(T):
                        nc.vector.bn_stats(stats[:, t, :], x_sb[:, u, t, :]).then_inc(stats_done, 1)
                    hold(dve, stats_done, T * b + T, passed)
                    for t in range(T):
                        nc.vector.bn_aggr(mv[:, t, :], stats[:, t, :]).then_inc(var_done, 1)
                    dve.wait_ge(var_done, T * b + T)
                    nc.vector.tensor_scalar(ve[:, :], mv[:, :, 1], LN_EPS, None, ALU.add).then_inc(ve_done, 1)

                def norm(b, u, j):
                    t, h = j // H4, j % H4
                    dve.wait_ge(rstd_done, b + 1)
                    nc.vector.tensor_scalar(xn[:, u, t, h, :], x_sb[:, u, t, :], mv[:, t, 0:1], rstd_h[:, t, h:h + 1], ALU.subtract, ALU.mult).then_inc(xn_done, 1)

                def maximum(b, g, h):
                    dve.wait_ge(scores_done, UB * b + H4 * g + h + 1)
                    nc.vector.tensor_reduce(negmax[:, g % 2, h:h + 1], scores[:, h, :], AX.X, ALU.max, negate=True).then_inc(max_done, 1)

                def evacuate(b, g, h):
                    t, q = g // QC, g % QC
                    dve.wait_ge(turned, UB * b + H4 * g + h + 1)
                    await_if(dve, pv_done, T * b + t - 1)
                    nc.vector.tensor_copy(probT[:, t, h, :, q * P:(q + 1) * P], turn[:, h % 2, :, :]).then_inc(dve_out, 1)

                def invert(b, g):
                    G = GROUPS * b + g
                    dve.wait_ge(exp_done, H4 * G + H4)
                    await_if(dve, rsumT_done, G - 1)
                    nc.vector.reciprocal(rsum[:, g % 2, :, :], sums[:, g % 2, :].rearrange("p (h e) -> p h e", e=1).broadcast_to([P, H4, HDIM])).then_inc(rsum_done, 1)

                def finish(b, u, t):
                    half = T * b + t
                    dve.wait_ge(pv_done, half + 1)
                    dve.wait_ge(rsumT_moved, half + 1)
                    await_if(dve, out_done, half)
                    nc.vector.tensor_tensor(o_sb[:, :], pv[:, :], rsumT_sb[:, t, :], ALU.mult).then_inc(o_done, 1)
                    dve.wait_ge(o_done, half + 1)
                    dve.wait_ge(stored[t], 16 * b + 16)
                    nc.vector.scalar_tensor_tensor(out=x_new[:, t, :], in0=o_sb[:, :], scalar=keep["gate0"][:, 0:1], in1=x_sb[:, u, t, :],
                                                   op0=ALU.mult, op1=ALU.add).then_inc(out_done, 1)

                def element(b, u, next_load):
                    first, last = isinstance(b, int) and b == 0, isinstance(b, int) and b == B - 1
                    for g in range(GROUPS):
                        if g == QC and not last:
                            norm_stats(b + 1, 1 - u, next_load)
                        for h in range(H4):
                            if h % 2:
                                evacuate(b, g, h)
                            if g < GROUPS - 1:
                                maximum(b, g + 1, h)
                            elif not last:
                                maximum(b + 1, 0, h)
                            if g > QC and not last and h < H4 - 1:
                                j = (g - QC - 1) * (H4 - 1) + h
                                if j < T * H4:
                                    norm(b + 1, 1 - u, j)
                        invert(b, g)
                        chunk = B // 2 - 1 if last else next_load - u
                        lut.step(dve, chunk, GROUPS * u + g)
                        if g == 1 and not first:
                            finish(b - 1, 1 - u, 1)
                        if g == QC + 1:
                            finish(b, u, 0)

                for t in range(T):
                    dve.sem_inc(stored[t], 16)
                nc.vector.memset(head_scale[:, :, :], 0.0).then_inc(const_done, 1)
                dve.wait_ge(const_done, 1)
                for h in range(H4):
                    nc.vector.memset(head_scale[h * HDIM:(h + 1) * HDIM, :, h:h + 1], scale).then_inc(const_done, 1)
                norm_stats(0, 0, 0)
                for j in range(T * H4):
                    norm(0, 0, j)
                for h in range(H4):
                    maximum(0, 0, h)
                lut.begin(dve)
                elements(dve, element)
                finish(B - 1, 1, 1)

            @block.gpsimd
            def _(pool):
                pool.wait_ge(const_done, 1 + H4)
                with pool.Fori(0, B) as b:
                    pool.wait_ge(ve_done, b + 1)
                    nc.gpsimd.tensor_tensor(rstd[:, :], ve[:, :], keep["neg_half"][:, 0:T], ALU.pow).then_inc(pow_done, 1)
                    pool.wait_ge(pow_done, b + 1)
                    nc.gpsimd.tensor_tensor(rstd_h[:, :, :], rstd[:, :].rearrange("p (t e) -> p t e", e=1).broadcast_to([P, T, H4]),
                                            head_scale[:, :, :], ALU.mult).then_inc(rstd_done, 1)

            @block.scalar
            def _(act):
                def exponential(b, g, h):
                    n = UB * b + H4 * g + h
                    if h == 0:
                        await_if(act, rsum_done, GROUPS * b + g - 1)
                    await_if(act, turned, n + 1 - 2 * H4)
                    act.wait_ge(max_done, n + 1)
                    nc.scalar.activation(prob[:, g % 2, h, :], scores[:, h, :], ACT.Exp, bias=negmax[:, g % 2, h:h + 1], accum_out=sums[:, g % 2, h:h + 1]).then_inc(exp_done, 1)

                def evacuate(b, g, h):
                    t, q = g // QC, g % QC
                    act.wait_ge(turned, UB * b + H4 * g + h + 1)
                    await_if(act, pv_done, T * b + t - 1)
                    nc.scalar.activation(probT[:, t, h, :, q * P:(q + 1) * P], turn[:, h % 2, :, :], ACT.Copy).then_inc(act_out, 1)

                def move_sums(b, t):
                    half = T * b + t
                    act.wait_ge(rsumT_done, QC * half + QC)
                    await_if(act, out_done, half - 1)
                    nc.scalar.activation(rsumT_sb[:, t, :], rsumT[:, :], ACT.Copy).then_inc(rsumT_moved, 1)

                def element(b, u, next_load):
                    first, last = isinstance(b, int) and b == 0, isinstance(b, int) and b == B - 1
                    for g in range(GROUPS):
                        for h in range(H4):
                            if h % 2 == 0:
                                evacuate(b, g, h)
                            if g < GROUPS - 1:
                                exponential(b, g + 1, h)
                            elif not last:
                                exponential(b + 1, 0, h)
                        if g == 0 and not first:
                            move_sums(b - 1, 1)
                        if g == QC:
                            move_sums(b, 0)

                for h in range(H4):
                    exponential(0, 0, h)
                elements(act, element)
                move_sums(B - 1, 1)


F32R = mybir.dt.float32r
BLK = 512
NB = N // BLK
TB = BLK // P
HC = 11
HPAD = HC * P
TERNARY_HIDDEN = 1365
LUT_HIDDEN = 1376
LUT_SIZE = 16
LUT_FIRST = {0: 0, "experts": 4, "combine": 12, 2: 16, 3: 20, "end": 24}
WCOLS = DC * HPAD


def build_ternary_weights(nc, io, keep, weights, scales):
    with ExitStack() as ctx:
        sc = Scope(nc, ctx, "tern")
        raw = sc.sb("raw", [P, 2, WCOLS])
        low = sc.sb("low", [P, WCOLS], BF16)
        magnitude = sc.sb("magnitude", [P, WCOLS])
        part = sc.sb("part", [P, 3])
        thr = sc.sb("thr", [P, 3])
        nthr = sc.sb("nthr", [P, 3])
        total = sc.ps("total", [P, 512])
        loaded = sc.sems("loaded", 2)
        part_done = sc.sem("part_done")
        total_done = sc.sem("total_done")
        scale_done = sc.sem("scale_done")
        thr_done = sc.sem("thr_done")
        low_done = sc.sem("low_done")
        weight_done = sc.sem("weight_done")
        with nc.Block() as block:

            @block.sync
            def _(sp):
                for m, name in enumerate(("w1t", "w3t", "w2t")):
                    if m == 2:
                        sp.wait_ge(weight_done, 1)
                    sp.dma_start(raw[:, m % 2, :], io[name]).then_inc(loaded[m % 2], 16)

            @block.tensor
            def _(pe):
                for m in range(3):
                    pe.wait_ge(part_done, m + 1)
                    if m:
                        pe.wait_ge(scale_done, m)
                    nc.tensor.matmul(total[:, m:m + 1], keep["ones"][:, :], part[:, m:m + 1], start=True, stop=True).then_inc(total_done, 1)

            @block.scalar
            def _(act):
                for m in range(3):
                    act.wait_ge(loaded[m % 2], 16 * (m // 2) + 16)
                    if m:
                        act.wait_ge(part_done, m)
                    nc.scalar.activation(magnitude[:, :], raw[:, m % 2, :], ACT.Abs, accum_out=part[:, m:m + 1]).then_inc(part_done, 1)

            @block.vector
            def _(dve):
                for m in range(3):
                    w = raw[:, m % 2, :]
                    dve.wait_ge(loaded[m % 2], 16 * (m // 2) + 16)
                    if m:
                        dve.wait_ge(weight_done, m)
                    dve.wait_ge(total_done, m + 1)
                    nc.vector.tensor_scalar(scales[:, m:m + 1], total[:, m:m + 1], 1.0 / (TERNARY_HIDDEN * D), None, ALU.mult).then_inc(scale_done, 1)
                    dve.wait_ge(scale_done, m + 1)
                    nc.vector.tensor_scalar(thr[:, m:m + 1], scales[:, m:m + 1], 0.5, None, ALU.mult).then_inc(thr_done, 1)
                    nc.vector.tensor_scalar(nthr[:, m:m + 1], scales[:, m:m + 1], -0.5, None, ALU.mult).then_inc(thr_done, 1)
                    dve.wait_ge(thr_done, 2 * m + 2)
                    nc.vector.tensor_scalar(low[:, :], w, nthr[:, m:m + 1], None, ALU.is_lt).then_inc(low_done, 1)
                    dve.wait_ge(low_done, m + 1)
                    nc.vector.scalar_tensor_tensor(out=weights[:, m, :], in0=w, scalar=thr[:, m:m + 1], in1=low[:, :], op0=ALU.is_gt, op1=ALU.subtract).then_inc(weight_done, 1)


class LutDecoder:
    CH = 704
    CHUNKS = 3 * WCOLS // CH
    K = LUT_SIZE

    def __init__(self, nc, io, sc, first):
        self.nc, self.io, self.first = nc, io, first
        self.lut = sc.sb("lut", [P, self.K])
        self.idx = sc.sb("lut_idx", [P, self.CH], I32)
        self.idxb = sc.sb("lut_idxb", [P, self.CH], BF16)
        self.mask = sc.sb("lut_mask", [P, 2, self.CH], BF16)
        self.acc = sc.sb("lut_acc", [P, 2, self.CH])
        self.out = sc.sb("lut_out", [P, self.CH])
        self.table_loaded = sc.sem("lut_table_loaded")
        self.idx_loaded = sc.sem("lut_idx_loaded")
        self.idxb_done = sc.sem("lut_idxb_done")
        self.mask_done = sc.sem("lut_mask_done")
        self.acc_done = sc.sem("lut_acc_done")
        self.stored = sc.sem("lut_stored")

    def columns(self, c):
        return bass.ds((self.first + c) * self.CH, self.CH)

    def load_table(self, sp):
        sp.dma_start(self.lut[:, :], self.io["lut"].rearrange("(a g) -> a g", a=1).broadcast_to([P, self.K])).then_inc(self.table_loaded, 16)

    def load(self, sp, c):
        sp.wait_ge(self.idxb_done, c + 1)
        sp.dma_start(self.idx[:, :], self.io["lut_idx"][:, self.columns(c)]).then_inc(self.idx_loaded, 16)

    def store(self, sp, c):
        sp.wait_ge(self.acc_done, self.K * (c + 1) + 2)
        sp.dma_start(self.io["lut_weights"][:, self.columns(c)], self.out[:, :]).then_inc(self.stored, 16)

    def finish(self, sp, chunks):
        sp.wait_ge(self.stored, 16 * chunks + 16)

    def begin(self, dve):
        for sem, n in ((self.idxb_done, 1), (self.mask_done, 1), (self.acc_done, 2), (self.stored, 16)):
            dve.sem_inc(sem, n)
        dve.wait_ge(self.table_loaded, 16)

    def step(self, dve, c, k):
        nc, K = self.nc, self.K
        if k == 0:
            dve.wait_ge(self.idx_loaded, 16 * c + 16)
            dve.wait_ge(self.mask_done, K * c + 1)
            nc.vector.tensor_copy(self.idxb[:, :], self.idx[:, :]).then_inc(self.idxb_done, 1)
            dve.wait_ge(self.idxb_done, c + 2)
        dve.wait_ge(self.acc_done, K * c + k + 1)
        nc.vector.tensor_scalar(self.mask[:, k % 2, :], self.idxb[:, :], float(k), None, ALU.is_equal).then_inc(self.mask_done, 1)
        dve.wait_ge(self.mask_done, K * c + k + 2)
        dve.wait_ge(self.acc_done, K * c + k + 2)
        if k == 0:
            nc.vector.tensor_scalar(self.acc[:, 0, :], self.mask[:, 0, :], self.lut[:, 0:1], None, ALU.mult).then_inc(self.acc_done, 1)
        else:
            if k == K - 1:
                dve.wait_ge(self.stored, 16 * c + 16)
            out = self.acc[:, k % 2, :] if k < K - 1 else self.out[:, :]
            nc.vector.scalar_tensor_tensor(out=out, in0=self.mask[:, k % 2, :], scalar=self.lut[:, k:k + 1], in1=self.acc[:, (k - 1) % 2, :],
                                           op0=ALU.mult, op1=ALU.add).then_inc(self.acc_done, 1)

    def steps(self, dve, first, begin, end):
        for n in range(begin, end):
            self.step(dve, first + n // self.K, n % self.K)


def build_ffn(nc, io, keep, x_in, x_out, ternary):
    name = "tffn" if ternary else "lffn"
    hidden = TERNARY_HIDDEN if ternary else LUT_HIDDEN
    gate = keep["gates"][:, 5:6] if ternary else keep["gates"][:, 7:8]
    parts = 2 if ternary else 1
    WDT = F32R if ternary else F32
    with ExitStack() as outer:
        osc = Scope(nc, outer, name)
        weights = osc.sb("weights", [P, 3, WCOLS], WDT)
        scales = osc.sb("scales", [P, 3])
        if ternary:
            build_ternary_weights(nc, io, keep, weights, scales)
        w1 = weights[:, 0, :].rearrange("p (c h) -> p c h", c=DC)
        w3 = weights[:, 1, :].rearrange("p (c h) -> p c h", c=DC)
        w2 = weights[:, 2, :].rearrange("p (j d) -> p j d", j=HC)
        HM = [min(P, (P * HC if ternary else hidden) - P * j) for j in range(HC)]
        with ExitStack() as ctx:
            sc = Scope(nc, ctx, name)
            x_ln = sc.sb("x_ln", [P, TB, D])
            x_res = sc.sb("x_res", [P, TB, D])
            xn = sc.sb("xn", [P, TB, D])
            xnT = [sc.sb(f"xnT{q}", [P, DC, BLK], WDT) for q in range(parts)]
            stats = sc.sb("stats", [P, TB, 6])
            mv = sc.sb("mv", [P, TB, 2])
            ve = sc.sb("ve", [P, TB])
            rstd = sc.sb("rstd", [P, TB])
            sil = sc.sb("sil", [P, 2, BLK])
            g32 = sc.sb("g32", [P, 2, BLK])
            gp = [sc.sb(f"g_part{q}", [P, 2, BLK], WDT) for q in range(parts)] if ternary else [g32]
            x_new = sc.sb("x_new", [P, TB, D])
            lut = LutDecoder(nc, io, sc, LUT_FIRST[3]) if ternary else None
            LC = LUT_FIRST["end"] - LUT_FIRST[3]
            LI = LC // NB
            out_scale = sc.sb("out_scale", [P, 1])
            s23 = sc.sb("s23", [P, 1])
            h1 = sc.ps("h1", [P, 2, BLK])
            h3 = sc.ps("h3", [P, 2, BLK])
            y = sc.ps("y", [P, TB, D])

            w_loaded = sc.sems("w_loaded", 3)
            ln_loaded = sc.sem("ln_loaded")
            res_loaded = sc.sem("res_loaded")
            stored = sc.sem("stored")
            ln_free = sc.sem("ln_free")
            res_free = sc.sem("res_free")
            stats_done = sc.sem("stats_done")
            var_done = sc.sem("var_done")
            ve_done = sc.sem("ve_done")
            rstd_done = sc.sem("rstd_done")
            xn_done = sc.sem("xn_done")
            turned = sc.sem("turned")
            hi_done = sc.sem("hi_done")
            lo_done = sc.sem("lo_done")
            h1_done = sc.sem("h1_done")
            h3_done = sc.sem("h3_done")
            sil_done = sc.sem("sil_done")
            g_done = sc.sem("g_done")
            ghi_done = sc.sem("ghi_done")
            glo_done = sc.sem("glo_done")
            y_step = sc.sem("y_step")
            out_done = sc.sem("out_done")
            scale_done = sc.sem("scale_done")
            passed = sc.sem("passed")
            dve_passed = sc.sem("dve_passed")
            g_ready = glo_done if ternary else g_done

            def left(i, j):
                return HC * i + j + 1 + (j == 0)

            with nc.Block() as block:

                @block.sync
                def _(sp):
                    def load_ln(i):
                        sp.wait_ge(ln_free, i + 1)
                        sp.dma_start(x_ln[:, :, :], rows(x_in, i * BLK, BLK).rearrange("(t p) d -> p t d", p=P)).then_inc(ln_loaded, 16)

                    def load_res(i):
                        sp.wait_ge(res_free, i + 1)
                        sp.dma_start(x_res[:, :, :], rows(x_in, i * BLK, BLK).rearrange("(t p) d -> p t d", p=P)).then_inc(res_loaded, 16)

                    def iteration(i, last):
                        if not last:
                            load_ln(i + 1)
                        if ternary:
                            for n in range(LI):
                                if not (last and n == LI - 1):
                                    lut.load(sp, LI * i + n + 1)
                                lut.store(sp, LI * i + n)
                        if not last:
                            load_res(i + 1)

                    load_ln(0)
                    if ternary:
                        lut.load_table(sp)
                        lut.load(sp, 0)
                    else:
                        for m in range(3):
                            sp.dma_start(weights[:, m, :], io["lut_weights"][:, m * WCOLS:(m + 1) * WCOLS]).then_inc(w_loaded[m], 16)
                    load_res(0)
                    with sp.Fori(0, NB - 1) as i:
                        iteration(i, False)
                    iteration(NB - 1, True)
                    if ternary:
                        lut.finish(sp, LC)

                @block.tensor
                def _(pe):
                    def turn(i):
                        pe.wait_ge(sil_done, HC * i + 2)
                        pe.wait_ge(g_done, HC * i + 2)
                        for c in range(DC):
                            bank = (h1, h3)[c // 2][:, c % 2, :]
                            for t in range(TB):
                                if c == 0:
                                    pe.wait_ge(xn_done, TB * i + t + 1)
                                mm = nc.tensor.transpose(bank[:, t * P:(t + 1) * P], xn[:, t, c * P:(c + 1) * P], keep["ident"][:, :])
                            mm.then_inc(turned, 1)

                    def down(i, j):
                        if j == 0:
                            pe.wait_ge(out_done, TB * i + TB)
                            if not ternary:
                                pe.wait_ge(w_loaded[2], 16)
                        pe.wait_ge(g_ready, HC * i + j + 1 + (0 if ternary else 2))
                        for t in range(TB):
                            for q in range(parts):
                                mm = nc.tensor.matmul(y[:, t, :], gp[q][0:HM[j], j % 2, t * P:(t + 1) * P], w2[0:HM[j], j, :],
                                                      start=j == 0 and q == 0, stop=j == HC - 1 and q == parts - 1)
                        mm.then_inc(y_step, 1)

                    def main(i):
                        pe.wait_ge(lo_done if ternary else hi_done, DC * i + DC)
                        for j in range(HC):
                            for m, w, h, done, used in ((0, w1, h1, h1_done, sil_done), (1, w3, h3, h3_done, g_done)):
                                if j == 0 and not ternary:
                                    pe.wait_ge(w_loaded[m], 16)
                                pe.wait_ge(used, left(i, j))
                                n = 0
                                for c in range(DC):
                                    for q in range(parts):
                                        mm = nc.tensor.matmul(h[0:HM[j], j % 2, :], w[:, c, j * P:j * P + HM[j]], xnT[q][:, c, :],
                                                              start=n == 0, stop=n == DC * parts - 1)
                                        n += 1
                                mm.then_inc(done, 1)
                            if j >= 1:
                                down(i, j - 1)
                        down(i, HC - 1)

                    turn(0)
                    with pe.Fori(0, NB - 1) as i:
                        main(i)
                        turn(i + 1)
                    main(NB - 1)

                @block.vector
                def _(dve):
                    def norm(i):
                        dve.wait_ge(ln_loaded, 16 * i + 16)
                        for t in range(TB):
                            nc.vector.bn_stats(stats[:, t, :], x_ln[:, t, :]).then_inc(stats_done, 1)
                        hold(dve, stats_done, TB * i + TB, dve_passed)
                        for t in range(TB):
                            nc.vector.bn_aggr(mv[:, t, :], stats[:, t, :]).then_inc(var_done, 1)
                        dve.wait_ge(var_done, TB * i + TB)
                        nc.vector.tensor_scalar(ve[:, :], mv[:, :, 1], LN_EPS, None, ALU.add).then_inc(ve_done, 1)
                        dve.wait_ge(rstd_done, i + 1)
                        dve.wait_ge(turned, DC * i + 1)
                        for t in range(TB):
                            nc.vector.tensor_scalar(xn[:, t, :], x_ln[:, t, :], mv[:, t, 0:1], rstd[:, t:t + 1], ALU.subtract, ALU.mult).then_inc(xn_done, 1)
                        dve.wait_ge(xn_done, TB * i + TB)
                        dve.sem_inc(ln_free, 1)

                    def evacuate_low(i):
                        for c in range(DC):
                            dve.wait_ge(turned, DC * i + c + 2)
                            dve.wait_ge(hi_done, DC * i + c + 1)
                            nc.vector.tensor_tensor(xnT[1][:, c, :], (h1, h3)[c // 2][:, c % 2, :], xnT[0][:, c, :].bitcast(F32), ALU.subtract).then_inc(lo_done, 1)

                    def main(i, next_norm):
                        for j in range(HC):
                            m = HM[j]
                            dve.wait_ge(sil_done, HC * i + j + 3)
                            dve.wait_ge(h3_done, HC * i + j + 1)
                            if not ternary:
                                dve.wait_ge(y_step, left(i, j))
                            nc.vector.tensor_tensor(g32[0:m, j % 2, :], sil[0:m, j % 2, :], h3[0:m, j % 2, :], ALU.mult).then_inc(g_done, 1)
                            if ternary:
                                dve.wait_ge(y_step, left(i, j))
                                dve.wait_ge(ghi_done, HC * i + j + 1)
                                nc.vector.tensor_tensor(gp[1][0:m, j % 2, :], g32[0:m, j % 2, :], gp[0][0:m, j % 2, :].bitcast(F32), ALU.subtract).then_inc(glo_done, 1)
                            if ternary:
                                lut.steps(dve, LI * i, LI * LUT_SIZE * j // HC, LI * LUT_SIZE * (j + 1) // HC)
                            if j == 2 and next_norm:
                                norm(i + 1)

                    def finish(i):
                        dve.wait_ge(res_loaded, 16 * i + 16)
                        dve.wait_ge(stored, 16 * i + 16)
                        dve.wait_ge(y_step, HC * i + HC + 2)
                        for t in range(TB):
                            nc.vector.scalar_tensor_tensor(out=x_new[:, t, :], in0=y[:, t, :], scalar=out_scale[:, 0:1], in1=x_res[:, t, :],
                                                           op0=ALU.mult, op1=ALU.add).then_inc(out_done, 1)
                        dve.wait_ge(out_done, TB * i + 2 * TB)
                        dve.sem_inc(res_free, 1)

                    for sem, n in ((ln_free, 1), (res_free, 1), (out_done, TB), (turned, 1), (g_done, 2), (sil_done, 2), (y_step, 2), (stored, 16)):
                        dve.sem_inc(sem, n)
                    if ternary:
                        nc.vector.tensor_tensor(s23[:, :], scales[:, 1:2], scales[:, 2:3], ALU.mult).then_inc(scale_done, 1)
                        dve.wait_ge(scale_done, 1)
                        nc.vector.tensor_tensor(out_scale[:, :], s23[:, :], gate, ALU.mult)
                    else:
                        nc.vector.tensor_copy(out_scale[:, :], gate)
                    norm(0)
                    if ternary:
                        lut.begin(dve)
                        evacuate_low(0)
                    with dve.Fori(0, NB - 1) as i:
                        main(i, True)
                        if ternary:
                            evacuate_low(i + 1)
                        finish(i)
                    main(NB - 1, False)
                    finish(NB - 1)

                @block.gpsimd
                def _(pool):
                    with pool.Fori(0, NB) as i:
                        pool.wait_ge(ve_done, i + 1)
                        nc.gpsimd.tensor_tensor(rstd[:, :], ve[:, :], keep["neg_half"][:, 0:TB], ALU.pow).then_inc(rstd_done, 1)

                @block.scalar
                def _(act):
                    def evacuate(i):
                        for c in range(DC):
                            act.wait_ge(turned, DC * i + c + 2)
                            nc.scalar.activation(xnT[0][:, c, :], (h1, h3)[c // 2][:, c % 2, :], ACT.Copy).then_inc(hi_done, 1)

                    def main(i):
                        for j in range(HC):
                            m = HM[j]
                            act.wait_ge(h1_done, HC * i + j + 1)
                            act.wait_ge(g_done, left(i, j))
                            nc.scalar.activation(sil[0:m, j % 2, :], h1[0:m, j % 2, :], ACT.Silu, scale=scales[0:m, 0:1] if ternary else 1.0).then_inc(sil_done, 1)
                            if ternary:
                                act.wait_ge(y_step, left(i, j))
                                act.wait_ge(g_done, HC * i + j + 3)
                                nc.scalar.activation(gp[0][0:m, j % 2, :], g32[0:m, j % 2, :], ACT.Copy).then_inc(ghi_done, 1)

                    def store(i):
                        act.wait_ge(out_done, TB * i + 2 * TB)
                        act.dma_start(rows(x_out, i * BLK, BLK).rearrange("(t p) d -> p t d", p=P), x_new[:, :, :]).then_inc(stored, 16)

                    evacuate(0)
                    with act.Fori(0, NB - 1) as i:
                        main(i)
                        evacuate(i + 1)
                        store(i)
                    main(NB - 1)
                    store(NB - 1)
                    act.wait_ge(stored, 16 * NB + 16)


def build_ternary_ffn(nc, io, keep, x_in, x_out):
    build_ffn(nc, io, keep, x_in, x_out, True)


def build_lut_ffn(nc, io, keep, x_in, x_out):
    build_ffn(nc, io, keep, x_in, x_out, False)


HEADS = 16
HD = D // HEADS
FD = 64
VE = HD + 1
LB = 512
LT = LB // P


class Fills:

    def __init__(self, plan):
        self.names = [name for name, _ in plan]
        self.engine = [e for _, e in plan]
        self.count = len(plan)
        self.per = {e: self.engine.count(e) for e in ("act", "dve")}
        self.place = {name: n for n, name in enumerate(self.names)}

    def filled(self, i, name):
        return self.count * i + self.place[name] + 1

    def emptied(self, i, name):
        n = self.place[name]
        e = self.engine[n]
        return e, self.per[e] * (i + 1) + self.engine[:n].count(e) + 1

    def bank_free(self, i, name):
        n = self.place[name]
        if n >= 8:
            return self.emptied(i, self.names[n - 8])
        before = max(m for m in range(self.count) if m % 8 == n % 8)
        return self.emptied(i - 1, self.names[before])


PAIRS = HEADS // 2
EB = LB // S
NIT = N // LB


class ContextSums:

    def __init__(self, nc, io, keep, sc):
        self.nc, self.io = nc, io
        self.wk, self.wv = (sc.sb(n, [P, DC, D]) for n in ("wk", "wv"))
        self.bk = sc.sb("bk", [P, DC])
        self.bv = sc.sb("bv", [P, D])
        self.fmap = sc.sb("fmap", [P, 4 * FD])
        self.mask = sc.sb("mask", [P, N // P])
        self.cT = sc.sb("cT", [P, EB, DC, S])
        self.kT = sc.sb("kT", [P, DC, LB])
        self.v = sc.sb("v", [P, LT, HEADS, VE])
        self.relu = sc.sb("relu", [P, 2, D])
        self.kf = sc.sb("kf", [P, LT, HEADS * FD])
        self.kvd = sc.sb("kvd", [P, EB, PAIRS, 2 * VE])
        self.kT_ps, self.v_ps, self.kf_ps, self.kv_ps = (sc.ps(n, [P, 2, 512]) for n in ("kT_ps", "v_ps", "kf_ps", "kv_ps"))
        names = "weights_loaded zeroed c_loaded v_done v_moved kT_done kT_moved kf_done kf_moved kf_ready kv_done kv_moved kv_stored act_passed".split()
        self.s = {n: sc.sem("ctx_" + n) for n in names}

    LOADS = 9

    def load_weights(self, sp):
        s, io = self.s, self.io
        sp.dma_start(self.cT[:, :, :, :], io["ctxT"][0:EB].rearrange("b p c s -> p b c s")).then_inc(s["c_loaded"], 16)
        for w, n in ((self.wv, "wv"), (self.wk, "wk")):
            sp.dma_start(w[:, :, :], io[n].rearrange("p (c o) -> p c o", c=DC)).then_inc(s["weights_loaded"], 16)
        sp.dma_start(self.bk[:, :], io["bk"]).then_inc(s["weights_loaded"], 16)
        sp.dma_start(self.bv[:, :], io["bv"].broadcast_to([P, D])).then_inc(s["weights_loaded"], 16)
        sp.dma_start(self.mask[:, :], io["mask"]).then_inc(s["weights_loaded"], 16)
        sp.wait_ge(s["zeroed"], 2)
        for h in range(4):
            sp.dma_start(self.fmap[h * HD:(h + 1) * HD, h * FD:(h + 1) * FD], io["wkf"]).then_inc(s["weights_loaded"], 16)

    def load(self, sp, i):
        sp.wait_ge(self.s["kT_done"], DC * i)
        sp.dma_start(self.cT[:, :, :, :], self.io["ctxT"][bass.ds(EB * i, EB)].rearrange("b p c s -> p b c s")).then_inc(self.s["c_loaded"], 16)

    def store(self, sp, i):
        sp.wait_ge(self.s["kv_moved"], 2 * EB * (i + 1) + 2)
        sp.dma_start(self.io["lin_kv"][bass.ds(i, 1)].rearrange("i p w -> p (i w)"), self.kvd[:, :, :, :].rearrange("p e q w -> p (e q w)")).then_inc(self.s["kv_stored"], 16)

    def begin(self, dve):
        nc, s = self.nc, self.s
        for name in ("v_moved", "kT_moved", "kf_moved", "kv_moved"):
            dve.sem_inc(s[name], 2)
        dve.sem_inc(s["kv_stored"], 16)
        nc.vector.memset(self.fmap[0:64, :], 0.0).then_inc(s["zeroed"], 1)
        nc.vector.memset(self.fmap[64:128, :], 0.0).then_inc(s["zeroed"], 1)
        nc.vector.memset(self.kvd[:, :, :, :], 0.0).then_inc(s["zeroed"], 1)
        nc.vector.memset(self.v[:, :, :, HD:VE], 1.0).then_inc(s["zeroed"], 1)

    def step(self, dve, i, t):
        nc, s = self.nc, self.s
        if t == 0:
            dve.wait_ge(s["weights_loaded"], 16 * self.LOADS)
        dve.wait_ge(s["v_done"], LT * i + t + 1)
        nc.vector.tensor_tensor(self.v[:, t, :, 0:HD], self.v_ps[:, t % 2, :].rearrange("p (h e) -> p h e", h=HEADS),
                                self.bv[:, :].rearrange("p (h e) -> p h e", h=HEADS), ALU.add).then_inc(s["v_moved"], 1)

    def tensor(self, pe):
        nc, s, cT = self.nc, self.s, self.cT
        pe.wait_ge(s["weights_loaded"], 16 * self.LOADS)
        pe.wait_ge(s["zeroed"], 4)
        with pe.Fori(0, NIT) as i:
            pe.wait_ge(s["c_loaded"], 16 * i + 16)
            for t in range(LT):
                pe.wait_ge(s["v_moved"], LT * i + t + 1)
                for c in range(DC):
                    mm = nc.tensor.matmul(self.v_ps[:, t % 2, :], cT[:, t // 2, c, (t % 2) * P:(t % 2 + 1) * P], self.wv[:, c, :], start=c == 0, stop=c == DC - 1)
                mm.then_inc(s["v_done"], 1)
            for o in range(DC):
                pe.wait_ge(s["kT_moved"], DC * i + o + 1)
                for c in range(DC):
                    mm = nc.tensor.matmul(self.kT_ps[:, o % 2, :], self.wk[:, c, o * P:(o + 1) * P], cT[:, :, c, :], start=c == 0, stop=c == DC - 1)
                mm.then_inc(s["kT_done"], 1)
            for t in range(LT):
                for h in range(2):
                    pe.wait_ge(s["kT_moved"], DC * i + 2 * h + 4)
                    pe.wait_ge(s["kf_moved"], 2 * LT * i + 2 * t + h + 1)
                    for q in range(2):
                        mm = nc.tensor.matmul(self.kf_ps[:, h, q * 256:(q + 1) * 256], self.kT[:, 2 * h + q, t * P:(t + 1) * P], self.fmap[:, :], start=True, stop=True)
                    mm.then_inc(s["kf_done"], 1)
            pe.wait_ge(s["v_moved"], LT * i + LT + 2)
            for e in range(EB):
                pe.wait_ge(s["kf_ready"], 2 * LT * i + 4 * e + 4)
                for h in range(2):
                    pe.wait_ge(s["kv_moved"], 2 * EB * i + 2 * e + h + 1)
                    for q in range(4):
                        p = 4 * h + q
                        for t in (2 * e, 2 * e + 1):
                            mm = nc.tensor.matmul(self.kv_ps[:, h, q * 2 * VE:(q + 1) * 2 * VE], self.kf[:, t, p * P:(p + 1) * P],
                                                  self.v[:, t, 2 * p:2 * p + 2, :].rearrange("p h e -> p (h e)"), start=t == 2 * e, stop=t == 2 * e + 1)
                    mm.then_inc(s["kv_done"], 1)

    def scalar(self, act):
        nc, s = self.nc, self.s
        act.wait_ge(s["weights_loaded"], 16 * self.LOADS)
        act.wait_ge(s["zeroed"], 4)
        with act.Fori(0, NIT) as i:
            for o in range(DC):
                act.wait_ge(s["kT_done"], DC * i + o + 1)
                nc.scalar.activation(self.kT[:, o, :], self.kT_ps[:, o % 2, :], ACT.Identity, bias=self.bk[:, o:o + 1]).then_inc(s["kT_moved"], 1)
            for t in range(LT):
                for h in range(2):
                    n = 2 * LT * i + 2 * t + h + 1
                    act.wait_ge(s["kf_done"], n)
                    nc.scalar.activation(self.relu[:, h, :], self.kf_ps[:, h, :], ACT.Relu).then_inc(s["kf_moved"], 1)
                    hold(act, s["kf_moved"], n + 2, s["act_passed"])
                    nc.scalar.activation(self.kf[:, t, h * 512:(h + 1) * 512], self.relu[:, h, :], ACT.Copy, scale=self.mask[:, bass.ds(LT * i + t, 1)]).then_inc(s["kf_ready"], 1)
            act.wait_ge(s["kv_stored"], 16 * i + 16)
            for e in range(EB):
                for h in range(2):
                    act.wait_ge(s["kv_done"], 2 * EB * i + 2 * e + h + 1)
                    for r in range(2):
                        src = self.kv_ps[r * FD:(r + 1) * FD, h, 0:4 * 2 * VE].rearrange("p (q w) -> p q w", q=4)[:, :, r * VE:(r + 1) * VE]
                        ins = nc.scalar.activation(self.kvd[r * FD:(r + 1) * FD, e, 4 * h:4 * h + 4, r * VE:(r + 1) * VE], src, ACT.Identity)
                    ins.then_inc(s["kv_moved"], 1)


def build_linear_attention(nc, io, keep, x_in, x_out):
    with ExitStack() as ctx:
        sc = Scope(nc, ctx, "lin")
        wq, wo = (sc.sb(n, [P, DC, D]) for n in ("wq", "wo"))
        bq = sc.sb("bq", [P, DC])
        bo = sc.sb("bo", [P, D])
        fmap_q = sc.sb("fmap_q", [P, 4 * FD])
        x_sb = sc.sb("x", [P, LT, D])
        x_res = sc.sb("x_res", [P, LT, D])
        xn = sc.sb("xn", [P, LT, D])
        xnT = sc.sb("xnT", [P, DC, LB])
        qT = sc.sb("qT", [P, DC, LB])
        qf = sc.sb("qf", [P, PAIRS, LB])
        kvd = sc.sb("kvd", [P, EB, PAIRS, 2 * VE])
        den = sc.sb("den", [P, LT, HEADS])
        rden = sc.sb("rden", [P, LT, HEADS])
        att = sc.sb("att", [P, LT, D])
        attT = sc.sb("attT", [P, DC, LB])
        proj = sc.sb("proj", [P, LT, D])
        x_new = proj
        stats = sc.sb("stats", [P, LT, 6])
        mv = sc.sb("mv", [P, LT, 2])
        ve = sc.sb("ve", [P, LT])
        rstd = sc.sb("rstd", [P, LT])
        bank = sc.ps("bank", [P, 8, 512])
        lut = LutDecoder(nc, io, sc, LUT_FIRST[2])
        LI = (LUT_FIRST[3] - LUT_FIRST[2]) // NIT

        weights_loaded = sc.sem("weights_loaded")
        x_loaded = sc.sem("x_loaded")
        res_loaded = sc.sem("res_loaded")
        kv_loaded = sc.sem("kv_loaded")
        x_free = sc.sem("x_free")
        res_free = sc.sem("res_free")
        stored = sc.sem("stored")
        stats_done = sc.sem("stats_done")
        var_done = sc.sem("var_done")
        ve_done = sc.sem("ve_done")
        rstd_done = sc.sem("rstd_done")
        xn_done = sc.sem("xn_done")
        setup_done = sc.sem("setup_done")
        filled = sc.sem("filled")
        emptied = {"act": sc.sem("act_emptied"), "dve": sc.sem("dve_emptied")}
        den_done = sc.sem("den_done")
        rden_done = sc.sem("rden_done")
        out_done = sc.sem("out_done")
        passed = sc.sem("passed")

        plan = Fills([(("xnT", c), "act") for c in range(DC)] + [(("qT", o), "act") for o in range(DC)] + [(("qf", p), "act") for p in range(PAIRS)]
                     + [(("att", t, h), "dve") for t in range(LT) for h in range(2)] + [(("attT", c), "act") for c in range(DC)]
                     + [(("out", t), "dve") for t in range(LT)])

        def at(name):
            return bank[:, plan.place[name] % 8, :]

        def wait_emptied(eng, i, *names):
            for name in names:
                e, value = plan.emptied(i, name)
                eng.wait_ge(emptied[e], value)

        with nc.Block() as block:

            @block.sync
            def _(sp):
                sp.dma_start(x_sb[:, :, :], rows(x_in, 0, LB).rearrange("(t p) d -> p t d", p=P)).then_inc(x_loaded, 16)
                for w, n in ((wq, "wq"), (wo, "wo")):
                    sp.dma_start(w[:, :, :], io[n].rearrange("p (c o) -> p c o", c=DC)).then_inc(weights_loaded, 16)
                sp.dma_start(bq[:, :], io["bq"]).then_inc(weights_loaded, 16)
                sp.dma_start(bo[:, :], io["bo"].broadcast_to([P, D])).then_inc(weights_loaded, 16)
                sp.wait_ge(setup_done, 2)
                for h in range(4):
                    sp.dma_start(fmap_q[h * HD:(h + 1) * HD, h * FD:(h + 1) * FD], io["wqf"]).then_inc(weights_loaded, 16)

                def load_kv(i):
                    sp.wait_ge(out_done, LT * i + LT)
                    sp.dma_start(kvd[:, :, :, :].rearrange("p e q w -> p (e q w)"), io["lin_kv"][bass.ds(i, 1)].rearrange("i p w -> p (i w)")).then_inc(kv_loaded, 16)

                def load_x(i):
                    sp.wait_ge(x_free, i)
                    sp.dma_start(x_sb[:, :, :], rows(x_in, i * LB, LB).rearrange("(t p) d -> p t d", p=P)).then_inc(x_loaded, 16)

                def load_res(i):
                    sp.wait_ge(res_free, i + 1)
                    sp.dma_start(x_res[:, :, :], rows(x_in, i * LB, LB).rearrange("(t p) d -> p t d", p=P)).then_inc(res_loaded, 16)

                def iteration(i, last):
                    if not last:
                        load_x(i + 1)
                    for n in range(LI):
                        if not (last and n == LI - 1):
                            lut.load(sp, LI * i + n + 1)
                        lut.store(sp, LI * i + n)
                    if not last:
                        load_res(i + 1)
                        load_kv(i + 1)

                load_kv(0)
                lut.load_table(sp)
                lut.load(sp, 0)
                load_res(0)
                with sp.Fori(0, NIT - 1) as i:
                    iteration(i, False)
                iteration(NIT - 1, True)
                lut.finish(sp, LI * NIT)

            @block.tensor
            def _(pe):
                def begin(i, name):
                    e, value = plan.bank_free(i, name)
                    pe.wait_ge(emptied[e], value)
                    return at(name)

                def projection(i, name, lhsT, rhs):
                    out = begin(i, name)
                    for c in range(DC):
                        mm = nc.tensor.matmul(out, lhsT(c), rhs(c), start=c == 0, stop=c == DC - 1)
                    mm.then_inc(filled, 1)

                pe.wait_ge(weights_loaded, 16 * 8)
                with pe.Fori(0, NIT) as i:
                    pe.wait_ge(xn_done, LT * i + LT)
                    for c in range(DC):
                        out = begin(i, ("xnT", c))
                        for t in range(LT):
                            mm = nc.tensor.transpose(out[:, t * P:(t + 1) * P], xn[:, t, c * P:(c + 1) * P], keep["ident"][:, :])
                        mm.then_inc(filled, 1)
                    wait_emptied(pe, i, ("xnT", DC - 1))
                    for o in range(DC):
                        projection(i, ("qT", o), lambda c: wq[:, c, o * P:(o + 1) * P], lambda c: xnT[:, c, :])
                    for p in range(PAIRS):
                        wait_emptied(pe, i, ("qT", p // 2))
                        out = begin(i, ("qf", p))
                        nc.tensor.matmul(out, fmap_q[:, (p % 2) * P:(p % 2 + 1) * P], qT[:, p // 2, :], start=True, stop=True).then_inc(filled, 1)
                    pe.wait_ge(kv_loaded, 16 * i + 16)
                    for t in range(LT):
                        wait_emptied(pe, i, ("qf", PAIRS - 1))
                        for h in range(2):
                            out = begin(i, ("att", t, h))
                            for q in range(4):
                                p = 4 * h + q
                                mm = nc.tensor.matmul(out[:, q * 2 * VE:(q + 1) * 2 * VE], qf[:, p, t * P:(t + 1) * P], kvd[:, t // 2, p, :], start=True, stop=True)
                            mm.then_inc(filled, 1)
                    wait_emptied(pe, i, ("att", LT - 1, 1))
                    for c in range(DC):
                        out = begin(i, ("attT", c))
                        for t in range(LT):
                            mm = nc.tensor.transpose(out[:, t * P:(t + 1) * P], att[:, t, c * P:(c + 1) * P], keep["ident"][:, :])
                        mm.then_inc(filled, 1)
                    wait_emptied(pe, i, ("attT", DC - 1))
                    for t in range(LT):
                        projection(i, ("out", t), lambda c: attT[:, c, t * P:(t + 1) * P], lambda c: wo[:, c, :])

            @block.scalar
            def _(act):
                def evacuate(i, name, out, func, bias=0.0, src=None, inc=True):
                    act.wait_ge(filled, plan.filled(i, name))
                    ins = nc.scalar.activation(out, at(name) if src is None else src, func, bias=bias)
                    if inc:
                        ins.then_inc(emptied["act"], 1)

                act.sem_inc(emptied["act"], plan.per["act"])
                act.wait_ge(weights_loaded, 16 * 8)
                with act.Fori(0, NIT) as i:
                    for c in range(DC):
                        evacuate(i, ("xnT", c), xnT[:, c, :], ACT.Identity)
                    for o in range(DC):
                        evacuate(i, ("qT", o), qT[:, o, :], ACT.Identity, bq[:, o:o + 1])
                    for p in range(PAIRS):
                        evacuate(i, ("qf", p), qf[:, p, :], ACT.Relu)
                    for c in range(DC):
                        evacuate(i, ("attT", c), attT[:, c, :], ACT.Identity)
                    act.wait_ge(out_done, LT * i + 2 * LT)
                    act.dma_start(rows(x_out, i * LB, LB).rearrange("(t p) d -> p t d", p=P), x_new[:, :, :]).then_inc(stored, 16)
                act.wait_ge(stored, 16 * NIT + 16)

            @block.vector
            def _(dve):
                def norm(i):
                    dve.wait_ge(x_loaded, 16 * i + 16)
                    for t in range(LT):
                        nc.vector.bn_stats(stats[:, t, :], x_sb[:, t, :]).then_inc(stats_done, 1)
                    hold(dve, stats_done, LT * i + LT, passed)
                    for t in range(LT):
                        nc.vector.bn_aggr(mv[:, t, :], stats[:, t, :]).then_inc(var_done, 1)
                    dve.wait_ge(var_done, LT * i + LT)
                    nc.vector.tensor_scalar(ve[:, :], mv[:, :, 1], LN_EPS, None, ALU.add).then_inc(ve_done, 1)
                    dve.wait_ge(rstd_done, i + 1)
                    for t in range(LT):
                        nc.vector.tensor_scalar(xn[:, t, :], x_sb[:, t, :], mv[:, t, 0:1], rstd[:, t:t + 1], ALU.subtract, ALU.mult).then_inc(xn_done, 1)
                    dve.wait_ge(xn_done, LT * i + LT)
                    dve.sem_inc(x_free, 1)

                def main(i, next_norm):
                    place = [0]

                    def decode(n):
                        lut.steps(dve, LI * i, place[0], place[0] + n)
                        place[0] += n

                    decode(4)
                    if next_norm:
                        dve.wait_ge(filled, plan.filled(i, ("xnT", DC - 1)))
                        norm(i + 1)
                    decode(4)
                    for t in range(LT):
                        for h in range(2):
                            n = 2 * LT * i + 2 * t + h + 1
                            src = at(("att", t, h))[:, 0:8 * VE].rearrange("p (h e) -> p h e", h=8)
                            dve.wait_ge(filled, plan.filled(i, ("att", t, h)))
                            nc.vector.tensor_scalar(den[:, t, 8 * h:8 * h + 8], src[:, :, HD], 1e-8, None, ALU.add).then_inc(den_done, 1)
                            dve.wait_ge(den_done, n)
                            nc.vector.reciprocal(rden[:, t, 8 * h:8 * h + 8], den[:, t, 8 * h:8 * h + 8]).then_inc(rden_done, 1)
                            dve.wait_ge(rden_done, n)
                            nc.vector.tensor_tensor(att[:, t, h * 256:(h + 1) * 256].rearrange("p (h e) -> p h e", h=8), src[:, :, 0:HD],
                                                    rden[:, t, 8 * h:8 * h + 8].rearrange("p (h e) -> p h e", e=1).broadcast_to([P, 8, HD]), ALU.mult).then_inc(emptied["dve"], 1)
                    dve.wait_ge(stored, 16 * i + 16)
                    dve.wait_ge(res_loaded, 16 * i + 16)
                    for t in range(LT):
                        decode(2)
                        dve.wait_ge(filled, plan.filled(i, ("out", t)))
                        nc.vector.tensor_tensor(proj[:, t, :], at(("out", t)), bo[:, :], ALU.add).then_inc(emptied["dve"], 1)
                        dve.wait_ge(emptied["dve"], plan.emptied(i, ("out", t))[1])
                        nc.vector.scalar_tensor_tensor(out=x_new[:, t, :], in0=proj[:, t, :], scalar=keep["gates"][:, 1:2], in1=x_res[:, t, :],
                                                       op0=ALU.mult, op1=ALU.add).then_inc(out_done, 1)
                    dve.wait_ge(out_done, LT * i + 2 * LT)
                    dve.sem_inc(res_free, 1)

                for sem, n in ((res_free, 1), (out_done, LT), (stored, 16), (emptied["dve"], plan.per["dve"])):
                    dve.sem_inc(sem, n)
                nc.vector.memset(fmap_q[0:64, :], 0.0).then_inc(setup_done, 1)
                nc.vector.memset(fmap_q[64:128, :], 0.0).then_inc(setup_done, 1)
                norm(0)
                dve.wait_ge(weights_loaded, 16 * 8)
                lut.begin(dve)
                with dve.Fori(0, NIT - 1) as i:
                    main(i, True)
                main(NIT - 1, False)

            @block.gpsimd
            def _(pool):
                with pool.Fori(0, NIT) as i:
                    pool.wait_ge(ve_done, i + 1)
                    nc.gpsimd.tensor_tensor(rstd[:, :], ve[:, :], keep["neg_half"][:, 0:LT], ALU.pow).then_inc(rstd_done, 1)


CAP = 256


class Routing:

    def __init__(self, nc, sc, name, experts, topk, slots, spare):
        self.nc, self.name, self.experts, self.topk, self.slots = nc, name, experts, topk, slots
        NT = N // P
        self.slot_of = sc.sb("slot_of", [P, NT, topk], U32)
        self.weight = sc.sb("weight", [P, NT, topk])
        self.xn = nc.dram_tensor(f"{name}_xn", [N, D], F32, kind="Internal").ap()
        self.token_of = nc.dram_tensor(f"{name}_token_of", [slots + spare, 1], I32, kind="Internal").ap()
        self.y = nc.dram_tensor(f"{name}_y", [slots, D], F32, kind="Internal").ap()


def build_route(nc, io, keep, x_in, x_mid, r, shared, gate, late):
    E, K = r.experts, r.topk
    (n1, n3, n2), hidden, split = shared
    SC = -(-hidden // P)
    HM = [min(P, hidden - P * j) for j in range(SC)]
    parts = 2 if split else 1
    WDT = F32R if split else F32
    with ExitStack() as ctx:
        sc = Scope(nc, ctx, r.name + "_route")
        w1 = sc.sb("w1", [P, DC, hidden], WDT)
        w3 = sc.sb("w3", [P, DC, hidden], WDT)
        w2 = sc.sb("w2", [P, SC, D], WDT)
        raw = [sc.sb("w1b", [P, DC, hidden], BF16), sc.sb("w3b", [P, DC, hidden], BF16), sc.sb("w2b", [P, SC, D], BF16)] if split else [w1, w3, w2]
        wg = sc.sb("wg", [P, DC, E])
        bias = sc.sb("bias", [P, E])
        x_all = sc.sb("x_all", [P, NB * TB, D])
        x_new = sc.sb("x_new", [P, TB, D])
        xn = sc.sb("xn", [P, TB, D])
        xnT = sc.sb("xnT", [P, DC, BLK])
        xp = [sc.sb(f"x_part{q}", [P, DC, BLK], WDT) for q in range(parts)] if split else [xnT]
        g32 = sc.sb("g32", [P, SC, BLK])
        gp = [sc.sb(f"g_part{q}", [P, SC, BLK], WDT) for q in range(parts)] if split else [g32]
        sil = sc.sb("sil", [P, SC, BLK])
        stats = sc.sb("stats", [P, NB * TB, 6])
        mv = sc.sb("mv", [P, NB * TB, 2])
        ve = sc.sb("ve", [P, NB * TB])
        rstd = sc.sb("rstd", [P, NB * TB])
        score = sc.sb("score", [P, TB, E])
        biased = sc.sb("biased", [P, TB, E]) if late else score
        tmp1 = sc.sb("tmp1", [P, TB, E])
        tmp2 = sc.sb("tmp2", [P, TB, E])
        top = sc.sb("top", [P, TB, 8])
        top_at = sc.sb("top_at", [P, TB, 8], U32)
        idx = sc.sb("idx", [P, TB, 8])
        is_kth = sc.sb("is_kth", [P, TB, K, E])
        at_kth = sc.sb("at_kth", [P, TB, K, E])
        at_kth_w = sc.sb("at_kth_w", [P, TB, K, E]) if late else None
        chosen = sc.sb("chosen", [P, TB, E], BF16)
        before = sc.sb("before", [P, E], BF16)
        pos = sc.sb("pos", [P, TB, K])
        decay = sc.sb("decay", [P, TB, E])
        wraw = sc.sb("wraw", [P, TB, K])
        wsum = sc.sb("wsum", [P, TB])
        wrec = sc.sb("wrec", [P, TB])
        valid = sc.sb("valid", [P, TB, K])
        wnorm = sc.sb("wnorm", [P, TB, K])
        posc = sc.sb("posc", [P, TB, K])
        slotf = sc.sb("slotf", [P, TB, K])
        slotd = sc.sb("slotd", [P, TB, K])
        slot_now = sc.sb("slot_now", [P, TB, K], U32)
        token_now = sc.sb("token_now", [P, TB], I32)
        turn = sc.ps("turn", [P, 2, BLK])
        h = sc.ps("h", [P, 2, BLK])
        y = sc.ps("y", [P, 2, D])
        logits = sc.ps("logits", [P, TB, P])
        places = sc.ps("places", [P, TB, P])

        x_loaded = sc.sems("x_loaded", NB)
        names = ("w_loaded raw_done xn_stored stored stats_done var_done ve_done rstd_done xn_done turned "
                 "xnT_done hi_done lo_done logits_done h1_done h3_done sil_done g_done ghi_done glo_done y_done out_done abs_done exp_done ln_done "
                 "soft_done score_done biased_done top_done top_at_done idx_done is_kth_done chosen_done init_done places_done at_kth_done pos_done weight_done "
                 "before_done before_step slots_ready slots_free scattered passed pool_passed").split()
        s = {n: sc.sem(n) for n in names}

        with nc.Block() as block:

            @block.sync
            def _(sp):
                for i in range(NB):
                    sp.dma_start(x_all[:, TB * i:TB * i + TB, :], rows(x_in, i * BLK, BLK).rearrange("(t p) d -> p t d", p=P)).then_inc(x_loaded[i], 16)
                sp.dma_start(wg[:, :, :], io[r.name + "_wg"].rearrange("p (c e) -> p c e", c=DC)).then_inc(s["w_loaded"], 16)
                for w, n in zip(raw, (n1, n3, n2)):
                    sp.dma_start(w[:, :, :], io[n].rearrange("p (c h) -> p c h", c=w.shape[1])).then_inc(s["w_loaded"], 16)
                if late:
                    sp.dma_start(bias[:, :], io[r.name + "_bias"].broadcast_to([P, E])).then_inc(s["w_loaded"], 16)
                rows_total = r.token_of.shape[0]
                sp.wait_ge(s["init_done"], 1)
                sp.dma_start(r.token_of.rearrange("(p c) a -> p (c a)", p=P), keep["zeros_i"][:, 0:rows_total // P]).then_inc(s["w_loaded"], 16)
                with sp.Fori(0, NB) as i:
                    sp.wait_ge(s["xn_done"], TB * i + TB)
                    sp.dma_start(rows(r.xn, i * BLK, BLK).rearrange("(t p) d -> p t d", p=P), xn[:, :, :]).then_inc(s["xn_stored"], 16)
                sp.wait_ge(s["xn_stored"], 16 * NB + 16)

            NW = 16 * (6 if late else 5)

            @block.tensor
            def _(pe):
                pe.wait_ge(s["w_loaded"], NW)
                if split:
                    pe.wait_ge(s["raw_done"], 3)
                pe.wait_ge(s["init_done"], 1)

                def turn_rows(i):
                    for c in range(DC):
                        pe.wait_ge(s["xnT_done"], DC * i + c + 1)
                        if split:
                            pe.wait_ge(s["hi_done"], DC * i + c + 1)
                        for t in range(TB):
                            if c == 0:
                                pe.wait_ge(s["xn_done"], TB * i + t + 1)
                            mm = nc.tensor.transpose(turn[:, c % 2, t * P:(t + 1) * P], xn[:, t, c * P:(c + 1) * P], keep["ident"][:, :])
                        mm.then_inc(s["turned"], 1)

                def main(i, last):
                    pe.wait_ge(s["xnT_done"], DC * i + DC + 2)
                    pe.wait_ge(s["score_done"], i + 1)
                    for t in range(TB):
                        for c in range(DC):
                            mm = nc.tensor.matmul(logits[:, t, 0:E], xnT[:, c, t * P:(t + 1) * P], wg[:, c, :], start=c == 0, stop=c == DC - 1)
                    mm.then_inc(s["logits_done"], 1)
                    if split:
                        pe.wait_ge(s["lo_done"], DC * i + DC)
                    for j in range(SC):
                        m = HM[j]
                        for which, w, done, used in ((0, w1, "h1_done", "sil_done"), (1, w3, "h3_done", "g_done")):
                            pe.wait_ge(s[used], SC * i + j + 1)
                            n = 0
                            for c in range(DC):
                                for q in range(parts):
                                    mm = nc.tensor.matmul(h[0:m, which, :], w[:, c, j * P:j * P + m], xp[q][:, c, :], start=n == 0, stop=n == DC * parts - 1)
                                    n += 1
                            mm.then_inc(s[done], 1)
                    if not last:
                        turn_rows(i + 1)
                    for t in range(TB):
                        pe.wait_ge(s["out_done"], TB * i + t + 1)
                        n = 0
                        for j in range(SC):
                            pe.wait_ge(s["glo_done" if split else "g_done"], SC * i + j + 1 + (0 if split else 1))
                            for q in range(parts):
                                mm = nc.tensor.matmul(y[:, t % 2, :], gp[q][0:HM[j], j, t * P:(t + 1) * P], w2[0:HM[j], j, :], start=n == 0, stop=n == SC * parts - 1)
                                n += 1
                        mm.then_inc(s["y_done"], 1)
                    pe.wait_ge(s["at_kth_done"], i + 1)
                    pe.wait_ge(s["chosen_done"], i + 1)
                    pe.wait_ge(s["before_done"], i + 1)
                    for t in range(TB):
                        nc.tensor.matmul(places[:, t, 0:E], keep["ones_bf"][:, :], before[:, :], start=True, stop=False)
                        for e in range(t):
                            nc.tensor.matmul(places[:, t, 0:E], keep["ones_bf"][:, :], chosen[:, e, :], start=False, stop=False)
                        mm = nc.tensor.matmul(places[:, t, 0:E], keep["earlier"][:, :], chosen[:, t, :], start=False, stop=True)
                    mm.then_inc(s["places_done"], 1)

                turn_rows(0)
                with pe.Fori(0, NB - 1) as i:
                    main(i, False)
                main(NB - 1, True)

            @block.vector
            def _(dve):
                def statistics():
                    for i in range(NB):
                        dve.wait_ge(x_loaded[i], 16)
                        for t in range(TB * i, TB * i + TB):
                            nc.vector.bn_stats(stats[:, t, :], x_all[:, t, :]).then_inc(s["stats_done"], 1)
                    hold(dve, s["stats_done"], NB * TB, s["passed"])
                    for t in range(NB * TB):
                        nc.vector.bn_aggr(mv[:, t, :], stats[:, t, :]).then_inc(s["var_done"], 1)
                    dve.wait_ge(s["var_done"], NB * TB)
                    nc.vector.tensor_scalar(ve[:, :], mv[:, :, 1], LN_EPS, None, ALU.add).then_inc(s["ve_done"], 1)
                    dve.wait_ge(s["rstd_done"], 1)

                def norm(i):
                    dve.wait_ge(s["turned"], DC * i + 1)
                    dve.wait_ge(s["xn_stored"], 16 * i + 16)
                    for t in range(TB):
                        at = bass.ds(TB * i + t, 1)
                        nc.vector.tensor_scalar(xn[:, t, :], x_all[:, at, :].rearrange("p a d -> p (a d)"), mv[:, at, 0:1].rearrange("p a b -> p (a b)"),
                                                rstd[:, at], ALU.subtract, ALU.mult).then_inc(s["xn_done"], 1)

                def hidden_product(i, j):
                    m = HM[j]
                    dve.wait_ge(s["sil_done"], SC * i + j + 2)
                    dve.wait_ge(s["h3_done"], SC * i + j + 1)
                    if j == 0:
                        dve.wait_ge(s["y_done"], TB * i + 1)
                    nc.vector.tensor_tensor(g32[0:m, j, :], sil[0:m, j, :], h[0:m, 1, :], ALU.mult).then_inc(s["g_done"], 1)
                    if split:
                        dve.wait_ge(s["ghi_done"], SC * i + j + 1)
                        nc.vector.tensor_tensor(gp[1][0:m, j, :], g32[0:m, j, :], gp[0][0:m, j, :].bitcast(F32), ALU.subtract).then_inc(s["glo_done"], 1)

                def softplus(i):
                    dve.wait_ge(s["ln_done"], i + 1)
                    nc.vector.scalar_tensor_tensor(out=tmp1[:, :, :], in0=logits[:, :, 0:E], scalar=0.0, in1=tmp2[:, :, :], op0=ALU.max, op1=ALU.add).then_inc(s["soft_done"], 1)

                def choose(i):
                    if late:
                        dve.wait_ge(s["score_done"], i + 2)
                        for t in range(TB):
                            nc.vector.tensor_tensor(biased[:, t, :], score[:, t, :], bias[:, :], ALU.add).then_inc(s["biased_done"], 1)
                    ready = (s["biased_done"], TB * i + TB) if late else (s["score_done"], i + 2)
                    hold(dve, *ready, s["passed"])
                    for t in range(TB):
                        nc.vector.max(top[:, t, :], biased[:, t, :]).then_inc(s["top_done"], 1)
                    hold(dve, s["top_done"], TB * i + TB, s["passed"])
                    for t in range(TB):
                        nc.vector.max_index(top_at[:, t, :], top[:, t, :], biased[:, t, :]).then_inc(s["top_at_done"], 1)
                    dve.wait_ge(s["top_at_done"], TB * i + TB)
                    nc.vector.tensor_copy(idx[:, :, :], top_at[:, :, :]).then_inc(s["idx_done"], 1)
                    dve.wait_ge(s["idx_done"], i + 1)
                    nc.vector.tensor_tensor(is_kth[:, :, :, :], keep["iota"][:, 0:E].rearrange("p (t k e) -> p t k e", t=1, k=1).broadcast_to([P, TB, K, E]),
                                            idx[:, :, 0:K].rearrange("p t (k e) -> p t k e", e=1).broadcast_to([P, TB, K, E]), ALU.is_equal).then_inc(s["is_kth_done"], 1)
                    dve.wait_ge(s["is_kth_done"], i + 1)
                    with nc.allow_low_precision(reason="sums of zeros and at most a one"):
                        nc.vector.tensor_reduce(chosen[:, :, :], is_kth[:, :, :, :].rearrange("p t k e -> p t e k"), AX.X, ALU.add).then_inc(s["chosen_done"], 1)

                def place(i):
                    def over_k4(ap):
                        return ap.rearrange("p t (k e) -> p t k e", k=1).broadcast_to([P, TB, K, E])

                    dve.wait_ge(s["places_done"], i + 1)
                    nc.vector.tensor_tensor(at_kth[:, :, :, :], is_kth[:, :, :, :], over_k4(places[:, :, 0:E]), ALU.mult).then_inc(s["at_kth_done"], 1)
                    if late:
                        nc.vector.tensor_tensor(at_kth_w[:, :, :, :], is_kth[:, :, :, :], over_k4(score[:, :, :]), ALU.mult).then_inc(s["weight_done"], 1)
                    dve.wait_ge(s["at_kth_done"], i + 2)
                    nc.vector.tensor_reduce(pos[:, :, :], at_kth[:, :, :, :], AX.X, ALU.add).then_inc(s["pos_done"], 1)
                    if late:
                        dve.wait_ge(s["weight_done"], i + 2)
                        nc.vector.tensor_reduce(wraw[:, :, :], at_kth_w[:, :, :, :], AX.X, ALU.add).then_inc(s["pos_done"], 1)
                    dve.wait_ge(s["pos_done"], (2 if late else 1) * (i + 1))
                    for t in range(TB):
                        last = t == TB - 1
                        nc.vector.tensor_tensor(before[:, :], before[:, :], chosen[:, t, :], ALU.add).then_inc(s["before_step"], 1)
                        dve.wait_ge(s["before_step"], TB * i + t + 1)
                        if last:
                            dve.sem_inc(s["before_done"], 1)
                    ti = bass.ds(TB * i, TB)
                    step = [0]

                    def then(ins):
                        step[0] += 1
                        ins.then_inc(s["slots_ready"], 1)
                        dve.wait_ge(s["slots_ready"], per_block * i + step[0])

                    def over_k(ap):
                        return ap.rearrange("p (t k) -> p t k", k=1).broadcast_to([P, TB, K])

                    if late:
                        per_block = 3
                        then(nc.vector.tensor_copy(late["idx"][:, ti, :], idx[:, :, 0:K]))
                        then(nc.vector.tensor_copy(late["pos"][:, ti, :], pos[:, :, :]))
                        then(nc.vector.tensor_scalar(r.weight[:, ti, :], wraw[:, :, :], gate, None, ALU.mult))
                    else:
                        per_block = 11
                        then(nc.vector.tensor_reduce(wsum[:, :], top[:, :, 0:K], AX.X, ALU.add))
                        then(nc.vector.reciprocal(wrec[:, :], wsum[:, :]))
                        then(nc.vector.tensor_tensor(wnorm[:, :, :], top[:, :, 0:K], over_k(wrec[:, :]), ALU.mult))
                        then(nc.vector.tensor_scalar(valid[:, :, :], pos[:, :, :], float(CAP), None, ALU.is_lt))
                        then(nc.vector.scalar_tensor_tensor(out=r.weight[:, ti, :], in0=wnorm[:, :, :], scalar=gate, in1=valid[:, :, :], op0=ALU.mult, op1=ALU.mult))
                        then(nc.vector.tensor_scalar(posc[:, :, :], pos[:, :, :], float(CAP - 1), None, ALU.min))
                        then(nc.vector.scalar_tensor_tensor(out=slotf[:, :, :], in0=idx[:, :, 0:K], scalar=float(CAP), in1=posc[:, :, :], op0=ALU.mult, op1=ALU.add))
                        then(nc.vector.tensor_copy(r.slot_of[:, ti, :], slotf[:, :, :]))
                        then(nc.vector.scalar_tensor_tensor(out=slotd[:, :, :], in0=slotf[:, :, :], scalar=keep["spare"][:, 0:1], in1=valid[:, :, :], op0=ALU.subtract, op1=ALU.mult))
                        dve.wait_ge(s["slots_free"], i + 1)
                        then(nc.vector.tensor_copy(token_now[:, :], keep["row_id"][:, ti]))
                        then(nc.vector.tensor_scalar(slot_now[:, :, :], slotd[:, :, :], keep["spare"][:, 0:1], None, ALU.add))

                def finish(i):
                    dve.wait_ge(s["stored"], 16 * i + 16)
                    for t in range(TB):
                        dve.wait_ge(s["y_done"], TB * i + t + 2)
                        nc.vector.scalar_tensor_tensor(out=x_new[:, t, :], in0=y[:, t % 2, :], scalar=gate,
                                                       in1=x_all[:, bass.ds(TB * i + t, 1), :].rearrange("p a d -> p (a d)"), op0=ALU.mult, op1=ALU.add).then_inc(s["out_done"], 1)

                def main(i, next_norm):
                    if split:
                        for c in range(DC):
                            dve.wait_ge(s["hi_done"], DC * i + c + 1 + 2)
                            dve.wait_ge(s["xnT_done"], DC * i + c + 1 + 2)
                            nc.vector.tensor_tensor(xp[1][:, c, :], xnT[:, c, :], xp[0][:, c, :].bitcast(F32), ALU.subtract).then_inc(s["lo_done"], 1)
                    if next_norm:
                        norm(i + 1)
                    if late:
                        softplus(i)
                    first = SC - 1 if late else 0
                    for j in range(first):
                        hidden_product(i, j)
                    choose(i)
                    for j in range(first, SC):
                        hidden_product(i, j)
                    finish(i)
                    place(i)

                for name, n in (("xn_stored", 16), ("stored", 16), ("turned", 1), ("out_done", 2), ("y_done", 1),
                                ("g_done", 1), ("sil_done", 1), ("at_kth_done", 1), ("weight_done", 1), ("slots_free", 1)):
                    dve.sem_inc(s[name], n)
                nc.vector.memset(before[:, :], 0.0).then_inc(s["before_done"], 1)
                dve.sem_inc(s["init_done"], 1)
                dve.wait_ge(s["before_done"], 1)
                statistics()
                norm(0)
                dve.wait_ge(s["w_loaded"], NW)
                if split:
                    for src, dst in zip(raw, (w1, w3, w2)):
                        nc.vector.tensor_copy(dst[:, :, :], src[:, :, :]).then_inc(s["raw_done"], 1)
                with dve.Fori(0, NB - 1) as i:
                    main(i, True)
                main(NB - 1, False)
                if late:
                    dve.wait_ge(s["before_done"], NB + 1)
                    nc.vector.tensor_copy(late["counts"][:, :], before[:, :])

            @block.scalar
            def _(act):
                act.sem_inc(s["xnT_done"], 2)
                act.sem_inc(s["hi_done"], 2)
                if not late:
                    act.sem_inc(s["score_done"], 1)
                def move_rows(i):
                    for c in range(DC):
                        act.wait_ge(s["turned"], DC * i + c + 2)
                        nc.scalar.activation(xnT[:, c, :], turn[:, c % 2, :], ACT.Copy).then_inc(s["xnT_done"], 1)
                        if split:
                            nc.scalar.activation(xp[0][:, c, :], turn[:, c % 2, :], ACT.Copy).then_inc(s["hi_done"], 1)

                def main(i, last):
                    act.wait_ge(s["logits_done"], i + 1)
                    if late:
                        act.wait_ge(s["soft_done"], i + 1)
                        nc.scalar.activation(tmp2[:, :, :], logits[:, :, 0:E], ACT.Abs).then_inc(s["abs_done"], 1)
                        act.wait_ge(s["abs_done"], i + 1)
                        nc.scalar.activation(decay[:, :, :], tmp2[:, :, :], ACT.Exp, scale=-1.0).then_inc(s["exp_done"], 1)
                        act.wait_ge(s["exp_done"], i + 1)
                        nc.scalar.activation(tmp2[:, :, :], decay[:, :, :], ACT.Ln, bias=1.0).then_inc(s["ln_done"], 1)
                    else:
                        nc.scalar.activation(score[:, :, :], logits[:, :, 0:E], ACT.Sigmoid).then_inc(s["score_done"], 1)
                    for j in range(SC):
                        m = HM[j]
                        act.wait_ge(s["h1_done"], SC * i + j + 1)
                        act.wait_ge(s["g_done"], SC * i + j + 1)
                        nc.scalar.activation(sil[0:m, j, :], h[0:m, 0, :], ACT.Silu).then_inc(s["sil_done"], 1)
                        if split:
                            act.wait_ge(s["g_done"], SC * i + j + 2)
                            nc.scalar.activation(gp[0][0:m, j, :], g32[0:m, j, :], ACT.Copy).then_inc(s["ghi_done"], 1)
                    if not last:
                        move_rows(i + 1)
                    act.wait_ge(s["out_done"], TB * i + TB + 2)
                    act.dma_start(rows(x_mid, i * BLK, BLK).rearrange("(t p) d -> p t d", p=P), x_new[:, :, :]).then_inc(s["stored"], 16)

                move_rows(0)
                with act.Fori(0, NB - 1) as i:
                    main(i, False)
                main(NB - 1, True)
                act.wait_ge(s["stored"], 16 * NB + 16)

            @block.gpsimd
            def _(pool):
                def root():
                    pool.wait_ge(s["ve_done"], 1)
                    nc.gpsimd.tensor_tensor(rstd[:, :], ve[:, :], keep["neg_half"][:, 0:NB * TB], ALU.pow).then_inc(s["rstd_done"], 1)

                def square_root(i):
                    pool.wait_ge(s["weight_done"], i + 1)
                    pool.wait_ge(s["soft_done"], i + 2)
                    nc.gpsimd.tensor_tensor(score[:, :, :], tmp1[:, :, :], keep["half"][:, :].rearrange("p (t e) -> p t e", t=TB), ALU.pow).then_inc(s["score_done"], 1)

                def scatter(i):
                    hold(pool, s["slots_ready"], 11 * i + 11, s["pool_passed"])
                    for t in range(TB):
                        for k in range(K):
                            nc.gpsimd.indirect_dma_start(out=r.token_of, out_offset=bass.IndirectOffsetOnAxis(ap=slot_now[:, t, k:k + 1], axis=0),
                                                         in_=token_now[:, t:t + 1], in_offset=None).then_inc(s["scattered"], 16)
                    pool.wait_ge(s["scattered"], 16 * TB * K * (i + 1))
                    pool.sem_inc(s["slots_free"], 1)

                if late:
                    pool.sem_inc(s["score_done"], 1)
                    pool.sem_inc(s["soft_done"], 1)
                root()
                with pool.Fori(0, NB) as i:
                    if late:
                        square_root(i)
                    else:
                        scatter(i)


def load_tokens(nc, r, tokens):
    tiles = r.slots // P
    with ExitStack() as ctx:
        sc = Scope(nc, ctx, r.name + "_tokens")
        raw = sc.sb("raw", [tiles, P], I32)
        asf = sc.sb("asf", [tiles, P])
        turned = sc.ps("turned", [P, 512])
        loaded, asf_done, turn_done, done = (sc.sem(n) for n in ("loaded", "asf_done", "turn_done", "done"))
        with nc.Block() as block:

            @block.sync
            def _(sp):
                sp.dma_start(raw[:, :], r.token_of[0:r.slots, :].rearrange("(n p) a -> n (p a)", p=P)).then_inc(loaded, 16)

            @block.vector
            def _(dve):
                dve.wait_ge(loaded, 16)
                nc.vector.tensor_copy(asf[:, :], raw[:, :]).then_inc(asf_done, 1)
                dve.wait_ge(turn_done, 1)
                nc.vector.tensor_copy(tokens[:, :], turned[:, 0:tiles]).then_inc(done, 1)

            @block.tensor
            def _(pe):
                pe.wait_ge(asf_done, 1)
                nc.tensor.transpose(turned[:, 0:tiles], asf[:, :], r.ident[0:tiles, 0:tiles]).then_inc(turn_done, 1)


def build_small_experts(nc, io, keep, r):
    TT = CAP // P
    HU = 64
    PAIRS = r.experts // 2
    QUADS = PAIRS // 4
    OUTS = 2 * TT
    with ExitStack() as ctx:
        sc = Scope(nc, ctx, "small")
        tokens = sc.sb("tokens", [P, r.slots // P], U32)
        load_tokens(nc, r, tokens)
        now = sc.sb("now", [P, 2, OUTS], U32)
        w_up = sc.sb("w_up", [P, 2, 2, DC, 2 * HU])
        w_down = sc.sb("w_down", [P, 2, 2, D])
        xg = sc.sb("xg", [P, 2, 2, TT, D])
        xgT = sc.sb("xgT", [P, 2, DC, CAP])
        sil = sc.sb("sil", [P, CAP])
        hid = sc.sb("hid", [P, CAP])
        y_sb = sc.sb("y", [P, 2, 2, TT, D])
        wide = sc.ps("wide", [P, 2, 2, 512])
        narrow = sc.ps("narrow", [P, 2, CAP])
        out = sc.ps("out", [P, 3, 512])
        w_loaded = sc.sems("w_loaded", 2)
        gathered = sc.sems("gathered", 2)
        stored = sc.sems("stored", 2)
        names = "zeroed now_done turned xT_act xT_dve up_done sil_done hid_done y_done y_act y_dve pool_passed".split()
        s = {n: sc.sem(n) for n in names}

        lut = LutDecoder(nc, io, sc, LUT_FIRST["experts"])

        def pairs(eng, pair):
            def four(q, last):
                for n in range(4):
                    pair(4 * q + n, n % 2, 2 * q + n // 2, last and n == 3, q, n)

            with eng.Fori(0, QUADS - 1) as q:
                four(q, False)
            four(QUADS - 1, True)

        with nc.Block() as block:

            @block.sync
            def _(sp):
                def load(i, par):
                    sp.dma_start(w_up[:, par], io["w_up"][bass.ds(2 * i, 2)].rearrange("e p (c h) -> p e c h", c=DC)).then_inc(w_loaded[par], 16)
                    for u in range(2):
                        sp.dma_start(w_down[u * HU:(u + 1) * HU, par, u, :], io["w_down"][bass.ds(2 * i + u, 1)].rearrange("e p d -> p (e d)")).then_inc(w_loaded[par], 16)

                def store(i, par):
                    for u in range(2):
                        sp.wait_ge(s["y_act"], 2 * i + u + 3)
                        sp.wait_ge(s["y_dve"], 2 * i + u + 3)
                        sp.dma_start(rows(r.y, (2 * i + u) * CAP, CAP).rearrange("(t p) d -> p t d", p=P), y_sb[:, par, u]).then_inc(stored[par], 16)

                def four(q, last):
                    for n in range(4):
                        store(4 * q + n, n % 2)
                        if not (last and n >= 2):
                            load(4 * q + n + 2, n % 2)
                        if n == 0 and not last:
                            lut.load(sp, q + 1)
                    lut.store(sp, q)

                load(0, 0)
                load(1, 1)
                lut.load_table(sp)
                lut.load(sp, 0)
                with sp.Fori(0, QUADS - 1) as q:
                    four(q, False)
                four(QUADS - 1, True)
                for par in range(2):
                    sp.wait_ge(stored[par], 16 * PAIRS + 32)
                lut.finish(sp, QUADS)

            @block.gpsimd
            def _(pool):
                with pool.Fori(0, PAIRS // 2) as k:
                    for par in range(2):
                        i = 2 * k + par
                        hold(pool, s["turned"], 4 * i + 4, s["pool_passed"])
                        nc.gpsimd.tensor_copy(now[:, par, :], tokens[:, bass.ds(OUTS * i, OUTS)]).then_inc(s["now_done"], 1)
                        hold(pool, s["now_done"], i + 1, s["pool_passed"])
                        for n in range(OUTS):
                            nc.gpsimd.indirect_dma_start(out=xg[:, par, n // TT, n % TT, :], out_offset=None, in_=r.xn,
                                                         in_offset=bass.IndirectOffsetOnAxis(ap=now[:, par, n:n + 1], axis=0)).then_inc(gathered[par], 16)

            @block.tensor
            def _(pe):
                def turn(par, k):
                    pe.wait_ge(gathered[par], 16 * OUTS * (k + 1))
                    for u in range(2):
                        for half in range(2):
                            for c in (2 * half, 2 * half + 1):
                                for t in range(TT):
                                    at = (c % 2) * CAP + t * P
                                    mm = nc.tensor.transpose(wide[:, u, half, at:at + P], xg[:, par, u, t, c * P:(c + 1) * P], keep["ident"][:, :])
                            mm.then_inc(s["turned"], 1)

                def pair(i, par, k, last, q, n):
                    pe.wait_ge(w_loaded[par], 48 * k + 48)
                    pe.wait_ge(s["xT_act"], 2 * i + 2)
                    pe.wait_ge(s["xT_dve"], 2 * i + 2)
                    for which in range(2):
                        for c in range(DC):
                            for u in range(2):
                                mm = nc.tensor.matmul(narrow[u * HU:(u + 1) * HU, which, :], w_up[:, par, u, c, which * HU:(which + 1) * HU], xgT[:, u, c, :],
                                                      start=c == 0, stop=c == DC - 1, tile_position=(0, u * HU))
                    mm.then_inc(s["up_done"], 1)
                    if not last:
                        turn(1 - par, k + par)
                    pe.wait_ge(s["hid_done"], i + 1)
                    for o in range(OUTS):
                        if o == 0:
                            pe.wait_ge(s["y_dve"], 2 * i + 2)
                        elif o == 2:
                            pe.wait_ge(s["y_act"], 2 * i + 2)
                        elif o == 3:
                            pe.wait_ge(s["y_act"], 2 * i + 3)
                        u, t = o // TT, o % TT
                        nc.tensor.matmul(out[:, o % 3, :], hid[:, t * P:(t + 1) * P], w_down[:, par, u, :], start=True, stop=True).then_inc(s["y_done"], 1)

                pe.sem_inc(s["turned"], 8)
                pe.wait_ge(s["zeroed"], 2)
                turn(0, 0)
                pairs(pe, pair)

            def turned(eng, i, u, half, move):
                eng.wait_ge(s["turned"], 4 * i + 2 * u + half + 1 + 8)
                move(xgT[:, u, 2 * half:2 * half + 2, :], wide[:, u, half, :].rearrange("p (c s) -> p c s", c=2)).then_inc(s["xT_dve" if half else "xT_act"], 1)

            @block.scalar
            def _(act):
                def copy(to, of):
                    return nc.scalar.activation(to, of, ACT.Copy)

                def pair(i, par, k, last, q, n):
                    act.wait_ge(s["up_done"], i + 1)
                    nc.scalar.activation(sil[:, :], narrow[:, 0, :], ACT.Silu).then_inc(s["sil_done"], 1)
                    if not last:
                        for u in range(2):
                            turned(act, i + 1, u, 0, copy)
                    act.wait_ge(stored[par], 32 * k + 32)
                    for n in (0, 2):
                        act.wait_ge(s["y_done"], OUTS * i + n + 1)
                        copy(y_sb[:, par, n // TT, n % TT, :], out[:, n % 3, :]).then_inc(s["y_act"], 1)

                act.sem_inc(s["y_act"], 2)
                for u in range(2):
                    turned(act, 0, u, 0, copy)
                pairs(act, pair)

            @block.vector
            def _(dve):
                def pair(i, par, k, last, q, n):
                    dve.wait_ge(s["sil_done"], i + 1)
                    nc.vector.tensor_tensor(hid[:, :], sil[:, :], narrow[:, 1, :], ALU.mult).then_inc(s["hid_done"], 1)
                    if not last:
                        for u in range(2):
                            turned(dve, i + 1, u, 1, nc.vector.tensor_copy)
                    dve.wait_ge(stored[par], 32 * k + 32)
                    lut.steps(dve, q, 4 * n, 4 * n + 2)
                    for out_n in (1, 3):
                        dve.wait_ge(s["y_done"], OUTS * i + out_n + 1)
                        nc.vector.tensor_copy(y_sb[:, par, out_n // TT, out_n % TT, :], out[:, out_n % 3, :]).then_inc(s["y_dve"], 1)
                    lut.steps(dve, q, 4 * n + 2, 4 * n + 4)

                for sem, n in ((s["y_dve"], 2), (stored[0], 32), (stored[1], 32)):
                    dve.sem_inc(sem, n)
                lut.begin(dve)
                nc.vector.memset(w_down[HU:P, :, 0, :], 0.0).then_inc(s["zeroed"], 1)
                nc.vector.memset(w_down[0:HU, :, 1, :], 0.0).then_inc(s["zeroed"], 1)
                for u in range(2):
                    turned(dve, 0, u, 1, nc.vector.tensor_copy)
                pairs(dve, pair)


def build_combine(nc, io, keep, r, x_mid, x_out, first):
    K = r.topk
    NT = N // P
    with ExitStack() as ctx:
        sc = Scope(nc, ctx, r.name + "_comb")
        AHEAD = 4
        now = sc.sb("now", [P, AHEAD, K], U32)
        x_sb = sc.sb("x", [P, AHEAD, D])
        yk = sc.sb("yk", [P, AHEAD, K, D])
        acc = sc.sb("acc", [P, 2, D])
        x_new = sc.sb("x_new", [P, AHEAD, D])
        loaded = sc.sems("loaded", AHEAD)
        gathered = sc.sems("gathered", AHEAD)
        stored = sc.sems("stored", AHEAD)
        x_free, now_done, acc_done, pool_passed = (sc.sem(n) for n in ("x_free", "now_done", "acc_done", "pool_passed"))
        lut = LutDecoder(nc, io, sc, first) if first is not None else None
        sums = ContextSums(nc, io, keep, sc) if first is not None else None
        ROUNDS = NT // AHEAD

        with nc.Block() as block:

            @block.sync
            def _(sp):
                def load(t, u):
                    sp.wait_ge(x_free, t + 1)
                    sp.dma_start(x_sb[:, u, :], rows(x_mid, t * P, P)).then_inc(loaded[u], 16)

                def store(t, u):
                    sp.wait_ge(acc_done, K * t + K)
                    sp.dma_start(rows(x_out, t * P, P), x_new[:, u, :]).then_inc(stored[u], 16)

                for u in range(AHEAD):
                    load(u, u)
                if lut:
                    lut.load_table(sp)
                    lut.load(sp, 0)
                    sums.load_weights(sp)
                with sp.Fori(0, ROUNDS - 1) as q:
                    if lut:
                        lut.load(sp, q + 1)
                    for u in range(AHEAD):
                        store(AHEAD * q + u, u)
                        load(AHEAD * (q + 1) + u, u)
                    if lut:
                        lut.store(sp, q)
                        sums.load(sp, q + 1)
                        sums.store(sp, q)
                for u in range(AHEAD):
                    store(AHEAD * (ROUNDS - 1) + u, u)
                if lut:
                    lut.store(sp, ROUNDS - 1)
                    sums.store(sp, ROUNDS - 1)
                    lut.finish(sp, ROUNDS)
                    sp.wait_ge(sums.s["kv_stored"], 16 * ROUNDS + 16)
                for u in range(AHEAD):
                    sp.wait_ge(stored[u], 16 * ROUNDS + 16)

            if sums:
                @block.tensor
                def _(pe):
                    sums.tensor(pe)

                @block.scalar
                def _(act):
                    sums.scalar(act)

            @block.gpsimd
            def _(pool):
                with pool.Fori(0, ROUNDS) as q:
                    for u in range(AHEAD):
                        t = AHEAD * q + u
                        hold(pool, x_free, t + 1, pool_passed)
                        nc.gpsimd.tensor_copy(now[:, u, :], r.slot_of[:, bass.ds(t, 1), :].rearrange("p a k -> p (a k)")).then_inc(now_done, 1)
                        hold(pool, now_done, t + 1, pool_passed)
                        for k in range(K):
                            nc.gpsimd.indirect_dma_start(out=yk[:, u, k, :], out_offset=None, in_=r.y, in_offset=bass.IndirectOffsetOnAxis(ap=now[:, u, k:k + 1], axis=0))\
                                .then_inc(gathered[u], 16)

            @block.vector
            def _(dve):
                def tile(q, u):
                    t = AHEAD * q + u
                    dve.wait_ge(loaded[u], 16 * q + 16)
                    dve.wait_ge(gathered[u], 16 * K * q + 16 * K)
                    dve.wait_ge(stored[u], 16 * q + 16)
                    for k in range(K):
                        if k:
                            dve.wait_ge(acc_done, K * t + k)
                        src = x_sb[:, u, :] if k == 0 else acc[:, (k - 1) % 2, :]
                        dst = x_new[:, u, :] if k == K - 1 else acc[:, k % 2, :]
                        nc.vector.scalar_tensor_tensor(out=dst, in0=yk[:, u, k, :], scalar=r.weight[:, bass.ds(t, 1), k:k + 1].rearrange("p a k -> p (a k)"), in1=src,
                                                       op0=ALU.mult, op1=ALU.add).then_inc(acc_done, 1)
                        if lut and k < LUT_SIZE // AHEAD:
                            lut.step(dve, q, LUT_SIZE // AHEAD * u + k)
                    dve.wait_ge(acc_done, K * t + K)
                    dve.sem_inc(x_free, 1)
                    if sums:
                        sums.step(dve, q, u)

                dve.sem_inc(x_free, AHEAD)
                for u in range(AHEAD):
                    dve.sem_inc(stored[u], 16)
                if lut:
                    sums.begin(dve)
                    lut.begin(dve)
                with dve.Fori(0, ROUNDS) as q:
                    for u in range(AHEAD):
                        tile(q, u)


def build_small_mixture(nc, io, keep, x_in, x_out):
    with ExitStack() as ctx:
        gate = keep["gates"][:, 4:5]
        r = Routing(nc, Scope(nc, ctx, "moe0"), "moe0", 64, 6, 64 * CAP, P)
        r.ident = keep["ident"]
        x_mid = nc.dram_tensor("moe0_x_mid", [N, D], F32, kind="Internal").ap()
        build_route(nc, io, keep, x_in, x_mid, r, (("moe0_w1", "moe0_w3", "moe0_w2"), 128, False), gate, None)
        build_small_experts(nc, io, keep, r)
        build_combine(nc, io, keep, r, x_mid, x_out, LUT_FIRST["combine"])


INTER = 352
INTER_C = 3
WIDE_TILES = N * 2 // P + 8


def build_late_slots(nc, io, keep, r, late, tile_expert, weights):
    E, K, NT = r.experts, r.topk, N // P
    WC = weights.shape[1] // E
    with ExitStack() as ctx:
        sc = Scope(nc, ctx, r.name + "_slots")
        counts_ps = sc.ps("counts_ps", [P, 512])
        counts = sc.sb("counts", [P, E])
        steps = sc.sb("steps", [P, NT])
        over = sc.sb("over", [P, E, NT])
        tiles = sc.sb("tiles", [P, E])
        start = sc.sb("start", [P, E])
        start_slot = sc.sb("start_slot", [P, E])
        first = sc.sb("first", [P, NT, K])
        slotf = sc.sb("slotf", [P, 2, NT, K])
        te = sc.sb("te", [P, 2, WIDE_TILES])
        slot_now = sc.sb("slot_now", [P, TB, K], U32)
        token_now = sc.sb("token_now", [P, TB], I32)
        raw = sc.sb("raw", [P, 2, WC], BF16)
        raw_loaded = sc.sems("raw_loaded", 2)
        weights_done = sc.sem("weights_done")
        counted, dve_step, slots_ready, slots_free, scattered, pool_passed = (sc.sem(n) for n in ("counted", "dve_step", "slots_ready", "slots_free", "scattered", "pool_passed"))
        with nc.Block() as block:

            @block.sync
            def _(sp):
                with sp.Fori(0, E // 2) as i:
                    for u in range(2):
                        e = 2 * i + u
                        sp.wait_ge(weights_done, e + 1)
                        sp.dma_start(raw[:, u, :], io["moe2_w"][bass.ds(e, 1)].rearrange("e p c -> p (e c)")).then_inc(raw_loaded[u], 16)

            @block.scalar
            def _(act):
                act.sem_inc(weights_done, 2)
                with act.Fori(0, E // 2) as i:
                    for u in range(2):
                        e = 2 * i + u
                        act.wait_ge(raw_loaded[u], 16 * i + 16)
                        nc.scalar.activation(weights[:, bass.ds(e * WC, WC)], raw[:, u, :], ACT.Copy).then_inc(weights_done, 1)

            @block.tensor
            def _(pe):
                nc.tensor.matmul(counts_ps[:, 0:E], keep["ones_bf"][:, :], late["counts"][:, :], start=True, stop=True).then_inc(counted, 1)

            @block.vector
            def _(dve):
                n = [0]

                def then(ins):
                    n[0] += 1
                    ins.then_inc(dve_step, 1)
                    dve.wait_ge(dve_step, n[0])

                dve.sem_inc(slots_free, 1)
                then(nc.vector.tensor_scalar(steps[:, :], keep["iota"][:, 0:NT], float(P), None, ALU.mult))
                dve.wait_ge(counted, 1)
                then(nc.vector.tensor_copy(counts[:, :], counts_ps[:, 0:E]))
                then(nc.vector.tensor_tensor(over[:, :, :], counts[:, :].rearrange("p (e m) -> p e m", m=1).broadcast_to([P, E, NT]),
                                             steps[:, :].rearrange("p (e m) -> p e m", e=1).broadcast_to([P, E, NT]), ALU.is_gt))
                then(nc.vector.tensor_reduce(tiles[:, :], over[:, :, :], AX.X, ALU.add))
                then(nc.vector.memset(start[:, 0:1], 0.0))
                for e in range(1, E):
                    then(nc.vector.tensor_tensor(start[:, e:e + 1], start[:, e - 1:e], tiles[:, e - 1:e], ALU.add))
                then(nc.vector.tensor_scalar(start_slot[:, :], start[:, :], float(P), None, ALU.mult))
                for e in range(E):
                    src = late["pos"] if e == 0 else slotf[:, (e - 1) % 2]
                    then(nc.vector.tensor_scalar(first[:, :, :], late["idx"][:, :, :], float(e), start_slot[:, e:e + 1], ALU.is_equal, ALU.mult))
                    then(nc.vector.tensor_tensor(slotf[:, e % 2], src[:, :, :], first[:, :, :], ALU.add))
                then(nc.vector.tensor_copy(r.slot_of[:, :, :], slotf[:, (E - 1) % 2]))
                then(nc.vector.memset(te[:, 0, :], 0.0))
                for e in range(1, E):
                    then(nc.vector.scalar_tensor_tensor(out=te[:, e % 2, :], in0=keep["iota"][:, 0:WIDE_TILES], scalar=start[:, e:e + 1], in1=te[:, (e - 1) % 2, :],
                                                        op0=ALU.is_ge, op1=ALU.add))
                then(nc.vector.tensor_copy(tile_expert[:, :], te[:, (E - 1) % 2, :]))
                with dve.Fori(0, NB) as i:
                    dve.wait_ge(slots_free, i + 1)
                    nc.vector.tensor_copy(token_now[:, :], keep["row_id"][:, bass.ds(TB * i, TB)]).then_inc(slots_ready, 1)
                    nc.vector.tensor_copy(slot_now[:, :, :], r.slot_of[:, bass.ds(TB * i, TB), :]).then_inc(slots_ready, 1)

            @block.gpsimd
            def _(pool):
                with pool.Fori(0, NB) as i:
                    hold(pool, slots_ready, 2 * i + 2, pool_passed)
                    for t in range(TB):
                        for k in range(K):
                            nc.gpsimd.indirect_dma_start(out=r.token_of, out_offset=bass.IndirectOffsetOnAxis(ap=slot_now[:, t, k:k + 1], axis=0),
                                                         in_=token_now[:, t:t + 1], in_offset=None).then_inc(scattered, 16)
                    pool.wait_ge(scattered, 16 * TB * K * (i + 1))
                    pool.sem_inc(slots_free, 1)


def build_wide_experts(nc, io, keep, r, tile_expert, weights):
    E = r.experts
    UPC = DC * INTER
    WC = 2 * UPC + INTER_C * D
    PAIRS = WIDE_TILES // 2
    HM = [min(P, INTER - P * j) for j in range(INTER_C)]
    with ExitStack() as ctx:
        sc = Scope(nc, ctx, "wide")
        tokens = sc.sb("tokens", [P, WIDE_TILES], U32)
        load_tokens(nc, r, tokens)
        now = sc.sb("now", [P, 2, 2], U32)
        xg = sc.sb("xg", [P, 2, 2, D])
        xT = [sc.sb(f"xT{q}", [P, 2, DC, P], F32R) for q in range(2)]
        sil = sc.sb("sil", [P, 2, INTER])
        hid = sc.sb("hid", [P, 2, INTER])
        hT = [sc.sb(f"hT{q}", [P, 2, INTER_C, P], F32R) for q in range(2)]
        y_sb = sc.sb("y", [P, 2, D])
        turn = sc.ps("turn", [P, 2, 512])
        up1 = sc.ps("up1", [P, 2, 512])
        up3 = sc.ps("up3", [P, 2, 512])
        out = sc.ps("out", [P, 2, 512])
        gathered = sc.sems("gathered", 2)
        stored = sc.sems("stored", 2)
        names = "now_done turned hi_done lo_done up_done sil_done hid_done hturned hhi_done hlo_done y_done y_moved pool_passed".split()
        s = {n: sc.sem(n) for n in names}

        def pairs(eng, pair):
            with eng.Fori(0, PAIRS // 2 - 1) as k:
                pair(2 * k, 0, k, False)
                pair(2 * k + 1, 1, k, False)
            pair(PAIRS - 2, 0, PAIRS // 2 - 1, False)
            pair(PAIRS - 1, 1, PAIRS // 2 - 1, True)

        with nc.Block() as block:

            @block.gpsimd
            def _(pool):
                with pool.Fori(0, PAIRS // 2) as k:
                    for par in range(2):
                        i = 2 * k + par
                        hold(pool, s["turned"], 2 * i + 2, s["pool_passed"])
                        nc.gpsimd.tensor_copy(now[:, par, :], tokens[:, bass.ds(2 * i, 2)]).then_inc(s["now_done"], 1)
                        hold(pool, s["now_done"], i + 1, s["pool_passed"])
                        for u in range(2):
                            nc.gpsimd.indirect_dma_start(out=xg[:, par, u, :], out_offset=None, in_=r.xn, in_offset=bass.IndirectOffsetOnAxis(ap=now[:, par, u:u + 1], axis=0))\
                                .then_inc(gathered[par], 16)

            @block.tensor
            def _(pe):
                def turn_slots(par, u, k):
                    pe.wait_ge(gathered[par], 32 * k + 32)
                    for c in range(DC):
                        mm = nc.tensor.transpose(turn[:, u, c * P:(c + 1) * P], xg[:, par, u, c * P:(c + 1) * P], keep["ident"][:, :])
                    mm.then_inc(s["turned"], 1)

                def pair(i, par, k, last):
                    base = [nc.tensor.value_load(tile_expert[0:1, bass.ds(2 * i + u, 1)], min_val=0, max_val=E - 1) * WC for u in range(2)]
                    for u in range(2):
                        j = 2 * i + u
                        pe.wait_ge(s["lo_done"], j + 1)
                        for bank, at in ((up1, 0), (up3, UPC)):
                            n = 0
                            for c in range(DC):
                                for q in range(2):
                                    mm = nc.tensor.matmul(bank[:, u, 0:INTER], xT[q][:, u, c, :], weights[:, bass.ds(base[u] + (at + c * INTER), INTER)], start=n == 0, stop=n == 2 * DC - 1)
                                    n += 1
                        mm.then_inc(s["up_done"], 1)
                    for u in range(2):
                        j = 2 * i + u
                        if not last:
                            turn_slots(1 - par, u, k + par)
                        pe.wait_ge(s["hid_done"], j + 1)
                        pe.wait_ge(s["y_moved"], j + 1)
                        for c in range(INTER_C):
                            mm = nc.tensor.transpose(out[0:HM[c], u, c * P:(c + 1) * P], hid[:, u, c * P:c * P + HM[c]], keep["ident"][:, :])
                        mm.then_inc(s["hturned"], 1)
                    for u in range(2):
                        j = 2 * i + u
                        pe.wait_ge(s["hlo_done"], j + 1)
                        n = 0
                        for c in range(INTER_C):
                            for q in range(2):
                                mm = nc.tensor.matmul(out[:, u, :], hT[q][0:HM[c], u, c, :], weights[0:HM[c], bass.ds(base[u] + (2 * UPC + c * D), D)], start=n == 0, stop=n == 2 * INTER_C - 1)
                                n += 1
                        mm.then_inc(s["y_done"], 1)

                pe.sem_inc(s["turned"], 4)
                for u in range(2):
                    turn_slots(0, u, 0)
                pairs(pe, pair)

            @block.scalar
            def _(act):
                def high(j, u):
                    act.wait_ge(s["turned"], j + 1 + 4)
                    nc.scalar.activation(xT[0][:, u, :, :], turn[:, u, :].rearrange("p (c s) -> p c s", c=DC), ACT.Copy).then_inc(s["hi_done"], 1)

                def pair(i, par, k, last):
                    for u in range(2):
                        act.wait_ge(s["up_done"], 2 * i + u + 1)
                        nc.scalar.activation(sil[:, u, :], up1[:, u, 0:INTER], ACT.Silu).then_inc(s["sil_done"], 1)
                    for u in range(2):
                        if not last:
                            high(2 * i + 2 + u, u)
                        act.wait_ge(s["hturned"], 2 * i + u + 1)
                        nc.scalar.activation(hT[0][:, u, 0:2, :], out[:, u, 0:2 * P].rearrange("p (c s) -> p c s", c=2), ACT.Copy)
                        nc.scalar.activation(hT[0][0:HM[2], u, 2, :], out[0:HM[2], u, 2 * P:3 * P], ACT.Copy).then_inc(s["hhi_done"], 1)
                    for u in range(2):
                        j = 2 * i + u
                        act.wait_ge(stored[u], 16 * i + 16)
                        act.wait_ge(s["y_done"], j + 1)
                        nc.scalar.activation(y_sb[:, u, :], out[:, u, :], ACT.Copy).then_inc(s["y_moved"], 1)
                        act.wait_ge(s["y_moved"], j + 3)
                        act.dma_start(rows(r.y, j * P, P), y_sb[:, u, :]).then_inc(stored[u], 16)

                act.sem_inc(s["y_moved"], 2)
                for u in range(2):
                    high(u, u)
                pairs(act, pair)
                for u in range(2):
                    act.wait_ge(stored[u], 16 * PAIRS + 16)

            @block.vector
            def _(dve):
                def low(j, u):
                    dve.wait_ge(s["hi_done"], j + 1)
                    nc.vector.tensor_tensor(xT[1][:, u, :, :], turn[:, u, :].rearrange("p (c s) -> p c s", c=DC), xT[0][:, u, :, :].bitcast(F32), ALU.subtract).then_inc(s["lo_done"], 1)

                def pair(i, par, k, last):
                    for u in range(2):
                        dve.wait_ge(s["sil_done"], 2 * i + u + 1)
                        nc.vector.tensor_tensor(hid[:, u, :], sil[:, u, :], up3[:, u, 0:INTER], ALU.mult).then_inc(s["hid_done"], 1)
                    for u in range(2):
                        if not last:
                            low(2 * i + 2 + u, u)
                        dve.wait_ge(s["hhi_done"], 2 * i + u + 1)
                        nc.vector.tensor_tensor(hT[1][:, u, 0:2, :], out[:, u, 0:2 * P].rearrange("p (c s) -> p c s", c=2), hT[0][:, u, 0:2, :].bitcast(F32), ALU.subtract)
                        nc.vector.tensor_tensor(hT[1][0:HM[2], u, 2, :], out[0:HM[2], u, 2 * P:3 * P], hT[0][0:HM[2], u, 2, :].bitcast(F32), ALU.subtract).then_inc(s["hlo_done"], 1)

                for u in range(2):
                    dve.sem_inc(stored[u], 16)
                for u in range(2):
                    low(u, u)
                pairs(dve, pair)


def build_wide_mixture(nc, io, keep, x_in, x_out):
    with ExitStack() as ctx:
        gate = keep["gates"][:, 6:7]
        sc = Scope(nc, ctx, "moe2")
        r = Routing(nc, sc, "moe2", 8, 2, WIDE_TILES * P, 0)
        r.ident = keep["ident"]
        late = {"idx": sc.sb("late_idx", [P, N // P, 2]), "pos": sc.sb("late_pos", [P, N // P, 2]), "counts": sc.sb("late_counts", [P, 8], BF16)}
        tile_expert = sc.sb("tile_expert", [P, WIDE_TILES], I32)
        x_mid = nc.dram_tensor("moe2_x_mid", [N, D], F32, kind="Internal").ap()
        build_route(nc, io, keep, x_in, x_mid, r, (("moe2_w1", "moe2_w3", "moe2_w2"), INTER, True), gate, late)
        with ExitStack() as inner:
            WC = 2 * DC * INTER + INTER_C * D
            weights = Scope(nc, inner, "moe2_experts").sb("weights", [P, r.experts * WC], F32R)
            build_late_slots(nc, io, keep, r, late, tile_expert, weights)
            build_wide_experts(nc, io, keep, r, tile_expert, weights)
        build_combine(nc, io, keep, r, x_mid, x_out, None)


GN = 8
GROUPS = S // GN
KPAD = D + P


def build_gated_conv(nc, io, keep, x_in, x_out):
    T = S // P
    NS = 2
    with ExitStack() as outer:
        osc = Scope(nc, outer, "conv")
        vT = osc.sb("vT", [P, DC, B, S])
        cT = osc.sb("cT", [P, B, DC, S])
        cTr = osc.sb("cTr", [P, B, DC, S])
        oT = osc.sb("oT", [P, DC, B, S])
        cT_loaded = osc.sem("cT_loaded")
        cTr_loaded = osc.sem("cTr_loaded")

        with ExitStack() as ctx:
            sc = Scope(nc, ctx, "skip")
            RB = 4
            x_sb = sc.sb("x", [P, RB, T, D])
            c_sb = sc.sb("c", [P, 2, T, D])
            xn = sc.sb("xn", [P, 2, T, D])
            z = sc.sb("z", [P, 2, T, D])
            group8 = sc.sb("group8", [P, P])
            skip = sc.sb("skip", [P, T])
            skip_m = sc.sb("skip_m", [P, T, P])
            sk = sc.sb("sk", [P, T, D])
            x_mid = sc.sb("x_mid", [P, 2, T, D])
            stats = sc.sb("stats", [P, RB, T, 6])
            mv = sc.sb("mv", [P, RB, T, 2])
            ve = sc.sb("ve", [P, RB, T])
            rstd = sc.sb("rstd", [P, RB, T])
            turn = sc.ps("turn", [P, DC, 512])
            ssum = sc.ps("ssum", [P, T, D])
            const_loaded = sc.sem("const_loaded")
            x_loaded = sc.sems("x_loaded", RB)
            c_loaded = sc.sems("c_loaded", 2)
            stored = sc.sems("stored", 2)
            stats_done = sc.sem("stats_done")
            var_done = sc.sem("var_done")
            ve_done = sc.sem("ve_done")
            rstd_done = sc.sem("rstd_done")
            xn_done = sc.sem("xn_done")
            z_done = sc.sem("z_done")
            skip_done = sc.sem("skip_done")
            turned = sc.sem("turned")
            vT_done = sc.sem("vT_done")
            ssum_done = sc.sem("ssum_done")
            sk_done = sc.sem("sk_done")
            mid_done = sc.sem("mid_done")
            passed = sc.sem("passed")
            with nc.Block() as block:

                @block.sync
                def _(sp):
                    sp.dma_start(group8[:, :], io["group8"]).then_inc(const_loaded, 16)
                    sp.dma_start(skip[:, :], io["skip"]).then_inc(const_loaded, 16)
                    def load_x(b, u):
                        sp.dma_start(x_sb[:, u], rows(x_in, b * S, S).rearrange("(t p) d -> p t d", p=P)).then_inc(x_loaded[u], 16)

                    def load_c(b, u):
                        sp.dma_start(c_sb[:, u], rows(io["ctx"], b * S, S).rearrange("(t p) d -> p t d", p=P)).then_inc(c_loaded[u], 16)

                    for u in range(RB):
                        load_x(u, u)
                        if u < 2:
                            load_c(u, u)
                    for b in range(B - 2):
                        sp.wait_ge(mid_done, T * b + T)
                        load_c(b + 2, b % 2)
                        if b < B - RB:
                            load_x(b + RB, b % RB)
                        if b == B - RB:
                            sp.dma_start(cT[:, :, :, :], io["ctxT"].rearrange("b p c s -> p b c s")).then_inc(cT_loaded, 16)
                    sp.dma_start(cTr[:, :, :, :], io["ctxTr"].rearrange("b p c s -> p b c s")).then_inc(cTr_loaded, 16)

                @block.tensor
                def _(pe):
                    pe.wait_ge(skip_done, T)
                    with pe.Fori(0, B // 2) as i:
                        for u in range(2):
                            b = 2 * i + u
                            for c in range(DC):
                                pe.wait_ge(vT_done, DC * b + c + 1)
                                for t in range(T):
                                    if c == 0:
                                        pe.wait_ge(xn_done, T * b + t + 1)
                                    mm = nc.tensor.transpose(turn[:, c, t * P:(t + 1) * P], xn[:, u, t, c * P:(c + 1) * P], keep["ident"][:, :])
                                mm.then_inc(turned, 1)
                            for t in range(T):
                                pe.wait_ge(z_done, T * b + t + 1)
                                pe.wait_ge(sk_done, T * b + t + 1)
                                nc.tensor.matmul(ssum[:, t, :], skip_m[:, t, :], z[:, u, t, :], start=True, stop=True).then_inc(ssum_done, 1)

                @block.vector
                def _(dve):
                    for sem, n in ((sk_done, T), (turned, DC + 1), (ssum_done, 2 * T), (stored[0], 16), (stored[1], 16)):
                        dve.sem_inc(sem, n)

                    def statistics(r):
                        for u in range(RB):
                            dve.wait_ge(x_loaded[u], 16 * r + 16)
                            for t in range(T):
                                nc.vector.bn_stats(stats[:, u, t, :], x_sb[:, u, t, :]).then_inc(stats_done, 1)
                        hold(dve, stats_done, RB * T * (r + 1), passed)
                        for u in range(RB):
                            for t in range(T):
                                nc.vector.bn_aggr(mv[:, u, t, :], stats[:, u, t, :]).then_inc(var_done, 1)
                        dve.wait_ge(var_done, RB * T * (r + 1))
                        nc.vector.tensor_scalar(ve[:, :, :], mv[:, :, :, 1], LN_EPS, None, ALU.add).then_inc(ve_done, 1)
                        dve.wait_ge(rstd_done, r + 1)

                    def gate_rows(r, u):
                        b = RB * r + u
                        dve.wait_ge(turned, DC * b + 1)
                        for t in range(T):
                            nc.vector.tensor_scalar(xn[:, u % 2, t, :], x_sb[:, u, t, :], mv[:, u, t, 0:1], rstd[:, u, t:t + 1], ALU.subtract, ALU.mult).then_inc(xn_done, 1)
                        dve.wait_ge(c_loaded[u % 2], 16 * (RB // 2 * r + u // 2) + 16)
                        for t in range(T):
                            dve.wait_ge(xn_done, T * b + t + 1)
                            dve.wait_ge(ssum_done, T * b + t + 1)
                            nc.vector.tensor_tensor(z[:, u % 2, t, :], xn[:, u % 2, t, :], c_sb[:, u % 2, t, :], ALU.mult).then_inc(z_done, 1)

                    def skip_rows(r, u):
                        b = RB * r + u
                        dve.wait_ge(stored[u % 2], 16 * (RB // 2 * r + u // 2) + 16)
                        for t in range(T):
                            dve.wait_ge(ssum_done, T * b + t + 1 + 2 * T)
                            nc.vector.tensor_tensor(sk[:, t, :], ssum[:, t, :], c_sb[:, u % 2, t, :], ALU.mult).then_inc(sk_done, 1)
                            dve.wait_ge(sk_done, T * b + t + 1 + T)
                            nc.vector.scalar_tensor_tensor(out=x_mid[:, u % 2, t, :], in0=sk[:, t, :], scalar=keep["gates"][:, 3:4], in1=x_sb[:, u, t, :],
                                                           op0=ALU.mult, op1=ALU.add).then_inc(mid_done, 1)

                    dve.wait_ge(const_loaded, 32)
                    for t in range(T):
                        nc.vector.tensor_scalar(skip_m[:, t, :], group8[:, :], skip[:, t:t + 1], None, ALU.mult).then_inc(skip_done, 1)
                    with dve.Fori(0, B // RB) as r:
                        statistics(r)
                        for u in range(RB):
                            gate_rows(r, u)
                            if u:
                                skip_rows(r, u - 1)
                        skip_rows(r, RB - 1)

                @block.gpsimd
                def _(pool):
                    with pool.Fori(0, B // RB) as r:
                        pool.wait_ge(ve_done, r + 1)
                        nc.gpsimd.tensor_tensor(rstd[:, :, :], ve[:, :, :], keep["neg_half"][:, 0:RB * T].rearrange("p (u t) -> p u t", u=RB), ALU.pow).then_inc(rstd_done, 1)

                @block.scalar
                def _(act):
                    act.sem_inc(vT_done, DC)
                    with act.Fori(0, B // 2) as i:
                        for u in range(2):
                            b = 2 * i + u
                            for c in range(DC):
                                act.wait_ge(turned, DC * b + c + 2 + DC)
                                nc.scalar.activation(vT[:, c, bass.ds(b, 1), :].rearrange("p a s -> p (a s)"), turn[:, c, 0:S], ACT.Copy).then_inc(vT_done, 1)
                            act.wait_ge(mid_done, T * b + T)
                            act.dma_start(rows(x_out, b * S, S).rearrange("(t p) d -> p t d", p=P), x_mid[:, u]).then_inc(stored[u], 16)
                    for u in range(2):
                        act.wait_ge(stored[u], 16 * (B // 2) + 16)

        with ExitStack() as ctx:
            sc = Scope(nc, ctx, "toep")
            toep = sc.sb("toep", [P, NS, D])
            kv = sc.sb("kv", [P, NS, DC, 512])
            gated = sc.sb("gated", [P, 2, 512])
            y = sc.ps("y", [P, NS, DC, 512])
            loaded = sc.sems("loaded", NS)
            kv_done = sc.sem("kv_done")
            y_done = sc.sem("y_done")
            gated_done = sc.sem("gated_done")
            o_done = sc.sem("o_done")
            fourths = [P, B, GN, GN]

            with nc.Block() as block:

                @block.sync
                def _(sp):
                    with sp.Fori(0, GROUPS // NS) as i:
                        for u in range(NS):
                            h = NS * i + u
                            sp.wait_ge(y_done, DC * h + DC)
                            windows = bass.AP(io["filt"].tensor, h * KPAD, [[1, P], [1, D]])
                            sp.dma_start(toep[:, u, :], windows).then_inc(loaded[u], 16)

                @block.tensor
                def _(pe):
                    pe.sem_inc(y_done, NS * DC)
                    with pe.Fori(0, GROUPS // NS) as i:
                        for u in range(NS):
                            h = NS * i + u
                            pe.wait_ge(loaded[u], 16 * i + 16)
                            for lc in range(DC):
                                pe.wait_ge(kv_done, DC * h + lc + 1)
                                pe.wait_ge(gated_done, DC * h + lc + 1)
                                for mc in range(lc + 1):
                                    at = 384 - P * (lc - mc)
                                    mm = nc.tensor.matmul(y[:, u, lc, :], toep[:, u, at:at + P], kv[:, u, mc, :], start=mc == 0, stop=mc == lc)
                                mm.then_inc(y_done, 1)

                @block.vector
                def _(dve):
                    def pairs(h, u, c):
                        dve.wait_ge(y_done, DC * h + DC)
                        nc.vector.tensor_tensor(kv[:, u, c, :].rearrange("p (b i j) -> p b i j", b=B, i=GN),
                                                vT[:, c, :, bass.ds(GN * h, GN)].rearrange("p b (i j) -> p b i j", j=1).broadcast_to(fourths),
                                                cT[:, :, c, bass.ds(GN * h, GN)].rearrange("p b (i j) -> p b i j", i=1).broadcast_to(fourths),
                                                ALU.mult).then_inc(kv_done, 1)

                    def combine(h, u, lc):
                        n = DC * h + lc
                        dve.wait_ge(y_done, n + 1 + NS * DC)
                        dve.wait_ge(o_done, n + 1)
                        nc.vector.tensor_tensor(gated[:, lc % 2, :].rearrange("p (b i j) -> p b i j", b=B, i=GN), y[:, u, lc, :].rearrange("p (b i j) -> p b i j", b=B, i=GN),
                                                cTr[:, :, lc, bass.ds(GN * h, GN)].rearrange("p b (i j) -> p b i j", j=1).broadcast_to(fourths),
                                                ALU.mult).then_inc(gated_done, 1)
                        dve.wait_ge(gated_done, n + 1 + NS * DC)
                        nc.vector.tensor_reduce(oT[:, lc, :, bass.ds(GN * h, GN)], gated[:, lc % 2, :].rearrange("p (b i j) -> p b j i", b=B, i=GN), AX.X, ALU.add)\
                            .then_inc(o_done, 1)

                    dve.sem_inc(gated_done, NS * DC)
                    dve.sem_inc(o_done, 2)
                    dve.wait_ge(cT_loaded, 16)
                    for c in range(DC):
                        pairs(0, 0, c)
                    dve.wait_ge(cTr_loaded, 16)
                    with dve.Fori(0, GROUPS // NS - 1) as i:
                        for u in range(NS):
                            for c in range(DC):
                                pairs(NS * i + u + 1, 1 - u, c)
                                combine(NS * i + u, u, c)
                    for c in range(DC):
                        pairs(GROUPS - 1, 1, c)
                        combine(GROUPS - 2, 0, c)
                    for c in range(DC):
                        combine(GROUPS - 1, 1, c)

        with ExitStack() as ctx:
            sc = Scope(nc, ctx, "back")
            o_b = sc.sb("o_b", [P, 2, DC, S])
            x_mid = sc.sb("x_mid", [P, 2, T, D])
            x_new = sc.sb("x_new", [P, 2, T, D])
            rows_ps = sc.ps("rows", [P, 2, T, D])
            loaded = sc.sems("loaded", 2)
            stored = sc.sems("stored", 2)
            o_copied = sc.sem("o_copied")
            rows_done = sc.sem("rows_done")
            out_done = sc.sem("out_done")
            with nc.Block() as block:

                @block.sync
                def _(sp):
                    def of(b):
                        return rows(x_out, b * S, S).rearrange("(t p) d -> p t d", p=P)

                    def store(b, u):
                        sp.wait_ge(out_done, T * b + 3 * T)
                        sp.dma_start(of(b), x_new[:, u]).then_inc(stored[u], 16)

                    for u in range(2):
                        sp.dma_start(x_mid[:, u], of(u)).then_inc(loaded[u], 16)
                    with sp.Fori(0, B // 2 - 1) as i:
                        for u in range(2):
                            b = 2 * i + u
                            store(b, u)
                            sp.dma_start(x_mid[:, u], of(b + 2)).then_inc(loaded[u], 16)
                    for u in range(2):
                        store(B - 2 + u, u)
                    for u in range(2):
                        sp.wait_ge(stored[u], 16 * (B // 2) + 16)

                @block.tensor
                def _(pe):
                    with pe.Fori(0, B // 2) as i:
                        for u in range(2):
                            b = 2 * i + u
                            pe.wait_ge(o_copied, b + 1)
                            pe.wait_ge(out_done, T * b + T)
                            for t in range(T):
                                for c in range(DC):
                                    mm = nc.tensor.matmul(rows_ps[:, u, t, c * P:(c + 1) * P], o_b[:, u, c, t * P:(t + 1) * P], keep["anti"][:, :], start=True, stop=True)
                                mm.then_inc(rows_done, 1)

                @block.vector
                def _(dve):
                    for sem, n in ((out_done, 2 * T), (rows_done, 2 * T), (stored[0], 16), (stored[1], 16)):
                        dve.sem_inc(sem, n)
                    with dve.Fori(0, B // 2) as i:
                        for u in range(2):
                            b = 2 * i + u
                            dve.wait_ge(loaded[u], 16 * i + 16)
                            dve.wait_ge(stored[u], 16 * i + 16)
                            for t in range(T):
                                dve.wait_ge(rows_done, T * b + t + 1 + 2 * T)
                                nc.vector.scalar_tensor_tensor(out=x_new[:, u, t, :], in0=rows_ps[:, u, t, :], scalar=keep["gates"][:, 3:4], in1=x_mid[:, u, t, :],
                                                               op0=ALU.mult, op1=ALU.add).then_inc(out_done, 1)

                @block.scalar
                def _(act):
                    with act.Fori(0, B // 2) as i:
                        for u in range(2):
                            b = 2 * i + u
                            act.wait_ge(rows_done, T * b + T)
                            nc.scalar.activation(o_b[:, u, :, :], oT[:, :, bass.ds(b, 1), :].rearrange("p c a s -> p c (a s)"), ACT.Copy).then_inc(o_copied, 1)


STAGES = [build_channel_attention, build_small_mixture, build_linear_attention, build_ternary_ffn, build_feature_attention, build_wide_mixture, build_gated_conv, build_lut_ffn]

INPUTS = {"x": "x", "ctx": "ctx_2048", "g_xattn": "g_xattn", "g_ffn": "g_ffn", "gamma": "L0_xattn_gamma"}


def build(nc, io, out):
    with ExitStack() as ctx:
        keep = {name: ctx.enter_context(nc.sbuf_tensor(f"keep_{name}", shape, dt)) for name, shape, dt in [
            ("ident", [P, P], F32), ("anti", [P, P], F32), ("ident_bf", [P, P], BF16), ("gates", [P, 8], F32), ("gate0", [P, 1], F32),
            ("neg_half", [P, 16], F32), ("half", [P, 32], F32), ("ones", [P, P], F32), ("ones_bf", [P, P], BF16),
            ("earlier_f", [P, P], F32), ("earlier", [P, P], BF16), ("iota", [P, 64], F32), ("spare", [P, 1], F32), ("row_id", [P, N // P], I32), ("zeros_i", [P, 136], I32)]}
        state = nc.dram_tensor("x_state", [N, D], F32, kind="Internal").ap()
        io = io | {"lin_kv": nc.dram_tensor("lin_kv", [NIT, P, EB * PAIRS * 2 * VE], F32, kind="Internal").ap(),
                   "lut_weights": nc.dram_tensor("lut_weights", [P, 3 * WCOLS], F32, kind="Internal").ap()}
        build_setup(nc, io, keep)
        for n, stage in enumerate(STAGES):
            stage(nc, io, keep, io["x"] if n == 0 else state, out if n == len(STAGES) - 1 else state)


def kernel(**inputs):
    import concourse.bacc as _bacc
    from concourse.bass_utils import run_bass_kernel_spmd as _run

    a = {k: np.asarray(v) for k, v in inputs.items()}
    ctx = a["ctx_2048"]
    arrays = {
        "x": a["x"].reshape(N, D), "ctx": ctx.reshape(N, D),
        "ctxT": ctx.transpose(0, 2, 1).reshape(B, DC, P, S).transpose(0, 2, 1, 3),
        "g_xattn": a["g_xattn"], "g_ffn": a["g_ffn"], "gamma": a["L0_xattn_gamma"].reshape(1, 1),
    }

    def contraction_first(w, pad):
        w = np.concatenate([w, np.zeros((pad - w.shape[0], D), w.dtype)])
        return w.T.reshape(DC, P, pad).transpose(1, 0, 2).reshape(P, DC * pad)

    def units_first(w, pad):
        w = np.concatenate([w.T, np.zeros((pad - w.shape[1], D), w.dtype)])
        return w.reshape(pad // P, P, D).transpose(1, 0, 2).reshape(P, pad // P * D)

    def square(w):
        return w.T.reshape(DC, P, D).transpose(1, 0, 2).reshape(P, DC * D)

    filt = a["L3_xattn_k"][:, ::-1]
    arrays |= {
        "filt": np.concatenate([filt, np.zeros((filt.shape[0], P), filt.dtype)], axis=1).reshape(-1),
        "ctxTr": arrays["ctxT"][:, ::-1],
        "skip": a["fside_S2_0"].reshape(S // P, P).T,
        "group8": np.kron(np.eye(P // GN, dtype=np.float32), np.ones((GN, GN), np.float32)),
    }
    def chunks(w):
        return w.reshape(-1, P, w.shape[1]).transpose(1, 0, 2).reshape(P, -1)

    up = a["L0_ffn_w_shared_up"]
    arrays |= {
        "moe0_w1": chunks(up[:, 128:]), "moe0_w3": chunks(up[:, :128]), "moe0_w2": chunks(a["L0_ffn_w_shared_down"]), "moe0_wg": chunks(a["L0_ffn_w_gate"]),
        "w_up": a["L0_ffn_w_up"].reshape(64, DC, P, 128).transpose(0, 2, 1, 3).reshape(64, P, DC * 128), "w_down": a["L0_ffn_w_down"],
    }
    def padded_rows(w):
        return np.concatenate([w, np.zeros((-w.shape[0] % P, w.shape[1]), w.dtype)])

    arrays |= {
        "moe2_w1": chunks(a["L2_ffn_sw1"].T), "moe2_w3": chunks(a["L2_ffn_sw3"].T), "moe2_w2": chunks(padded_rows(a["L2_ffn_sw2"].T)),
        "moe2_wg": chunks(a["L2_ffn_gate_w"].T), "moe2_bias": a["L2_ffn_gate_b"].reshape(1, -1),
        "moe2_w": np.stack([np.concatenate([chunks(a["L2_ffn_w1"][e].T), chunks(a["L2_ffn_w3"][e].T), chunks(padded_rows(a["L2_ffn_w2"][e].T))], axis=1)
                            for e in range(8)]),
    }
    arrays |= {n.lower(): square(a[f"L1_xattn_{n}"]) for n in ("Wq", "Wk", "Wv", "Wo")}
    arrays |= {n: a[f"L1_xattn_{n}"].reshape(DC, P).T for n in ("bq", "bk")}
    arrays |= {n: a[f"L1_xattn_{n}"].reshape(1, D) for n in ("bv", "bo")}
    arrays |= {"wqf": a["L1_xattn_Wqf"].T, "wkf": a["L1_xattn_Wkf"].T, "mask": a["mask_BxS2_ff1"].reshape(N // P, P).T}
    arrays |= {
        "w1t": contraction_first(a["L1_ffn_w1"], HPAD), "w3t": contraction_first(a["L1_ffn_w3"], HPAD), "w2t": units_first(a["L1_ffn_w2"], HPAD),
        "lut": a["L3_ffn_lut"],
        "lut_idx": np.concatenate([contraction_first(a["L3_ffn_gate_idx"], HPAD), contraction_first(a["L3_ffn_up_idx"], HPAD),
                                   units_first(a["L3_ffn_down_idx"], HPAD)], axis=1),
    }
    arrays = {f"in_{k}": np.ascontiguousarray(v) for k, v in arrays.items()}
    nc = _bacc.Bacc("TRN2", target_bir_lowering=False, num_devices=1)
    io = {k[3:]: nc.dram_tensor(k, v.shape, mybir.dt.from_np(v.dtype), kind="ExternalInput").ap() for k, v in arrays.items()}
    out = nc.dram_tensor("x_out", [N, D], F32, kind="ExternalOutput").ap()
    build(nc, io, out)
    r = _run(nc, [arrays], core_ids=[0])
    return r.results[0]["x_out"].reshape(B, S, D)
```
